# Optimizing a Trainium2 kernel written in Bass

```python
import numpy as np
import jax
import jax.numpy as jnp

def _softmax(x, axis=-1):
    return jax.nn.softmax(x, axis=axis)

def _gelu(x):
    return jax.nn.gelu(x, approximate=True)

def _silu(x):
    return jax.nn.silu(x)

def _sigmoid(x):
    return jax.nn.sigmoid(x)

def _layernorm(x, axis=-1, eps=1e-05):
    m = jnp.mean(x, axis=axis, keepdims=True)
    v = jnp.var(x, axis=axis, keepdims=True)
    return (x - m) / jnp.sqrt(v + eps)

def _scatter_add(tgt, idx, src, axis=0):
    return tgt.at[idx].add(src)

def _segment_sum(src, seg, n):
    return jax.ops.segment_sum(src, seg, n)
kernel_name = 'mk_perceiver_d4_seqx_r4_9edc8f'

def setup_inputs(seed: int=0):
    np.random.seed(seed)
    _w = jnp.asarray

    def _rec_inputs():
        import jax
        import jax.numpy as jnp
        _rk = jax.random.key(seed)
        x = -0.0003929 + 0.9999 * jax.random.normal(jax.random.fold_in(_rk, 1), (64, 32, 256), jnp.float32)
        _lenS = 32 - jax.random.randint(jax.random.fold_in(_rk, 7), (64,), 0, max(1, 32 // 4) + 1, jnp.int32)
        _lenS2 = 257 - jax.random.randint(jax.random.fold_in(_rk, 8), (64,), 0, max(1, 257 // 4) + 1, jnp.int32)
        _ctx_1024P = jax.random.normal(jax.random.fold_in(_rk, 11), (64, 16, 256), jnp.float32)
        _ctx_1024c = jax.random.dirichlet(jax.random.fold_in(_rk, 511), 0.3 * jnp.ones((16,), jnp.float32), (64, 257))
        _ctx_1024t = jnp.einsum('bsk,bkd->bsd', _ctx_1024c, _ctx_1024P)
        _ctx_1024t = _ctx_1024t * jax.lax.rsqrt(jnp.mean(jnp.square(_ctx_1024t)) + 1e-12) * 0.953939
        ctx_1024 = 4.13588e-05 + 0.999923 * (_ctx_1024t + 0.3 * jax.random.normal(jax.random.fold_in(_rk, 611), (64, 257, 256), jnp.float32))
        fside_1x1xSxS2_0 = 0.000376506 + 0.999991 * jax.random.normal(jax.random.fold_in(_rk, 14), (1, 1, 32, 257), jnp.float32)
        _validS = jnp.arange(32)[None, :] < _lenS[:, None]
        _validS2 = jnp.arange(257)[None, :] < _lenS2[:, None]
        _causal = jnp.tril(jnp.ones((32, 32), dtype=bool))
        mask_BxS2_ik0 = jnp.where(jnp.broadcast_to(_validS2[:, :], (64, 257)), 0, 1).astype(jnp.int32)
        mask_Bx1x1xS2_bf1 = jnp.ones((64, 1, 1, 257), dtype=bool)
        return (x, ctx_1024, fside_1x1xSxS2_0, mask_BxS2_ik0, mask_Bx1x1xS2_bf1)
    x, ctx_1024, fside_1x1xSxS2_0, mask_BxS2_ik0, mask_Bx1x1xS2_bf1 = _rec_inputs()

    def _L0_xattn_setup():
        import jax, jax.numpy as jnp
        import numpy as np
        H = 256
        B = 8
        L_CHAR = 512
        L_SUB = 256

        def _linear(x, W, b):
            return jnp.einsum('blh,oh->blo', x, W) + b

        def _interp_linear(x, out_len):
            L_in = x.shape[1]
            pos = (jnp.arange(out_len, dtype=x.dtype) + 0.5) * (L_in / out_len) - 0.5
            pos = jnp.clip(pos, 0.0, L_in - 1)
            lo = jnp.floor(pos).astype(jnp.int32)
            hi = jnp.minimum(lo + 1, L_in - 1)
            w = (pos - lo.astype(x.dtype))[None, :, None]
            return x[:, lo] * (1 - w) + x[:, hi] * w
        key = jax.random.key(seed)
        ks = jax.random.split(key, 18)
        s = 0.02
        inp = {'char_emb': jax.random.normal(ks[0], (B, L_CHAR, H), jnp.float32), 'subword_emb': jax.random.normal(ks[1], (B, L_SUB, H), jnp.float32)}
        names = ['Wq_c', 'Wk_s', 'Wv_s', 'Wq_s', 'Wk_c', 'Wv_c']
        for i, n in enumerate(names):
            inp[n] = jax.random.normal(ks[2 + 2 * i], (H, H), jnp.float32) * s
            inp['b' + n[1:]] = jax.random.normal(ks[3 + 2 * i], (H,), jnp.float32) * s
        inp['Wg'] = jax.random.normal(ks[14], (H, 2 * H), jnp.float32) * s
        inp['bg'] = jax.random.normal(ks[15], (H,), jnp.float32) * s
        return inp
    _L0_xattn_all = _L0_xattn_setup()
    _L0_xattn_in = {k: v for k, v in _L0_xattn_all.items() if k in ('Wq_c', 'bq_c', 'Wk_s', 'bk_s', 'Wv_s', 'bv_s', 'Wq_s', 'bq_s', 'Wk_c', 'bk_c', 'Wv_c', 'bv_c', 'Wg', 'bg')}
    del _L0_xattn_all

    def _L0_attn_setup():
        import jax, jax.numpy as jnp
        import numpy as np
        IMG_SIZE = 224
        PATCH_SIZE = 16
        CONTEXT_LEN = 79
        LATENT_DIM = 256
        NUM_HEADS = 16
        NUM_PATCHES = (IMG_SIZE // PATCH_SIZE) ** 2
        SEQ_LEN = NUM_PATCHES + CONTEXT_LEN
        BATCH = 8

        def prefix_lm_mask(num_img_patches, total):
            m = np.tril(np.ones((total, total), dtype=np.float32))
            m[:num_img_patches, :num_img_patches] = 1.0
            return jnp.asarray(m)
        key = jax.random.key(seed)
        k_x, k_q, k_k, k_v, k_o, k_b = jax.random.split(key, 6)
        d = LATENT_DIM
        scale = 1.0 / np.sqrt(d)
        return {'x': jax.random.normal(k_x, (BATCH, SEQ_LEN, d), dtype=jnp.float32), 'w_q': jax.random.normal(k_q, (d, d), dtype=jnp.float32) * scale, 'w_k': jax.random.normal(k_k, (d, d), dtype=jnp.float32) * scale, 'w_v': jax.random.normal(k_v, (d, d), dtype=jnp.float32) * scale, 'w_o': jax.random.normal(k_o, (d, d), dtype=jnp.float32) * scale, 'b_o': jax.random.normal(k_b, (d,), dtype=jnp.float32) * 0.01}
    _L0_attn_all = _L0_attn_setup()
    _L0_attn_in = {k: v for k, v in _L0_attn_all.items() if k in ('w_q', 'w_k', 'w_v', 'w_o', 'b_o')}
    del _L0_attn_all

    def _L0_ffn_setup():
        import jax, jax.numpy as jnp
        import numpy as np
        MICRO_BATCHES = 2
        TOP_K = 2
        NUM_EXPERTS = 8
        B, S, D = (4, 1024, 256)
        H = 4 * D
        key = jax.random.key(seed)
        ks = jax.random.split(key, 8)
        s = 0.02
        return {'x': jax.random.normal(ks[0], (B, S, D), jnp.float32), 'ln_scale': jnp.ones((D,), jnp.float32), 'ln_bias': jnp.zeros((D,), jnp.float32), 'attn_w': jax.random.normal(ks[1], (D, D), jnp.float32) * s, 'attn_b': jnp.zeros((D,), jnp.float32), 'gate_w': jax.random.normal(ks[2], (NUM_EXPERTS, D), jnp.float32) * s, 'w1': jax.random.normal(ks[3], (NUM_EXPERTS, D, H), jnp.float32) * s, 'b1': jnp.zeros((NUM_EXPERTS, H), jnp.float32), 'w2': jax.random.normal(ks[4], (NUM_EXPERTS, H, D), jnp.float32) * s, 'b2': jnp.zeros((NUM_EXPERTS, D), jnp.float32), 'next_w': jax.random.normal(ks[5], (D, D), jnp.float32) * s, 'next_b': jnp.zeros((D,), jnp.float32)}
    _L0_ffn_all = _L0_ffn_setup()
    _L0_ffn_in = {k: v for k, v in _L0_ffn_all.items() if k in ('ln_scale', 'ln_bias', 'attn_w', 'attn_b', 'gate_w', 'w1', 'b1', 'w2', 'b2', 'next_w', 'next_b')}
    del _L0_ffn_all

    def _L1_xattn_setup():
        import jax, jax.numpy as jnp
        import numpy as np
        DIM = 256
        NUM_HEADS = 16
        HEAD_DIM = DIM // NUM_HEADS
        SCALE = HEAD_DIM ** (-0.5)
        key = jax.random.key(seed)
        ks = jax.random.split(key, 12)
        B, N, M, C = (4, 128, 512, DIM)
        x = jax.random.normal(ks[0], (B, N, C), dtype=jnp.float32)
        context = jax.random.normal(ks[1], (B, M, C), dtype=jnp.float32)
        mask = jax.random.randint(ks[2], (B, M), 0, 2, dtype=jnp.int32)
        mask = mask.at[:, 0].set(1)
        w = 0.02
        Wq = jax.random.normal(ks[3], (C, C), dtype=jnp.float32) * w
        bq = jnp.zeros((C,), dtype=jnp.float32)
        Wk = jax.random.normal(ks[4], (C, C), dtype=jnp.float32) * w
        bk = jnp.zeros((C,), dtype=jnp.float32)
        Wv = jax.random.normal(ks[5], (C, C), dtype=jnp.float32) * w
        bv = jnp.zeros((C,), dtype=jnp.float32)
        Wo = jax.random.normal(ks[6], (C, C), dtype=jnp.float32) * w
        bo = jnp.zeros((C,), dtype=jnp.float32)
        return {'x': x, 'context': context, 'ctx_key_padding_mask': mask, 'Wq': Wq, 'bq': bq, 'Wk': Wk, 'bk': bk, 'Wv': Wv, 'bv': bv, 'Wo': Wo, 'bo': bo}
    _L1_xattn_all = _L1_xattn_setup()
    _L1_xattn_in = {k: v for k, v in _L1_xattn_all.items() if k in ('Wq', 'bq', 'Wk', 'bk', 'Wv', 'bv', 'Wo', 'bo')}
    del _L1_xattn_all

    def _L1_attn_setup():
        import math
        import jax, jax.numpy as jnp
        import numpy as np
        B, S, D = (4, 512, 256)

        def _complex_proj(x, W, b):
            p = jnp.einsum('bsd,ed->bse', x, W) + b
            p = p.reshape(*x.shape[:-1], x.shape[-1], 2)
            return (p[..., 0], p[..., 1])
        key = jax.random.key(seed)
        ks = jax.random.split(key, 9)
        sd = 1.0 / math.sqrt(D)
        return {'hidden_states': jax.random.normal(ks[0], (B, S, D), jnp.float32), 'Wq': jax.random.normal(ks[1], (2 * D, D), jnp.float32) * sd, 'bq': jax.random.normal(ks[2], (2 * D,), jnp.float32) * 0.01, 'Wk': jax.random.normal(ks[3], (2 * D, D), jnp.float32) * sd, 'bk': jax.random.normal(ks[4], (2 * D,), jnp.float32) * 0.01, 'Wv': jax.random.normal(ks[5], (2 * D, D), jnp.float32) * sd, 'bv': jax.random.normal(ks[6], (2 * D,), jnp.float32) * 0.01, 'Wo': jax.random.normal(ks[7], (D, 2 * D), jnp.float32) * sd, 'bo': jax.random.normal(ks[8], (D,), jnp.float32) * 0.01}
    _L1_attn_all = _L1_attn_setup()
    _L1_attn_in = {k: v for k, v in _L1_attn_all.items() if k in ('Wq', 'bq', 'Wk', 'bk', 'Wv', 'bv', 'Wo', 'bo')}
    del _L1_attn_all

    def _L1_ffn_setup():
        import jax, jax.numpy as jnp
        import numpy as np
        TOPK = 8
        BN_EPS = 1e-05
        key = jax.random.key(seed)
        ks = jax.random.split(key, 5)
        b, n, d = (2, 256, 256)
        h, nk, kd = (8, 64, 128)
        ne = nk * nk
        scale = 0.02
        return {'inputs': jax.random.normal(ks[0], (b, n, d), jnp.float32), 'gamma': jnp.ones((d,), jnp.float32), 'beta': jnp.zeros((d,), jnp.float32), 'w_q': jax.random.normal(ks[1], (2 * h * kd, d), jnp.float32) * scale, 'keys': jax.random.normal(ks[2], (h, nk, 2, kd), jnp.float32) * scale, 'key_in': jax.random.normal(ks[3], (ne, d), jnp.float32) * scale, 'key_out': jax.random.normal(ks[4], (ne, d), jnp.float32) * scale}
    _L1_ffn_all = _L1_ffn_setup()
    _L1_ffn_in = {k: v for k, v in _L1_ffn_all.items() if k in ('gamma', 'beta', 'w_q', 'keys', 'key_in', 'key_out')}
    del _L1_ffn_all

    def _L2_xattn_setup():
        import jax, jax.numpy as jnp
        import numpy as np
        import math
        D_MODEL = 256
        N_HEADS = 16
        HEAD_DIM = D_MODEL // N_HEADS
        B, S = (4, 512)

        def _split_heads(x):
            b, s, _ = x.shape
            return x.reshape(b, s, N_HEADS, HEAD_DIM).transpose(0, 2, 1, 3)
        key = jax.random.key(seed)
        ks = jax.random.split(key, 12)
        scale = 1.0 / math.sqrt(D_MODEL)
        inp = {'query': jax.random.normal(ks[0], (B, S, D_MODEL), jnp.float32), 'key': jax.random.normal(ks[1], (B, S, D_MODEL), jnp.float32), 'value': jax.random.normal(ks[2], (B, S, D_MODEL), jnp.float32), 'mask': jnp.ones((B, 1, 1, S), dtype=bool), 'Wq': jax.random.normal(ks[3], (D_MODEL, D_MODEL), jnp.float32) * scale, 'bq': jnp.zeros((D_MODEL,), jnp.float32), 'Wk': jax.random.normal(ks[4], (D_MODEL, D_MODEL), jnp.float32) * scale, 'bk': jnp.zeros((D_MODEL,), jnp.float32), 'Wv': jax.random.normal(ks[5], (D_MODEL, D_MODEL), jnp.float32) * scale, 'bv': jnp.zeros((D_MODEL,), jnp.float32), 'Wo': jax.random.normal(ks[6], (D_MODEL, D_MODEL), jnp.float32) * scale, 'bo': jnp.zeros((D_MODEL,), jnp.float32)}
        return inp
    _L2_xattn_all = _L2_xattn_setup()
    _L2_xattn_in = {k: v for k, v in _L2_xattn_all.items() if k in ('Wq', 'bq', 'Wk', 'bk', 'Wv', 'bv', 'Wo', 'bo')}
    del _L2_xattn_all

    def _L2_attn_setup():
        import jax, jax.numpy as jnp
        import numpy as np
        D_MODEL = 256
        N_HEADS = 16
        HEAD_DIM = D_MODEL // N_HEADS

        def _rope_tables(L, dtype):
            inv_freq = 1.0 / 10000.0 ** (jnp.arange(0, HEAD_DIM, 2, dtype=dtype) / HEAD_DIM)
            t = jnp.arange(L, dtype=dtype)
            freqs = t[:, None] * inv_freq[None, :]
            emb = jnp.concatenate([freqs, freqs], axis=-1)
            return (jnp.cos(emb), jnp.sin(emb))

        def _rotate_half(x):
            x1, x2 = (x[..., :HEAD_DIM // 2], x[..., HEAD_DIM // 2:])
            return jnp.concatenate([-x2, x1], axis=-1)
        key = jax.random.key(seed)
        ks = jax.random.split(key, 9)
        B, L = (2, 512)
        s = 1.0 / np.sqrt(D_MODEL)
        return {'x': jax.random.normal(ks[0], (B, L, D_MODEL), dtype=jnp.float32), 'q_w': jax.random.normal(ks[1], (D_MODEL, D_MODEL), dtype=jnp.float32) * s, 'q_b': jnp.zeros((D_MODEL,), dtype=jnp.float32), 'k_w': jax.random.normal(ks[2], (D_MODEL, D_MODEL), dtype=jnp.float32) * s, 'k_b': jnp.zeros((D_MODEL,), dtype=jnp.float32), 'v_w': jax.random.normal(ks[3], (D_MODEL, D_MODEL), dtype=jnp.float32) * s, 'v_b': jnp.zeros((D_MODEL,), dtype=jnp.float32), 'o_w': jax.random.normal(ks[4], (D_MODEL, D_MODEL), dtype=jnp.float32) * s, 'o_b': jnp.zeros((D_MODEL,), dtype=jnp.float32)}
    _L2_attn_all = _L2_attn_setup()
    _L2_attn_in = {k: v for k, v in _L2_attn_all.items() if k in ('q_w', 'q_b', 'k_w', 'k_b', 'v_w', 'v_b', 'o_w', 'o_b')}
    del _L2_attn_all

    def _L2_ffn_setup():
        import jax, jax.numpy as jnp
        import numpy as np
        D, H, E, K, S = (256, 512, 8, 2, 1)
        B, L = (4, 512)
        key = jax.random.key(seed)
        ks = jax.random.split(key, 9)
        std = 0.02
        return {'x': jax.random.normal(ks[0], (B, L, D), dtype=jnp.float32), 'router_w': jax.random.normal(ks[1], (E, D), dtype=jnp.float32) * std, 'experts_bias': jnp.zeros((E,), dtype=jnp.float32), 'w1': jax.random.normal(ks[2], (E, D, H), dtype=jnp.float32) * std, 'w3': jax.random.normal(ks[3], (E, D, H), dtype=jnp.float32) * std, 'w2': jax.random.normal(ks[4], (E, H, D), dtype=jnp.float32) * std, 'sw1': jax.random.normal(ks[5], (S, D, H), dtype=jnp.float32) * std, 'sw3': jax.random.normal(ks[6], (S, D, H), dtype=jnp.float32) * std, 'sw2': jax.random.normal(ks[7], (S, H, D), dtype=jnp.float32) * std}
    _L2_ffn_all = _L2_ffn_setup()
    _L2_ffn_in = {k: v for k, v in _L2_ffn_all.items() if k in ('router_w', 'experts_bias', 'w1', 'w3', 'w2', 'sw1', 'sw3', 'sw2')}
    del _L2_ffn_all

    def _L3_xattn_setup():
        import jax, jax.numpy as jnp
        import numpy as np
        HIDDEN = 256
        HEADS = 16
        DEPTH = HIDDEN // HEADS
        B, F, T = (2, 512, 512)
        key = jax.random.key(seed)
        ks = jax.random.split(key, 7)
        a_qkv = np.sqrt(2.0) * np.sqrt(6.0 / (HIDDEN + HEADS * DEPTH))
        a_out = np.sqrt(2.0) * np.sqrt(6.0 / (HEADS * DEPTH + HIDDEN))
        return {'query_input': jax.random.normal(ks[0], (B, F, HIDDEN), jnp.float32), 'source_input': jax.random.normal(ks[1], (B, T, HIDDEN), jnp.float32), 'bias': jax.random.normal(ks[2], (1, 1, F, T), jnp.float32), 'Wq': jax.random.normal(ks[3], (HIDDEN, HEADS, DEPTH), jnp.float32) * a_qkv, 'Wk': jax.random.normal(ks[4], (HIDDEN, HEADS, DEPTH), jnp.float32) * a_qkv, 'Wv': jax.random.normal(ks[5], (HIDDEN, HEADS, DEPTH), jnp.float32) * a_qkv, 'Wo': jax.random.normal(ks[6], (HEADS, DEPTH, HIDDEN), jnp.float32) * a_out}
    _L3_xattn_all = _L3_xattn_setup()
    _L3_xattn_in = {k: v for k, v in _L3_xattn_all.items() if k in ('Wq', 'Wk', 'Wv', 'Wo')}
    del _L3_xattn_all

    def _L3_attn_setup():
        import jax, jax.numpy as jnp
        import numpy as np
        B, S, E, H = (2, 512, 256, 16)
        D = E // H
        NEG_INF = -1e+30

        def alibi_slopes(n_head):
            return jnp.asarray([2.0 ** (-8.0 * (i + 1) / n_head) for i in range(n_head)], dtype=jnp.float32)
        key = jax.random.key(seed)
        ks = jax.random.split(key, 5)
        scale = 0.02
        return {'x': jax.random.normal(ks[0], (B, S, E), dtype=jnp.float32), 'W_kqv': jax.random.normal(ks[1], (E, 3 * E), dtype=jnp.float32) * scale, 'b_kqv': jnp.zeros((3 * E,), dtype=jnp.float32), 'W_proj': jax.random.normal(ks[2], (E, E), dtype=jnp.float32) * scale, 'b_proj': jnp.zeros((E,), dtype=jnp.float32), 'slopes': alibi_slopes(H)}
    _L3_attn_all = _L3_attn_setup()
    _L3_attn_in = {k: v for k, v in _L3_attn_all.items() if k in ('W_kqv', 'b_kqv', 'W_proj', 'b_proj', 'slopes')}
    del _L3_attn_all

    def _L3_ffn_setup():
        import jax, jax.numpy as jnp
        import numpy as np
        D_MODEL = 256
        H_SHARED = 512
        H_ROUTED = 256
        N_EXPERTS = 8
        TOP_K = 2
        key = jax.random.key(seed)
        ks = jax.random.split(key, 8)
        B, T = (2, 512)
        sc_d = 1.0 / np.sqrt(D_MODEL)
        sc_hs = 1.0 / np.sqrt(H_SHARED)
        sc_hr = 1.0 / np.sqrt(H_ROUTED)
        return {'x': jax.random.normal(ks[0], (B, T, D_MODEL), dtype=jnp.float32), 'router_w': jax.random.normal(ks[1], (N_EXPERTS, D_MODEL), dtype=jnp.float32) * sc_d, 'router_bias': jnp.zeros((N_EXPERTS,), dtype=jnp.float32), 'sw1': jax.random.normal(ks[2], (D_MODEL, H_SHARED), dtype=jnp.float32) * sc_d, 'sw3': jax.random.normal(ks[3], (D_MODEL, H_SHARED), dtype=jnp.float32) * sc_d, 'sw2': jax.random.normal(ks[4], (H_SHARED, D_MODEL), dtype=jnp.float32) * sc_hs, 'ew1': jax.random.normal(ks[5], (N_EXPERTS, D_MODEL, H_ROUTED), dtype=jnp.float32) * sc_d, 'ew2': jax.random.normal(ks[6], (N_EXPERTS, H_ROUTED, D_MODEL), dtype=jnp.float32) * sc_hr}
    _L3_ffn_all = _L3_ffn_setup()
    _L3_ffn_in = {k: v for k, v in _L3_ffn_all.items() if k in ('router_w', 'router_bias', 'sw1', 'sw3', 'sw2', 'ew1', 'ew2')}
    del _L3_ffn_all
    return {'x': x, 'ctx_1024': ctx_1024, 'fside_1x1xSxS2_0': fside_1x1xSxS2_0, 'mask_BxS2_ik0': mask_BxS2_ik0, 'mask_Bx1x1xS2_bf1': mask_Bx1x1xS2_bf1, 'L0_xattn_Wq_c': _L0_xattn_in['Wq_c'], 'L0_xattn_bq_c': _L0_xattn_in['bq_c'], 'L0_xattn_Wk_s': _L0_xattn_in['Wk_s'], 'L0_xattn_bk_s': _L0_xattn_in['bk_s'], 'L0_xattn_Wv_s': _L0_xattn_in['Wv_s'], 'L0_xattn_bv_s': _L0_xattn_in['bv_s'], 'L0_xattn_Wq_s': _L0_xattn_in['Wq_s'], 'L0_xattn_bq_s': _L0_xattn_in['bq_s'], 'L0_xattn_Wk_c': _L0_xattn_in['Wk_c'], 'L0_xattn_bk_c': _L0_xattn_in['bk_c'], 'L0_xattn_Wv_c': _L0_xattn_in['Wv_c'], 'L0_xattn_bv_c': _L0_xattn_in['bv_c'], 'L0_xattn_Wg': _L0_xattn_in['Wg'], 'L0_xattn_bg': _L0_xattn_in['bg'], 'L0_attn_w_q': _L0_attn_in['w_q'], 'L0_attn_w_k': _L0_attn_in['w_k'], 'L0_attn_w_v': _L0_attn_in['w_v'], 'L0_attn_w_o': _L0_attn_in['w_o'], 'L0_attn_b_o': _L0_attn_in['b_o'], 'L0_ffn_ln_scale': _L0_ffn_in['ln_scale'], 'L0_ffn_ln_bias': _L0_ffn_in['ln_bias'], 'L0_ffn_attn_w': _L0_ffn_in['attn_w'], 'L0_ffn_attn_b': _L0_ffn_in['attn_b'], 'L0_ffn_gate_w': _L0_ffn_in['gate_w'], 'L0_ffn_w1': _L0_ffn_in['w1'], 'L0_ffn_b1': _L0_ffn_in['b1'], 'L0_ffn_w2': _L0_ffn_in['w2'], 'L0_ffn_b2': _L0_ffn_in['b2'], 'L0_ffn_next_w': _L0_ffn_in['next_w'], 'L0_ffn_next_b': _L0_ffn_in['next_b'], 'L1_xattn_Wq': _L1_xattn_in['Wq'], 'L1_xattn_bq': _L1_xattn_in['bq'], 'L1_xattn_Wk': _L1_xattn_in['Wk'], 'L1_xattn_bk': _L1_xattn_in['bk'], 'L1_xattn_Wv': _L1_xattn_in['Wv'], 'L1_xattn_bv': _L1_xattn_in['bv'], 'L1_xattn_Wo': _L1_xattn_in['Wo'], 'L1_xattn_bo': _L1_xattn_in['bo'], 'L1_attn_Wq': _L1_attn_in['Wq'], 'L1_attn_bq': _L1_attn_in['bq'], 'L1_attn_Wk': _L1_attn_in['Wk'], 'L1_attn_bk': _L1_attn_in['bk'], 'L1_attn_Wv': _L1_attn_in['Wv'], 'L1_attn_bv': _L1_attn_in['bv'], 'L1_attn_Wo': _L1_attn_in['Wo'], 'L1_attn_bo': _L1_attn_in['bo'], 'L1_ffn_gamma': _L1_ffn_in['gamma'], 'L1_ffn_beta': _L1_ffn_in['beta'], 'L1_ffn_w_q': _L1_ffn_in['w_q'], 'L1_ffn_keys': _L1_ffn_in['keys'], 'L1_ffn_key_in': _L1_ffn_in['key_in'], 'L1_ffn_key_out': _L1_ffn_in['key_out'], 'L2_xattn_Wq': _L2_xattn_in['Wq'], 'L2_xattn_bq': _L2_xattn_in['bq'], 'L2_xattn_Wk': _L2_xattn_in['Wk'], 'L2_xattn_bk': _L2_xattn_in['bk'], 'L2_xattn_Wv': _L2_xattn_in['Wv'], 'L2_xattn_bv': _L2_xattn_in['bv'], 'L2_xattn_Wo': _L2_xattn_in['Wo'], 'L2_xattn_bo': _L2_xattn_in['bo'], 'L2_attn_q_w': _L2_attn_in['q_w'], 'L2_attn_q_b': _L2_attn_in['q_b'], 'L2_attn_k_w': _L2_attn_in['k_w'], 'L2_attn_k_b': _L2_attn_in['k_b'], 'L2_attn_v_w': _L2_attn_in['v_w'], 'L2_attn_v_b': _L2_attn_in['v_b'], 'L2_attn_o_w': _L2_attn_in['o_w'], 'L2_attn_o_b': _L2_attn_in['o_b'], 'L2_ffn_router_w': _L2_ffn_in['router_w'], 'L2_ffn_experts_bias': _L2_ffn_in['experts_bias'], 'L2_ffn_w1': _L2_ffn_in['w1'], 'L2_ffn_w3': _L2_ffn_in['w3'], 'L2_ffn_w2': _L2_ffn_in['w2'], 'L2_ffn_sw1': _L2_ffn_in['sw1'], 'L2_ffn_sw3': _L2_ffn_in['sw3'], 'L2_ffn_sw2': _L2_ffn_in['sw2'], 'L3_xattn_Wq': _L3_xattn_in['Wq'], 'L3_xattn_Wk': _L3_xattn_in['Wk'], 'L3_xattn_Wv': _L3_xattn_in['Wv'], 'L3_xattn_Wo': _L3_xattn_in['Wo'], 'L3_attn_W_kqv': _L3_attn_in['W_kqv'], 'L3_attn_b_kqv': _L3_attn_in['b_kqv'], 'L3_attn_W_proj': _L3_attn_in['W_proj'], 'L3_attn_b_proj': _L3_attn_in['b_proj'], 'L3_attn_slopes': _L3_attn_in['slopes'], 'L3_ffn_router_w': _L3_ffn_in['router_w'], 'L3_ffn_router_bias': _L3_ffn_in['router_bias'], 'L3_ffn_sw1': _L3_ffn_in['sw1'], 'L3_ffn_sw3': _L3_ffn_in['sw3'], 'L3_ffn_sw2': _L3_ffn_in['sw2'], 'L3_ffn_ew1': _L3_ffn_in['ew1'], 'L3_ffn_ew2': _L3_ffn_in['ew2']}

def reference(x, ctx_1024, fside_1x1xSxS2_0, mask_BxS2_ik0, mask_Bx1x1xS2_bf1, L0_xattn_Wq_c, L0_xattn_bq_c, L0_xattn_Wk_s, L0_xattn_bk_s, L0_xattn_Wv_s, L0_xattn_bv_s, L0_xattn_Wq_s, L0_xattn_bq_s, L0_xattn_Wk_c, L0_xattn_bk_c, L0_xattn_Wv_c, L0_xattn_bv_c, L0_xattn_Wg, L0_xattn_bg, L0_attn_w_q, L0_attn_w_k, L0_attn_w_v, L0_attn_w_o, L0_attn_b_o, L0_ffn_ln_scale, L0_ffn_ln_bias, L0_ffn_attn_w, L0_ffn_attn_b, L0_ffn_gate_w, L0_ffn_w1, L0_ffn_b1, L0_ffn_w2, L0_ffn_b2, L0_ffn_next_w, L0_ffn_next_b, L1_xattn_Wq, L1_xattn_bq, L1_xattn_Wk, L1_xattn_bk, L1_xattn_Wv, L1_xattn_bv, L1_xattn_Wo, L1_xattn_bo, L1_attn_Wq, L1_attn_bq, L1_attn_Wk, L1_attn_bk, L1_attn_Wv, L1_attn_bv, L1_attn_Wo, L1_attn_bo, L1_ffn_gamma, L1_ffn_beta, L1_ffn_w_q, L1_ffn_keys, L1_ffn_key_in, L1_ffn_key_out, L2_xattn_Wq, L2_xattn_bq, L2_xattn_Wk, L2_xattn_bk, L2_xattn_Wv, L2_xattn_bv, L2_xattn_Wo, L2_xattn_bo, L2_attn_q_w, L2_attn_q_b, L2_attn_k_w, L2_attn_k_b, L2_attn_v_w, L2_attn_v_b, L2_attn_o_w, L2_attn_o_b, L2_ffn_router_w, L2_ffn_experts_bias, L2_ffn_w1, L2_ffn_w3, L2_ffn_w2, L2_ffn_sw1, L2_ffn_sw3, L2_ffn_sw2, L3_xattn_Wq, L3_xattn_Wk, L3_xattn_Wv, L3_xattn_Wo, L3_attn_W_kqv, L3_attn_b_kqv, L3_attn_W_proj, L3_attn_b_proj, L3_attn_slopes, L3_ffn_router_w, L3_ffn_router_bias, L3_ffn_sw1, L3_ffn_sw3, L3_ffn_sw2, L3_ffn_ew1, L3_ffn_ew2):
    import jax
    import jax.numpy as jnp

    def _L0_xattn_ref(char_emb, subword_emb, Wq_c, bq_c, Wk_s, bk_s, Wv_s, bv_s, Wq_s, bq_s, Wk_c, bk_c, Wv_c, bv_c, Wg, bg):
        import jax, jax.numpy as jnp
        import numpy as np
        H = 256
        B = 8
        L_CHAR = 512
        L_SUB = 256

        def _linear(x, W, b):
            return jnp.einsum('blh,oh->blo', x, W) + b

        def _interp_linear(x, out_len):
            L_in = x.shape[1]
            pos = (jnp.arange(out_len, dtype=x.dtype) + 0.5) * (L_in / out_len) - 0.5
            pos = jnp.clip(pos, 0.0, L_in - 1)
            lo = jnp.floor(pos).astype(jnp.int32)
            hi = jnp.minimum(lo + 1, L_in - 1)
            w = (pos - lo.astype(x.dtype))[None, :, None]
            return x[:, lo] * (1 - w) + x[:, hi] * w
        h = char_emb.shape[-1]
        scale = 1.0 / jnp.sqrt(jnp.asarray(h, char_emb.dtype))
        Q_char = _linear(char_emb, Wq_c, bq_c)
        K_sub = _linear(subword_emb, Wk_s, bk_s)
        V_sub = _linear(subword_emb, Wv_s, bv_s)
        scores = jnp.einsum('bqh,bkh->bqk', Q_char, K_sub) * scale
        char2sub = jnp.einsum('bqk,bkh->bqh', jax.nn.softmax(scores, axis=-1), V_sub)
        Q_sub = _linear(subword_emb, Wq_s, bq_s)
        K_char = _linear(char_emb, Wk_c, bk_c)
        V_char = _linear(char_emb, Wv_c, bv_c)
        scores2 = jnp.einsum('bqh,bkh->bqk', Q_sub, K_char) * scale
        sub2char = jnp.einsum('bqk,bkh->bqh', jax.nn.softmax(scores2, axis=-1), V_char)
        L_char = char_emb.shape[1]
        if sub2char.shape[1] != L_char:
            sub2char = _interp_linear(sub2char, L_char)
        gate_in = jnp.concatenate([char2sub, sub2char], axis=-1)
        gate = jax.nn.sigmoid(jnp.einsum('blh,oh->blo', gate_in, Wg) + bg)
        return gate * char2sub + (1 - gate) * sub2char

    def _L0_attn_ref(x, w_q, w_k, w_v, w_o, b_o):
        import jax, jax.numpy as jnp
        import numpy as np
        IMG_SIZE = 224
        PATCH_SIZE = 16
        CONTEXT_LEN = 79
        LATENT_DIM = 256
        NUM_HEADS = 16
        NUM_PATCHES = (IMG_SIZE // PATCH_SIZE) ** 2
        SEQ_LEN = NUM_PATCHES + CONTEXT_LEN
        BATCH = 8

        def prefix_lm_mask(num_img_patches, total):
            m = np.tril(np.ones((total, total), dtype=np.float32))
            m[:num_img_patches, :num_img_patches] = 1.0
            return jnp.asarray(m)
        B, S, D = x.shape
        H = NUM_HEADS
        hd = D // H
        q = (x @ w_q.T).reshape(B, S, H, hd).transpose(0, 2, 1, 3)
        k = (x @ w_k.T).reshape(B, S, H, hd).transpose(0, 2, 1, 3)
        v = (x @ w_v.T).reshape(B, S, H, hd).transpose(0, 2, 1, 3)
        scores = jnp.einsum('bhqd,bhkd->bhqk', q, k) / jnp.sqrt(jnp.float32(hd))
        mask = prefix_lm_mask(NUM_PATCHES, S)
        scores = jnp.where(mask == 0, jnp.float32(-jnp.inf), scores)
        attn = jax.nn.softmax(scores, axis=-1)
        ctx = jnp.einsum('bhqk,bhkd->bhqd', attn, v)
        ctx = ctx.transpose(0, 2, 1, 3).reshape(B, S, D)
        return ctx @ w_o.T + b_o

    def _L0_ffn_ref(x, ln_scale, ln_bias, attn_w, attn_b, gate_w, w1, b1, w2, b2, next_w, next_b):
        import jax, jax.numpy as jnp
        import numpy as np
        MICRO_BATCHES = 2
        TOP_K = 2
        NUM_EXPERTS = 8
        B, S, D = (4, 1024, 256)
        H = 4 * D
        b, s, d = x.shape
        flat = x.reshape(b * s, d)
        mu = jnp.mean(flat, axis=-1, keepdims=True)
        var = jnp.mean((flat - mu) ** 2, axis=-1, keepdims=True)
        xn = (flat - mu) * jax.lax.rsqrt(var + 1e-05) * ln_scale + ln_bias
        x_attn = xn @ attn_w.T + attn_b + flat
        logits = x_attn @ gate_w.T
        _vals, _idx = jax.lax.top_k(logits, TOP_K)
        e = w1.shape[0]
        n = b * s // (MICRO_BATCHES * e)
        xe = x_attn.reshape(MICRO_BATCHES, e, n, d)
        h = jax.nn.gelu(jnp.einsum('mend,edh->menh', xe, w1) + b1[None, :, None, :], approximate=False)
        eo = jnp.einsum('menh,ehd->mend', h, w2) + b2[None, :, None, :]
        eo = eo.reshape(b * s, d)
        out = jax.nn.gelu(eo @ next_w.T + next_b, approximate=False)
        return out.reshape(b, s, d)

    def _L1_xattn_ref(x, context, ctx_key_padding_mask, Wq, bq, Wk, bk, Wv, bv, Wo, bo):
        import jax, jax.numpy as jnp
        import numpy as np
        DIM = 256
        NUM_HEADS = 16
        HEAD_DIM = DIM // NUM_HEADS
        SCALE = HEAD_DIM ** (-0.5)
        B, N, C = x.shape
        M = context.shape[1]
        H, D = (NUM_HEADS, HEAD_DIM)
        q = (x @ Wq.T + bq).reshape(B, N, H, D)
        k = (context @ Wk.T + bk).reshape(B, M, H, D)
        v = (context @ Wv.T + bv).reshape(B, M, H, D)
        scores = jnp.einsum('bnhd,bmhd->bhnm', q, k) * SCALE
        neg = jnp.finfo(scores.dtype).min
        bias = jnp.where(ctx_key_padding_mask[:, None, None, :] != 0, 0.0, neg).astype(scores.dtype)
        attn = jax.nn.softmax(scores + bias, axis=-1)
        out = jnp.einsum('bhnm,bmhd->bnhd', attn, v).reshape(B, N, C)
        return out @ Wo.T + bo

    def _L1_attn_ref(hidden_states, Wq, bq, Wk, bk, Wv, bv, Wo, bo):
        import math
        import jax, jax.numpy as jnp
        import numpy as np
        B, S, D = (4, 512, 256)

        def _complex_proj(x, W, b):
            p = jnp.einsum('bsd,ed->bse', x, W) + b
            p = p.reshape(*x.shape[:-1], x.shape[-1], 2)
            return (p[..., 0], p[..., 1])
        dim = hidden_states.shape[-1]
        qr, qi = _complex_proj(hidden_states, Wq, bq)
        kr, ki = _complex_proj(hidden_states, Wk, bk)
        vr, vi = _complex_proj(hidden_states, Wv, bv)
        scale = 1.0 / math.sqrt(dim)
        scores = (jnp.einsum('bsd,btd->bst', qr, kr) + jnp.einsum('bsd,btd->bst', qi, ki)) * scale
        w = jax.nn.softmax(scores, axis=-1)
        o_r = jnp.einsum('bst,btd->bsd', w, vr)
        o_i = jnp.einsum('bst,btd->bsd', w, vi)
        out = jnp.stack([o_r, o_i], axis=-1).reshape(*hidden_states.shape[:-1], 2 * dim)
        return jnp.einsum('bse,de->bsd', out, Wo) + bo

    def _L1_ffn_ref(inputs, gamma, beta, w_q, keys, key_in, key_out):
        import jax, jax.numpy as jnp
        import numpy as np
        TOPK = 8
        BN_EPS = 1e-05
        b, n, d = inputs.shape
        h, nk, _, kd = keys.shape
        k = TOPK
        x = inputs.reshape(b * n, d)
        mu = jnp.mean(x, axis=0)
        var = jnp.mean(jnp.square(x - mu), axis=0)
        xn = (x - mu) * jax.lax.rsqrt(var + BN_EPS) * gamma + beta
        q = (xn @ w_q.T).reshape(b, n, 2, h, kd).transpose(2, 0, 1, 3, 4)
        sim = jnp.einsum('pbnhd,hkpd->pbnhk', q, keys)
        s, i = jax.lax.top_k(sim, k)
        sx, sy = (s[0], s[1])
        ix, iy = (i[0], i[1])
        all_scores = (sx[..., :, None] + sy[..., None, :]).reshape(b, n, h, k * k)
        all_idx = (ix[..., :, None] * nk + iy[..., None, :]).reshape(b, n, h, k * k)
        scores, pk = jax.lax.top_k(all_scores, k)
        idx = jnp.take_along_axis(all_idx, pk, axis=-1)
        w_down = key_in[idx]
        w_up = key_out[idx]
        o = jnp.einsum('bnd,bnhkd->bnhk', inputs, w_down)
        o = jax.nn.gelu(o, approximate=False) * jax.nn.softmax(scores, axis=-1)
        return jnp.einsum('bnhk,bnhkd->bnd', o, w_up)

    def _L2_xattn_ref(query, key, value, mask, Wq, bq, Wk, bk, Wv, bv, Wo, bo):
        import jax, jax.numpy as jnp
        import numpy as np
        import math
        D_MODEL = 256
        N_HEADS = 16
        HEAD_DIM = D_MODEL // N_HEADS
        B, S = (4, 512)

        def _split_heads(x):
            b, s, _ = x.shape
            return x.reshape(b, s, N_HEADS, HEAD_DIM).transpose(0, 2, 1, 3)
        q = _split_heads(query @ Wq.T + bq)
        k = _split_heads(key @ Wk.T + bk)
        v = _split_heads(value @ Wv.T + bv)
        scores = jnp.einsum('bhqd,bhkd->bhqk', q, k) / math.sqrt(HEAD_DIM)
        scores = jnp.where(mask, scores, -jnp.inf)
        attn = jax.nn.softmax(scores, axis=-1)
        ctx = jnp.einsum('bhqk,bhkd->bhqd', attn, v)
        ctx = ctx.transpose(0, 2, 1, 3).reshape(query.shape[0], -1, D_MODEL)
        return ctx @ Wo.T + bo

    def _L2_attn_ref(x, q_w, q_b, k_w, k_b, v_w, v_b, o_w, o_b):
        import jax, jax.numpy as jnp
        import numpy as np
        D_MODEL = 256
        N_HEADS = 16
        HEAD_DIM = D_MODEL // N_HEADS

        def _rope_tables(L, dtype):
            inv_freq = 1.0 / 10000.0 ** (jnp.arange(0, HEAD_DIM, 2, dtype=dtype) / HEAD_DIM)
            t = jnp.arange(L, dtype=dtype)
            freqs = t[:, None] * inv_freq[None, :]
            emb = jnp.concatenate([freqs, freqs], axis=-1)
            return (jnp.cos(emb), jnp.sin(emb))

        def _rotate_half(x):
            x1, x2 = (x[..., :HEAD_DIM // 2], x[..., HEAD_DIM // 2:])
            return jnp.concatenate([-x2, x1], axis=-1)
        B, L, D = x.shape
        H, hd = (N_HEADS, HEAD_DIM)

        def proj(w, b):
            y = jnp.einsum('bld,ed->ble', x, w) + b
            return y.reshape(B, L, H, hd).transpose(0, 2, 1, 3)
        q, k, v = (proj(q_w, q_b), proj(k_w, k_b), proj(v_w, v_b))
        cos, sin = _rope_tables(L, x.dtype)
        q = q * cos + _rotate_half(q) * sin
        k = k * cos + _rotate_half(k) * sin
        scores = jnp.einsum('bhqd,bhkd->bhqk', q, k) / jnp.sqrt(jnp.asarray(hd, x.dtype))
        attn = jax.nn.softmax(scores, axis=-1)
        out = jnp.einsum('bhqk,bhkd->bhqd', attn, v)
        out = out.transpose(0, 2, 1, 3).reshape(B, L, D)
        return jnp.einsum('bld,ed->ble', out, o_w) + o_b

    def _L2_ffn_ref(x, router_w, experts_bias, w1, w3, w2, sw1, sw3, sw2):
        import jax, jax.numpy as jnp
        import numpy as np
        D, H, E, K, S = (256, 512, 8, 2, 1)
        B, L = (4, 512)
        b, l, d = x.shape
        xf = x.reshape(-1, d)
        sg = jnp.einsum('td,sdh->tsh', xf, sw1)
        su = jnp.einsum('td,sdh->tsh', xf, sw3)
        shared_out = jnp.einsum('tsh,shd->td', jax.nn.silu(sg) * su, sw2)
        logits = xf @ router_w.T + experts_bias
        rw, sel = jax.lax.top_k(logits, K)
        rw = jax.nn.softmax(rw.astype(jnp.float32), axis=-1).astype(x.dtype)
        cw = (jax.nn.one_hot(sel, E, dtype=x.dtype) * rw[..., None]).sum(axis=1)
        g = jnp.einsum('td,edh->teh', xf, w1)
        u = jnp.einsum('td,edh->teh', xf, w3)
        eo = jax.nn.silu(g) * u
        moe_out = jnp.einsum('te,teh,ehd->td', cw, eo, w2)
        return (moe_out + shared_out).reshape(b, l, d)

    def _L3_xattn_ref(query_input, source_input, bias, Wq, Wk, Wv, Wo):
        import jax, jax.numpy as jnp
        import numpy as np
        HIDDEN = 256
        HEADS = 16
        DEPTH = HIDDEN // HEADS
        B, F, T = (2, 512, 512)
        q = jnp.einsum('bfc,cnh->bfnh', query_input, Wq)
        k = jnp.einsum('btc,cnh->btnh', source_input, Wk)
        v = jnp.einsum('btc,cnh->btnh', source_input, Wv)
        q = q * DEPTH ** (-0.5)
        logits = jnp.einsum('btnh,bfnh->bnft', k, q)
        logits = logits + bias
        weights = jax.nn.softmax(logits, axis=3)
        att = jnp.einsum('bnft,btnh->bfnh', weights, v)
        out = jnp.einsum('bfnh,nhe->bfe', att, Wo)
        return out

    def _L3_attn_ref(x, W_kqv, b_kqv, W_proj, b_proj, slopes):
        import jax, jax.numpy as jnp
        import numpy as np
        B, S, E, H = (2, 512, 256, 16)
        D = E // H
        NEG_INF = -1e+30

        def alibi_slopes(n_head):
            return jnp.asarray([2.0 ** (-8.0 * (i + 1) / n_head) for i in range(n_head)], dtype=jnp.float32)
        b, s, e = x.shape
        kqv = x @ W_kqv + b_kqv
        k, q, v = jnp.split(kqv, 3, axis=-1)
        k = k.reshape(b, s, H, D)
        q = q.reshape(b, s, H, D)
        v = v.reshape(b, s, H, D)
        attn = jnp.einsum('bqhd,bkhd->bhqk', q, k) * (1.0 / jnp.sqrt(jnp.float32(D)))
        i = jnp.arange(s)[:, None]
        j = jnp.arange(s)[None, :]
        rel = (j - i).astype(jnp.float32)
        bias = slopes[:, None, None] * jnp.tril(rel)
        bias = jnp.where(j > i, NEG_INF, bias)
        attn = jax.nn.softmax(attn + bias[None], axis=-1)
        y = jnp.einsum('bhqk,bkhd->bqhd', attn, v).reshape(b, s, e)
        return y @ W_proj + b_proj

    def _L3_ffn_ref(x, router_w, router_bias, sw1, sw3, sw2, ew1, ew2):
        import jax, jax.numpy as jnp
        import numpy as np
        D_MODEL = 256
        H_SHARED = 512
        H_ROUTED = 256
        N_EXPERTS = 8
        TOP_K = 2
        B, T, C = x.shape
        xf = x.reshape(-1, C)
        shared_out = jax.nn.silu(xf @ sw1) * (xf @ sw3) @ sw2
        s = jax.nn.sigmoid((xf @ router_w.T).astype(jnp.float32))
        sel_scores = s + router_bias.astype(jnp.float32)
        _, topk_idx = jax.lax.top_k(sel_scores, TOP_K)
        s_sel = jnp.take_along_axis(s, topk_idx, axis=1)
        denom = s_sel.sum(axis=1, keepdims=True)
        gates = jnp.where(denom > 1e-09, s_sel / (denom + 1e-09), 1.0 / TOP_K).astype(x.dtype)
        one_hot = jax.nn.one_hot(topk_idx, N_EXPERTS, dtype=x.dtype)
        comb = jnp.einsum('nke,nk->ne', one_hot, gates)
        h = jax.nn.gelu(jnp.einsum('nd,edh->neh', xf, ew1), approximate=False)
        y = jnp.einsum('neh,ehd->ned', h, ew2)
        routed_out = jnp.einsum('ned,ne->nd', y, comb)
        return (shared_out + routed_out).reshape(B, T, C)
    x = x + _L0_xattn_ref(_layernorm(x, axis=-1), ctx_1024, L0_xattn_Wq_c, L0_xattn_bq_c, L0_xattn_Wk_s, L0_xattn_bk_s, L0_xattn_Wv_s, L0_xattn_bv_s, L0_xattn_Wq_s, L0_xattn_bq_s, L0_xattn_Wk_c, L0_xattn_bk_c, L0_xattn_Wv_c, L0_xattn_bv_c, L0_xattn_Wg, L0_xattn_bg)
    x = x + _L0_attn_ref(_layernorm(x, axis=-1), L0_attn_w_q, L0_attn_w_k, L0_attn_w_v, L0_attn_w_o, L0_attn_b_o)
    x = x + _L0_ffn_ref(_layernorm(x, axis=-1), L0_ffn_ln_scale, L0_ffn_ln_bias, L0_ffn_attn_w, L0_ffn_attn_b, L0_ffn_gate_w, L0_ffn_w1, L0_ffn_b1, L0_ffn_w2, L0_ffn_b2, L0_ffn_next_w, L0_ffn_next_b)
    x = x + _L1_xattn_ref(_layernorm(x, axis=-1), ctx_1024, mask_BxS2_ik0, L1_xattn_Wq, L1_xattn_bq, L1_xattn_Wk, L1_xattn_bk, L1_xattn_Wv, L1_xattn_bv, L1_xattn_Wo, L1_xattn_bo)
    x = x + _L1_attn_ref(_layernorm(x, axis=-1), L1_attn_Wq, L1_attn_bq, L1_attn_Wk, L1_attn_bk, L1_attn_Wv, L1_attn_bv, L1_attn_Wo, L1_attn_bo)
    x = x + _L1_ffn_ref(_layernorm(x, axis=-1), L1_ffn_gamma, L1_ffn_beta, L1_ffn_w_q, L1_ffn_keys, L1_ffn_key_in, L1_ffn_key_out)
    x = x + _L2_xattn_ref(_layernorm(x, axis=-1), ctx_1024, ctx_1024, mask_Bx1x1xS2_bf1, L2_xattn_Wq, L2_xattn_bq, L2_xattn_Wk, L2_xattn_bk, L2_xattn_Wv, L2_xattn_bv, L2_xattn_Wo, L2_xattn_bo)
    x = x + _L2_attn_ref(_layernorm(x, axis=-1), L2_attn_q_w, L2_attn_q_b, L2_attn_k_w, L2_attn_k_b, L2_attn_v_w, L2_attn_v_b, L2_attn_o_w, L2_attn_o_b)
    x = x + _L2_ffn_ref(_layernorm(x, axis=-1), L2_ffn_router_w, L2_ffn_experts_bias, L2_ffn_w1, L2_ffn_w3, L2_ffn_w2, L2_ffn_sw1, L2_ffn_sw3, L2_ffn_sw2)
    x = x + _L3_xattn_ref(_layernorm(x, axis=-1), ctx_1024, fside_1x1xSxS2_0, L3_xattn_Wq, L3_xattn_Wk, L3_xattn_Wv, L3_xattn_Wo)
    x = x + _L3_attn_ref(_layernorm(x, axis=-1), L3_attn_W_kqv, L3_attn_b_kqv, L3_attn_W_proj, L3_attn_b_proj, L3_attn_slopes)
    x = x + _L3_ffn_ref(_layernorm(x, axis=-1), L3_ffn_router_w, L3_ffn_router_bias, L3_ffn_sw1, L3_ffn_sw3, L3_ffn_sw2, L3_ffn_ew1, L3_ffn_ew2)
    return x

_drawn_inputs = setup_inputs


def setup_inputs(seed=0):
    import zlib

    import numpy as np

    out = dict(_drawn_inputs(seed))
    spreads = {'L0_ffn_ln_scale': (1.0, 0.6),
     'L0_ffn_ln_bias': (0.0, 0.8),
     'L0_ffn_attn_b': (0.0, 0.8),
     'L0_ffn_b1': (0.0, 0.502),
     'L0_ffn_b2': (0.0, 0.1),
     'L0_ffn_next_b': (0.0, 0.1),
     'L1_xattn_bq': (0.0, 0.8),
     'L1_xattn_bk': (0.0, 0.8),
     'L1_xattn_bv': (0.0, 0.1),
     'L1_xattn_bo': (0.0, 0.1),
     'L1_ffn_gamma': (1.0, 0.6),
     'L1_ffn_beta': (0.0, 0.8),
     'L2_xattn_bq': (0.0, 0.1),
     'L2_xattn_bk': (0.0, 0.8),
     'L2_xattn_bv': (0.0, 0.1),
     'L2_xattn_bo': (0.0, 0.1),
     'L2_attn_q_b': (0.0, 0.343),
     'L2_attn_k_b': (0.0, 0.53),
     'L2_attn_v_b': (0.0, 0.1),
     'L2_attn_o_b': (0.0, 0.1),
     'L2_ffn_experts_bias': (0.0, 0.77),
     'L3_attn_b_kqv': (0.0, 0.8),
     'L3_attn_b_proj': (0.0, 0.41),
     'L3_ffn_router_bias': (0.0, 0.1)}
    factors = {'L0_xattn_Wq_c': 8.0,
     'L0_xattn_bq_c': 8.0,
     'L0_xattn_Wk_s': 8.0,
     'L0_xattn_bk_s': 8.0,
     'L0_xattn_Wq_s': 6.842,
     'L0_xattn_bq_s': 8.0,
     'L0_xattn_Wk_c': 7.06,
     'L0_xattn_bk_c': 8.0,
     'L0_xattn_Wg': 5.662,
     'L0_xattn_bg': 8.0,
     'L0_ffn_attn_w': 4.778,
     'L1_xattn_Wq': 8.0,
     'L1_xattn_Wk': 8.0,
     'L1_attn_bq': 7.206,
     'L1_attn_bk': 8.0,
     'L1_attn_bo': 3.81,
     'L1_ffn_w_q': 8.0,
     'L1_ffn_keys': 8.0,
     'L1_ffn_key_in': 8.0,
     'L1_ffn_key_out': 8.0,
     'L2_ffn_router_w': 3.227,
     'L2_ffn_w1': 2.819,
     'L2_ffn_w3': 2.819,
     'L2_ffn_w2': 2.764,
     'L3_attn_W_kqv': 4.395,
     'L3_attn_W_proj': 4.045,
     'L3_attn_slopes': 8.0}
    for name, (base, spread) in spreads.items():
        noise = np.random.default_rng([zlib.crc32(name.encode()), seed]).standard_normal(out[name].shape)
        drawn = base * np.exp(spread * noise) if base else spread * noise
        out[name] = jnp.asarray(drawn.astype(out[name].dtype))
    for name, factor in factors.items():
        out[name] = (out[name] * factor).astype(out[name].dtype)
    return out
```

```python
from contextlib import ExitStack

import numpy as np

import concourse.bass as bass
from concourse import mybir
from concourse.alu_op_type import AluOpType as ALU

ACT = mybir.ActivationFunctionType
F32 = mybir.dt.float32
BF16 = mybir.dt.bfloat16
I32 = mybir.dt.int32
U8 = mybir.dt.uint8
U32 = mybir.dt.uint32
X = mybir.AxisListType.X

P = 128
D = 256
C = D // P
B = 64
S = 32
KEYS = 257
T = B * S
NT = T // P
BT = P // S
H = 16
HD = D // H
G = 4
HG = H // G
GD = HG * HD
MASKED = -3.4028234663852886e38
EPS = 1e-5


def constant_tables():
    p = np.arange(P)
    parts = {
        "ident": np.eye(P),
        "minus_half": np.full((P, 1), -0.5),
        "head_of_feature": 0.25 * ((p[:, None] % GD) // HD == np.arange(HG)[None]),
        "quarter": (p[:, None] // S == np.arange(4)[None]),
        "relative": np.minimum(np.arange(S)[None] - (p % S)[:, None], 0),
        "later": np.where(np.arange(S)[None] > (p % S)[:, None], -1e30, 0.0),
        "iota": np.broadcast_to(np.arange(P), (P, P)),
        "group_rows": np.repeat((p[:, None] % S == (np.arange(G) % 2 * 2 + np.arange(G) // 2)[None]), GD, axis=1),
    }
    inv = (1.0 / 10000.0 ** (np.arange(0, HD, 2, dtype=np.float32) / HD)).astype(np.float32)
    freq = np.arange(S, dtype=np.float32)[:, None] * inv[None]
    emb = np.concatenate([freq, freq], axis=-1).astype(np.float32)
    sign = np.where(np.arange(HD) < HD // 2, -1.0, 1.0)
    parts["cosine"] = np.cos(emb).T[p % HD]
    parts["sine"] = (np.sin(emb).T * sign[:, None])[p % HD]
    pos = np.clip((np.arange(S, dtype=np.float32) + 0.5) * np.float32(KEYS / S) - 0.5, 0.0, KEYS - 1)
    lo = np.floor(pos).astype(np.int64)
    hi = np.minimum(lo + 1, KEYS - 1)
    w = (pos - lo).astype(np.float32)
    inter = np.zeros((64, S), np.float32)
    inter[2 * np.arange(S), np.arange(S)] = 1 - w
    inter[2 * np.arange(S) + 1, np.arange(S)] = w
    parts["interpolate"] = np.concatenate([inter, inter], axis=0)
    where, at = {}, 0
    for name, a in parts.items():
        where[name] = (at, a.shape[1])
        at += a.shape[1]
    table = np.concatenate([np.asarray(a, np.float32) for a in parts.values()], axis=1)
    return np.ascontiguousarray(table), where, np.stack([lo, hi], axis=1).reshape(-1)


class Core:

    def __init__(self, nc, inputs, x_sb, const, where):
        self.nc, self.inputs, self.x, self.const, self.where = nc, inputs, x_sb, const, where

    def table(self, name, rows=P):
        at, n = self.where[name]
        return self.const[0:rows, at:at + n]

    def weight(self, name):
        return self.inputs[name].rearrange("(c p) n -> p c n", p=P)

    def column(self, name):
        return self.inputs[name + "_col"]

    def rows(self, name, n=P):
        a = self.inputs[name].rearrange("(a d) -> a d", a=1)
        return a.broadcast_to([n, a.shape[1]])


def semaphores(nc, tag, names):
    return {n: nc.alloc_semaphore(f"{tag}_{n}") for n in names.split()}


LN_SEMS = "var_ready stats_ready mean_ready rstd_ready xn_ready"


def wait(engine, sem, n):
    engine.wait_ge(sem, n)
    engine.nop(nofuse=True)


def layer_norm(dve, nc, s, n, x_tile, xn, stats, mean, rstd):
    nc.vector.bn_stats(stats, x_tile).then_inc(s["stats_ready"], 1)
    wait(dve, s["stats_ready"], n)
    nc.vector.bn_aggr(mean, stats).then_inc(s["mean_ready"], 1)
    dve.wait_ge(s["rstd_ready"], n)
    nc.vector.tensor_scalar(xn, x_tile, mean[:, 0:1], rstd, ALU.subtract, ALU.mult).then_inc(s["xn_ready"], 1)


def layer_norm_root(pool, nc, s, n, mean, rstd, minus_half):
    wait(pool, s["mean_ready"], n)
    nc.gpsimd.tensor_scalar(mean[:, 1:2], mean[:, 1:2], EPS, None, ALU.add).then_inc(s["var_ready"], 1)
    pool.wait_ge(s["var_ready"], n)
    nc.gpsimd.tensor_tensor(rstd, mean[:, 1:2], minus_half, ALU.pow).then_inc(s["rstd_ready"], 1)


def self_attention(core, tag, w, rope=False, alibi=None):
    nc = core.nc
    with ExitStack() as ctx:
        def sb(name, shape, dt=F32):
            return ctx.enter_context(nc.sbuf_tensor(f"{tag}_{name}", shape, dt))

        def ps(name, shape):
            return ctx.enter_context(nc.psum_tensor(f"{tag}_{name}", shape, F32))

        s = semaphores(nc, tag, LN_SEMS + """ weights_loaded xn_turned xnT_ready xnT4_ready qk_ready v_ready
            qT_ready kT_ready q_spread v_spread scores_ready biased_ready max_ready shifted_ready exp_ready
            sum_ready inv_ready probs_ready probs_turned ctx_ready ctxT_ready y_ready x_biased x_done
            bias_1 bias_2 rot_1 rot_2 rot_3 rot_4 rot_ready rotq_mult rotk_mult""")
        names = [k for k in ("q", "k", "v", "o", "qr", "kr") if w.get(k)]
        wt = {k: sb(f"w{k}", [P, C, D]) for k in names}
        cols = {k: sb(k, [P, C]) for k in ("bq", "bk", "bv", "bqr", "bkr") if w.get(k)}
        bo = sb("bo", [P, D])
        n_loads = len(names) + len(cols) + 1 + (HG if alibi else 0)
        stats, mean, rstd = sb("stats", [P, 6]), sb("mean", [P, 2]), sb("rstd", [P, 1])
        xn = sb("xn", [P, D])
        xnT = sb("xnT", [P, C, P])
        xnT_four = sb("xnT_four", [P, C, BT, HG, S])
        qT, kT = sb("qT", [P, C, P]), sb("kT", [P, C, P])
        q_by_head = sb("q_by_head", [P, C, BT, HG, S])
        v_by_head = sb("v_by_head", [P, BT, G, HG, HD])
        biased = sb("biased", [P, BT * G, S])
        big, rsum, rinv = sb("big", [P, BT * G]), sb("rsum", [P, BT * G]), sb("rinv", [P, BT * G])
        shifted = sb("shifted", [P, BT * G, S])
        probs = sb("probs", [P, BT * G, S])
        probsT = sb("probsT", [P, BT * G, S])
        ctxT = sb("ctxT", [P, C, P])
        x_plus_bo = sb("x_plus_bo", [P, D])
        if rope:
            qrot, krot = sb("qrot", [P, C, P]), sb("krot", [P, C, P])
        if alibi:
            slope = sb("slope", [P, 2, C])
            bias = sb("bias", [P, G, S])
        ps_t = ps("ps_t", [P, C, P])
        ps_qk = ps("ps_qk", [P, 2, C, P])
        ps_qkr = ps("ps_qkr", [P, 2, C, P]) if rope else None
        ps_v = ps("ps_v", [P, BT, D])
        ps_s = ps("ps_s", [P, 2, 512])[:, :, 0:BT * C * S]
        ps_oy = ps("ps_oy", [P, 2, C, P])
        ps_o, ps_y = ps_oy[:, 0], ps_oy[:, 1].rearrange("p c n -> p (c n)")
        ident = core.table("ident")
        head_of_feature = core.table("head_of_feature")
        quarter = core.table("quarter")
        block = ctx.enter_context(nc.Block())

        @block.sync
        def _(sp):
            for k in names:
                sp.dma_start(wt[k][:], core.weight(w[k])).then_inc(s["weights_loaded"], 16)
            for k in cols:
                sp.dma_start(cols[k][:], core.column(w[k])).then_inc(s["weights_loaded"], 16)
            sp.dma_start(bo[:], core.rows(w["bo"])).then_inc(s["weights_loaded"], 16)
            if alibi:
                by_head = core.inputs[alibi + "_by_head"]
                for h in range(HG):
                    sp.dma_start(slope[S * h:S * h + S].rearrange("p j c -> p (j c)"),
                                 by_head[h:h + 1].broadcast_to([S, G])).then_inc(
                        s["weights_loaded"], 16)

        @block.gpsimd
        def _(pool):
            pool.wait_ge(s["weights_loaded"], 16 * n_loads)
            with pool.Fori(0, NT) as i:
                layer_norm_root(pool, nc, s, i + 1, mean[:], rstd[:], core.table("minus_half"))
                pool.wait_ge(s["x_done"], i + 1)
                nc.gpsimd.tensor_tensor(x_plus_bo[:], core.x[:, i, :], bo[:], ALU.add).then_inc(s["x_biased"], 1)

        @block.tensor
        def _(pe):
            pe.wait_ge(s["weights_loaded"], 16 * n_loads)
            with pe.Fori(0, NT) as i:
                n = i + 1
                pe.wait_ge(s["xn_ready"], n)
                nc.tensor.transpose(ps_t[:, 0, :], xn[:, 0:P], ident)
                nc.tensor.transpose(ps_t[:, 1, :], xn[:, P:D], ident).then_inc(s["xn_turned"], 1)
                pe.wait_ge(s["xnT_ready"], n)
                for a, k in enumerate(("q", "k")):
                    for dst, kk in ((ps_qk, k), (ps_qkr, k + "r")):
                        if kk in wt:
                            for o in range(C):
                                for c in range(C):
                                    last = nc.tensor.matmul(dst[:, a, o, :], wt[kk][:, c, o * P:o * P + P],
                                                            xnT[:, c, :], start=(c == 0), stop=(c == C - 1))
                last.then_inc(s["qk_ready"], 1)
                pe.wait_ge(s["xnT4_ready"], n)
                for b in range(BT):
                    for c in range(C):
                        last = nc.tensor.matmul(ps_v[:, b, :], xnT_four[:, c, b, :, :], wt["v"][:, c, :],
                                                start=(c == 0), stop=(c == C - 1))
                last.then_inc(s["v_ready"], 1)
                pe.wait_ge(s["kT_ready"], n)
                wait(pe, s["q_spread"], n)
                for b in range(BT):
                    for g in range(G):
                        at = slice(GD * (g % 2), GD * (g % 2) + GD)
                        last = nc.tensor.matmul(ps_s[:, g % 2, (b * C + g // 2) * S:(b * C + g // 2 + 1) * S],
                                                q_by_head[at, g // 2, b, :, :],
                                                kT[at, g // 2, S * b:S * b + S], start=True, stop=True)
                last.then_inc(s["scores_ready"], 1)
                pe.wait_ge(s["v_spread"], n)
                wait(pe, s["probs_turned"], n)
                for b in range(BT):
                    for g in range(G):
                        at = slice(GD * (g % 2), GD * (g % 2) + GD)
                        last = nc.tensor.matmul(ps_o[at, g // 2, S * b:S * b + S], v_by_head[:, b, g, :, :],
                                                probsT[:, (g % 2) * BT * C + b * C + g // 2, :], start=True, stop=True)
                last.then_inc(s["ctx_ready"], 1)
                pe.wait_ge(s["ctxT_ready"], n)
                for c in range(C):
                    last = nc.tensor.matmul(ps_y[:], ctxT[:, c, :], wt["o"][:, c, :], start=(c == 0), stop=(c == C - 1))
                last.then_inc(s["y_ready"], 1)

        @block.scalar
        def _(act):
            act.wait_ge(s["weights_loaded"], 16 * n_loads)
            with act.Fori(0, NT) as i:
                n = i + 1
                act.wait_ge(s["xn_turned"], n)
                nc.scalar.copy(xnT[:], ps_t[:]).then_inc(s["xnT_ready"], 1)
                for c in range(C):
                    last = nc.scalar.copy(xnT_four[:, c], ps_t[:, c, :].rearrange("p (b k) -> p b k", b=BT)
                                          .unsqueeze(2).broadcast_to([P, BT, HG, S]))
                last.then_inc(s["xnT4_ready"], 1)
                act.wait_ge(s["qk_ready"], n)
                for a, (dst, bb) in enumerate(((qT, "bq"), (kT, "bk"))):
                    done = s["qT_ready"] if a == 0 else (s["rotk_mult"] if rope else s["kT_ready"])
                    for c in range(C):
                        if bb in cols:
                            last = nc.scalar.activation(dst[:, c, :], ps_qk[:, a, c, :], ACT.Identity,
                                                        bias=cols[bb][:, c:c + 1])
                        else:
                            last = nc.scalar.copy(dst[:, c, :], ps_qk[:, a, c, :])
                    last.then_inc(done, 1)
                if rope:
                    for a, (dst, bb) in enumerate(((qrot, "bqr"), (krot, "bkr"))):
                        for c in range(C):
                            last = nc.scalar.activation(dst[:, c, :], ps_qkr[:, a, c, :], ACT.Identity,
                                                        bias=cols[bb][:, c:c + 1])
                    last.then_inc(s["rotq_mult"], 1)
                act.wait_ge(s["v_ready"], n)
                for h in range(HG):
                    last = nc.scalar.activation(
                        v_by_head[:, :, :, h, :], ps_v[:].rearrange("p b (g h d) -> p b g h d", g=G, h=HG)[:, :, :, h, :],
                        ACT.Copy, scale=quarter[:, h:h + 1])
                last.then_inc(s["v_spread"], 1)
                act.wait_ge(s["shifted_ready"], n)
                nc.scalar.activation(shifted[:], shifted[:], ACT.Exp).then_inc(s["exp_ready"], 1)
                act.wait_ge(s["ctx_ready"], n)
                for c in range(C):
                    if "bv" in cols:
                        last = nc.scalar.activation(ctxT[:, c, :], ps_o[:, c, :], ACT.Identity,
                                                    bias=cols["bv"][:, c:c + 1])
                    else:
                        last = nc.scalar.copy(ctxT[:, c, :], ps_o[:, c, :])
                last.then_inc(s["ctxT_ready"], 1)

        @block.vector
        def _(dve):
            dve.sem_inc(s["x_done"], 1)
            dve.wait_ge(s["weights_loaded"], 16 * n_loads)
            if alibi:
                for g in range(G):
                    last = nc.vector.tensor_scalar(bias[:, g, :], core.table("relative"), slope[:, g // C, g % C:g % C + 1], None,
                                                   ALU.mult)
                last.then_inc(s["bias_1"], 1)
                dve.wait_ge(s["bias_1"], 1)
                nc.vector.tensor_tensor(bias[:], bias[:], core.table("later").unsqueeze(1).broadcast_to([P, G, S]),
                                        ALU.add).then_inc(s["bias_2"], 1)
                dve.wait_ge(s["bias_2"], 1)
            with dve.Fori(0, NT) as i:
                n = i + 1
                x_tile = core.x[:, i, :]
                layer_norm(dve, nc, s, n, x_tile, xn[:], stats[:], mean[:], rstd[:])
                dve.wait_ge(s["qT_ready"], n)
                if rope:
                    def turns(name):
                        return core.table(name).unsqueeze(1).broadcast_to([P, C * BT, S])
                    dve.wait_ge(s["rotq_mult"], n)
                    def flat(t):
                        return t[:].rearrange("p c (b q) -> p (c b) q", b=BT)
                    nc.vector.tensor_tensor(flat(qT), flat(qT), turns("cosine"), ALU.mult)
                    nc.vector.tensor_tensor(flat(qrot), flat(qrot), turns("sine"), ALU.mult).then_inc(s["rot_1"], 1)
                    dve.wait_ge(s["rotk_mult"], n)
                    nc.vector.tensor_tensor(flat(kT), flat(kT), turns("cosine"), ALU.mult)
                    nc.vector.tensor_tensor(flat(krot), flat(krot), turns("sine"), ALU.mult).then_inc(s["rot_2"], 1)
                    dve.wait_ge(s["rot_1"], n)
                    nc.vector.tensor_tensor(qT[:], qT[:], qrot[:], ALU.add).then_inc(s["rot_3"], 1)
                    dve.wait_ge(s["rot_2"], n)
                    nc.vector.tensor_tensor(kT[:], kT[:], krot[:], ALU.add).then_inc(s["kT_ready"], 1)
                    dve.wait_ge(s["rot_3"], n)
                for c in range(C):
                    last = nc.vector.tensor_tensor(
                        q_by_head[:, c], qT[:, c, :].rearrange("p (b q) -> p b q", b=BT).unsqueeze(2).broadcast_to(
                            [P, BT, HG, S]),
                        head_of_feature.unsqueeze(1).unsqueeze(3).broadcast_to([P, BT, HG, S]), ALU.mult)
                last.then_inc(s["q_spread"], 1)
                dve.wait_ge(s["scores_ready"], n)
                scores = ps_s
                if alibi:
                    nc.vector.tensor_tensor(
                        biased[:].rearrange("p (j b c) k -> p j b (c k)", j=2, b=BT),
                        ps_s.rearrange("p j (b n) -> p j b n", b=BT),
                        bias[:].rearrange("p (j c) k -> p j (c k)", j=2).unsqueeze(2).broadcast_to([P, 2, BT, C * S]),
                        ALU.add).then_inc(s["biased_ready"], 1)
                    dve.wait_ge(s["biased_ready"], n)
                    scores = biased[:].rearrange("p (j n) k -> p j (n k)", j=2)
                halves = scores.rearrange("p j (n k) -> p j n k", k=S)
                nc.vector.tensor_reduce(big[:].rearrange("p (j n) -> p j n", j=2), halves, X, ALU.max).then_inc(s["max_ready"], 1)
                dve.wait_ge(s["max_ready"], n)
                nc.vector.tensor_tensor(shifted[:].rearrange("p (j n) k -> p j n k", j=2), halves,
                                        big[:].rearrange("p (j n) -> p j n", j=2).unsqueeze(3).broadcast_to(
                                            [P, 2, BT * C, S]),
                                        ALU.subtract).then_inc(s["shifted_ready"], 1)
                dve.wait_ge(s["exp_ready"], n)
                nc.vector.tensor_reduce(rsum[:], shifted[:], X, ALU.add).then_inc(s["sum_ready"], 1)
                dve.wait_ge(s["sum_ready"], n)
                nc.vector.reciprocal(rinv[:], rsum[:]).then_inc(s["inv_ready"], 1)
                dve.wait_ge(s["inv_ready"], n)
                nc.vector.tensor_tensor(probs[:], shifted[:], rinv[:].unsqueeze(2).broadcast_to([P, BT * G, S]),
                                        ALU.mult).then_inc(s["probs_ready"], 1)
                dve.wait_ge(s["probs_ready"], n)
                nc.vector.transpose(probsT[:].rearrange("p a k -> p (a k)"),
                                    probs[:].rearrange("p a k -> p (a k)")).then_inc(s["probs_turned"], 1)
                dve.wait_ge(s["y_ready"], n)
                dve.wait_ge(s["x_biased"], n)
                nc.vector.tensor_tensor(x_tile, ps_y[:], x_plus_bo[:], ALU.add).then_inc(s["x_done"], 1)


def cross_attention(core, tag, w, mask=None, mask_type=None, bias_rows=None):
    nc = core.nc
    K2 = KEYS - 1
    with ExitStack() as ctx:
        def sb(name, shape, dt=F32):
            return ctx.enter_context(nc.sbuf_tensor(f"{tag}_{name}", shape, dt))

        def ps(name, shape):
            return ctx.enter_context(nc.psum_tensor(f"{tag}_{name}", shape, F32))

        s = semaphores(nc, tag, LN_SEMS + """ weights_loaded ctx_tail_loaded xn_turned xnT_ready q_ready
            qT_ready q_spread tail_copied tail_cleared tail_keys_ready tail_keys tail_values_ready tail_values tail_half
            tail_scores_ready tail_scores y_ready x_biased x_done mask_loaded mask_bias_ready mask_read""")
        per_batch = {k: [nc.alloc_semaphore(f"{tag}_{k}{b}") for b in range(BT)] for k in
                     """ctx_loaded ctx_used k_ready kT_ready v_ready v_kept scores_ready biased_ready row_ready max_ready
                     exp_ready inv_ready probs_turned_1 probs_turned probsT_1 probsT_2 o_ready o_kept oT_ready
                     oT_kept""".split()}
        wt = {k: sb(f"w{k}", [P, C, D]) for k in "qkv"}
        wo = sb("wo", [GD, HG, D])
        cols = {k: sb(k, [P, C]) for k in ("bq", "bk") if w.get(k)}
        rows = {k: sb(k, [P, D]) for k in ("bv", "bo") if w.get(k)}
        n_loads = 4 + len(cols) + len(rows) + (HG if bias_rows else 0)
        ctx_tail = sb("ctx_tail", [P, C, B])
        ctx_sb = sb("ctx_sb", [P, BT, C, K2])
        stats, mean, rstd = sb("stats", [P, 6]), sb("mean", [P, 2]), sb("rstd", [P, 1])
        xn, xnT, qT = sb("xn", [P, D]), sb("xnT", [P, C, P]), sb("qT", [P, C, P])
        q_by_head = sb("q_by_head", [P, C, BT, HG, S])
        tail_rep = sb("tail_rep", [P, C, BT, S])
        k_tail = sb("k_tail", [P, C, BT, 2])
        s_tail = sb("s_tail", [P, BT, G])
        v_tail = sb("v_tail", [P, D])
        kT = sb("kT", [P, 2, C, K2])
        v = sb("v", [P, BT, 2, D])
        scores = sb("scores", [P, BT, G, KEYS])
        n_bias = BT if mask else 1
        bias = sb("bias", [P, n_bias, KEYS]) if mask or bias_rows else None
        mask_raw = sb("mask_raw", [P, BT, KEYS], mask_type) if mask else None
        minus_big, rsum, rinv = sb("minus_big", [P, BT, G]), sb("rsum", [P, BT, G]), sb("rinv", [P, BT, G])
        probsT = sb("probsT", [P, 2, G, P])
        probsT_tail = sb("probsT_tail", [P, P])
        o = sb("o", [P, BT, G, HD])
        oT = sb("oT", [GD, HG, BT, S])
        x_plus_bo = sb("x_plus_bo", [P, D])
        ps_s = ps("ps_s", [P, 2, 2, K2])
        ps_k = ps("ps_k", [P, C, K2])
        ps_v = ps("ps_v", [P, 2, D])
        ps_p = ps("ps_p", [P, 2, G, P])
        ps_a = ps("ps_a", [P, 512])
        ps_o, ps_oT, ps_pt = ps_a[:, 0:256], ps_a[0:GD, 256:384], ps_a[:, 384:512]
        ps_b = ps("ps_b", [P, 512])
        ps_t, ps_vt = ps_b[:, 0:256], ps_b[:, 256:512]
        ident = core.table("ident")
        block = ctx.enter_context(nc.Block())

        def j_of(g):
            return (g % 2) * 2 + g // 2

        @block.sync
        def _(sp):
            for k in "qkv":
                sp.dma_start(wt[k][:], core.weight(w[k])).then_inc(s["weights_loaded"], 16)
            sp.dma_start(wo[:], core.inputs[w["o"]]).then_inc(s["weights_loaded"], 16)
            for k in cols:
                sp.dma_start(cols[k][:], core.column(w[k])).then_inc(s["weights_loaded"], 16)
            for k in rows:
                sp.dma_start(rows[k][:], core.rows(w[k])).then_inc(s["weights_loaded"], 16)
            if bias_rows:
                for h in range(HG):
                    sp.dma_start(bias[S * h:S * h + S, 0, :], core.inputs[bias_rows]).then_inc(
                        s["weights_loaded"], 16)
            sp.dma_start(ctx_tail[:], core.inputs["ctx_tail"].rearrange("(c p) b -> p c b", p=P)).then_inc(
                s["ctx_tail_loaded"], 16)
            context = core.inputs["ctx_T"].rearrange("(c p) (t b k) -> p t b c k", p=P, b=BT, k=KEYS)
            if mask:
                mask_rows = core.inputs[mask].rearrange("(t n) -> t n", n=BT * KEYS)
            with sp.Fori(0, NT) as i:
                if mask:
                    wait(sp, s["mask_read"], i + 1)
                    sp.dma_start(mask_raw[:].rearrange("p b k -> p (b k)"),
                                 mask_rows[bass.ds(i, 1), :].broadcast_to([P, BT * KEYS])).then_inc(s["mask_loaded"], 16)
                for b in range(BT):
                    wait(sp, per_batch["ctx_used"][b], i + 1)
                    sp.dma_start(ctx_sb[:, b], context[:, i, b, :, 0:K2]).then_inc(
                        per_batch["ctx_loaded"][b], 16)

        def after(engine, sem, count, alone=False):
            if isinstance(count, int) and count < 1:
                return
            if alone:
                wait(engine, sem, count)
            else:
                engine.wait_ge(sem, count)

        def all_tiles(engine, turn):
            turn(0, first=True, last=False)
            with engine.Fori(1, NT - 1) as i:
                turn(i, first=False, last=False)
            turn(NT - 1, first=False, last=True)

        def batch(t, n, first, last):
            if (t < 0 and first) or (t >= BT and last):
                return None
            return t % BT, n + t // BT

        @block.gpsimd
        def _(pool):
            pool.wait_ge(s["weights_loaded"], 16 * n_loads)
            pool.wait_ge(s["ctx_tail_loaded"], 16)
            if mask:
                pool.sem_inc(s["mask_read"], 1)

            def front(i, n):
                layer_norm_root(pool, nc, s, n, mean[:], rstd[:], core.table("minus_half"))
                after(pool, s["tail_values_ready"], n - 1)
                for c in range(C):
                    last = nc.gpsimd.tensor_copy(tail_rep[:, c], ctx_tail[:, c, bass.ds(i * BT, BT)].unsqueeze(2)
                                                 .broadcast_to([P, BT, S]))
                last.then_inc(s["tail_copied"], 1)

            def mask_bias(n):
                if mask:
                    after(pool, per_batch["biased_ready"][BT - 1], n - 1)
                    wait(pool, s["mask_loaded"], n * 16)
                    nc.gpsimd.tensor_scalar(bias[:], mask_raw[:], 0.0, MASKED, ALU.is_equal, ALU.mult).then_inc(
                        s["mask_bias_ready"], 1)
                    wait(pool, s["mask_bias_ready"], n)
                    pool.sem_inc(s["mask_read"], 1)

            def turn(i, first, last):
                n = i + 1
                if not last:
                    front(i + 1, n + 1)
                if "bo" in rows:
                    after(pool, s["x_done"], n - 1)
                    nc.gpsimd.tensor_tensor(x_plus_bo[:], core.x[:, i, :], rows["bo"][:], ALU.add).then_inc(
                        s["x_biased"], 1)
                if not last:
                    mask_bias(n + 1)

            front(0, 1)
            mask_bias(1)
            all_tiles(pool, turn)

        @block.tensor
        def _(pe):
            for b in range(BT):
                pe.sem_inc(per_batch["ctx_used"][b], 1)
            pe.wait_ge(s["weights_loaded"], 16 * n_loads)

            def turn_xn(n):
                after(pe, s["x_done"], n - 2)
                after(pe, s["tail_values"], n - 1)
                pe.wait_ge(s["xn_ready"], n)
                nc.tensor.transpose(ps_t[:, 0:P], xn[:, 0:P], ident)
                nc.tensor.transpose(ps_t[:, P:D], xn[:, P:D], ident).then_inc(s["xn_turned"], 1)

            def queries(n):
                pe.wait_ge(s["xnT_ready"], n)
                for oc in range(C):
                    for c in range(C):
                        last = nc.tensor.matmul(ps_t[:, oc * P:oc * P + P], wt["q"][:, c, oc * P:oc * P + P],
                                                xnT[:, c, :], start=(c == 0), stop=(c == C - 1))
                last.then_inc(s["q_ready"], 1)

            def tail_keys(n):
                pe.wait_ge(s["tail_copied"], n)
                pe.wait_ge(s["qT_ready"], n)
                for oc in range(C):
                    for c in range(C):
                        last = nc.tensor.matmul(ps_vt[:, oc * BT:oc * BT + BT], wt["k"][:, c, oc * P:oc * P + P],
                                                tail_rep[:, c, :, 0], start=(c == 0), stop=(c == C - 1))
                last.then_inc(s["tail_keys_ready"], 1)

            def tail_scores(n):
                pe.wait_ge(s["q_spread"], n)
                wait(pe, s["tail_keys"], n)
                for b in range(BT):
                    for c in range(C):
                        last = nc.tensor.matmul(ps_vt[:, (b * C + c) * 2:(b * C + c) * 2 + 2],
                                                q_by_head[:, c, b, :, :], k_tail[:, c, b, :], start=True, stop=True)
                last.then_inc(s["tail_scores_ready"], 1)

            def tail_values(n):
                pe.wait_ge(s["tail_scores"], n)
                for c in range(C):
                    last = nc.tensor.matmul(ps_vt, tail_rep[:, c, :, :], wt["v"][:, c, :],
                                            start=(c == 0), stop=(c == C - 1))
                last.then_inc(s["tail_values_ready"], 1)

            def keys_and_values(at, before):
                b, n = at
                pe.wait_ge(per_batch["ctx_loaded"][b], n * 16)
                if before:
                    pe.wait_ge(per_batch["kT_ready"][before[0]], before[1])
                for oc in range(C):
                    for c in range(C):
                        last = nc.tensor.matmul(ps_k[:, oc, :], wt["k"][:, c, oc * P:oc * P + P],
                                                ctx_sb[:, b, c, :], start=(c == 0), stop=(c == C - 1))
                last.then_inc(per_batch["k_ready"][b], 1)
                if before:
                    pe.wait_ge(per_batch["v_kept"][before[0]], before[1])
                for kc in range(2):
                    for c in range(C):
                        last = nc.tensor.matmul(ps_v[:, kc, :], ctx_sb[:, b, c, kc * P:kc * P + P],
                                                wt["v"][:, c, :], start=(c == 0), stop=(c == C - 1))
                last.then_inc(per_batch["v_ready"][b], 1)

            def score(at, before):
                b, n = at
                if before:
                    pe.wait_ge(per_batch["biased_ready"][before[0]], before[1])
                pe.wait_ge(s["q_spread"], n)
                wait(pe, per_batch["kT_ready"][b], n)
                for g in range(G):
                    rows_g = slice(GD * (g % 2), GD * (g % 2) + GD)
                    last = nc.tensor.matmul(ps_s[:, g % 2, g // 2, :], q_by_head[rows_g, g // 2, b, :, :],
                                            kT[rows_g, b % 2, g // 2, :], start=True, stop=True)
                last.then_inc(per_batch["scores_ready"][b], 1)

            def turn_probs(at, before):
                b, n = at
                pe.wait_ge(per_batch["exp_ready"][b], n)
                if before:
                    pe.wait_ge(per_batch["probsT_2"][before[0]], before[1])
                    pe.wait_ge(per_batch["probsT_1"][before[0]], before[1])
                for kc in range(2):
                    for j in range(G):
                        last = nc.tensor.transpose(ps_p[:, kc, j, :], scores[:, b, j, kc * P:kc * P + P], ident)
                    if kc == 0:
                        last.then_inc(per_batch["probs_turned_1"][b], 1)
                if before:
                    pe.wait_ge(per_batch["oT_kept"][before[0]], before[1])
                nc.tensor.matmul(ps_pt[S * b:S * b + G, :], scores[:, b, :, K2], ident, start=True,
                                 stop=True).then_inc(per_batch["probs_turned"][b], 1)

            def outputs(at):
                b, n = at
                pe.wait_ge(s["tail_values"], n)
                pe.wait_ge(per_batch["v_kept"][b], n)
                pe.wait_ge(per_batch["probsT_1"][b], n)
                wait(pe, per_batch["probsT_2"][b], n)
                nc.tensor.matmul(ps_o, probsT_tail[S * b:S * b + G, :], v_tail[S * b:S * b + G, :],
                                 start=True, stop=False, skip_group_check=True, tile_position=(S * b, 0))
                for g in range(G):
                    for kc in range(2):
                        last = nc.tensor.matmul(ps_o[:, g * GD:g * GD + GD], probsT[:, kc, j_of(g), :],
                                                v[:, b, kc, g * GD:g * GD + GD], start=False,
                                                stop=(kc == 1), skip_group_check=True)
                last.then_inc(per_batch["o_ready"][b], 1)

            def turn_outputs(at):
                b, n = at
                wait(pe, per_batch["o_kept"][b], n)
                nc.tensor.transpose(ps_oT, o[:, b].rearrange("p g d -> p (g d)"), ident).then_inc(
                    per_batch["oT_ready"][b], 1)

            def tile_output(n):
                pe.wait_ge(per_batch["oT_kept"][BT - 1], n)
                for h in range(HG):
                    last = nc.tensor.matmul(ps_t, oT[:, h, :, :], wo[:, h, :], start=(h == 0), stop=(h == HG - 1))
                last.then_inc(s["y_ready"], 1)

            def turn(i, first, last):
                n = i + 1
                for t in range(BT):
                    now, before, ahead, ahead2 = (batch(t + k, n, first, last) for k in (0, -1, 1, 2))
                    if ahead:
                        score(ahead, now)
                    if before:
                        turn_outputs(before)
                    if t == 0:
                        tail_values(n)
                    if not last and t == 1:
                        turn_xn(n + 1)
                    if not last and t == 2:
                        tail_keys(n + 1)
                    if not last and t == 3:
                        tail_scores(n + 1)
                    turn_probs(now, before)
                    if ahead2:
                        keys_and_values(ahead2, ahead)
                        wait(pe, per_batch["v_ready"][ahead2[0]], ahead2[1])
                        pe.sem_inc(per_batch["ctx_used"][ahead2[0]], 1)
                    if not last and t == 1:
                        queries(n + 1)
                    if not first and t == 0:
                        wait(pe, s["tail_values"], n)
                        tile_output(n - 1)
                    outputs(now)

            keys_and_values((0, 1), None)
            keys_and_values((1, 1), (0, 1))
            for b in range(2):
                wait(pe, per_batch["v_ready"][b], 1)
                pe.sem_inc(per_batch["ctx_used"][b], 1)
            turn_xn(1)
            queries(1)
            tail_keys(1)
            score((0, 1), None)
            tail_scores(1)
            all_tiles(pe, turn)
            turn_outputs((BT - 1, NT))
            tile_output(NT)

        @block.scalar
        def _(act):
            act.wait_ge(s["weights_loaded"], 16 * n_loads)
            nc.scalar.activation(k_tail[:], core.table("iota")[:, 0:C * BT * 2], ACT.Copy, scale=0.0).then_inc(s["tail_cleared"], 1)
            act.wait_ge(s["tail_cleared"], 1)

            def keep_xnT(n):
                act.wait_ge(s["xn_turned"], n)
                nc.scalar.copy(xnT[:].rearrange("p c n -> p (c n)"), ps_t).then_inc(s["xnT_ready"], 1)

            def keep_q(n):
                act.wait_ge(s["q_ready"], n)
                for c in range(C):
                    if "bq" in cols:
                        last = nc.scalar.activation(qT[:, c, :], ps_t[:, c * P:c * P + P], ACT.Identity,
                                                    bias=cols["bq"][:, c:c + 1])
                    else:
                        last = nc.scalar.copy(qT[:, c, :], ps_t[:, c * P:c * P + P])
                last.then_inc(s["qT_ready"], 1)

            def keep_tail_keys(n):
                act.wait_ge(s["tail_keys_ready"], n)
                for c in range(C):
                    for half in range(2):
                        at = slice(GD * half, GD * half + GD)
                        if "bk" in cols:
                            last = nc.scalar.activation(k_tail[at, c, :, half], ps_vt[at, c * BT:c * BT + BT],
                                                        ACT.Identity, bias=cols["bk"][at, c:c + 1])
                        else:
                            last = nc.scalar.copy(k_tail[at, c, :, half], ps_vt[at, c * BT:c * BT + BT])
                last.then_inc(s["tail_keys"], 1)

            def keep_keys(at, used):
                b, n = at
                act.wait_ge(per_batch["k_ready"][b], n)
                if used:
                    act.wait_ge(per_batch["scores_ready"][used[0]], used[1])
                for c in range(C):
                    if "bk" in cols:
                        last = nc.scalar.activation(kT[:, b % 2, c, :], ps_k[:, c, :], ACT.Identity,
                                                    bias=cols["bk"][:, c:c + 1])
                    else:
                        last = nc.scalar.copy(kT[:, b % 2, c, :], ps_k[:, c, :])
                last.then_inc(per_batch["kT_ready"][b], 1)

            def exps(at):
                b, n = at
                act.wait_ge(per_batch["max_ready"][b], n)
                for j in range(G):
                    last = nc.scalar.activation(scores[:, b, j, :], scores[:, b, j, :], ACT.Exp,
                                                bias=minus_big[:, b, j:j + 1], accum_out=rsum[:, b, j:j + 1])
                last.then_inc(per_batch["exp_ready"][b], 1)

            def keep_probs(at, before):
                b, n = at
                act.wait_ge(per_batch["probs_turned_1"][b], n)
                if before:
                    act.wait_ge(per_batch["o_ready"][before[0]], before[1])
                nc.scalar.copy(probsT[:, 0], ps_p[:, 0]).then_inc(per_batch["probsT_1"][b], 1)

            def keep_outputs(at):
                b, n = at
                if b == 0:
                    after(act, s["y_ready"], n - 1)
                act.wait_ge(per_batch["oT_ready"][b], n)
                nc.scalar.copy(oT[:, :, b, :], ps_oT.rearrange("p (h q) -> p h q", h=HG)).then_inc(
                    per_batch["oT_kept"][b], 1)

            def turn(i, first, last):
                n = i + 1
                for t in range(BT):
                    now, before, ahead, ahead2 = (batch(t + k, n, first, last) for k in (0, -1, 1, 2))
                    if before:
                        keep_outputs(before)
                    if not last and t == 1:
                        keep_xnT(n + 1)
                    if not last and t == 2:
                        keep_tail_keys(n + 1)
                    keep_probs(now, before)
                    if ahead:
                        exps(ahead)
                    if ahead2:
                        keep_keys(ahead2, now)
                    if not last and t == 1:
                        keep_q(n + 1)

            keep_keys((0, 1), None)
            keep_keys((1, 1), None)
            keep_xnT(1)
            keep_q(1)
            keep_tail_keys(1)
            exps((0, 1))
            all_tiles(act, turn)
            keep_outputs((BT - 1, NT))

        @block.vector
        def _(dve):
            dve.wait_ge(s["weights_loaded"], 16 * n_loads)

            def norm_stats(i, n):
                nc.vector.bn_stats(stats[:], core.x[:, i, :]).then_inc(s["stats_ready"], 1)
                wait(dve, s["stats_ready"], n)
                nc.vector.bn_aggr(mean[:], stats[:]).then_inc(s["mean_ready"], 1)

            def normed(i, n):
                dve.wait_ge(s["rstd_ready"], n)
                nc.vector.tensor_scalar(xn[:], core.x[:, i, :], mean[:, 0:1], rstd[:], ALU.subtract,
                                        ALU.mult).then_inc(s["xn_ready"], 1)

            def spread_q(n):
                dve.wait_ge(s["qT_ready"], n)
                after(dve, per_batch["scores_ready"][BT - 1], n - 1)
                for c in range(C):
                    last = nc.vector.tensor_tensor(
                        q_by_head[:, c], qT[:, c, :].rearrange("p (b q) -> p b q", b=BT).unsqueeze(2).broadcast_to(
                            [P, BT, HG, S]),
                        core.table("head_of_feature").unsqueeze(1).unsqueeze(3).broadcast_to([P, BT, HG, S]),
                        ALU.mult)
                last.then_inc(s["q_spread"], 1)

            def keep_tail_scores(n):
                if mask:
                    dve.wait_ge(s["mask_bias_ready"], n)
                dve.wait_ge(s["tail_scores_ready"], n)
                raw = ps_vt[:, 0:BT * G].rearrange("p (b c j) -> p b j c", b=BT, j=2)
                kept = s_tail[:].rearrange("p b (j c) -> p b j c", j=2)
                if bias is None:
                    last = nc.vector.tensor_copy(kept, raw)
                else:
                    of_tail = bias[:, :, K2:KEYS] if mask else bias[:, 0:1, K2:KEYS].broadcast_to([P, BT, 1])
                    last = nc.vector.tensor_tensor(kept, raw, of_tail.unsqueeze(3).broadcast_to([P, BT, 2, C]),
                                                   ALU.add)
                last.then_inc(s["tail_scores"], 1)

            def keep_tail_values(n):
                dve.wait_ge(s["tail_values_ready"], n)
                after(dve, per_batch["o_ready"][BT - 1], n - 1)
                if "bv" in rows:
                    nc.vector.tensor_tensor(v_tail[:], ps_vt, rows["bv"][:], ALU.add).then_inc(s["tail_half"], 1)
                else:
                    nc.vector.tensor_copy(v_tail[:], ps_vt).then_inc(s["tail_half"], 1)
                dve.wait_ge(s["tail_half"], n)
                nc.vector.tensor_tensor(v_tail[:], v_tail[:], core.table("group_rows"), ALU.mult).then_inc(
                    s["tail_values"], 1)

            def maxima(at):
                b, n = at
                dve.wait_ge(per_batch["scores_ready"][b], n)
                after(dve, per_batch["probs_turned"][b], n - 1)
                nc.vector.tensor_tensor(
                    scores[:, b, :, 0:K2], ps_s[:].rearrange("p j c k -> p (j c) k"),
                    bias[:, b if mask else 0, 0:K2].unsqueeze(1).broadcast_to([P, G, K2]), ALU.add).then_inc(
                        per_batch["biased_ready"][b], 1)
                dve.wait_ge(s["tail_scores"], n)
                nc.vector.tensor_copy(scores[:, b, :, K2], s_tail[:, b, :]).then_inc(per_batch["row_ready"][b], 1)
                dve.wait_ge(per_batch["biased_ready"][b], n)
                dve.wait_ge(per_batch["row_ready"][b], n)
                nc.vector.tensor_reduce(minus_big[:, b, :], scores[:, b], X, ALU.max, negate=True).then_inc(
                    per_batch["max_ready"][b], 1)

            def keep_values(at):
                b, n = at
                dve.wait_ge(per_batch["v_ready"][b], n)
                after(dve, per_batch["o_ready"][b], n - 1)
                if "bv" in rows:
                    last = nc.vector.tensor_tensor(v[:, b], ps_v[:], rows["bv"][:].unsqueeze(1).broadcast_to(
                        [P, 2, D]), ALU.add)
                else:
                    last = nc.vector.tensor_copy(v[:, b], ps_v[:])
                last.then_inc(per_batch["v_kept"][b], 1)

            def keep_probs(at, before):
                b, n = at
                dve.wait_ge(per_batch["probs_turned"][b], n)
                if before:
                    dve.wait_ge(per_batch["o_ready"][before[0]], before[1])
                nc.vector.tensor_copy(probsT_tail[S * b:S * b + G, :], ps_pt[S * b:S * b + G, :])
                nc.vector.tensor_copy(probsT[:, 1], ps_p[:, 1]).then_inc(per_batch["probsT_2"][b], 1)

            def keep_outputs(at):
                b, n = at
                dve.wait_ge(per_batch["exp_ready"][b], n)
                nc.vector.reciprocal(rinv[:, b, :], rsum[:, b, :]).then_inc(per_batch["inv_ready"][b], 1)
                dve.wait_ge(per_batch["o_ready"][b], n)
                dve.wait_ge(per_batch["inv_ready"][b], n)
                for h in range(HG):
                    at_h = slice(S * h, S * h + S)
                    last = nc.vector.tensor_tensor(
                        o[at_h, b].rearrange("p (c j) d -> p c j d", j=2),
                        ps_o[at_h, :].rearrange("p (c j h d) -> p c j h d", c=C, j=2, h=HG)[:, :, :, h, :],
                        rinv[at_h, b, :].rearrange("p (j c) -> p c j", j=2).unsqueeze(3).broadcast_to(
                            [S, C, 2, HD]), ALU.mult)
                last.then_inc(per_batch["o_kept"][b], 1)

            def add_output(i, n):
                dve.wait_ge(s["y_ready"], n)
                if "bo" in rows:
                    dve.wait_ge(s["x_biased"], n)
                    nc.vector.tensor_tensor(core.x[:, i, :], ps_t, x_plus_bo[:], ALU.add).then_inc(s["x_done"], 1)
                else:
                    nc.vector.tensor_tensor(core.x[:, i, :], ps_t, core.x[:, i, :], ALU.add).then_inc(s["x_done"], 1)

            def turn(i, first, last):
                n = i + 1
                for t in range(BT):
                    now, before, ahead, ahead2 = (batch(t + k, n, first, last) for k in (0, -1, 1, 2))
                    if before:
                        keep_outputs(before)
                    if not last and t == 0:
                        norm_stats(i + 1, n + 1)
                    if not last and t == 3:
                        keep_tail_scores(n + 1)
                    if ahead:
                        maxima(ahead)
                    if t == 0:
                        keep_tail_values(n)
                    keep_probs(now, before)
                    if not last and t == 2:
                        spread_q(n + 1)
                    if ahead2:
                        keep_values(ahead2)
                    if not first and t == 0:
                        add_output(i - 1, n - 1)
                    if not last and t == 0:
                        normed(i + 1, n + 1)

            norm_stats(0, 1)
            normed(0, 1)
            keep_values((0, 1))
            keep_values((1, 1))
            spread_q(1)
            keep_tail_scores(1)
            maxima((0, 1))
            all_tiles(dve, turn)
            keep_outputs((BT - 1, NT))
            add_output(NT - 1, NT)


def complex_attention(core, tag, w):
    nc = core.nc
    E = 2 * D
    CE = E // P
    scale = 1.0 / np.sqrt(D)
    with ExitStack() as ctx:
        def sb(name, shape, dt=F32):
            return ctx.enter_context(nc.sbuf_tensor(f"{tag}_{name}", shape, dt))

        def ps(name, shape):
            return ctx.enter_context(nc.psum_tensor(f"{tag}_{name}", shape, F32))

        s = semaphores(nc, tag, LN_SEMS + """ weights_loaded cleared xn_turned xnT_ready q_ready k_ready v_ready
            qT_ready kT_ready v_kept scores_ready max_ready bias_ready exp_ready inv_ready probs_ready probs_turned
            o_ready oT_ready y_ready x_biased x_done""")
        wt = {k: sb(f"w{k}", [P, C, E]) for k in "qkv"}
        wo = sb("wo", [P, CE, D])
        cols = {k: sb(k, [P, CE]) for k in ("bq", "bk", "bv")}
        bo = sb("bo", [P, D])
        stats, mean, rstd = sb("stats", [P, 6]), sb("mean", [P, 2]), sb("rstd", [P, 1])
        xn, xnT = sb("xn", [P, D]), sb("xnT", [P, C, P])
        qT, kT, v = sb("qT", [P, CE, P]), sb("kT", [P, CE, P]), sb("v", [P, E])
        big, minus_big = sb("big", [P, 1]), sb("minus_big", [P, 1])
        rsum, rinv = sb("rsum", [P, 1]), sb("rinv", [P, 1])
        probs, probsT = sb("probs", [P, S]), sb("probsT", [P, P])
        oT = sb("oT", [P, CE, P])
        x_plus_bo = sb("x_plus_bo", [P, D])
        ps_t, ps_q, ps_k = ps("ps_t", [P, D]), ps("ps_q", [P, CE, P]), ps("ps_k", [P, CE, P])
        ps_v, ps_s, ps_o, ps_y = ps("ps_v", [P, E]), ps("ps_s", [P, S]), ps("ps_o", [P, CE, P]), ps("ps_y", [P, D])
        ident = core.table("ident")
        block = ctx.enter_context(nc.Block())

        @block.sync
        def _(sp):
            for k in "qkv":
                sp.dma_start(wt[k][:], core.weight(w[k])).then_inc(s["weights_loaded"], 16)
            sp.dma_start(wo[:], core.weight(w["o"])).then_inc(s["weights_loaded"], 16)
            for k in cols:
                sp.dma_start(cols[k][:], core.column(w[k])).then_inc(s["weights_loaded"], 16)
            sp.dma_start(bo[:], core.rows(w["bo"])).then_inc(s["weights_loaded"], 16)

        @block.gpsimd
        def _(pool):
            pool.wait_ge(s["weights_loaded"], 16 * 8)
            with pool.Fori(0, NT) as i:
                layer_norm_root(pool, nc, s, i + 1, mean[:], rstd[:], core.table("minus_half"))
                pool.wait_ge(s["x_done"], i + 1)
                nc.gpsimd.tensor_tensor(x_plus_bo[:], core.x[:, i, :], bo[:], ALU.add).then_inc(s["x_biased"], 1)

        @block.tensor
        def _(pe):
            pe.wait_ge(s["weights_loaded"], 16 * 8)
            with pe.Fori(0, NT) as i:
                n = i + 1
                pe.wait_ge(s["xn_ready"], n)
                for c in range(C):
                    last = nc.tensor.transpose(ps_t[:, c * P:c * P + P], xn[:, c * P:c * P + P], ident)
                last.then_inc(s["xn_turned"], 1)
                pe.wait_ge(s["xnT_ready"], n)
                for k, dst in (("q", ps_q), ("k", ps_k)):
                    for oc in range(CE):
                        for c in range(C):
                            last = nc.tensor.matmul(dst[:, oc, :], wt[k][:, c, oc * P:oc * P + P], xnT[:, c, :],
                                                    start=(c == 0), stop=(c == C - 1))
                    last.then_inc(s[k + "_ready"], 1)
                for c in range(C):
                    last = nc.tensor.matmul(ps_v[:], xnT[:, c, :], wt["v"][:, c, :], start=(c == 0), stop=(c == C - 1))
                last.then_inc(s["v_ready"], 1)
                pe.wait_ge(s["qT_ready"], n)
                wait(pe, s["kT_ready"], n)
                for b in range(BT):
                    at = slice(S * b, S * b + S)
                    for c in range(CE):
                        last = nc.tensor.matmul(ps_s[at, :], qT[:, c, at], kT[:, c, at],
                                                start=(c == 0), stop=(c == CE - 1))
                last.then_inc(s["scores_ready"], 1)
                pe.wait_ge(s["v_kept"], n)
                pe.wait_ge(s["probs_turned"], n)
                for c in range(CE):
                    last = nc.tensor.matmul(ps_o[:, c, :], v[:, c * P:c * P + P], probsT[:], start=True, stop=True)
                last.then_inc(s["o_ready"], 1)
                pe.wait_ge(s["oT_ready"], n)
                for c in range(CE):
                    last = nc.tensor.matmul(ps_y[:], oT[:, c, :], wo[:, c, :], start=(c == 0), stop=(c == CE - 1))
                last.then_inc(s["y_ready"], 1)

        @block.scalar
        def _(act):
            act.wait_ge(s["weights_loaded"], 16 * 8)
            with act.Fori(0, NT) as i:
                n = i + 1
                act.wait_ge(s["xn_turned"], n)
                nc.scalar.copy(xnT[:].rearrange("p c n -> p (c n)"), ps_t[:]).then_inc(s["xnT_ready"], 1)
                for k, dst, src in (("q", qT, ps_q), ("k", kT, ps_k)):
                    act.wait_ge(s[k + "_ready"], n)
                    for c in range(CE):
                        last = nc.scalar.activation(dst[:, c, :], src[:, c, :], ACT.Identity,
                                                    bias=cols["b" + k][:, c:c + 1])
                    last.then_inc(s[k + "T_ready"], 1)
                act.wait_ge(s["bias_ready"], n)
                nc.scalar.activation(probs[:], ps_s[:], ACT.Exp, bias=minus_big[:], scale=float(scale),
                                     accum_out=rsum[:]).then_inc(s["exp_ready"], 1)
                act.wait_ge(s["o_ready"], n)
                for c in range(CE):
                    last = nc.scalar.activation(oT[:, c, :], ps_o[:, c, :], ACT.Identity, bias=cols["bv"][:, c:c + 1])
                last.then_inc(s["oT_ready"], 1)

        @block.vector
        def _(dve):
            dve.sem_inc(s["x_done"], 1)
            nc.vector.memset(probsT[:], 0.0).then_inc(s["cleared"], 1)
            dve.wait_ge(s["cleared"], 1)
            with dve.Fori(0, NT) as i:
                n = i + 1
                x_tile = core.x[:, i, :]
                layer_norm(dve, nc, s, n, x_tile, xn[:], stats[:], mean[:], rstd[:])
                dve.wait_ge(s["v_ready"], n)
                nc.vector.tensor_copy(v[:], ps_v[:]).then_inc(s["v_kept"], 1)
                dve.wait_ge(s["scores_ready"], n)
                nc.vector.tensor_reduce(big[:], ps_s[:], X, ALU.max, negate=True).then_inc(s["max_ready"], 1)
                dve.wait_ge(s["max_ready"], n)
                nc.vector.tensor_scalar(minus_big[:], big[:], float(scale), None, ALU.mult).then_inc(s["bias_ready"], 1)
                dve.wait_ge(s["exp_ready"], n)
                nc.vector.reciprocal(rinv[:], rsum[:]).then_inc(s["inv_ready"], 1)
                dve.wait_ge(s["inv_ready"], n)
                nc.vector.tensor_scalar(probs[:], probs[:], rinv[:], None, ALU.mult).then_inc(s["probs_ready"], 1)
                dve.wait_ge(s["probs_ready"], n)
                for b in range(BT):
                    at = slice(S * b, S * b + S)
                    last = nc.vector.transpose(probsT[at, at], probs[at, :])
                last.then_inc(s["probs_turned"], 1)
                dve.wait_ge(s["y_ready"], n)
                dve.wait_ge(s["x_biased"], n)
                nc.vector.tensor_tensor(x_tile, ps_y[:], x_plus_bo[:], ALU.add).then_inc(s["x_done"], 1)


SEL = 2 * S


def gated_cross_attention(core, tag):
    nc = core.nc
    K2 = KEYS - 1
    scale = float(1.0 / np.sqrt(D))
    w = "L0_xattn_"
    with ExitStack() as ctx:
        def sb(name, shape, dt=F32):
            return ctx.enter_context(nc.sbuf_tensor(f"{tag}_{name}", shape, dt))

        def ps(name):
            return ctx.enter_context(nc.psum_tensor(f"{tag}_{name}", [P, 512], F32))

        s = semaphores(nc, tag, LN_SEMS + """ weights_loaded cleared ctx_loaded ctx_used xn_turned xnT_ready
            qk_ready qkT_ready v_ready v_kept folded_ready folded_kept sel_ready sel_kept s1_ready max1_ready
            shift1_ready bias1_ready exp1_ready inv1_ready probs1_turned probs1T_ready pc_ready pcT_ready c2s_ready
            c2s_kept s2_ready max2_ready bias2_ready exp2_ready inv2_ready probs2_ready ip_ready ip_kept s2c_ready
            s2c_kept diff_ready gate_in_turned gate_in_ready z_ready z_kept e_ready one_plus gate_ready mixed x_plus
            x_done""")
        names = ("Wq_c_T", "Wk_c_T", "Wv_c_T", "Wk_s", "Wv_s_T", "Wq_s_T")
        wt = {k: sb(k, [P, C, D]) for k in names}
        wg = sb("wg", [P, 2 * C, D])
        cols = {k: sb(k, [P, C]) for k in ("bq_c", "bk_c", "bk_s", "bq_s")}
        rows = {k: sb(k, [P, D]) for k in ("bv_c", "bv_s", "bg")}
        n_loads = len(names) + 1 + len(cols) + len(rows)
        ctxT = sb("ctxT", [P, C, BT, KEYS])
        ctx_rows = sb("ctx_rows", [P, BT, 2, D])
        ctx_last = sb("ctx_last", [1, BT, D])
        ctx_sel = sb("ctx_sel", [P, C, BT * SEL])
        stats, mean, rstd = sb("stats", [P, 6]), sb("mean", [P, 2]), sb("rstd", [P, 1])
        xn, xnT = sb("xn", [P, D]), sb("xnT", [P, C, P])
        qT, kT, v = sb("qT", [P, C, P]), sb("kT", [P, C, P]), sb("v", [P, D])
        folded = sb("folded", [P, C, P])
        q_bk = sb("q_bk", [P, 1])
        selT = sb("selT", [P, C, BT * SEL])
        big1, sum1, bias1, rsum1, rinv1 = (sb(k, [P, 1]) for k in ("big1", "sum1", "bias1", "rsum1", "rinv1"))
        probs1, probs1T = sb("probs1", [P, KEYS]), sb("probs1T", [P, 3, P])
        pcT = sb("pcT", [P, C, P])
        c2s, s2c = sb("c2s", [P, D]), sb("s2c", [P, D])
        big2, bias2, rsum2, rinv2 = (sb(k, [P, 2]) for k in ("big2", "bias2", "rsum2", "rinv2"))
        probs2 = sb("probs2", [P, 2, S])
        ip = sb("ip", [P, P])
        gate_in = sb("gate_in", [P, 2 * C, P])
        z, e, diff = sb("z", [P, D]), sb("e", [P, D]), sb("diff", [P, D])
        ps_t, ps_qk, ps_s1, ps_v, ps_f, ps_sel, ps_x, ps_y = (ps(f"bank{k}") for k in range(8))
        ident = core.table("ident")
        block = ctx.enter_context(nc.Block())

        @block.sync
        def _(sp):
            for k in names:
                sp.dma_start(wt[k][:], core.weight(w + k)).then_inc(s["weights_loaded"], 16)
            sp.dma_start(wg[:], core.weight(w + "Wg_T")).then_inc(s["weights_loaded"], 16)
            for k in cols:
                sp.dma_start(cols[k][:], core.column(w + k)).then_inc(s["weights_loaded"], 16)
            for k in rows:
                sp.dma_start(rows[k][:], core.rows(w + k)).then_inc(s["weights_loaded"], 16)
            by_feature = core.inputs["ctx_T"].rearrange("(c p) (t n) -> p t c n", p=P, n=BT * KEYS)
            by_row = core.inputs["ctx"].rearrange("(t b) k d -> t b k d", b=BT)
            selected = core.inputs["ctx_sel_T"].rearrange("(c p) (t n) -> p t c n", p=P, n=BT * SEL)
            with sp.Fori(0, NT) as i:
                wait(sp, s["ctx_used"], i + 1)
                for c in range(C):
                    sp.dma_start(ctxT[:, c].rearrange("p b k -> p (b k)"), by_feature[:, i, c, :]).then_inc(
                        s["ctx_loaded"], 16)
                    sp.dma_start(ctx_sel[:, c, :], selected[:, i, c, :]).then_inc(s["ctx_loaded"], 16)
                for b in range(BT):
                    sp.dma_start(ctx_rows[:, b], by_row[i, b, 0:K2, :].rearrange("(k p) d -> p k d", p=P)).then_inc(
                        s["ctx_loaded"], 16)
                sp.dma_start(ctx_last[:], by_row[bass.ds(i, 1), :, K2, :]).then_inc(s["ctx_loaded"], 16)

        @block.gpsimd
        def _(pool):
            with pool.Fori(0, NT) as i:
                layer_norm_root(pool, nc, s, i + 1, mean[:], rstd[:], core.table("minus_half"))

        @block.tensor
        def _(pe):
            pe.sem_inc(s["ctx_used"], 1)
            pe.wait_ge(s["weights_loaded"], 16 * n_loads)
            with pe.Fori(0, NT) as i:
                n = i + 1
                n_ctx = n * (16 * (2 * C + BT + 1))

                def product(dst, lhsT, rhs, count=C):
                    for c in range(count):
                        last = nc.tensor.matmul(dst, lhsT(c), rhs(c), start=(c == 0), stop=(c == count - 1))
                    return last

                def chunk(oc):
                    return slice(oc * P, oc * P + P)

                pe.wait_ge(s["xn_ready"], n)
                for c in range(C):
                    last = nc.tensor.transpose(ps_t[:, chunk(c)], xn[:, chunk(c)], ident)
                last.then_inc(s["xn_turned"], 1)
                pe.wait_ge(s["ctx_loaded"], n_ctx)
                for oc in range(C):
                    last = product(ps_sel[:, oc * 256:oc * 256 + 256], lambda c: wt["Wq_s_T"][:, c, chunk(oc)],
                                   lambda c: ctx_sel[:, c, :])
                last.then_inc(s["sel_ready"], 1)
                pe.wait_ge(s["xnT_ready"], n)
                for a, k in enumerate(("Wq_c_T", "Wk_c_T")):
                    for oc in range(C):
                        last = product(ps_qk[:, chunk(2 * a + oc)], lambda c: wt[k][:, c, chunk(oc)],
                                       lambda c: xnT[:, c, :])
                last.then_inc(s["qk_ready"], 1)
                product(ps_v[:, 0:D], lambda c: xnT[:, c, :], lambda c: wt["Wv_c_T"][:, c, :]).then_inc(s["v_ready"], 1)
                pe.wait_ge(s["qkT_ready"], n)
                for oc in range(C):
                    product(ps_f[:, chunk(oc)], lambda c: wt["Wk_s"][:, c, chunk(oc)], lambda c: qT[:, c, :])
                product(ps_f[:, D:D + 1], lambda c: qT[:, c, :], lambda c: cols["bk_s"][:, c:c + 1]).then_inc(
                    s["folded_ready"], 1)
                wait(pe, s["sel_kept"], n)
                for b in range(BT):
                    last = product(ps_x[64 * (b % 2):64 * (b % 2) + 64, S * (b // 2):S * (b // 2) + S],
                                   lambda c: selT[:, c, SEL * b:SEL * b + SEL], lambda c: kT[:, c, S * b:S * b + S])
                last.then_inc(s["s2_ready"], 1)
                wait(pe, s["folded_kept"], n)
                for b in range(BT):
                    at = slice(S * b, S * b + S)
                    last = product(ps_s1[at, 0:KEYS], lambda c: folded[:, c, at], lambda c: ctxT[:, c, b, :])
                last.then_inc(s["s1_ready"], 1)
                wait(pe, s["probs2_ready"], n)
                for b in range(BT):
                    half = slice(64 * (b % 2), 64 * (b % 2) + 64)
                    last = nc.tensor.matmul((ps_x if b % 2 == 0 else ps_y)[S * b:S * b + S, 0:S],
                                            probs2[half, b // 2, :], core.table("interpolate")[half, :],
                                            start=True, stop=True)
                last.then_inc(s["ip_ready"], 1)
                pe.wait_ge(s["v_kept"], n)
                pe.wait_ge(s["ip_kept"], n)
                nc.tensor.matmul(ps_v[:, 0:D], ip[:], v[:], start=True, stop=True).then_inc(s["s2c_ready"], 1)
                pe.wait_ge(s["exp1_ready"], n)
                for kc in range(2):
                    nc.tensor.transpose(ps_qk[:, chunk(kc)], probs1[:, chunk(kc)], ident)
                nc.tensor.transpose(ps_qk[0:1, chunk(2)], probs1[:, K2:KEYS], ident).then_inc(s["probs1_turned"], 1)
                wait(pe, s["probs1T_ready"], n)
                for oc in range(C):
                    for b in range(BT):
                        at = slice(S * b, S * b + S)
                        dst = ps_f[:, oc * P + S * b:oc * P + S * b + S]
                        for kc in range(2):
                            nc.tensor.matmul(dst, ctx_rows[:, b, kc, chunk(oc)], probs1T[:, kc, at],
                                             start=(kc == 0), stop=False)
                        last = nc.tensor.matmul(dst, ctx_last[0:1, b, chunk(oc)], probs1T[0:1, 2, at],
                                                start=False, stop=True)
                last.then_inc(s["pc_ready"], 1)
                pe.wait_ge(s["pcT_ready"], n)
                pe.sem_inc(s["ctx_used"], 1)
                product(ps_t[:, 0:D], lambda c: pcT[:, c, :], lambda c: wt["Wv_s_T"][:, c, :]).then_inc(
                    s["c2s_ready"], 1)
                pe.wait_ge(s["s2c_kept"], n)
                pe.wait_ge(s["c2s_kept"], n)
                for c in range(C):
                    nc.tensor.transpose(ps_sel[:, chunk(c)], c2s[:, chunk(c)], ident)
                for c in range(C):
                    last = nc.tensor.transpose(ps_sel[:, chunk(C + c)], s2c[:, chunk(c)], ident)
                last.then_inc(s["gate_in_turned"], 1)
                pe.wait_ge(s["gate_in_ready"], n)
                product(ps_x[:, 0:D], lambda c: gate_in[:, c, :], lambda c: wg[:, c, :], 2 * C).then_inc(
                    s["z_ready"], 1)
                pe.wait_ge(s["z_kept"], n)

        @block.scalar
        def _(act):
            act.wait_ge(s["weights_loaded"], 16 * n_loads)
            with act.Fori(0, NT) as i:
                n = i + 1

                def with_bias(dst, src, column):
                    return nc.scalar.activation(dst, src, ACT.Identity, bias=column)

                act.wait_ge(s["xn_turned"], n)
                nc.scalar.copy(xnT[:].rearrange("p c n -> p (c n)"), ps_t[:, 0:D]).then_inc(s["xnT_ready"], 1)
                act.wait_ge(s["sel_ready"], n)
                for c in range(C):
                    last = with_bias(selT[:, c, :], ps_sel[:, c * 256:c * 256 + 256], cols["bq_s"][:, c:c + 1])
                last.then_inc(s["sel_kept"], 1)
                act.wait_ge(s["qk_ready"], n)
                for a, (dst, k) in enumerate(((qT, "bq_c"), (kT, "bk_c"))):
                    for c in range(C):
                        last = with_bias(dst[:, c, :], ps_qk[:, (2 * a + c) * P:(2 * a + c + 1) * P],
                                         cols[k][:, c:c + 1])
                last.then_inc(s["qkT_ready"], 1)
                act.wait_ge(s["folded_ready"], n)
                nc.scalar.copy(q_bk[:], ps_f[:, D:D + 1])
                nc.scalar.copy(folded[:].rearrange("p c n -> p (c n)"), ps_f[:, 0:D]).then_inc(s["folded_kept"], 1)
                act.wait_ge(s["bias2_ready"], n)
                for j in range(2):
                    last = nc.scalar.activation(probs2[:, j, :], ps_x[:, S * j:S * j + S], ACT.Exp, scale=scale,
                                                bias=bias2[:, j:j + 1], accum_out=rsum2[:, j:j + 1])
                last.then_inc(s["exp2_ready"], 1)
                act.wait_ge(s["bias1_ready"], n)
                nc.scalar.activation(probs1[:], ps_s1[:, 0:KEYS], ACT.Exp, scale=scale, bias=bias1[:],
                                     accum_out=rsum1[:]).then_inc(s["exp1_ready"], 1)
                act.wait_ge(s["probs1_turned"], n)
                nc.scalar.copy(probs1T[:, 0:2].rearrange("p k n -> p (k n)"), ps_qk[:, 0:2 * P])
                nc.scalar.copy(probs1T[0:1, 2, :], ps_qk[0:1, 2 * P:3 * P]).then_inc(s["probs1T_ready"], 1)
                act.wait_ge(s["pc_ready"], n)
                nc.scalar.copy(pcT[:].rearrange("p c n -> p (c n)"), ps_f[:, 0:D]).then_inc(s["pcT_ready"], 1)
                act.wait_ge(s["gate_in_turned"], n)
                nc.scalar.copy(gate_in[:].rearrange("p c n -> p (c n)"), ps_sel[:]).then_inc(s["gate_in_ready"], 1)
                act.wait_ge(s["z_kept"], n)
                nc.scalar.activation(e[:], z[:], ACT.Exp, scale=-1.0).then_inc(s["e_ready"], 1)

        @block.vector
        def _(dve):
            nc.vector.memset(ip[:], 0.0).then_inc(s["cleared"], 1)
            dve.wait_ge(s["cleared"], 1)
            dve.wait_ge(s["weights_loaded"], 16 * n_loads)
            with dve.Fori(0, NT) as i:
                n = i + 1
                x_tile = core.x[:, i, :]

                def then(ins, name):
                    ins.then_inc(s[name], 1)
                    dve.wait_ge(s[name], n)

                layer_norm(dve, nc, s, n, x_tile, xn[:], stats[:], mean[:], rstd[:])
                dve.wait_ge(s["v_ready"], n)
                nc.vector.tensor_tensor(v[:], ps_v[:, 0:D], rows["bv_c"][:], ALU.add).then_inc(s["v_kept"], 1)
                dve.wait_ge(s["s2_ready"], n)
                then(nc.vector.tensor_reduce(big2[:], ps_x[:, 0:2 * S].rearrange("p (j k) -> p j k", j=2), X, ALU.max,
                                             negate=True), "max2_ready")
                nc.vector.tensor_scalar(bias2[:], big2[:], scale, None, ALU.mult).then_inc(s["bias2_ready"], 1)
                dve.wait_ge(s["exp2_ready"], n)
                then(nc.vector.reciprocal(rinv2[:], rsum2[:]), "inv2_ready")
                nc.vector.tensor_tensor(probs2[:], probs2[:], rinv2[:].unsqueeze(2).broadcast_to([P, 2, S]),
                                        ALU.mult).then_inc(s["probs2_ready"], 1)
                dve.wait_ge(s["s1_ready"], n)
                then(nc.vector.tensor_reduce(big1[:], ps_s1[:, 0:KEYS], X, ALU.max), "max1_ready")
                dve.wait_ge(s["folded_kept"], n)
                then(nc.vector.tensor_tensor(sum1[:], big1[:], q_bk[:], ALU.add), "shift1_ready")
                nc.vector.tensor_scalar(bias1[:], q_bk[:], sum1[:], scale, ALU.subtract, ALU.mult).then_inc(
                    s["bias1_ready"], 1)
                dve.wait_ge(s["ip_ready"], n)
                for b in range(BT):
                    at = slice(S * b, S * b + S)
                    last = nc.vector.tensor_copy(ip[at, at], (ps_x if b % 2 == 0 else ps_y)[at, 0:S])
                last.then_inc(s["ip_kept"], 1)
                dve.wait_ge(s["s2c_ready"], n)
                nc.vector.tensor_copy(s2c[:], ps_v[:, 0:D]).then_inc(s["s2c_kept"], 1)
                dve.wait_ge(s["exp1_ready"], n)
                then(nc.vector.reciprocal(rinv1[:], rsum1[:]), "inv1_ready")
                dve.wait_ge(s["c2s_ready"], n)
                then(nc.vector.scalar_tensor_tensor(c2s[:], ps_t[:, 0:D], rinv1[:], rows["bv_s"][:], ALU.mult,
                                                    ALU.add), "c2s_kept")
                dve.wait_ge(s["s2c_kept"], n)
                nc.vector.tensor_tensor(diff[:], c2s[:], s2c[:], ALU.subtract).then_inc(s["diff_ready"], 1)
                then(nc.vector.tensor_tensor(x_tile, x_tile, s2c[:], ALU.add), "x_plus")
                dve.wait_ge(s["z_ready"], n)
                nc.vector.tensor_tensor(z[:], ps_x[:, 0:D], rows["bg"][:], ALU.add).then_inc(s["z_kept"], 1)
                dve.wait_ge(s["e_ready"], n)
                then(nc.vector.tensor_scalar(e[:], e[:], 1.0, None, ALU.add), "one_plus")
                then(nc.vector.reciprocal(e[:], e[:]), "gate_ready")
                dve.wait_ge(s["diff_ready"], n)
                then(nc.vector.tensor_tensor(diff[:], diff[:], e[:], ALU.mult), "mixed")
                then(nc.vector.tensor_tensor(x_tile, x_tile, diff[:], ALU.add), "x_done")


def fixed_experts_ffn(core, tag):
    nc = core.nc
    E, HID = 8, 4 * D
    HC = HID // P
    U = NT // E
    N = U * P
    w = "L0_ffn_"
    with ExitStack() as ctx:
        def sb(name, shape, dt=F32):
            return ctx.enter_context(nc.sbuf_tensor(f"{tag}_{name}", shape, dt))

        def ps(name, shape):
            return ctx.enter_context(nc.psum_tensor(f"{tag}_{name}", shape, F32))

        s = semaphores(nc, tag, """weights_loaded w1_loaded w2_loaded w1_used w2_used ps_t_used flatT_ready
            xn2T_ready attn_ready xaT_ready out_ready eoT_ready y_ready y_kept gelu_ready x_done""")
        ln = [[semaphores(nc, f"{tag}_ln{a}{u}", LN_SEMS) for u in range(U)] for a in range(2)]
        turned = [nc.alloc_semaphore(f"{tag}_turned{u}") for u in range(U)]
        half_read = [nc.alloc_semaphore(f"{tag}_half_read{u}") for u in range(U)]
        flat_read = [nc.alloc_semaphore(f"{tag}_flat_read{u}") for u in range(U)]
        h_ready = [nc.alloc_semaphore(f"{tag}_h_ready{k}") for k in range(HC // 2)]
        h_kept = [nc.alloc_semaphore(f"{tag}_h_kept{k}") for k in range(HC // 2)]
        attn_w, next_w = sb("attn_w", [P, C, D]), sb("next_w", [P, C, D])
        cols = {k: sb(k, [P, C]) for k in ("ln_scale", "ln_bias", "attn_b")}
        next_b = sb("next_b", [P, D])
        w1, w2 = sb("w1", [P, C, HID]), sb("w2", [P, HC, D])
        b1, b2 = sb("b1", [P, HC]), sb("b2", [P, C])
        stats, mean, rstd = sb("stats", [P, 2, U, 6]), sb("mean", [P, 2, U, 2]), sb("rstd", [P, 2, U])
        flat, xn2 = sb("flat", [P, U, D]), sb("xn2", [P, U, D])
        flatT, xn2T, xaT = sb("flatT", [P, C, N]), sb("xn2T", [P, C, N]), sb("xaT", [P, C, N])
        hT = sb("hT", [P, HC, N])
        eoT = sb("eoT", [P, C, N])
        y = sb("y", [P, U, D])
        ps_t, ps_a = ps("ps_t", [P, 4, P]), ps("ps_a", [P, C, N])
        ps_h = ps("ps_h", [P, HC // 2, 2, N])
        ps_e, ps_y = ps("ps_e", [P, C, N]), ps("ps_y", [P, U, D])
        ident = core.table("ident")
        block = ctx.enter_context(nc.Block())

        @block.sync
        def _(sp):
            for t, k in ((attn_w, "attn_w_T"), (next_w, "next_w_T")):
                sp.dma_start(t[:], core.weight(w + k)).then_inc(s["weights_loaded"], 16)
            for k in cols:
                sp.dma_start(cols[k][:], core.column(w + k)).then_inc(s["weights_loaded"], 16)
            sp.dma_start(next_b[:], core.rows(w + "next_b")).then_inc(s["weights_loaded"], 16)
            w1_by_expert = core.inputs[w + "w1"].rearrange("e (c p) n -> e p c n", p=P)
            w2_by_expert = core.inputs[w + "w2"].rearrange("e (c p) n -> e p c n", p=P)
            with sp.Fori(0, E) as e:
                wait(sp, s["w1_used"], e + 1)
                sp.dma_start(w1[:], w1_by_expert[e]).then_inc(s["w1_loaded"], 16)
                sp.dma_start(b1[:], core.inputs[w + "b1_col"][e]).then_inc(s["w1_loaded"], 16)
                wait(sp, s["w2_used"], e + 1)
                sp.dma_start(w2[:], w2_by_expert[e]).then_inc(s["w2_loaded"], 16)
                sp.dma_start(b2[:], core.inputs[w + "b2_col"][e]).then_inc(s["w2_loaded"], 16)

        @block.gpsimd
        def _(pool):
            with pool.Fori(0, E) as e:
                for a in range(2):
                    for u in range(U):
                        layer_norm_root(pool, nc, ln[a][u], e + 1, mean[:, a, u], rstd[:, a, u:u + 1],
                                        core.table("minus_half"))

        @block.tensor
        def _(pe):
            pe.wait_ge(s["weights_loaded"], 16 * 6)
            with pe.Fori(0, E) as e:
                n = e + 1
                for u in range(U):
                    if u:
                        pe.wait_ge(half_read[u - 1], n)
                        pe.wait_ge(flat_read[u - 1], n)
                    pe.wait_ge(ln[1][u]["xn_ready"], n)
                    for c in range(C):
                        nc.tensor.transpose(ps_t[:, c, :], flat[:, u, c * P:c * P + P], ident)
                    for c in range(C):
                        last = nc.tensor.transpose(ps_t[:, C + c, :], xn2[:, u, c * P:c * P + P], ident)
                    last.then_inc(turned[u], 1)
                pe.wait_ge(half_read[U - 1], n)
                for oc in range(C):
                    for c in range(C):
                        last = nc.tensor.matmul(ps_a[:, oc, :], attn_w[:, c, oc * P:oc * P + P], xn2T[:, c, :],
                                                start=(c == 0), stop=(c == C - 1))
                last.then_inc(s["attn_ready"], 1)
                pe.wait_ge(s["w1_loaded"], n * 32)
                pe.wait_ge(s["xaT_ready"], n)
                for k in range(HC // 2):
                    for hc in (2 * k, 2 * k + 1):
                        for c in range(C):
                            last = nc.tensor.matmul(ps_h[:, k, hc % 2, :], w1[:, c, hc * P:hc * P + P], xaT[:, c, :],
                                                    start=(c == 0), stop=(c == C - 1))
                    last.then_inc(h_ready[k], 1)
                pe.wait_ge(s["w2_loaded"], n * 32)
                for oc in range(C):
                    for hc in range(HC):
                        if oc == 0 and hc % 2 == 0:
                            pe.wait_ge(h_kept[hc // 2], n)
                        last = nc.tensor.matmul(ps_e[:, oc, :], w2[:, hc, oc * P:oc * P + P], hT[:, hc, :],
                                                start=(hc == 0), stop=(hc == HC - 1))
                last.then_inc(s["out_ready"], 1)
                pe.wait_ge(s["eoT_ready"], n)
                for u in range(U):
                    for c in range(C):
                        last = nc.tensor.matmul(ps_y[:, u, :], eoT[:, c, u * P:u * P + P], next_w[:, c, :],
                                                start=(c == 0), stop=(c == C - 1))
                last.then_inc(s["y_ready"], 1)

        @block.scalar
        def _(act):
            act.sem_inc(s["w1_used"], 1)
            act.sem_inc(s["w2_used"], 1)
            act.wait_ge(s["weights_loaded"], 16 * 6)
            with act.Fori(0, E) as e:
                n = e + 1
                for u in range(U):
                    act.wait_ge(turned[u], n)
                    for c in range(C):
                        last = nc.scalar.copy(flatT[:, c, u * P:u * P + P], ps_t[:, c, :])
                    last.then_inc(flat_read[u], 1)
                    for c in range(C):
                        last = nc.scalar.activation(xn2T[:, c, u * P:u * P + P], ps_t[:, C + c, :], ACT.Identity,
                                                    bias=cols["ln_bias"][:, c:c + 1], scale=cols["ln_scale"][:, c:c + 1])
                    last.then_inc(half_read[u], 1)
                for k in range(HC // 2):
                    act.wait_ge(h_ready[k], n)
                    if k == 0:
                        act.wait_ge(s["w1_loaded"], n * 32)
                    for hc in (2 * k, 2 * k + 1):
                        last = nc.scalar.activation(hT[:, hc, :], ps_h[:, k, hc % 2, :], ACT.Gelu,
                                                    bias=b1[:, hc:hc + 1])
                    last.then_inc(h_kept[k], 1)
                act.wait_ge(h_kept[HC // 2 - 1], n)
                act.sem_inc(s["w1_used"], 1)
                act.wait_ge(s["out_ready"], n)
                for c in range(C):
                    last = nc.scalar.activation(eoT[:, c, :], ps_e[:, c, :], ACT.Identity, bias=b2[:, c:c + 1])
                last.then_inc(s["eoT_ready"], 1)
                act.wait_ge(s["eoT_ready"], n)
                act.sem_inc(s["w2_used"], 1)
                act.wait_ge(s["y_kept"], n)
                nc.scalar.activation(y[:], y[:], ACT.Gelu).then_inc(s["gelu_ready"], 1)

        @block.vector
        def _(dve):
            dve.wait_ge(s["weights_loaded"], 16 * 6)
            with dve.Fori(0, E) as e:
                n = e + 1
                for u in range(U):
                    layer_norm(dve, nc, ln[0][u], n, core.x[:, e + E * u, :], flat[:, u], stats[:, 0, u],
                               mean[:, 0, u], rstd[:, 0, u:u + 1])
                for u in range(U):
                    dve.wait_ge(ln[0][u]["xn_ready"], n)
                    layer_norm(dve, nc, ln[1][u], n, flat[:, u], xn2[:, u], stats[:, 1, u],
                               mean[:, 1, u], rstd[:, 1, u:u + 1])
                dve.wait_ge(s["attn_ready"], n)
                dve.wait_ge(flat_read[U - 1], n)
                for c in range(C):
                    last = nc.vector.scalar_tensor_tensor(xaT[:, c, :], ps_a[:, c, :], cols["attn_b"][:, c:c + 1],
                                                          flatT[:, c, :], ALU.add, ALU.add)
                last.then_inc(s["xaT_ready"], 1)
                dve.wait_ge(s["y_ready"], n)
                nc.vector.tensor_tensor(y[:], ps_y[:], next_b[:].unsqueeze(1).broadcast_to([P, U, D]), ALU.add).then_inc(
                    s["y_kept"], 1)
                dve.wait_ge(s["gelu_ready"], n)
                for u in range(U):
                    last = nc.vector.tensor_tensor(core.x[:, e + E * u, :], core.x[:, e + E * u, :], y[:, u],
                                                   ALU.add)
                last.then_inc(s["x_done"], 1)
                dve.wait_ge(s["x_done"], n)


def normed_features(core, tag, xnT_all, router=None):
    nc = core.nc
    E = 8
    with ExitStack() as ctx:
        def sb(name, shape, dt=F32):
            return ctx.enter_context(nc.sbuf_tensor(f"{tag}_{name}", shape, dt))

        def ps(name, shape):
            return ctx.enter_context(nc.psum_tensor(f"{tag}_{name}", shape, F32))

        s = semaphores(nc, tag, LN_SEMS + """ weights_loaded xn_turned xnT_ready logits_ready exp_ready
            one_plus sigmoid_ready chosen_by top_ready place_ready kept bank_read""")
        stats, mean, rstd = sb("stats", [P, 6]), sb("mean", [P, 2]), sb("rstd", [P, 1])
        xn, xnT = sb("xn", [P, D]), sb("xnT", [P, C, P])
        ps_t = ps("ps_t", [P, C, P])
        if router:
            weights, bias_row, kind, gates = router
            rw, rb = sb("rw", [P, C, E]), sb("rb", [P, E])
            ps_r = ps("ps_r", [P, E])
            e, sig, by = sb("e", [P, E]), sb("sig", [P, E]), sb("by", [P, E])
            top, place = sb("top", [P, E]), sb("place", [P, E], U32)
            sig_all = sb("sig_all", [P, NT, E])
            top_all, place_all = sb("top_all", [P, NT, 2]), sb("place_all", [P, NT, 2])
            weigh, share = sb("weigh", [P, NT, 2]), sb("share", [P, NT, 2])
            one_hot = sb("one_hot", [P, 2, NT, E])
            total, enough = sb("total", [P, NT]), sb("enough", [P, NT])
            after = semaphores(nc, tag + "g", "hot picked gap exps a b c d e f h")
        ident = core.table("ident")
        block = ctx.enter_context(nc.Block())

        @block.sync
        def _(sp):
            if router:
                sp.dma_start(rw[:], core.inputs[weights]).then_inc(s["weights_loaded"], 16)
                sp.dma_start(rb[:], core.rows(bias_row)).then_inc(s["weights_loaded"], 16)

        @block.gpsimd
        def _(pool):
            with pool.Fori(0, NT) as i:
                layer_norm_root(pool, nc, s, i + 1, mean[:], rstd[:], core.table("minus_half"))

        @block.tensor
        def _(pe):
            if router:
                pe.wait_ge(s["weights_loaded"], 32)
            with pe.Fori(0, NT) as i:
                n = i + 1
                pe.wait_ge(s["xn_ready"], n)
                pe.wait_ge(s["bank_read"], n)
                for c in range(C):
                    last = nc.tensor.transpose(ps_t[:, c, :], xn[:, c * P:c * P + P], ident)
                last.then_inc(s["xn_turned"], 1)
                if router:
                    pe.wait_ge(s["xnT_ready"], n)
                    for c in range(C):
                        last = nc.tensor.matmul(ps_r[:], xnT[:, c, :], rw[:, c, :], start=(c == 0), stop=(c == C - 1))
                    last.then_inc(s["logits_ready"], 1)

        @block.scalar
        def _(act):
            act.sem_inc(s["bank_read"], 1)
            with act.Fori(0, NT) as i:
                n = i + 1
                act.wait_ge(s["xn_turned"], n)
                nc.scalar.copy(xnT[:], ps_t[:]).then_inc(s["xnT_ready"], 1)
                nc.scalar.copy(xnT_all[:, :, bass.ts(i, P)], ps_t[:]).then_inc(s["bank_read"], 1)
                if router and kind == "sigmoid":
                    act.wait_ge(s["logits_ready"], n)
                    nc.scalar.activation(e[:], ps_r[:], ACT.Exp, scale=-1.0).then_inc(s["exp_ready"], 1)
            if router and kind == "softmax":
                act.wait_ge(after["gap"], 1)
                nc.scalar.activation(weigh[:, :, 1], weigh[:, :, 1], ACT.Exp).then_inc(after["exps"], 1)

        @block.vector
        def _(dve):
            if router:
                dve.wait_ge(s["weights_loaded"], 32)
            with dve.Fori(0, NT) as i:
                n = i + 1

                def then(ins, name):
                    ins.then_inc(s[name], 1)
                    wait(dve, s[name], n)

                dve.wait_ge(s["bank_read"], n)
                layer_norm(dve, nc, s, n, core.x[:, i, :], xn[:], stats[:], mean[:], rstd[:])
                if router:
                    if kind == "sigmoid":
                        dve.wait_ge(s["exp_ready"], n)
                        then(nc.vector.tensor_scalar(e[:], e[:], 1.0, None, ALU.add), "one_plus")
                        then(nc.vector.reciprocal(sig[:], e[:]), "sigmoid_ready")
                        nc.vector.tensor_copy(sig_all[:, i, :], sig[:])
                        then(nc.vector.tensor_tensor(by[:], sig[:], rb[:], ALU.add), "chosen_by")
                    else:
                        dve.wait_ge(s["logits_ready"], n)
                        then(nc.vector.tensor_tensor(by[:], ps_r[:], rb[:], ALU.add), "chosen_by")
                    then(nc.vector.max(top[:], by[:]), "top_ready")
                    then(nc.vector.max_index(place[:], top[:], by[:]), "place_ready")
                    nc.vector.tensor_copy(top_all[:, i, :], top[:, 0:2])
                    then(nc.vector.tensor_copy(place_all[:, i, :], place[:, 0:2]), "kept")
            if not router:
                return

            def step(ins, name):
                ins.then_inc(after[name], 1)
                dve.wait_ge(after[name], 1)

            for k in range(2):
                last = nc.vector.tensor_tensor(one_hot[:, k], place_all[:, :, k].unsqueeze(2).broadcast_to([P, NT, E]),
                                               core.table("iota")[:, 0:E].unsqueeze(1).broadcast_to([P, NT, E]),
                                               ALU.is_equal)
            step(last, "hot")
            if kind == "softmax":
                nc.vector.memset(weigh[:, :, 0], 1.0)
                step(nc.vector.tensor_tensor(weigh[:, :, 1], top_all[:, :, 1], top_all[:, :, 0], ALU.subtract), "gap")
                dve.wait_ge(after["exps"], 1)
            else:
                for k in range(2):
                    step(nc.vector.tensor_tensor(gates[:, :, 0:E], one_hot[:, k], sig_all[:], ALU.mult), "ab"[k])
                    step(nc.vector.tensor_reduce(weigh[:, :, k], gates[:, :, 0:E], X, ALU.add), "cd"[k])
            step(nc.vector.tensor_tensor(total[:], weigh[:, :, 0], weigh[:, :, 1], ALU.add), "e")
            if kind == "sigmoid":
                nc.vector.tensor_scalar(enough[:], total[:], 1e-9, None, ALU.is_gt)
                step(nc.vector.tensor_scalar(total[:], total[:], 1e-9, None, ALU.add), "f")
            step(nc.vector.reciprocal(total[:], total[:]), "h")
            many = after["picked"]
            nc.vector.tensor_tensor(share[:], weigh[:], total[:].unsqueeze(2).broadcast_to([P, NT, 2]),
                                    ALU.mult).then_inc(many, 1)
            dve.wait_ge(many, 1)
            if kind == "sigmoid":
                nc.vector.tensor_scalar(share[:], share[:], 0.5, None, ALU.subtract).then_inc(many, 1)
                dve.wait_ge(many, 2)
                nc.vector.tensor_tensor(share[:], share[:], enough[:].unsqueeze(2).broadcast_to([P, NT, 2]),
                                        ALU.mult).then_inc(many, 1)
                dve.wait_ge(many, 3)
                nc.vector.tensor_scalar(share[:], share[:], 0.5, None, ALU.add).then_inc(many, 1)
                dve.wait_ge(many, 4)
            for k in range(2):
                last = nc.vector.tensor_tensor(one_hot[:, k], one_hot[:, k],
                                               share[:, :, k].unsqueeze(2).broadcast_to([P, NT, E]), ALU.mult)
            last.then_inc(many, 1)
            dve.wait_ge(many, 5 if kind == "sigmoid" else 2)
            nc.vector.tensor_tensor(gates[:, :, 0:E], one_hot[:, 0], one_hot[:, 1], ALU.add)
            nc.vector.memset(gates[:, :, E], 1.0)


def dense_experts(core, tag, xnT_all, gates, first, count, hidden, names, swiglu):
    nc = core.nc
    HC = hidden // P
    TB = 512
    NB = T // TB
    TT = TB // P
    ups = 2 if swiglu else 1
    slots = 2 if count > 1 else 1
    with ExitStack() as ctx:
        def sb(name, shape, dt=F32):
            return ctx.enter_context(nc.sbuf_tensor(f"{tag}_{name}", shape, dt))

        def ps(name, shape):
            return ctx.enter_context(nc.psum_tensor(f"{tag}_{name}", shape, F32))

        s = semaphores(nc, tag, "up_ready activated hidden_ready out_ready x_done gate_ready")
        loaded = [nc.alloc_semaphore(f"{tag}_loaded{k}") for k in range(slots)]
        used = [nc.alloc_semaphore(f"{tag}_used{k}") for k in range(slots)]
        w_up = sb("w_up", [P, slots, ups, C, hidden])
        w_down = sb("w_down", [P, slots, HC, D])
        act_out = sb("act_out", [P, 2, TB])
        hiddenT = sb("hiddenT", [P, 2, HC, TB])
        gate = sb("gate", [P, NT])
        ps_up = ps("ps_up", [P, 2, ups, TB])
        ps_d = ps("ps_d", [P, 2, TT, D])
        block = ctx.enter_context(nc.Block())
        per_load = 16 * (ups + 1)

        def each(engine, body):
            if count >= 2:
                with engine.Fori(0, count // 2) as i:
                    body(0, i * 2, i + 1)
                    body(1, i * 2 + 1, i + 1)
            if count % 2:
                body(0, count - 1, count // 2 + 1)

        @block.sync
        def _(sp):
            views = [core.inputs[k].rearrange("e (c p) n -> e p c n", p=P) for k in names]

            def load(slot, e, turn):
                wait(sp, used[slot], turn)
                for k in range(ups):
                    sp.dma_start(w_up[:, slot, k], views[k][e]).then_inc(loaded[slot], 16)
                sp.dma_start(w_down[:, slot], views[ups][e]).then_inc(loaded[slot], 16)

            each(sp, load)

        @block.tensor
        def _(pe):
            for slot in range(slots):
                pe.sem_inc(used[slot], 1)
            pe.sem_inc(s["out_ready"], 2)

            def expert(slot, e, turn):
                pe.wait_ge(loaded[slot], turn * per_load)

                def up(tb, hc):
                    k = (tb * HC + hc) % 2
                    pe.wait_ge(s["hidden_ready"], e * (NB * HC) + (tb * HC + hc + 1))
                    for a in range(ups):
                        for c in range(C):
                            last = nc.tensor.matmul(ps_up[:, k, a, :], w_up[:, slot, a, c, hc * P:hc * P + P],
                                                    xnT_all[:, c, tb * TB:tb * TB + TB],
                                                    start=(c == 0), stop=(c == C - 1))
                    last.then_inc(s["up_ready"], 1)

                def down(tb):
                    pe.wait_ge(s["hidden_ready"], e * (NB * HC) + (tb * HC + HC + 2))
                    pe.wait_ge(s["x_done"], e * NB + (tb + 1))
                    for tt in range(TT):
                        for hc in range(HC):
                            last = nc.tensor.matmul(ps_d[:, tb % 2, tt, :], hiddenT[:, tb % 2, hc, tt * P:tt * P + P],
                                                    w_down[:, slot, hc, :], start=(hc == 0), stop=(hc == HC - 1))
                    last.then_inc(s["out_ready"], 1)

                for tb in range(NB):
                    for hc in range(HC):
                        up(tb, hc)
                        if hc == 1 and tb:
                            down(tb - 1)
                down(NB - 1)
                pe.wait_ge(s["out_ready"], e * NB + (NB + 2))
                pe.sem_inc(used[slot], 1)

            each(pe, expert)

        @block.scalar
        def _(act):
            def expert(slot, e, turn):
                for tb in range(NB):
                    for hc in range(HC):
                        k = (tb * HC + hc) % 2
                        if swiglu:
                            act.wait_ge(s["hidden_ready"], e * (NB * HC) + (tb * HC + hc + 1))
                        elif hc == 0:
                            act.wait_ge(s["out_ready"], e * NB + (tb + 1))
                        act.wait_ge(s["up_ready"], e * (NB * HC) + (tb * HC + hc + 1))
                        if swiglu:
                            nc.scalar.activation(act_out[:, k, :], ps_up[:, k, 0, :], ACT.Silu).then_inc(
                                s["activated"], 1)
                        else:
                            nc.scalar.activation(hiddenT[:, tb % 2, hc, :], ps_up[:, k, 0, :], ACT.Gelu).then_inc(
                                s["hidden_ready"], 1)

            if not swiglu:
                act.sem_inc(s["hidden_ready"], 2)
            each(act, expert)

        @block.vector
        def _(dve):
            if swiglu:
                dve.sem_inc(s["hidden_ready"], 2)
            dve.sem_inc(s["x_done"], 2)

            def expert(slot, e, turn):
                wait(dve, s["x_done"], e * NB + 2)
                nc.vector.tensor_copy(gate[:], gates[:, :, first + e]).then_inc(s["gate_ready"], 1)
                dve.wait_ge(s["gate_ready"], e + 1)

                def add(tb):
                    dve.wait_ge(s["out_ready"], e * NB + (tb + 3))
                    for tt in range(TT):
                        t = tb * TT + tt
                        last = nc.vector.scalar_tensor_tensor(core.x[:, t, :], ps_d[:, tb % 2, tt, :], gate[:, t:t + 1],
                                                              core.x[:, t, :], ALU.mult, ALU.add)
                    last.then_inc(s["x_done"], 1)

                for tb in range(NB):
                    for hc in range(HC):
                        if swiglu:
                            k = (tb * HC + hc) % 2
                            if hc == 0:
                                dve.wait_ge(s["out_ready"], e * NB + (tb + 1))
                            dve.wait_ge(s["activated"], e * (NB * HC) + (tb * HC + hc + 1))
                            nc.vector.tensor_tensor(hiddenT[:, tb % 2, hc, :], act_out[:, k, :], ps_up[:, k, 1, :],
                                                    ALU.mult).then_inc(s["hidden_ready"], 1)
                        if hc == 1 and tb:
                            add(tb - 1)
                add(NB - 1)

            each(dve, expert)


def routed_ffn(core, tag, router, parts):
    with ExitStack() as ctx:
        xnT_all = ctx.enter_context(core.nc.sbuf_tensor(f"{tag}_xnT_all", [P, C, T], F32))
        gates = ctx.enter_context(core.nc.sbuf_tensor(f"{tag}_gates", [P, NT, 9], F32))
        normed_features(core, tag + "n", xnT_all, (*router, gates))
        for k, (first, count, hidden, names, swiglu) in enumerate(parts):
            dense_experts(core, f"{tag}e{k}", xnT_all, gates, first, count, hidden, names, swiglu)


PH = 8
NK = 64
K8 = 8
EN = PH * K8


def product_key_ffn(core, tag):
    nc = core.nc
    w = "L1_ffn_"
    with ExitStack() as whole:
        def keep(name, shape, dt=F32):
            return whole.enter_context(nc.sbuf_tensor(f"{tag}_{name}", shape, dt))

        xnT_all = keep("xnT_all", [P, C, T])
        norm_scale, norm_bias = keep("norm_scale", [P, C]), keep("norm_bias", [P, C])
        normed_features(core, tag + "n", xnT_all)
        folded = keep("folded", [P, C, 2 * PH * NK])
        fold_keys(core, tag + "f", xnT_all, folded, norm_scale, norm_bias)
        chosen_units(core, tag + "u", xnT_all, folded, norm_scale, norm_bias)


def fold_keys(core, tag, xnT_all, folded, norm_scale, norm_bias):
    nc = core.nc
    PARTS = T // 512
    with ExitStack() as ctx:
        def sb(name, shape, dt=F32):
            return ctx.enter_context(nc.sbuf_tensor(f"{tag}_{name}", shape, dt))

        s = semaphores(nc, tag, """weights_loaded folded_ready stats_ready mean_ready var_ready rstd_ready
            scale_ready shift_ready bias_ready""")
        w_q = sb("w_q", [P, 2 * PH, D])
        keys = sb("keys", [P, 2 * PH, NK])
        gamma, beta = sb("gamma", [P, C]), sb("beta", [P, C])
        stats, mean, rstd = sb("stats", [P, C, PARTS, 6]), sb("mean", [P, C, 2]), sb("rstd", [P, C])
        shift = sb("shift", [P, C])
        ps_f = ctx.enter_context(nc.psum_tensor(f"{tag}_ps_f", [P, C, 2 * PH * NK], F32))
        block = ctx.enter_context(nc.Block())

        @block.sync
        def _(sp):
            sp.dma_start(w_q[:], core.inputs["L1_ffn_w_q"].rearrange("(a p) d -> p a d", p=P)).then_inc(
                s["weights_loaded"], 16)
            sp.dma_start(keys[:], core.inputs["L1_ffn_keys_by_dim"]).then_inc(s["weights_loaded"], 16)
            sp.dma_start(gamma[:], core.column("L1_ffn_gamma")).then_inc(s["weights_loaded"], 16)
            sp.dma_start(beta[:], core.column("L1_ffn_beta")).then_inc(s["weights_loaded"], 16)

        @block.tensor
        def _(pe):
            pe.wait_ge(s["weights_loaded"], 64)
            for c in range(C):
                for a in range(2 * PH):
                    last = nc.tensor.matmul(ps_f[:, c, a * NK:a * NK + NK], w_q[:, a, c * P:c * P + P], keys[:, a, :],
                                            start=True, stop=True)
            last.then_inc(s["folded_ready"], 1)

        @block.scalar
        def _(act):
            act.wait_ge(s["folded_ready"], 1)
            for c in range(C):
                nc.scalar.copy(folded[:, c, :], ps_f[:, c, :])

        @block.gpsimd
        def _(pool):
            pool.wait_ge(s["mean_ready"], C)
            nc.gpsimd.tensor_scalar(mean[:, :, 1], mean[:, :, 1], EPS, None, ALU.add).then_inc(s["var_ready"], 1)
            pool.wait_ge(s["var_ready"], 1)
            nc.gpsimd.tensor_tensor(rstd[:], mean[:, :, 1], core.table("minus_half").broadcast_to([P, C]),
                                    ALU.pow).then_inc(s["rstd_ready"], 1)

        @block.vector
        def _(dve):
            for c in range(C):
                for k in range(PARTS):
                    last = nc.vector.bn_stats(stats[:, c, k], xnT_all[:, c, k * 512:k * 512 + 512])
            last.then_inc(s["stats_ready"], 1)
            dve.wait_ge(s["stats_ready"], 1)
            for c in range(C):
                nc.vector.bn_aggr(mean[:, c], stats[:, c].rearrange("p k n -> p (k n)")).then_inc(s["mean_ready"], 1)
            dve.wait_ge(s["weights_loaded"], 64)
            dve.wait_ge(s["rstd_ready"], 1)
            nc.vector.tensor_tensor(norm_scale[:], rstd[:], gamma[:], ALU.mult).then_inc(s["scale_ready"], 1)
            dve.wait_ge(s["scale_ready"], 1)
            nc.vector.tensor_tensor(shift[:], mean[:, :, 0], norm_scale[:], ALU.mult).then_inc(s["shift_ready"], 1)
            dve.wait_ge(s["shift_ready"], 1)
            nc.vector.tensor_tensor(norm_bias[:], beta[:], shift[:], ALU.subtract).then_inc(s["bias_ready"], 1)


def chosen_units(core, tag, xnT_all, folded, norm_scale, norm_bias):
    nc = core.nc
    J = NK // 2
    K = 8
    TC = NK // K
    JS = J // K
    W3 = 3
    with ExitStack() as ctx:
        def sb(name, shape, dt=F32):
            return ctx.enter_context(nc.sbuf_tensor(f"{tag}_{name}", shape, dt))

        def ps(name, shape):
            return ctx.enter_context(nc.psum_tensor(f"{tag}_{name}", shape, F32))

        s = semaphores(nc, tag, """weights_loaded part_ready first_ready second_hot second_ready plane_ready
            plane_kept units_ready activated weighed step_done x_done
            normed sim_ready sim_kept top_ready place_ready place_f_ready sums_ready best_ready
            rank_ready rows_ready digits_ready hot_ready weighed_ready picked_ready
            gap_ready exp_ready total_ready inv_ready weight_ready upper_ready split_ready doubled turned entries_kept""")
        key_in = sb("key_in", [P, C, J, P])
        key_out = sb("key_out", [P, J, D])
        entries = sb("entries", [P, 2, 3, NK])
        parts, rest = sb("parts", [P, 2, W3, NK], BF16), sb("rest", [P, 2, NK])
        first = sb("first", [P, 2, TC, P], BF16)
        second = sb("second", [P, 2, TC, J], BF16)
        second_weighed = sb("second_weighed", [P, 2, W3, TC, J], BF16)
        plane = sb("plane", [P, 2, P, J])
        act_out, weighed = sb("act_out", [P, 2, JS, P]), sb("weighed", [P, 2, JS, P])
        xbT = sb("xbT", [P, C, P])
        sim = sb("sim", [P, 2 * PH, NK])
        top, place = sb("top", [P, 2 * PH, K8]), sb("place", [P, 2 * PH, K8], U32)
        place_f = sb("place_f", [P, 2 * PH, K8])
        sums = sb("sums", [P, PH, K8, K8])
        best, rank = sb("best", [P, PH, K8]), sb("rank", [P, PH, K8], U32)
        digit = sb("digit", [P, 2, PH, K8], U32)
        digit_f = sb("digit_f", [P, 2, PH, K8])
        hot = sb("hot", [P, 2, PH, K8, K8])
        trio = sb("trio", [P, 3, EN])
        upper = sb("upper", [P, EN])
        gap, total, inv = sb("gap", [P, PH, K8]), sb("total", [P, PH]), sb("inv", [P, PH])
        doubled = sb("doubled", [P, 3, 2, EN])
        ps_p = ps("ps_p", [P, 2, 512])[:, :, 0:TC * J].rearrange("p h (n j) -> p h n j", j=J)
        ps_u = ps("ps_u", [P, 2, JS, P])
        ps_y = ps("ps_y", [P, 512])[:, 0:D]
        ps_sim = ps("ps_sim", [P, 2, 512])
        ps_e = ps("ps_e", [P, 4, P])
        ident = core.table("ident")
        iota8 = core.table("iota")[:, 0:K8]

        def iota(n):
            return core.table("iota")[:, 0:n].unsqueeze(1).broadcast_to([P, TC, n])
        block = ctx.enter_context(nc.Block())

        def after(engine, sem, count, alone=False):
            if isinstance(count, int) and count < 1:
                return
            if alone:
                wait(engine, sem, count)
            else:
                engine.wait_ge(sem, count)

        def all_turns(engine, turn):
            turn(-2, 0, True, False, False)
            turn(-1, 1, True, True, False)
            with engine.Fori(0, NT // 2 - 1) as g:
                turn(g * 2, 0, True, True, True)
                turn(g * 2 + 1, 1, True, True, True)
            turn(NT - 2, 0, False, True, True)
            turn(NT - 1, 1, False, False, True)

        def spread(par, value, k, n):
            return entries[:, par, value, TC * k:TC * k + TC].unsqueeze(2).broadcast_to([P, TC, n])

        @block.sync
        def _(sp):
            sp.dma_start(key_in[:], core.inputs["L1_ffn_key_in_by_expert"].rearrange("(c p) j m -> p c j m", p=P)
                         ).then_inc(s["weights_loaded"], 16)
            sp.dma_start(key_out[:], core.inputs["L1_ffn_key_out_by_expert"]).then_inc(s["weights_loaded"], 16)

        @block.gpsimd
        def _(pool):
            def turn(t, par, choose, build, units):
                if build:
                    for k in range(K):
                        pool.wait_ge(s["second_hot"], (t + 1) * K + (k + 1))
                        after(pool, s["plane_ready"], (t + 1) * K + (k - 1))
                        for part in range(W3):
                            last = nc.gpsimd.tensor_tensor(
                                second_weighed[:, k % 2, part], second[:, k % 2],
                                parts[:, 1 - par, part, TC * k:TC * k + TC].unsqueeze(2).broadcast_to([P, TC, J]),
                                ALU.mult)
                        last.then_inc(s["second_ready"], 1)

            all_turns(pool, turn)

        @block.tensor
        def _(pe):
            pe.sem_inc(s["step_done"], 2)

            def similarities(tile):
                pe.wait_ge(s["normed"], tile + 1)
                after(pe, s["sim_kept"], tile)
                for k in range(2):
                    for c in range(C):
                        last = nc.tensor.matmul(ps_sim[:, k, :], xbT[:, c, :], folded[:, c, k * 512:k * 512 + 512],
                                                start=(c == 0), stop=(c == C - 1))
                last.then_inc(s["sim_ready"], 1)

            def turn_entries(tile):
                pe.wait_ge(s["doubled"], tile + 1)
                after(pe, s["entries_kept"], tile)
                for k in range(3):
                    last = nc.tensor.transpose(ps_e[:, k, :], doubled[:, k].rearrange("p r e -> p (r e)"), ident)
                last.then_inc(s["turned"], 1)

            def build_plane(tile, k):
                pe.wait_ge(s["first_ready"], tile * K + (k + 1))
                after(pe, s["plane_kept"], tile * K + k)
                wait(pe, s["second_ready"], tile * K + (k + 1))
                for token in range(TC):
                    for half in range(2):
                        rows = slice(EN * half, EN * half + EN)
                        for part in range(W3):
                            last = nc.tensor.matmul(ps_p[:, half, token, :], first[rows, k % 2, token, :],
                                                    second_weighed[rows, k % 2, part, token, :],
                                                    start=(part == 0), stop=(part == W3 - 1))
                last.then_inc(s["plane_ready"], 1)

            def hidden(tile, k):
                pe.wait_ge(s["activated"], tile * K + (k + 1))
                for j in range(JS):
                    for c in range(C):
                        last = nc.tensor.matmul(ps_u[:, k % 2, j, :], key_in[:, c, JS * k + j, :],
                                                xnT_all[:, c, bass.ts(tile, P)], start=(c == 0), stop=(c == C - 1))
                last.then_inc(s["units_ready"], 1)

            def outputs(tile, k):
                if k == 0:
                    pe.wait_ge(s["x_done"], tile + 1)
                pe.wait_ge(s["weighed"], tile * K + (k + 3))
                for j in range(JS):
                    last = nc.tensor.matmul(ps_y, weighed[:, k % 2, j, :], key_out[:, JS * k + j, :],
                                            start=(k + j == 0), stop=(k == K - 1 and j == JS - 1))
                last.then_inc(s["step_done"], 1)

            def turn(t, par, choose, build, units):
                if units:
                    hidden(t, 0)
                for k in range(K):
                    if units and k + 1 < K:
                        hidden(t, k + 1)
                    if build:
                        build_plane(t + 1, k)
                    if units:
                        outputs(t, k)
                    if choose and k == 0:
                        similarities(t + 2)
                    if choose and k == K - 1:
                        turn_entries(t + 2)
                if build and not units:
                    pe.wait_ge(s["weights_loaded"], 32)

            all_turns(pe, turn)

        @block.scalar
        def _(act):
            act.sem_inc(s["activated"], 2)

            def normed(tile):
                after(act, s["sim_ready"], tile, alone=True)
                for c in range(C):
                    last = nc.scalar.activation(xbT[:, c, :], xnT_all[:, c, bass.ts(tile, P)], ACT.Identity,
                                                bias=norm_bias[:, c:c + 1], scale=norm_scale[:, c:c + 1])
                last.then_inc(s["normed"], 1)

            def keep_similarities(tile):
                act.wait_ge(s["sim_ready"], tile + 1)
                after(act, s["place_ready"], tile)
                nc.scalar.copy(sim[:].rearrange("p a k -> p (a k)"), ps_sim[:].rearrange("p a k -> p (a k)")).then_inc(
                    s["sim_kept"], 1)

            def exps(tile):
                act.wait_ge(s["gap_ready"], tile + 1)
                nc.scalar.activation(gap[:], gap[:], ACT.Exp).then_inc(s["exp_ready"], 1)

            def keep_entries(tile, par):
                after(act, s["plane_ready"], tile * K - K)
                wait(act, s["turned"], tile + 1)
                for half in range(2):
                    at = slice(EN * half, EN * half + EN)
                    last = nc.scalar.copy(entries[at, par], ps_e[at, 0:3, NK * half:NK * half + NK])
                last.then_inc(s["entries_kept"], 1)

            def keep_plane(tile, par, k):
                if k == 0:
                    after(act, s["weighed"], tile * K + (2 - K))
                act.wait_ge(s["plane_ready"], tile * K + (k + 1))
                nc.scalar.copy(
                    plane[:, par].rearrange("p (h n) j -> p h (n j)", h=2)[:, :, TC * J * k:TC * J * k + TC * J],
                    ps_p.rearrange("p h n j -> p h (n j)")).then_inc(s["plane_kept"], 1)

            def gelus(tile, k):
                act.wait_ge(s["units_ready"], tile * K + (k + 1))
                act.wait_ge(s["weighed"], tile * K + (k + 1))
                nc.scalar.activation(act_out[:, k % 2], ps_u[:, k % 2], ACT.Gelu).then_inc(s["activated"], 1)

            def turn(t, par, choose, build, units):
                if choose:
                    normed(t + 2)
                if units:
                    gelus(t, 0)
                for k in range(K):
                    if units and k + 1 < K:
                        gelus(t, k + 1)
                    if build:
                        keep_plane(t + 1, 1 - par, k)
                    if choose and k == 0:
                        keep_similarities(t + 2)
                    if choose and k == 5:
                        exps(t + 2)
                    if choose and k == K - 1:
                        keep_entries(t + 2, par)

            all_turns(act, turn)

        @block.vector
        def _(dve):
            dve.sem_inc(s["weighed"], 2)
            dve.sem_inc(s["x_done"], 1)

            def choose_step(tile, k):
                n = tile + 1

                def then(ins, name):
                    ins.then_inc(s[name], 1)
                    wait(dve, s[name], n)

                if k == 1:
                    wait(dve, s["sim_kept"], n)
                    for a in range(2 * PH):
                        last = nc.vector.max(top[:, a, :], sim[:, a, :])
                    then(last, "top_ready")
                if k == 2:
                    for a in range(2 * PH):
                        last = nc.vector.max_index(place[:, a, :], top[:, a, :], sim[:, a, :])
                    then(last, "place_ready")
                if k == 3:
                    nc.vector.tensor_copy(place_f[:], place[:]).then_inc(s["place_f_ready"], 1)
                    then(nc.vector.tensor_tensor(sums[:], top[:, 0:PH, :].unsqueeze(3).broadcast_to([P, PH, K8, K8]),
                                                 top[:, PH:, :].unsqueeze(2).broadcast_to([P, PH, K8, K8]), ALU.add),
                         "sums_ready")
                    for h in range(PH):
                        last = nc.vector.max(best[:, h, :], sums[:, h].rearrange("p a b -> p (a b)"))
                    then(last, "best_ready")
                if k == 4:
                    for h in range(PH):
                        last = nc.vector.max_index(rank[:, h, :], best[:, h, :],
                                                   sums[:, h].rearrange("p a b -> p (a b)"))
                    then(last, "rank_ready")
                    nc.vector.tensor_tensor(gap[:], best[:], best[:, :, 0:1].broadcast_to([P, PH, K8]),
                                            ALU.subtract).then_inc(s["gap_ready"], 1)
                    nc.vector.tensor_scalar(digit[:, 0], rank[:], 3, None, ALU.logical_shift_right)
                    then(nc.vector.tensor_scalar(digit[:, 1], rank[:], 7, None, ALU.bitwise_and), "rows_ready")
                    then(nc.vector.tensor_copy(digit_f[:], digit[:]), "digits_ready")
                if k == 5:
                    for p in range(2):
                        last = nc.vector.tensor_tensor(
                            hot[:, p], digit_f[:, p].unsqueeze(3).broadcast_to([P, PH, K8, K8]),
                            iota8.unsqueeze(1).unsqueeze(1).broadcast_to([P, PH, K8, K8]), ALU.is_equal)
                    then(last, "hot_ready")
                    dve.wait_ge(s["place_f_ready"], n)
                    for p in range(2):
                        last = nc.vector.tensor_tensor(
                            hot[:, p], hot[:, p], place_f[:, PH * p:PH * p + PH, :].unsqueeze(2).broadcast_to(
                                [P, PH, K8, K8]), ALU.mult)
                    then(last, "weighed_ready")
                if k == 6:
                    for p in range(2):
                        last = nc.vector.tensor_reduce(trio[:, p].rearrange("p (h k) -> p h k", h=PH), hot[:, p], X,
                                                       ALU.add)
                    last.then_inc(s["picked_ready"], 1)
                    dve.wait_ge(s["exp_ready"], n)
                    then(nc.vector.tensor_reduce(total[:], gap[:], X, ALU.add), "total_ready")
                    then(nc.vector.reciprocal(inv[:], total[:]), "inv_ready")
                    then(nc.vector.tensor_tensor(trio[:, 2].rearrange("p (h k) -> p h k", h=PH), gap[:],
                                                 inv[:].unsqueeze(2).broadcast_to([P, PH, K8]), ALU.mult),
                         "weight_ready")
                    dve.wait_ge(s["picked_ready"], n)
                    then(nc.vector.tensor_scalar(upper[:], trio[:, 1], float(J), float(J), ALU.is_ge, ALU.mult),
                         "upper_ready")
                    nc.vector.scalar_tensor_tensor(trio[:, 0], upper[:], NK / J, trio[:, 0], ALU.mult, ALU.add)
                    then(nc.vector.tensor_tensor(trio[:, 1], trio[:, 1], upper[:], ALU.subtract), "split_ready")
                    after(dve, s["turned"], tile, alone=True)
                    nc.vector.tensor_copy(doubled[:], trio[:].unsqueeze(2).broadcast_to([P, 3, 2, EN])).then_inc(
                        s["doubled"], 1)

            def one_hot_rows(tile, par, k):
                if k == 0:
                    dve.wait_ge(s["entries_kept"], tile + 1)
                    left = entries[:, par, 2]
                    for part in range(W3):
                        nc.vector.tensor_copy(parts[:, par, part], left).then_inc(s["part_ready"], 1)
                        dve.wait_ge(s["part_ready"], tile * (2 * W3 - 1) + (2 * part + 1))
                        if part < W3 - 1:
                            nc.vector.tensor_tensor(rest[:, part], left, parts[:, par, part],
                                                    ALU.subtract).then_inc(s["part_ready"], 1)
                            dve.wait_ge(s["part_ready"], tile * (2 * W3 - 1) + (2 * part + 2))
                            left = rest[:, part]
                after(dve, s["plane_ready"], tile * K + (k - 1))
                nc.vector.tensor_tensor(first[:, k % 2], spread(par, 0, k, P), iota(P), ALU.is_equal).then_inc(
                    s["first_ready"], 1)
                after(dve, s["second_ready"], tile * K + (k - 1))
                nc.vector.tensor_tensor(second[:, k % 2], spread(par, 1, k, J), iota(J), ALU.is_equal).then_inc(
                    s["second_hot"], 1)

            def weigh(tile, par, k):
                if k == 0:
                    dve.wait_ge(s["plane_kept"], tile * K + K)
                dve.wait_ge(s["activated"], tile * K + (k + 3))
                dve.wait_ge(s["step_done"], tile * K + (k + 1))
                nc.vector.tensor_tensor(weighed[:, k % 2], act_out[:, k % 2],
                                        plane[:, par, :, JS * k:JS * k + JS].rearrange("p n j -> p j n"),
                                        ALU.mult).then_inc(s["weighed"], 1)

            def add_outputs(tile):
                wait(dve, s["step_done"], tile * K + (K + 2))
                nc.vector.tensor_tensor(core.x[:, tile, :], core.x[:, tile, :], ps_y, ALU.add).then_inc(s["x_done"], 1)

            def turn(t, par, choose, build, units):
                if build:
                    one_hot_rows(t + 1, 1 - par, 0)
                for k in range(K):
                    if units:
                        weigh(t, par, k)
                    if build and k + 1 < K:
                        one_hot_rows(t + 1, 1 - par, k + 1)
                    if choose:
                        choose_step(t + 2, k)
                if units:
                    add_outputs(t)

            all_turns(dve, turn)


SUBLAYERS = range(12)


def perceiver(nc, inputs, where, out):
    with ExitStack() as ctx:
        x_sb = ctx.enter_context(nc.sbuf_tensor("x_sb", [P, NT, D], F32))
        const = ctx.enter_context(nc.sbuf_tensor("const", [P, inputs["const"].shape[1]], F32))
        core = Core(nc, inputs, x_sb, const, where)
        with nc.semaphore("x_loaded") as x_loaded, nc.Block() as block:
            @block.sync
            def _(sp):
                sp.dma_start(const[:], inputs["const"]).then_inc(x_loaded, 16)
                sp.dma_start(x_sb[:], inputs["x"].rearrange("(t p) d -> p t d", p=P)).then_inc(x_loaded, 16)
                sp.wait_ge(x_loaded, 32)
        for n in SUBLAYERS:
            with nc.cleanup_on_exit():
                sublayer(core, n)
        with nc.semaphore("x_stored") as x_stored, nc.Block() as block:
            @block.sync
            def _(sp):
                sp.dma_start(out.rearrange("(t p) d -> p t d", p=P), x_sb[:]).then_inc(x_stored, 16)
                sp.wait_ge(x_stored, 16)


def sublayer(core, n):
    if n == 1:
        self_attention(core, "l0a", dict(q="L0_attn_w_q_T", k="L0_attn_w_k_T", v="L0_attn_w_v_T", o="L0_attn_w_o_T",
                                         bo="L0_attn_b_o"))
    if n == 0:
        gated_cross_attention(core, "l0x")
    if n == 4:
        complex_attention(core, "l1a", dict(q="L1_attn_Wq_T", k="L1_attn_Wk_T", v="L1_attn_Wv_T", o="L1_attn_Wo_T",
                                            bq="L1_attn_bq", bk="L1_attn_bk", bv="L1_attn_bv", bo="L1_attn_bo"))
    if n == 2:
        fixed_experts_ffn(core, "l0f")
    if n == 5:
        product_key_ffn(core, "l1f")
    if n == 8:
        routed_ffn(core, "l2f", ("L2_ffn_router", "L2_ffn_experts_bias", "softmax"), [
            (0, 9, 512, ("L2_ffn_w1_all", "L2_ffn_w3_all", "L2_ffn_w2_all"), True)])
    if n == 11:
        routed_ffn(core, "l3f", ("L3_ffn_router", "L3_ffn_router_bias", "sigmoid"), [
            (0, 8, 256, ("L3_ffn_ew1", "L3_ffn_ew2"), False),
            (8, 1, 512, ("L3_ffn_sw1", "L3_ffn_sw3", "L3_ffn_sw2"), True)])
    if n == 3:
        cross_attention(core, "l1x", dict(q="L1_xattn_Wq_T", k="L1_xattn_Wk_T", v="L1_xattn_Wv_T", o="L1_xattn_o",
                                          bq="L1_xattn_bq", bk="L1_xattn_bk", bv="L1_xattn_bv", bo="L1_xattn_bo"),
                        mask="mask_int", mask_type=I32)
    if n == 6:
        cross_attention(core, "l2x", dict(q="L2_xattn_Wq_T", k="L2_xattn_Wk_T", v="L2_xattn_Wv_T", o="L2_xattn_o",
                                          bq="L2_xattn_bq", bk="L2_xattn_bk", bv="L2_xattn_bv", bo="L2_xattn_bo"),
                        mask="mask_bool", mask_type=U8)
    if n == 9:
        cross_attention(core, "l3x", dict(q="L3_xattn_Wq", k="L3_xattn_Wk", v="L3_xattn_Wv", o="L3_xattn_o"),
                        bias_rows="fside")
    if n == 7:
        self_attention(core, "l2a", dict(
            q="L2_attn_q_w_T", k="L2_attn_k_w_T", v="L2_attn_v_w_T", o="L2_attn_o_w_T", bq="L2_attn_q_b",
            bk="L2_attn_k_b", bv="L2_attn_v_b", bo="L2_attn_o_b", qr="L2_attn_q_w_rot", kr="L2_attn_k_w_rot",
            bqr="L2_attn_q_b_rot", bkr="L2_attn_k_b_rot"), rope=True)
    if n == 10:
        self_attention(core, "l3a", dict(
            q="L3_attn_W_q", k="L3_attn_W_k", v="L3_attn_W_v", o="L3_attn_W_proj", bq="L3_attn_b_q",
            bk="L3_attn_b_k", bv="L3_attn_b_v", bo="L3_attn_b_proj"), alibi="L3_attn_slopes")


COLUMNS = ["L1_ffn_gamma", "L1_ffn_beta", "L0_ffn_ln_scale", "L0_ffn_ln_bias", "L0_ffn_attn_b", "L0_xattn_bq_c", "L0_xattn_bk_c", "L0_xattn_bk_s", "L0_xattn_bq_s",
           "L1_attn_bq", "L1_attn_bk", "L1_attn_bv", "L1_xattn_bq", "L1_xattn_bk", "L2_xattn_bq", "L2_xattn_bk",
           "L2_attn_q_b", "L2_attn_k_b", "L2_attn_v_b", "L2_attn_q_b_rot", "L2_attn_k_b_rot",
           "L3_attn_b_q", "L3_attn_b_k", "L3_attn_b_v"]


def laid_out(inputs):
    a = {k: np.asarray(v) for k, v in inputs.items()}
    table, where, rows = constant_tables()
    d = dict(const=table)
    d["x"] = a["x"].reshape(T, D)
    for n in ("L0_attn_w_q", "L0_attn_w_k", "L0_attn_w_v", "L0_attn_w_o",
              "L2_attn_q_w", "L2_attn_k_w", "L2_attn_v_w", "L2_attn_o_w"):
        d[n + "_T"] = a[n].T
    other = np.arange(D).reshape(H, 2, HD // 2)[:, ::-1].reshape(-1)
    for n in ("L2_attn_q", "L2_attn_k"):
        d[n + "_w_rot"] = a[n + "_w"][other].T
        d[n + "_b_rot"] = a[n + "_b"][other]
    for j, n in enumerate("kqv"):
        d["L3_attn_W_" + n] = a["L3_attn_W_kqv"][:, j * D:j * D + D]
        d["L3_attn_b_" + n] = a["L3_attn_b_kqv"][j * D:j * D + D]
    for n in ("L0_attn_b_o", "L2_attn_o_b", "L3_attn_W_proj", "L3_attn_b_proj"):
        d[n] = a[n]
    context = a["ctx_1024"].transpose(2, 0, 1)
    d["ctx_T"] = context.reshape(D, -1)
    d["ctx"] = a["ctx_1024"]
    d["ctx_sel_T"] = context[:, :, rows].reshape(D, -1)
    for n in ("Wq_c", "Wk_c", "Wv_c", "Wv_s", "Wq_s", "Wg"):
        d[f"L0_xattn_{n}_T"] = a["L0_xattn_" + n].T
    for n in ("Wk_s", "bv_c", "bv_s", "bg"):
        d["L0_xattn_" + n] = a["L0_xattn_" + n]
    for n in ("Wq", "Wk", "Wv", "Wo"):
        d[f"L1_attn_{n}_T"] = a["L1_attn_" + n].T
    d["L1_attn_bo"] = a["L1_attn_bo"]
    d["ctx_tail"] = context[:, :, KEYS - 1]
    d["mask_int"] = a["mask_BxS2_ik0"].reshape(-1)
    d["mask_bool"] = a["mask_Bx1x1xS2_bf1"].view(np.uint8).reshape(-1)
    d["fside"] = a["fside_1x1xSxS2_0"].reshape(S, KEYS)
    for n in ("L1_xattn_", "L2_xattn_"):
        for k in "qkv":
            d[n + "W" + k + "_T"] = a[n + "W" + k].T
        d[n + "o"] = a[n + "Wo"].T.reshape(G, HG, HD, D).transpose(0, 2, 1, 3).reshape(GD, HG, D)
        d[n + "bv"], d[n + "bo"] = a[n + "bv"], a[n + "bo"]
    for k in "qkv":
        d["L3_xattn_W" + k] = a["L3_xattn_W" + k].reshape(D, D)
    d["L3_xattn_o"] = a["L3_xattn_Wo"].reshape(G, HG, HD, D).transpose(0, 2, 1, 3).reshape(GD, HG, D)
    for n in ("attn_w", "next_w"):
        d[f"L0_ffn_{n}_T"] = a["L0_ffn_" + n].T
    for n in ("next_b", "w1", "w2"):
        d["L0_ffn_" + n] = a["L0_ffn_" + n]
    for n in ("b1", "b2"):
        d[f"L0_ffn_{n}_col"] = a["L0_ffn_" + n].reshape(8, -1, P).transpose(0, 2, 1)
    for n in ("L2_ffn_router", "L3_ffn_router"):
        d[n] = a[n + "_w"].T.reshape(C, P, 8).transpose(1, 0, 2)
    for n in ("L2_ffn_experts_bias", "L3_ffn_router_bias", "L3_ffn_ew1", "L3_ffn_ew2"):
        d[n] = a[n]
    for n in ("w1", "w3", "w2"):
        d[f"L2_ffn_{n}_all"] = np.concatenate([a["L2_ffn_" + n], a["L2_ffn_s" + n]])
        d["L3_ffn_s" + n] = a["L3_ffn_s" + n][None]
    d["L1_ffn_w_q"] = a["L1_ffn_w_q"]
    d["L1_ffn_keys_by_dim"] = a["L1_ffn_keys"].transpose(3, 2, 0, 1).reshape(P, 2 * PH, NK)
    experts = a["L1_ffn_key_in"].reshape(NK, 2, NK // 2, D)
    d["L1_ffn_key_in_by_expert"] = experts.transpose(3, 2, 1, 0).reshape(D, NK // 2, P)
    experts = a["L1_ffn_key_out"].reshape(NK, 2, NK // 2, D)
    d["L1_ffn_key_out_by_expert"] = experts.transpose(1, 0, 2, 3).reshape(P, NK // 2, D)
    for n in COLUMNS:
        v = d.pop(n) if n in d else a[n]
        d[n + "_col"] = v.reshape(-1, P).T
    d["L3_attn_slopes_by_head"] = a["L3_attn_slopes"].reshape(C, 2, HG).transpose(2, 1, 0).reshape(HG, G)
    return {k: np.ascontiguousarray(v) for k, v in d.items()}, where


def kernel(**inputs):
    import concourse.bacc as bacc
    from concourse.bass_utils import run_bass_kernel_spmd

    nc = bacc.Bacc("TRN2", target_bir_lowering=False, num_devices=1)
    arrays, where = laid_out(inputs)
    aps, fed = {}, {}
    for name, a in arrays.items():
        fed[f"in_{name}_dram"] = a
        aps[name] = nc.dram_tensor(f"in_{name}_dram", a.shape, mybir.dt.from_np(a.dtype), kind="ExternalInput").ap()
    out = nc.dram_tensor("out_0_dram", (T, D), F32, kind="ExternalOutput").ap()
    perceiver(nc, aps, where, out)
    r = run_bass_kernel_spmd(nc, [fed], core_ids=[0])
    return r.results[0]["out_0_dram"].reshape(B, S, D)
```

```python
from contextlib import ExitStack

import numpy as np

import concourse.bass as bass
from concourse import mybir
from concourse.alu_op_type import AluOpType as ALU

ACT = mybir.ActivationFunctionType
F32 = mybir.dt.float32
BF16 = mybir.dt.bfloat16
I32 = mybir.dt.int32
U8 = mybir.dt.uint8
U32 = mybir.dt.uint32
X = mybir.AxisListType.X

P = 128
D = 256
C = D // P
B = 64
S = 32
KEYS = 257
T = B * S
NT = T // P
BT = P // S
H = 16
HD = D // H
G = 4
HG = H // G
GD = HG * HD
MASKED = -3.4028234663852886e38
EPS = 1e-5


def constant_tables():
    p = np.arange(P)
    parts = {
        "ident": np.eye(P),
        "minus_half": np.full((P, 1), -0.5),
        "head_of_feature": 0.25 * ((p[:, None] % GD) // HD == np.arange(HG)[None]),
        "quarter": (p[:, None] // S == np.arange(4)[None]),
        "relative": np.minimum(np.arange(S)[None] - (p % S)[:, None], 0),
        "later": np.where(np.arange(S)[None] > (p % S)[:, None], -1e30, 0.0),
        "iota": np.broadcast_to(np.arange(P), (P, P)),
        "group_rows": np.repeat((p[:, None] % S == (np.arange(G) % 2 * 2 + np.arange(G) // 2)[None]), GD, axis=1),
    }
    inv = (1.0 / 10000.0 ** (np.arange(0, HD, 2, dtype=np.float32) / HD)).astype(np.float32)
    freq = np.arange(S, dtype=np.float32)[:, None] * inv[None]
    emb = np.concatenate([freq, freq], axis=-1).astype(np.float32)
    sign = np.where(np.arange(HD) < HD // 2, -1.0, 1.0)
    parts["cosine"] = np.cos(emb).T[p % HD]
    parts["sine"] = (np.sin(emb).T * sign[:, None])[p % HD]
    pos = np.clip((np.arange(S, dtype=np.float32) + 0.5) * np.float32(KEYS / S) - 0.5, 0.0, KEYS - 1)
    lo = np.floor(pos).astype(np.int64)
    hi = np.minimum(lo + 1, KEYS - 1)
    w = (pos - lo).astype(np.float32)
    inter = np.zeros((64, S), np.float32)
    inter[2 * np.arange(S), np.arange(S)] = 1 - w
    inter[2 * np.arange(S) + 1, np.arange(S)] = w
    parts["interpolate"] = np.concatenate([inter, inter], axis=0)
    where, at = {}, 0
    for name, a in parts.items():
        where[name] = (at, a.shape[1])
        at += a.shape[1]
    table = np.concatenate([np.asarray(a, np.float32) for a in parts.values()], axis=1)
    return np.ascontiguousarray(table), where, np.stack([lo, hi], axis=1).reshape(-1)


class Core:

    def __init__(self, nc, inputs, x_sb, const, where):
        self.nc, self.inputs, self.x, self.const, self.where = nc, inputs, x_sb, const, where

    def table(self, name, rows=P):
        at, n = self.where[name]
        return self.const[0:rows, at:at + n]

    def weight(self, name):
        return self.inputs[name].rearrange("(c p) n -> p c n", p=P)

    def column(self, name):
        return self.inputs[name + "_col"]

    def rows(self, name, n=P):
        a = self.inputs[name].rearrange("(a d) -> a d", a=1)
        return a.broadcast_to([n, a.shape[1]])


def semaphores(nc, tag, names):
    return {n: nc.alloc_semaphore(f"{tag}_{n}") for n in names.split()}


LN_SEMS = "var_ready stats_ready mean_ready rstd_ready xn_ready"


def wait(engine, sem, n):
    engine.wait_ge(sem, n)
    engine.nop(nofuse=True)


def layer_norm_root(pool, nc, s, n, mean, rstd, minus_half):
    wait(pool, s["mean_ready"], n)
    nc.gpsimd.tensor_scalar(mean[:, 1:2], mean[:, 1:2], EPS, None, ALU.add).then_inc(s["var_ready"], 1)
    pool.wait_ge(s["var_ready"], n)
    nc.gpsimd.tensor_tensor(rstd, mean[:, 1:2], minus_half, ALU.pow).then_inc(s["rstd_ready"], 1)


def after(engine, sem, count, alone=False):
    if isinstance(count, int) and count < 1:
        return
    if alone:
        wait(engine, sem, count)
    else:
        engine.wait_ge(sem, count)


def staged_tiles(engine, turn, count=NT):
    turn(-2, False, False, True)
    turn(-1, False, True, True)
    turn(0, True, True, True)
    with engine.Fori(1, count - 2) as i:
        turn(i, True, True, True)
    turn(count - 2, True, True, False)
    turn(count - 1, True, False, False)


def not_first(i):
    return not (isinstance(i, int) and i == 0)


def norm_stats(dve, nc, s, n, x_tile, stats, mean):
    nc.vector.bn_stats(stats, x_tile).then_inc(s["stats_ready"], 1)
    wait(dve, s["stats_ready"], n)
    nc.vector.bn_aggr(mean, stats).then_inc(s["mean_ready"], 1)


def normed(dve, nc, s, n, x_tile, xn, mean, rstd):
    dve.wait_ge(s["rstd_ready"], n)
    nc.vector.tensor_scalar(xn, x_tile, mean[:, 0:1], rstd, ALU.subtract, ALU.mult).then_inc(s["xn_ready"], 1)


def layer_norm(dve, nc, s, n, x_tile, xn, stats, mean, rstd):
    norm_stats(dve, nc, s, n, x_tile, stats, mean)
    normed(dve, nc, s, n, x_tile, xn, mean, rstd)


def self_attention(core, tag, w, rope=False, alibi=None):
    nc = core.nc
    with ExitStack() as ctx:
        def sb(name, shape, dt=F32):
            return ctx.enter_context(nc.sbuf_tensor(f"{tag}_{name}", shape, dt))

        def ps(name, shape):
            return ctx.enter_context(nc.psum_tensor(f"{tag}_{name}", shape, F32))

        s = semaphores(nc, tag, LN_SEMS + """ weights_loaded xn_turned xnT_ready xnT4_ready qk_ready v_ready
            qT_ready kT_ready qk_kept q_spread v_spread scores_ready biased_ready max_ready shifted_ready exp_ready
            sum_ready inv_ready probs_ready probs_turned ctx_ready ctxT_ready y_ready x_biased x_done
            cleared bias_1 bias_2 rot_1 rot_2 rot_3 rot_4 rot_ready rotq_mult rotk_mult""")
        names = [k for k in ("q", "k", "v", "o", "qr", "kr") if w.get(k)]
        wt = {k: sb(f"w{k}", [P, C, D]) for k in names}
        cols = {k: sb(k, [P, C]) for k in ("bq", "bk", "bv", "bqr", "bkr") if w.get(k)}
        bo = sb("bo", [P, D])
        n_loads = len(names) + len(cols) + 1 + (HG if alibi else 0)
        stats, mean, rstd = sb("stats", [P, 6]), sb("mean", [P, 2]), sb("rstd", [P, 1])
        xn = sb("xn", [P, D])
        xnT = sb("xnT", [P, C, P])
        xnT_four = sb("xnT_four", [P, C, BT, HG, S])
        qT, kT = sb("qT", [P, C, P]), sb("kT", [P, C, P]) if rope else None
        k_by_half = sb("k_by_half", [P, C, BT, 2, S])
        q_by_head = sb("q_by_head", [P, C, BT, HG, S])
        v_by_head = sb("v_by_head", [P, BT, G, HG, HD])
        biased = sb("biased", [P, BT * G, S])
        big, rsum, rinv = sb("big", [P, BT * G]), sb("rsum", [P, BT * G]), sb("rinv", [P, BT * G])
        shifted = sb("shifted", [P, BT * G, S])
        probs = sb("probs", [P, BT * G, S])
        probsT = sb("probsT", [P, BT * G, S])
        ctxT = sb("ctxT", [P, C, P])
        x_plus_bo = sb("x_plus_bo", [P, D])
        if rope:
            qrot, krot = sb("qrot", [P, C, P]), sb("krot", [P, C, P])
        if alibi:
            slope = sb("slope", [P, G])
            bias = sb("bias", [P, G, S])
        ps_t = ps("ps_t", [P, C, P])
        ps_qk = ps("ps_qk", [P, 2, C, P])
        ps_qkr = ps("ps_qkr", [P, 2, C, P]) if rope else None
        ps_v = ps("ps_v", [P, BT, D])
        ps_s = ps("ps_s", [P, BT * G, S])
        ps_oy = ps("ps_oy", [P, 2, C, P])
        ps_o, ps_y = ps_oy[:, 0], ps_oy[:, 1].rearrange("p c n -> p (c n)")
        ident = core.table("ident")
        head_of_feature = core.table("head_of_feature")
        quarter = core.table("quarter")
        block = ctx.enter_context(nc.Block())

        @block.sync
        def _(sp):
            for k in names:
                sp.dma_start(wt[k][:], core.weight(w[k])).then_inc(s["weights_loaded"], 16)
            for k in cols:
                sp.dma_start(cols[k][:], core.column(w[k])).then_inc(s["weights_loaded"], 16)
            sp.dma_start(bo[:], core.rows(w["bo"])).then_inc(s["weights_loaded"], 16)
            if alibi:
                by_head = core.inputs[alibi + "_by_head"]
                for h in range(HG):
                    sp.dma_start(slope[S * h:S * h + S],
                                 by_head[h:h + 1].broadcast_to([S, G])).then_inc(
                        s["weights_loaded"], 16)

        @block.gpsimd
        def _(pool):
            pool.wait_ge(s["weights_loaded"], 16 * n_loads)

            def turn(i, now, ahead, ahead2):
                if ahead2:
                    layer_norm_root(pool, nc, s, i + 3, mean[:], rstd[:], core.table("minus_half"))
                if now:
                    after(pool, s["x_done"], i)
                    nc.gpsimd.tensor_tensor(x_plus_bo[:], core.x[:, i, :], bo[:], ALU.add).then_inc(s["x_biased"], 1)

            staged_tiles(pool, turn)

        @block.tensor
        def _(pe):
            pe.wait_ge(s["weights_loaded"], 16 * n_loads)

            def turn_xn(n):
                after(pe, s["xnT4_ready"], n - 1)
                pe.wait_ge(s["xn_ready"], n)
                nc.tensor.transpose(ps_t[:, 0, :], xn[:, 0:P], ident)
                nc.tensor.transpose(ps_t[:, 1, :], xn[:, P:D], ident).then_inc(s["xn_turned"], 1)

            def queries_and_keys(n):
                after(pe, s["qk_kept"], n - 1)
                pe.wait_ge(s["xnT_ready"], n)
                for a, k in enumerate(("q", "k")):
                    for dst, kk in ((ps_qk, k), (ps_qkr, k + "r")):
                        if kk in wt:
                            for o in range(C):
                                for c in range(C):
                                    last = nc.tensor.matmul(dst[:, a, o, :], wt[kk][:, c, o * P:o * P + P],
                                                            xnT[:, c, :], start=(c == 0), stop=(c == C - 1))
                last.then_inc(s["qk_ready"], 1)

            def values(n):
                after(pe, s["v_spread"], n - 1)
                pe.wait_ge(s["xnT4_ready"], n)
                for b in range(BT):
                    for c in range(C):
                        last = nc.tensor.matmul(ps_v[:, b, :], xnT_four[:, c, b, :, :], wt["v"][:, c, :],
                                                start=(c == 0), stop=(c == C - 1))
                last.then_inc(s["v_ready"], 1)

            def scores(n):
                after(pe, s["biased_ready"] if alibi else s["shifted_ready"], n - 1)
                pe.wait_ge(s["kT_ready"], n)
                pe.wait_ge(s["q_spread"], n)
                for b in range(BT):
                    for c in range(C):
                        g = b * G + 2 * c
                        last = nc.tensor.matmul(ps_s[:, g:g + 2, :], q_by_head[:, c, b, :, :],
                                                k_by_half[:, c, b, :, :], start=True, stop=True)
                last.then_inc(s["scores_ready"], 1)

            def weighed_values(n):
                after(pe, s["x_done"], n - 1)
                pe.wait_ge(s["v_spread"], n)
                wait(pe, s["probs_turned"], n)
                for b in range(BT):
                    for g in range(G):
                        at = slice(GD * (g % 2), GD * (g % 2) + GD)
                        last = nc.tensor.matmul(ps_o[at, g // 2, S * b:S * b + S], v_by_head[:, b, g, :, :],
                                                probsT[:, b * G + g, :], start=True, stop=True)
                last.then_inc(s["ctx_ready"], 1)

            def output(n):
                pe.wait_ge(s["ctxT_ready"], n)
                for c in range(C):
                    last = nc.tensor.matmul(ps_y[:], ctxT[:, c, :], wt["o"][:, c, :], start=(c == 0), stop=(c == C - 1))
                last.then_inc(s["y_ready"], 1)

            def turn(i, now, ahead, ahead2):
                if now:
                    scores(i + 1)
                if ahead:
                    queries_and_keys(i + 2)
                    values(i + 2)
                if now:
                    weighed_values(i + 1)
                if ahead2:
                    turn_xn(i + 3)
                if now:
                    output(i + 1)

            staged_tiles(pe, turn)

        @block.scalar
        def _(act):
            act.wait_ge(s["weights_loaded"], 16 * n_loads)

            def keep_xnT(n):
                after(act, s["v_ready"], n - 1)
                act.wait_ge(s["xn_turned"], n)
                nc.scalar.copy(xnT[:], ps_t[:]).then_inc(s["xnT_ready"], 1)
                for c in range(C):
                    last = nc.scalar.copy(xnT_four[:, c], ps_t[:, c, :].rearrange("p (b k) -> p b k", b=BT)
                                          .unsqueeze(2).broadcast_to([P, BT, HG, S]))
                last.then_inc(s["xnT4_ready"], 1)

            def kept(dst, src, column, at=slice(0, P)):
                if column in cols:
                    return lambda c: nc.scalar.activation(dst(c), src(c), ACT.Identity,
                                                          bias=cols[column][at, c:c + 1])
                return lambda c: nc.scalar.copy(dst(c), src(c))

            def keep_queries_and_keys(n):
                after(act, s["q_spread"], n - 1)
                after(act, s["kT_ready"] if rope else s["scores_ready"], n - 1)
                act.wait_ge(s["qk_ready"], n)
                for c in range(C):
                    last = kept(lambda c: qT[:, c, :], lambda c: ps_qk[:, 0, c, :], "bq")(c)
                last.then_inc(s["qT_ready"], 1)
                for c in range(C):
                    if rope:
                        last = kept(lambda c: kT[:, c, :], lambda c: ps_qk[:, 1, c, :], "bk")(c)
                    else:
                        for half in range(2):
                            at = slice(GD * half, GD * half + GD)
                            last = kept(lambda c: k_by_half[at, c, :, half, :],
                                        lambda c: ps_qk[at, 1, c, :].rearrange("p (b k) -> p b k", b=BT), "bk",
                                        at)(c)
                last.then_inc(s["rotk_mult"] if rope else s["kT_ready"], 1)
                if rope:
                    for a, (dst, column) in enumerate(((qrot, "bqr"), (krot, "bkr"))):
                        for c in range(C):
                            last = kept(lambda c: dst[:, c, :], lambda c: ps_qkr[:, a, c, :], column)(c)
                    last.then_inc(s["rotq_mult"], 1)
                wait(act, s["rotq_mult"] if rope else s["kT_ready"], n)
                act.sem_inc(s["qk_kept"], 1)

            def exps(n):
                act.wait_ge(s["shifted_ready"], n)
                nc.scalar.activation(shifted[:], shifted[:], ACT.Exp).then_inc(s["exp_ready"], 1)

            def spread_values(n):
                after(act, s["ctx_ready"], n - 1)
                act.wait_ge(s["v_ready"], n)
                for h in range(HG):
                    last = nc.scalar.activation(
                        v_by_head[:, :, :, h, :], ps_v[:].rearrange("p b (g h d) -> p b g h d", g=G, h=HG)[:, :, :, h, :],
                        ACT.Copy, scale=quarter[:, h:h + 1])
                last.then_inc(s["v_spread"], 1)

            def keep_context(n):
                after(act, s["y_ready"], n - 1)
                act.wait_ge(s["ctx_ready"], n)
                for c in range(C):
                    last = kept(lambda c: ctxT[:, c, :], lambda c: ps_o[:, c, :], "bv")(c)
                last.then_inc(s["ctxT_ready"], 1)

            def turn(i, now, ahead, ahead2):
                if now:
                    exps(i + 1)
                if ahead:
                    keep_queries_and_keys(i + 2)
                if now:
                    keep_context(i + 1)
                if ahead:
                    spread_values(i + 2)
                if ahead2:
                    keep_xnT(i + 3)

            act.wait_ge(s["cleared"], 1)
            staged_tiles(act, turn)

        @block.vector
        def _(dve):
            nc.vector.memset(k_by_half[:], 0.0).then_inc(s["cleared"], 1)
            dve.wait_ge(s["cleared"], 1)
            dve.wait_ge(s["weights_loaded"], 16 * n_loads)
            if alibi:
                for g in range(G):
                    last = nc.vector.tensor_scalar(bias[:, g, :], core.table("relative"), slope[:, g:g + 1], None,
                                                   ALU.mult)
                last.then_inc(s["bias_1"], 1)
                dve.wait_ge(s["bias_1"], 1)
                nc.vector.tensor_tensor(bias[:], bias[:], core.table("later").unsqueeze(1).broadcast_to([P, G, S]),
                                        ALU.add).then_inc(s["bias_2"], 1)
                dve.wait_ge(s["bias_2"], 1)

            def rotate(n):
                def turns(name):
                    return core.table(name).unsqueeze(1).broadcast_to([P, C * BT, S])

                def flat(t):
                    return t[:].rearrange("p c (b q) -> p (c b) q", b=BT)

                dve.wait_ge(s["rotk_mult"], n)
                nc.vector.tensor_tensor(flat(kT), flat(kT), turns("cosine"), ALU.mult)
                dve.wait_ge(s["rotq_mult"], n)
                nc.vector.tensor_tensor(flat(krot), flat(krot), turns("sine"), ALU.mult).then_inc(s["rot_2"], 1)
                nc.vector.tensor_tensor(flat(qT), flat(qT), turns("cosine"), ALU.mult)
                nc.vector.tensor_tensor(flat(qrot), flat(qrot), turns("sine"), ALU.mult).then_inc(s["rot_1"], 1)
                dve.wait_ge(s["rot_2"], n)
                after(dve, s["scores_ready"], n - 1)
                for half in range(2):
                    at = slice(GD * half, GD * half + GD)
                    last = nc.vector.tensor_tensor(k_by_half[at, :, :, half, :],
                                                   kT[at].rearrange("p c (b k) -> p c b k", b=BT),
                                                   krot[at].rearrange("p c (b k) -> p c b k", b=BT), ALU.add)
                last.then_inc(s["kT_ready"], 1)
                dve.wait_ge(s["rot_1"], n)
                nc.vector.tensor_tensor(qT[:], qT[:], qrot[:], ALU.add).then_inc(s["rot_3"], 1)
                dve.wait_ge(s["rot_3"], n)

            def spread_queries(n):
                dve.wait_ge(s["qT_ready"], n)
                if rope:
                    rotate(n)
                after(dve, s["scores_ready"], n - 1)
                for c in range(C):
                    last = nc.vector.tensor_tensor(
                        q_by_head[:, c], qT[:, c, :].rearrange("p (b q) -> p b q", b=BT).unsqueeze(2).broadcast_to(
                            [P, BT, HG, S]),
                        head_of_feature.unsqueeze(1).unsqueeze(3).broadcast_to([P, BT, HG, S]), ALU.mult)
                last.then_inc(s["q_spread"], 1)

            def less_maximum(n):
                dve.wait_ge(s["scores_ready"], n)
                scores = ps_s[:]
                if alibi:
                    nc.vector.tensor_tensor(
                        biased[:].rearrange("p (b g) k -> p b (g k)", b=BT), ps_s[:].rearrange("p (b g) k -> p b (g k)", b=BT),
                        bias[:].rearrange("p g k -> p (g k)").unsqueeze(1).broadcast_to([P, BT, G * S]),
                        ALU.add).then_inc(s["biased_ready"], 1)
                    dve.wait_ge(s["biased_ready"], n)
                    scores = biased[:]
                nc.vector.tensor_reduce(big[:], scores, X, ALU.max).then_inc(s["max_ready"], 1)
                dve.wait_ge(s["max_ready"], n)
                nc.vector.tensor_tensor(shifted[:], scores, big[:].unsqueeze(2).broadcast_to([P, BT * G, S]),
                                        ALU.subtract).then_inc(s["shifted_ready"], 1)

            def probabilities(n):
                dve.wait_ge(s["exp_ready"], n)
                nc.vector.tensor_reduce(rsum[:], shifted[:], X, ALU.add).then_inc(s["sum_ready"], 1)
                dve.wait_ge(s["sum_ready"], n)
                nc.vector.reciprocal(rinv[:], rsum[:]).then_inc(s["inv_ready"], 1)
                dve.wait_ge(s["inv_ready"], n)
                nc.vector.tensor_tensor(probs[:], shifted[:], rinv[:].unsqueeze(2).broadcast_to([P, BT * G, S]),
                                        ALU.mult).then_inc(s["probs_ready"], 1)
                dve.wait_ge(s["probs_ready"], n)
                after(dve, s["ctx_ready"], n - 1)
                nc.vector.transpose(probsT[:].rearrange("p a k -> p (a k)"),
                                    probs[:].rearrange("p a k -> p (a k)")).then_inc(s["probs_turned"], 1)

            def add_output(i, n):
                dve.wait_ge(s["y_ready"], n)
                dve.wait_ge(s["x_biased"], n)
                nc.vector.tensor_tensor(core.x[:, i, :], ps_y[:], x_plus_bo[:], ALU.add).then_inc(s["x_done"], 1)

            def turn(i, now, ahead, ahead2):
                if now:
                    less_maximum(i + 1)
                if ahead2:
                    norm_stats(dve, nc, s, i + 3, core.x[:, i + 2, :], stats[:], mean[:])
                if now:
                    probabilities(i + 1)
                if ahead2:
                    after(dve, s["xn_turned"], i + 2)
                    normed(dve, nc, s, i + 3, core.x[:, i + 2, :], xn[:], mean[:], rstd[:])
                if ahead:
                    spread_queries(i + 2)
                if now:
                    add_output(i, i + 1)

            staged_tiles(dve, turn)


def cross_attention(core, tag, w, mask=None, mask_type=None, bias_rows=None):
    nc = core.nc
    K2 = KEYS - 1
    with ExitStack() as ctx:
        def sb(name, shape, dt=F32):
            return ctx.enter_context(nc.sbuf_tensor(f"{tag}_{name}", shape, dt))

        def ps(name, shape):
            return ctx.enter_context(nc.psum_tensor(f"{tag}_{name}", shape, F32))

        s = semaphores(nc, tag, LN_SEMS + """ weights_loaded ctx_tail_loaded xn_turned xnT_ready q_ready
            qT_ready q_spread tail_copied tail_cleared tail_keys_ready tail_keys tail_values_ready tail_values tail_half
            tail_scores_ready tail_scores y_ready x_biased x_done mask_loaded mask_bias_ready mask_read""")
        per_batch = {k: [nc.alloc_semaphore(f"{tag}_{k}{b}") for b in range(BT)] for k in
                     """ctx_loaded ctx_used k_ready kT_ready v_ready v_kept scores_ready biased_ready row_ready max_ready
                     exp_ready inv_ready probs_turned_1 probs_turned probsT_1 probsT_2 o_ready o_kept oT_ready
                     oT_kept""".split()}
        wt = {k: sb(f"w{k}", [P, C, D]) for k in "qkv"}
        wo = sb("wo", [GD, HG, D])
        cols = {k: sb(k, [P, C]) for k in ("bq", "bk") if w.get(k)}
        rows = {k: sb(k, [P, D]) for k in ("bv", "bo") if w.get(k)}
        n_loads = 4 + len(cols) + len(rows) + (HG if bias_rows else 0)
        ctx_tail = sb("ctx_tail", [P, C, B])
        ctx_sb = sb("ctx_sb", [P, BT, C, K2])
        stats, mean, rstd = sb("stats", [P, 6]), sb("mean", [P, 2]), sb("rstd", [P, 1])
        xn, xnT, qT = sb("xn", [P, D]), sb("xnT", [P, C, P]), sb("qT", [P, C, P])
        q_by_head = sb("q_by_head", [P, C, BT, HG, S])
        tail_rep = sb("tail_rep", [P, C, BT, S])
        k_tail = sb("k_tail", [P, C, BT, 2])
        s_tail = sb("s_tail", [P, BT, G])
        v_tail = sb("v_tail", [P, D])
        kT = sb("kT", [P, 2, C, K2])
        v = sb("v", [P, BT, 2, D])
        scores = sb("scores", [P, BT, G, KEYS])
        n_bias = BT if mask else 1
        bias = sb("bias", [P, n_bias, KEYS]) if mask or bias_rows else None
        mask_raw = sb("mask_raw", [P, BT, KEYS], mask_type) if mask else None
        minus_big, rsum, rinv = sb("minus_big", [P, BT, G]), sb("rsum", [P, BT, G]), sb("rinv", [P, BT, G])
        probsT = sb("probsT", [P, 2, G, P])
        probsT_tail = sb("probsT_tail", [P, P])
        o = sb("o", [P, BT, G, HD])
        oT = sb("oT", [GD, HG, BT, S])
        x_plus_bo = sb("x_plus_bo", [P, D])
        ps_s = ps("ps_s", [P, 2, 2, K2])
        ps_k = ps("ps_k", [P, C, K2])
        ps_v = ps("ps_v", [P, 2, D])
        ps_p = ps("ps_p", [P, 2, G, P])
        ps_a = ps("ps_a", [P, 512])
        ps_o, ps_oT, ps_pt = ps_a[:, 0:256], ps_a[0:GD, 256:384], ps_a[:, 384:512]
        ps_b = ps("ps_b", [P, 512])
        ps_t, ps_vt = ps_b[:, 0:256], ps_b[:, 256:512]
        ident = core.table("ident")
        block = ctx.enter_context(nc.Block())

        def j_of(g):
            return (g % 2) * 2 + g // 2

        @block.sync
        def _(sp):
            for k in "qkv":
                sp.dma_start(wt[k][:], core.weight(w[k])).then_inc(s["weights_loaded"], 16)
            sp.dma_start(wo[:], core.inputs[w["o"]]).then_inc(s["weights_loaded"], 16)
            for k in cols:
                sp.dma_start(cols[k][:], core.column(w[k])).then_inc(s["weights_loaded"], 16)
            for k in rows:
                sp.dma_start(rows[k][:], core.rows(w[k])).then_inc(s["weights_loaded"], 16)
            if bias_rows:
                for h in range(HG):
                    sp.dma_start(bias[S * h:S * h + S, 0, :], core.inputs[bias_rows]).then_inc(
                        s["weights_loaded"], 16)
            sp.dma_start(ctx_tail[:], core.inputs["ctx_tail"].rearrange("(c p) b -> p c b", p=P)).then_inc(
                s["ctx_tail_loaded"], 16)
            context = core.inputs["ctx_T"].rearrange("(c p) (t b k) -> p t b c k", p=P, b=BT, k=KEYS)
            if mask:
                mask_rows = core.inputs[mask].rearrange("(t n) -> t n", n=BT * KEYS)
            with sp.Fori(0, NT) as i:
                if mask:
                    wait(sp, s["mask_read"], i + 1)
                    sp.dma_start(mask_raw[:].rearrange("p b k -> p (b k)"),
                                 mask_rows[bass.ds(i, 1), :].broadcast_to([P, BT * KEYS])).then_inc(s["mask_loaded"], 16)
                for b in range(BT):
                    wait(sp, per_batch["ctx_used"][b], i + 1)
                    sp.dma_start(ctx_sb[:, b], context[:, i, b, :, 0:K2]).then_inc(
                        per_batch["ctx_loaded"][b], 16)

        def all_tiles(engine, turn):
            turn(0, first=True, last=False)
            with engine.Fori(1, NT - 1) as i:
                turn(i, first=False, last=False)
            turn(NT - 1, first=False, last=True)

        def batch(t, n, first, last):
            if (t < 0 and first) or (t >= BT and last):
                return None
            return t % BT, n + t // BT

        @block.gpsimd
        def _(pool):
            pool.wait_ge(s["weights_loaded"], 16 * n_loads)
            pool.wait_ge(s["ctx_tail_loaded"], 16)
            if mask:
                pool.sem_inc(s["mask_read"], 1)

            def front(i, n):
                layer_norm_root(pool, nc, s, n, mean[:], rstd[:], core.table("minus_half"))
                after(pool, s["tail_values_ready"], n - 1)
                for c in range(C):
                    last = nc.gpsimd.tensor_copy(tail_rep[:, c], ctx_tail[:, c, bass.ds(i * BT, BT)].unsqueeze(2)
                                                 .broadcast_to([P, BT, S]))
                last.then_inc(s["tail_copied"], 1)

            def mask_bias(n):
                if mask:
                    after(pool, per_batch["biased_ready"][BT - 1], n - 1)
                    wait(pool, s["mask_loaded"], n * 16)
                    nc.gpsimd.tensor_scalar(bias[:], mask_raw[:], 0.0, MASKED, ALU.is_equal, ALU.mult).then_inc(
                        s["mask_bias_ready"], 1)
                    wait(pool, s["mask_bias_ready"], n)
                    pool.sem_inc(s["mask_read"], 1)

            def turn(i, first, last):
                n = i + 1
                if not last:
                    front(i + 1, n + 1)
                if "bo" in rows:
                    after(pool, s["x_done"], n - 1)
                    nc.gpsimd.tensor_tensor(x_plus_bo[:], core.x[:, i, :], rows["bo"][:], ALU.add).then_inc(
                        s["x_biased"], 1)
                if not last:
                    mask_bias(n + 1)

            front(0, 1)
            mask_bias(1)
            all_tiles(pool, turn)

        @block.tensor
        def _(pe):
            for b in range(BT):
                pe.sem_inc(per_batch["ctx_used"][b], 1)
            pe.wait_ge(s["weights_loaded"], 16 * n_loads)

            def turn_xn(n):
                after(pe, s["x_done"], n - 2)
                after(pe, s["tail_values"], n - 1)
                pe.wait_ge(s["xn_ready"], n)
                nc.tensor.transpose(ps_t[:, 0:P], xn[:, 0:P], ident)
                nc.tensor.transpose(ps_t[:, P:D], xn[:, P:D], ident).then_inc(s["xn_turned"], 1)

            def queries(n):
                pe.wait_ge(s["xnT_ready"], n)
                for oc in range(C):
                    for c in range(C):
                        last = nc.tensor.matmul(ps_t[:, oc * P:oc * P + P], wt["q"][:, c, oc * P:oc * P + P],
                                                xnT[:, c, :], start=(c == 0), stop=(c == C - 1))
                last.then_inc(s["q_ready"], 1)

            def tail_keys(n):
                pe.wait_ge(s["tail_copied"], n)
                pe.wait_ge(s["qT_ready"], n)
                for oc in range(C):
                    for c in range(C):
                        last = nc.tensor.matmul(ps_vt[:, oc * BT:oc * BT + BT], wt["k"][:, c, oc * P:oc * P + P],
                                                tail_rep[:, c, :, 0], start=(c == 0), stop=(c == C - 1))
                last.then_inc(s["tail_keys_ready"], 1)

            def tail_scores(n):
                pe.wait_ge(s["q_spread"], n)
                wait(pe, s["tail_keys"], n)
                for b in range(BT):
                    for c in range(C):
                        last = nc.tensor.matmul(ps_vt[:, (b * C + c) * 2:(b * C + c) * 2 + 2],
                                                q_by_head[:, c, b, :, :], k_tail[:, c, b, :], start=True, stop=True)
                last.then_inc(s["tail_scores_ready"], 1)

            def tail_values(n):
                pe.wait_ge(s["tail_scores"], n)
                for c in range(C):
                    last = nc.tensor.matmul(ps_vt, tail_rep[:, c, :, :], wt["v"][:, c, :],
                                            start=(c == 0), stop=(c == C - 1))
                last.then_inc(s["tail_values_ready"], 1)

            def keys_and_values(at, before):
                b, n = at
                pe.wait_ge(per_batch["ctx_loaded"][b], n * 16)
                if before:
                    pe.wait_ge(per_batch["kT_ready"][before[0]], before[1])
                for oc in range(C):
                    for c in range(C):
                        last = nc.tensor.matmul(ps_k[:, oc, :], wt["k"][:, c, oc * P:oc * P + P],
                                                ctx_sb[:, b, c, :], start=(c == 0), stop=(c == C - 1))
                last.then_inc(per_batch["k_ready"][b], 1)
                if before:
                    pe.wait_ge(per_batch["v_kept"][before[0]], before[1])
                for kc in range(2):
                    for c in range(C):
                        last = nc.tensor.matmul(ps_v[:, kc, :], ctx_sb[:, b, c, kc * P:kc * P + P],
                                                wt["v"][:, c, :], start=(c == 0), stop=(c == C - 1))
                last.then_inc(per_batch["v_ready"][b], 1)

            def score(at, before):
                b, n = at
                if before:
                    pe.wait_ge(per_batch["biased_ready"][before[0]], before[1])
                pe.wait_ge(s["q_spread"], n)
                wait(pe, per_batch["kT_ready"][b], n)
                for g in range(G):
                    rows_g = slice(GD * (g % 2), GD * (g % 2) + GD)
                    last = nc.tensor.matmul(ps_s[:, g % 2, g // 2, :], q_by_head[rows_g, g // 2, b, :, :],
                                            kT[rows_g, b % 2, g // 2, :], start=True, stop=True)
                last.then_inc(per_batch["scores_ready"][b], 1)

            def turn_probs(at, before):
                b, n = at
                pe.wait_ge(per_batch["exp_ready"][b], n)
                if before:
                    pe.wait_ge(per_batch["probsT_2"][before[0]], before[1])
                    pe.wait_ge(per_batch["probsT_1"][before[0]], before[1])
                for kc in range(2):
                    for j in range(G):
                        last = nc.tensor.transpose(ps_p[:, kc, j, :], scores[:, b, j, kc * P:kc * P + P], ident)
                    if kc == 0:
                        last.then_inc(per_batch["probs_turned_1"][b], 1)
                if before:
                    pe.wait_ge(per_batch["oT_kept"][before[0]], before[1])
                nc.tensor.matmul(ps_pt[S * b:S * b + G, :], scores[:, b, :, K2], ident, start=True,
                                 stop=True).then_inc(per_batch["probs_turned"][b], 1)

            def outputs(at):
                b, n = at
                pe.wait_ge(s["tail_values"], n)
                pe.wait_ge(per_batch["v_kept"][b], n)
                pe.wait_ge(per_batch["probsT_1"][b], n)
                wait(pe, per_batch["probsT_2"][b], n)
                nc.tensor.matmul(ps_o, probsT_tail[S * b:S * b + G, :], v_tail[S * b:S * b + G, :],
                                 start=True, stop=False, skip_group_check=True, tile_position=(S * b, 0))
                for g in range(G):
                    for kc in range(2):
                        last = nc.tensor.matmul(ps_o[:, g * GD:g * GD + GD], probsT[:, kc, j_of(g), :],
                                                v[:, b, kc, g * GD:g * GD + GD], start=False,
                                                stop=(kc == 1), skip_group_check=True)
                last.then_inc(per_batch["o_ready"][b], 1)

            def turn_outputs(at):
                b, n = at
                wait(pe, per_batch["o_kept"][b], n)
                nc.tensor.transpose(ps_oT, o[:, b].rearrange("p g d -> p (g d)"), ident).then_inc(
                    per_batch["oT_ready"][b], 1)

            def tile_output(n):
                pe.wait_ge(per_batch["oT_kept"][BT - 1], n)
                for h in range(HG):
                    last = nc.tensor.matmul(ps_t, oT[:, h, :, :], wo[:, h, :], start=(h == 0), stop=(h == HG - 1))
                last.then_inc(s["y_ready"], 1)

            def turn(i, first, last):
                n = i + 1
                for t in range(BT):
                    now, before, ahead, ahead2 = (batch(t + k, n, first, last) for k in (0, -1, 1, 2))
                    if ahead:
                        score(ahead, now)
                    if before:
                        turn_outputs(before)
                    if t == 0:
                        tail_values(n)
                    if not last and t == 1:
                        turn_xn(n + 1)
                    if not last and t == 2:
                        tail_keys(n + 1)
                    if not last and t == 3:
                        tail_scores(n + 1)
                    turn_probs(now, before)
                    if ahead2:
                        keys_and_values(ahead2, ahead)
                        wait(pe, per_batch["v_ready"][ahead2[0]], ahead2[1])
                        pe.sem_inc(per_batch["ctx_used"][ahead2[0]], 1)
                    if not last and t == 1:
                        queries(n + 1)
                    if not first and t == 0:
                        wait(pe, s["tail_values"], n)
                        tile_output(n - 1)
                    outputs(now)

            keys_and_values((0, 1), None)
            keys_and_values((1, 1), (0, 1))
            for b in range(2):
                wait(pe, per_batch["v_ready"][b], 1)
                pe.sem_inc(per_batch["ctx_used"][b], 1)
            turn_xn(1)
            queries(1)
            tail_keys(1)
            score((0, 1), None)
            tail_scores(1)
            all_tiles(pe, turn)
            turn_outputs((BT - 1, NT))
            tile_output(NT)

        @block.scalar
        def _(act):
            act.wait_ge(s["weights_loaded"], 16 * n_loads)
            nc.scalar.activation(k_tail[:], core.table("iota")[:, 0:C * BT * 2], ACT.Copy, scale=0.0).then_inc(s["tail_cleared"], 1)
            act.wait_ge(s["tail_cleared"], 1)

            def keep_xnT(n):
                act.wait_ge(s["xn_turned"], n)
                nc.scalar.copy(xnT[:].rearrange("p c n -> p (c n)"), ps_t).then_inc(s["xnT_ready"], 1)

            def keep_q(n):
                act.wait_ge(s["q_ready"], n)
                for c in range(C):
                    if "bq" in cols:
                        last = nc.scalar.activation(qT[:, c, :], ps_t[:, c * P:c * P + P], ACT.Identity,
                                                    bias=cols["bq"][:, c:c + 1])
                    else:
                        last = nc.scalar.copy(qT[:, c, :], ps_t[:, c * P:c * P + P])
                last.then_inc(s["qT_ready"], 1)

            def keep_tail_keys(n):
                act.wait_ge(s["tail_keys_ready"], n)
                for c in range(C):
                    for half in range(2):
                        at = slice(GD * half, GD * half + GD)
                        if "bk" in cols:
                            last = nc.scalar.activation(k_tail[at, c, :, half], ps_vt[at, c * BT:c * BT + BT],
                                                        ACT.Identity, bias=cols["bk"][at, c:c + 1])
                        else:
                            last = nc.scalar.copy(k_tail[at, c, :, half], ps_vt[at, c * BT:c * BT + BT])
                last.then_inc(s["tail_keys"], 1)

            def keep_keys(at, used):
                b, n = at
                act.wait_ge(per_batch["k_ready"][b], n)
                if used:
                    act.wait_ge(per_batch["scores_ready"][used[0]], used[1])
                for c in range(C):
                    if "bk" in cols:
                        last = nc.scalar.activation(kT[:, b % 2, c, :], ps_k[:, c, :], ACT.Identity,
                                                    bias=cols["bk"][:, c:c + 1])
                    else:
                        last = nc.scalar.copy(kT[:, b % 2, c, :], ps_k[:, c, :])
                last.then_inc(per_batch["kT_ready"][b], 1)

            def exps(at):
                b, n = at
                act.wait_ge(per_batch["max_ready"][b], n)
                for j in range(G):
                    last = nc.scalar.activation(scores[:, b, j, :], scores[:, b, j, :], ACT.Exp,
                                                bias=minus_big[:, b, j:j + 1], accum_out=rsum[:, b, j:j + 1])
                last.then_inc(per_batch["exp_ready"][b], 1)

            def keep_probs(at, before):
                b, n = at
                act.wait_ge(per_batch["probs_turned_1"][b], n)
                if before:
                    act.wait_ge(per_batch["o_ready"][before[0]], before[1])
                nc.scalar.copy(probsT[:, 0], ps_p[:, 0]).then_inc(per_batch["probsT_1"][b], 1)

            def keep_outputs(at):
                b, n = at
                if b == 0:
                    after(act, s["y_ready"], n - 1)
                act.wait_ge(per_batch["oT_ready"][b], n)
                nc.scalar.copy(oT[:, :, b, :], ps_oT.rearrange("p (h q) -> p h q", h=HG)).then_inc(
                    per_batch["oT_kept"][b], 1)

            def turn(i, first, last):
                n = i + 1
                for t in range(BT):
                    now, before, ahead, ahead2 = (batch(t + k, n, first, last) for k in (0, -1, 1, 2))
                    if before:
                        keep_outputs(before)
                    if not last and t == 1:
                        keep_xnT(n + 1)
                    if not last and t == 2:
                        keep_tail_keys(n + 1)
                    keep_probs(now, before)
                    if ahead:
                        exps(ahead)
                    if ahead2:
                        keep_keys(ahead2, now)
                    if not last and t == 1:
                        keep_q(n + 1)

            keep_keys((0, 1), None)
            keep_keys((1, 1), None)
            keep_xnT(1)
            keep_q(1)
            keep_tail_keys(1)
            exps((0, 1))
            all_tiles(act, turn)
            keep_outputs((BT - 1, NT))

        @block.vector
        def _(dve):
            dve.wait_ge(s["weights_loaded"], 16 * n_loads)

            def norm_stats(i, n):
                nc.vector.bn_stats(stats[:], core.x[:, i, :]).then_inc(s["stats_ready"], 1)
                wait(dve, s["stats_ready"], n)
                nc.vector.bn_aggr(mean[:], stats[:]).then_inc(s["mean_ready"], 1)

            def normed(i, n):
                dve.wait_ge(s["rstd_ready"], n)
                nc.vector.tensor_scalar(xn[:], core.x[:, i, :], mean[:, 0:1], rstd[:], ALU.subtract,
                                        ALU.mult).then_inc(s["xn_ready"], 1)

            def spread_q(n):
                dve.wait_ge(s["qT_ready"], n)
                after(dve, per_batch["scores_ready"][BT - 1], n - 1)
                for c in range(C):
                    last = nc.vector.tensor_tensor(
                        q_by_head[:, c], qT[:, c, :].rearrange("p (b q) -> p b q", b=BT).unsqueeze(2).broadcast_to(
                            [P, BT, HG, S]),
                        core.table("head_of_feature").unsqueeze(1).unsqueeze(3).broadcast_to([P, BT, HG, S]),
                        ALU.mult)
                last.then_inc(s["q_spread"], 1)

            def keep_tail_scores(n):
                if mask:
                    dve.wait_ge(s["mask_bias_ready"], n)
                dve.wait_ge(s["tail_scores_ready"], n)
                raw = ps_vt[:, 0:BT * G].rearrange("p (b c j) -> p b j c", b=BT, j=2)
                kept = s_tail[:].rearrange("p b (j c) -> p b j c", j=2)
                if bias is None:
                    last = nc.vector.tensor_copy(kept, raw)
                else:
                    of_tail = bias[:, :, K2:KEYS] if mask else bias[:, 0:1, K2:KEYS].broadcast_to([P, BT, 1])
                    last = nc.vector.tensor_tensor(kept, raw, of_tail.unsqueeze(3).broadcast_to([P, BT, 2, C]),
                                                   ALU.add)
                last.then_inc(s["tail_scores"], 1)

            def keep_tail_values(n):
                dve.wait_ge(s["tail_values_ready"], n)
                after(dve, per_batch["o_ready"][BT - 1], n - 1)
                if "bv" in rows:
                    nc.vector.tensor_tensor(v_tail[:], ps_vt, rows["bv"][:], ALU.add).then_inc(s["tail_half"], 1)
                else:
                    nc.vector.tensor_copy(v_tail[:], ps_vt).then_inc(s["tail_half"], 1)
                dve.wait_ge(s["tail_half"], n)
                nc.vector.tensor_tensor(v_tail[:], v_tail[:], core.table("group_rows"), ALU.mult).then_inc(
                    s["tail_values"], 1)

            def maxima(at):
                b, n = at
                dve.wait_ge(per_batch["scores_ready"][b], n)
                after(dve, per_batch["probs_turned"][b], n - 1)
                nc.vector.tensor_tensor(
                    scores[:, b, :, 0:K2], ps_s[:].rearrange("p j c k -> p (j c) k"),
                    bias[:, b if mask else 0, 0:K2].unsqueeze(1).broadcast_to([P, G, K2]), ALU.add).then_inc(
                        per_batch["biased_ready"][b], 1)
                dve.wait_ge(s["tail_scores"], n)
                nc.vector.tensor_copy(scores[:, b, :, K2], s_tail[:, b, :]).then_inc(per_batch["row_ready"][b], 1)
                dve.wait_ge(per_batch["biased_ready"][b], n)
                dve.wait_ge(per_batch["row_ready"][b], n)
                nc.vector.tensor_reduce(minus_big[:, b, :], scores[:, b], X, ALU.max, negate=True).then_inc(
                    per_batch["max_ready"][b], 1)

            def keep_values(at):
                b, n = at
                dve.wait_ge(per_batch["v_ready"][b], n)
                after(dve, per_batch["o_ready"][b], n - 1)
                if "bv" in rows:
                    last = nc.vector.tensor_tensor(v[:, b], ps_v[:], rows["bv"][:].unsqueeze(1).broadcast_to(
                        [P, 2, D]), ALU.add)
                else:
                    last = nc.vector.tensor_copy(v[:, b], ps_v[:])
                last.then_inc(per_batch["v_kept"][b], 1)

            def keep_probs(at, before):
                b, n = at
                dve.wait_ge(per_batch["probs_turned"][b], n)
                if before:
                    dve.wait_ge(per_batch["o_ready"][before[0]], before[1])
                nc.vector.tensor_copy(probsT_tail[S * b:S * b + G, :], ps_pt[S * b:S * b + G, :])
                nc.vector.tensor_copy(probsT[:, 1], ps_p[:, 1]).then_inc(per_batch["probsT_2"][b], 1)

            def keep_outputs(at):
                b, n = at
                dve.wait_ge(per_batch["exp_ready"][b], n)
                nc.vector.reciprocal(rinv[:, b, :], rsum[:, b, :]).then_inc(per_batch["inv_ready"][b], 1)
                dve.wait_ge(per_batch["o_ready"][b], n)
                dve.wait_ge(per_batch["inv_ready"][b], n)
                for h in range(HG):
                    at_h = slice(S * h, S * h + S)
                    last = nc.vector.tensor_tensor(
                        o[at_h, b].rearrange("p (c j) d -> p c j d", j=2),
                        ps_o[at_h, :].rearrange("p (c j h d) -> p c j h d", c=C, j=2, h=HG)[:, :, :, h, :],
                        rinv[at_h, b, :].rearrange("p (j c) -> p c j", j=2).unsqueeze(3).broadcast_to(
                            [S, C, 2, HD]), ALU.mult)
                last.then_inc(per_batch["o_kept"][b], 1)

            def add_output(i, n):
                dve.wait_ge(s["y_ready"], n)
                if "bo" in rows:
                    dve.wait_ge(s["x_biased"], n)
                    nc.vector.tensor_tensor(core.x[:, i, :], ps_t, x_plus_bo[:], ALU.add).then_inc(s["x_done"], 1)
                else:
                    nc.vector.tensor_tensor(core.x[:, i, :], ps_t, core.x[:, i, :], ALU.add).then_inc(s["x_done"], 1)

            def turn(i, first, last):
                n = i + 1
                for t in range(BT):
                    now, before, ahead, ahead2 = (batch(t + k, n, first, last) for k in (0, -1, 1, 2))
                    if before:
                        keep_outputs(before)
                    if not last and t == 0:
                        norm_stats(i + 1, n + 1)
                    if not last and t == 3:
                        keep_tail_scores(n + 1)
                    if ahead:
                        maxima(ahead)
                    if t == 0:
                        keep_tail_values(n)
                    keep_probs(now, before)
                    if not last and t == 2:
                        spread_q(n + 1)
                    if ahead2:
                        keep_values(ahead2)
                    if not first and t == 0:
                        add_output(i - 1, n - 1)
                    if not last and t == 0:
                        normed(i + 1, n + 1)

            norm_stats(0, 1)
            normed(0, 1)
            keep_values((0, 1))
            keep_values((1, 1))
            spread_q(1)
            keep_tail_scores(1)
            maxima((0, 1))
            all_tiles(dve, turn)
            keep_outputs((BT - 1, NT))
            add_output(NT - 1, NT)


def complex_attention(core, tag, w):
    nc = core.nc
    E = 2 * D
    CE = E // P
    scale = 1.0 / np.sqrt(D)
    with ExitStack() as ctx:
        def sb(name, shape, dt=F32):
            return ctx.enter_context(nc.sbuf_tensor(f"{tag}_{name}", shape, dt))

        def ps(name, shape):
            return ctx.enter_context(nc.psum_tensor(f"{tag}_{name}", shape, F32))

        s = semaphores(nc, tag, LN_SEMS + """ weights_loaded cleared xn_turned xnT_ready q_ready k_ready v_ready
            qT_ready kT_ready v_kept scores_ready max_ready bias_ready exp_ready inv_ready probs_ready probs_turned
            o_ready oT_ready y_ready x_biased x_done""")
        wt = {k: sb(f"w{k}", [P, C, E]) for k in "qkv"}
        wo = sb("wo", [P, CE, D])
        cols = {k: sb(k, [P, CE]) for k in ("bq", "bk", "bv")}
        bo = sb("bo", [P, D])
        stats, mean, rstd = sb("stats", [P, 6]), sb("mean", [P, 2]), sb("rstd", [P, 1])
        xn, xnT = sb("xn", [P, D]), sb("xnT", [P, C, P])
        qT, kT, v = sb("qT", [P, CE, P]), sb("kT", [P, CE, P]), sb("v", [P, E])
        big, minus_big = sb("big", [P, 1]), sb("minus_big", [P, 1])
        rsum, rinv = sb("rsum", [P, 1]), sb("rinv", [P, 1])
        probs, probsT = sb("probs", [P, S]), sb("probsT", [P, P])
        oT = sb("oT", [P, CE, P])
        x_plus_bo = sb("x_plus_bo", [P, D])
        ps_t, ps_q, ps_k = ps("ps_t", [P, D]), ps("ps_q", [P, CE, P]), ps("ps_k", [P, CE, P])
        ps_v, ps_s, ps_o, ps_y = ps("ps_v", [P, E]), ps("ps_s", [P, S]), ps("ps_o", [P, CE, P]), ps("ps_y", [P, D])
        ident = core.table("ident")
        block = ctx.enter_context(nc.Block())

        @block.sync
        def _(sp):
            for k in "qkv":
                sp.dma_start(wt[k][:], core.weight(w[k])).then_inc(s["weights_loaded"], 16)
            sp.dma_start(wo[:], core.weight(w["o"])).then_inc(s["weights_loaded"], 16)
            for k in cols:
                sp.dma_start(cols[k][:], core.column(w[k])).then_inc(s["weights_loaded"], 16)
            sp.dma_start(bo[:], core.rows(w["bo"])).then_inc(s["weights_loaded"], 16)

        @block.gpsimd
        def _(pool):
            pool.wait_ge(s["weights_loaded"], 16 * 8)

            def turn(i, now, ahead, ahead2):
                if ahead2:
                    layer_norm_root(pool, nc, s, i + 3, mean[:], rstd[:], core.table("minus_half"))
                if now:
                    after(pool, s["x_done"], i)
                    nc.gpsimd.tensor_tensor(x_plus_bo[:], core.x[:, i, :], bo[:], ALU.add).then_inc(s["x_biased"], 1)

            staged_tiles(pool, turn)

        @block.tensor
        def _(pe):
            pe.wait_ge(s["weights_loaded"], 16 * 8)

            def turn_xn(n):
                after(pe, s["xnT_ready"], n - 1)
                pe.wait_ge(s["xn_ready"], n)
                for c in range(C):
                    last = nc.tensor.transpose(ps_t[:, c * P:c * P + P], xn[:, c * P:c * P + P], ident)
                last.then_inc(s["xn_turned"], 1)

            def queries_and_keys(n):
                pe.wait_ge(s["xnT_ready"], n)
                for k, dst in (("q", ps_q), ("k", ps_k)):
                    after(pe, s[k + "T_ready"], n - 1)
                    for oc in range(CE):
                        for c in range(C):
                            last = nc.tensor.matmul(dst[:, oc, :], wt[k][:, c, oc * P:oc * P + P], xnT[:, c, :],
                                                    start=(c == 0), stop=(c == C - 1))
                    last.then_inc(s[k + "_ready"], 1)

            def values(n):
                after(pe, s["v_kept"], n - 1)
                for c in range(C):
                    last = nc.tensor.matmul(ps_v[:], xnT[:, c, :], wt["v"][:, c, :], start=(c == 0), stop=(c == C - 1))
                last.then_inc(s["v_ready"], 1)

            def scores(n):
                after(pe, s["exp_ready"], n - 1)
                pe.wait_ge(s["qT_ready"], n)
                wait(pe, s["kT_ready"], n)
                for b in range(BT):
                    at = slice(S * b, S * b + S)
                    for c in range(CE):
                        last = nc.tensor.matmul(ps_s[at, :], qT[:, c, at], kT[:, c, at],
                                                start=(c == 0), stop=(c == CE - 1))
                last.then_inc(s["scores_ready"], 1)

            def weighed_values(n):
                pe.wait_ge(s["v_kept"], n)
                pe.wait_ge(s["probs_turned"], n)
                after(pe, s["oT_ready"], n - 1)
                for c in range(CE):
                    last = nc.tensor.matmul(ps_o[:, c, :], v[:, c * P:c * P + P], probsT[:], start=True, stop=True)
                last.then_inc(s["o_ready"], 1)

            def output(n):
                after(pe, s["x_done"], n - 1)
                pe.wait_ge(s["oT_ready"], n)
                for c in range(CE):
                    last = nc.tensor.matmul(ps_y[:], oT[:, c, :], wo[:, c, :], start=(c == 0), stop=(c == CE - 1))
                last.then_inc(s["y_ready"], 1)

            def turn(i, now, ahead, ahead2):
                if now:
                    scores(i + 1)
                if ahead:
                    queries_and_keys(i + 2)
                if now:
                    weighed_values(i + 1)
                if ahead:
                    values(i + 2)
                if ahead2:
                    turn_xn(i + 3)
                if now:
                    output(i + 1)

            staged_tiles(pe, turn)

        @block.scalar
        def _(act):
            act.wait_ge(s["weights_loaded"], 16 * 8)

            def keep_xnT(n):
                after(act, s["v_ready"], n - 1)
                act.wait_ge(s["xn_turned"], n)
                nc.scalar.copy(xnT[:].rearrange("p c n -> p (c n)"), ps_t[:]).then_inc(s["xnT_ready"], 1)

            def keep_queries_and_keys(n):
                after(act, s["scores_ready"], n - 1)
                for k, dst, src in (("q", qT, ps_q), ("k", kT, ps_k)):
                    act.wait_ge(s[k + "_ready"], n)
                    for c in range(CE):
                        last = nc.scalar.activation(dst[:, c, :], src[:, c, :], ACT.Identity,
                                                    bias=cols["b" + k][:, c:c + 1])
                    last.then_inc(s[k + "T_ready"], 1)

            def exps(n):
                act.wait_ge(s["bias_ready"], n)
                nc.scalar.activation(probs[:], ps_s[:], ACT.Exp, bias=minus_big[:], scale=float(scale),
                                     accum_out=rsum[:]).then_inc(s["exp_ready"], 1)

            def keep_context(n):
                after(act, s["y_ready"], n - 1)
                act.wait_ge(s["o_ready"], n)
                for c in range(CE):
                    last = nc.scalar.activation(oT[:, c, :], ps_o[:, c, :], ACT.Identity, bias=cols["bv"][:, c:c + 1])
                last.then_inc(s["oT_ready"], 1)

            def turn(i, now, ahead, ahead2):
                if now:
                    exps(i + 1)
                if ahead:
                    keep_queries_and_keys(i + 2)
                if now:
                    keep_context(i + 1)
                if ahead2:
                    keep_xnT(i + 3)

            staged_tiles(act, turn)

        @block.vector
        def _(dve):
            nc.vector.memset(probsT[:], 0.0).then_inc(s["cleared"], 1)
            dve.wait_ge(s["cleared"], 1)

            def maxima(n):
                dve.wait_ge(s["scores_ready"], n)
                nc.vector.tensor_reduce(big[:], ps_s[:], X, ALU.max, negate=True).then_inc(s["max_ready"], 1)
                dve.wait_ge(s["max_ready"], n)
                nc.vector.tensor_scalar(minus_big[:], big[:], float(scale), None, ALU.mult).then_inc(s["bias_ready"], 1)

            def probabilities(n):
                dve.wait_ge(s["exp_ready"], n)
                nc.vector.reciprocal(rinv[:], rsum[:]).then_inc(s["inv_ready"], 1)
                dve.wait_ge(s["inv_ready"], n)
                nc.vector.tensor_scalar(probs[:], probs[:], rinv[:], None, ALU.mult).then_inc(s["probs_ready"], 1)
                dve.wait_ge(s["probs_ready"], n)
                after(dve, s["o_ready"], n - 1)
                for b in range(BT):
                    at = slice(S * b, S * b + S)
                    last = nc.vector.transpose(probsT[at, at], probs[at, :])
                last.then_inc(s["probs_turned"], 1)

            def keep_values(n):
                dve.wait_ge(s["v_ready"], n)
                after(dve, s["o_ready"], n - 1)
                nc.vector.tensor_copy(v[:], ps_v[:]).then_inc(s["v_kept"], 1)

            def add_output(i, n):
                dve.wait_ge(s["y_ready"], n)
                dve.wait_ge(s["x_biased"], n)
                nc.vector.tensor_tensor(core.x[:, i, :], ps_y[:], x_plus_bo[:], ALU.add).then_inc(s["x_done"], 1)

            def turn(i, now, ahead, ahead2):
                if now:
                    maxima(i + 1)
                if ahead2:
                    norm_stats(dve, nc, s, i + 3, core.x[:, i + 2, :], stats[:], mean[:])
                if now:
                    probabilities(i + 1)
                if ahead2:
                    after(dve, s["xn_turned"], i + 2)
                    normed(dve, nc, s, i + 3, core.x[:, i + 2, :], xn[:], mean[:], rstd[:])
                if ahead:
                    keep_values(i + 2)
                if now:
                    add_output(i, i + 1)

            staged_tiles(dve, turn)


SEL = 2 * S


def gated_cross_attention(core, tag):
    nc = core.nc
    K2 = KEYS - 1
    scale = float(1.0 / np.sqrt(D))
    w = "L0_xattn_"
    with ExitStack() as ctx:
        def sb(name, shape, dt=F32):
            return ctx.enter_context(nc.sbuf_tensor(f"{tag}_{name}", shape, dt))

        def ps(name):
            return ctx.enter_context(nc.psum_tensor(f"{tag}_{name}", [P, 512], F32))

        s = semaphores(nc, tag, LN_SEMS + """ weights_loaded cleared sel_loaded ctx_loaded
            rows_loaded rows_used xn_turned xnT_ready
            qk_ready qkT_ready v_ready v_kept folded_ready folded_kept sel_ready sel_kept s1_ready max1_ready
            shift1_ready bias1_ready exp1_ready inv1_ready probs1_turned probs1T_ready pc_ready pcT_ready c2s_ready
            c2s_kept s2_ready max2_ready bias2_ready exp2_ready inv2_ready probs2_ready ip_ready ip_kept s2c_ready
            s2c_kept diff_ready gate_in_turned gate_in_ready z_ready z_kept e_ready one_plus gate_ready mixed x_plus
            x_done""")
        names = ("Wq_c_T", "Wk_c_T", "Wv_c_T", "Wk_s", "Wv_s_T", "Wq_s_T")
        wt = {k: sb(k, [P, C, D]) for k in names}
        wg = sb("wg", [P, 2 * C, D])
        cols = {k: sb(k, [P, C]) for k in ("bq_c", "bk_c", "bk_s", "bq_s")}
        rows = {k: sb(k, [P, D]) for k in ("bv_c", "bv_s", "bg")}
        n_loads = len(names) + 1 + len(cols) + len(rows)
        ctxT = sb("ctxT", [P, C, BT, KEYS])
        ctx_rows = sb("ctx_rows", [P, BT, 2, D])
        ctx_last = sb("ctx_last", [1, BT, D])
        ctx_sel = sb("ctx_sel", [P, C, BT * SEL])
        stats, mean, rstd = sb("stats", [P, 6]), sb("mean", [P, 2]), sb("rstd", [P, 1])
        xn, xnT = sb("xn", [P, D]), sb("xnT", [P, C, P])
        qT, kT, v = sb("qT", [P, C, P]), sb("kT", [P, C, P]), sb("v", [P, D])
        folded = sb("folded", [P, C, P])
        q_bk = sb("q_bk", [P, 1])
        selT = sb("selT", [P, C, BT * SEL])
        big1, sum1, bias1, rsum1, rinv1 = (sb(k, [P, 1]) for k in ("big1", "sum1", "bias1", "rsum1", "rinv1"))
        probs1, probs1T = sb("probs1", [P, KEYS]), sb("probs1T", [P, 3, P])
        pcT = sb("pcT", [P, C, P])
        c2s, s2c = sb("c2s", [P, D]), sb("s2c", [P, D])
        big2, bias2, rsum2, rinv2 = (sb(k, [P, 2]) for k in ("big2", "bias2", "rsum2", "rinv2"))
        probs2 = sb("probs2", [P, 2, S])
        ip = sb("ip", [P, P])
        gate_in = sb("gate_in", [P, 2 * C, P])
        z, e, diff = sb("z", [P, D]), sb("e", [P, D]), sb("diff", [P, D])
        ps_t, ps_qk, ps_s1, ps_v, ps_f, ps_sel, ps_x, ps_y = (ps(f"bank{k}") for k in range(8))
        ident = core.table("ident")
        block = ctx.enter_context(nc.Block())

        @block.sync
        def _(sp):
            for k in names:
                sp.dma_start(wt[k][:], core.weight(w + k)).then_inc(s["weights_loaded"], 16)
            sp.dma_start(wg[:], core.weight(w + "Wg_T")).then_inc(s["weights_loaded"], 16)
            for k in cols:
                sp.dma_start(cols[k][:], core.column(w + k)).then_inc(s["weights_loaded"], 16)
            for k in rows:
                sp.dma_start(rows[k][:], core.rows(w + k)).then_inc(s["weights_loaded"], 16)
            by_feature = core.inputs["ctx_T"].rearrange("(c p) (t n) -> p t c n", p=P, n=BT * KEYS)
            by_row = core.inputs["ctx"].rearrange("(t b) k d -> t b k d", b=BT)
            selected = core.inputs["ctx_sel_T"].rearrange("(c p) (t n) -> p t c n", p=P, n=BT * SEL)
            with sp.Fori(0, NT) as i:
                wait(sp, s["sel_ready"], i + 1)
                for c in range(C):
                    sp.dma_start(ctx_sel[:, c, :], selected[:, i, c, :]).then_inc(s["sel_loaded"], 16)
                wait(sp, s["s1_ready"], i + 1)
                for c in range(C):
                    sp.dma_start(ctxT[:, c].rearrange("p b k -> p (b k)"), by_feature[:, i, c, :]).then_inc(
                        s["ctx_loaded"], 16)
                wait(sp, s["rows_used"], i + 1)
                for b in range(BT):
                    sp.dma_start(ctx_rows[:, b], by_row[i, b, 0:K2, :].rearrange("(k p) d -> p k d", p=P)).then_inc(
                        s["rows_loaded"], 16)
                sp.dma_start(ctx_last[:], by_row[bass.ds(i, 1), :, K2, :]).then_inc(s["rows_loaded"], 16)

        @block.gpsimd
        def _(pool):
            def turn(i, now, ahead, ahead2):
                if ahead2:
                    layer_norm_root(pool, nc, s, i + 3, mean[:], rstd[:], core.table("minus_half"))

            staged_tiles(pool, turn)

        @block.tensor
        def _(pe):
            for k in ("sel_ready", "s1_ready", "rows_used"):
                pe.sem_inc(s[k], 1)
            pe.wait_ge(s["weights_loaded"], 16 * n_loads)

            def product(dst, lhsT, rhs, count=C):
                for c in range(count):
                    last = nc.tensor.matmul(dst, lhsT(c), rhs(c), start=(c == 0), stop=(c == count - 1))
                return last

            def chunk(oc):
                return slice(oc * P, oc * P + P)

            def turn_xn(n):
                after(pe, s["c2s_kept"], n - 2)
                pe.wait_ge(s["xn_ready"], n)
                for c in range(C):
                    last = nc.tensor.transpose(ps_t[:, chunk(c)], xn[:, chunk(c)], ident)
                last.then_inc(s["xn_turned"], 1)

            def context_queries(n):
                after(pe, s["gate_in_ready"], n - 2)
                pe.wait_ge(s["sel_loaded"], n * (16 * C))
                for oc in range(C):
                    last = product(ps_sel[:, oc * 256:oc * 256 + 256], lambda c: wt["Wq_s_T"][:, c, chunk(oc)],
                                   lambda c: ctx_sel[:, c, :])
                last.then_inc(s["sel_ready"], 1)

            def queries_and_keys(n):
                after(pe, s["probs1T_ready"], n - 2)
                pe.wait_ge(s["xnT_ready"], n)
                for a, k in enumerate(("Wq_c_T", "Wk_c_T")):
                    for oc in range(C):
                        last = product(ps_qk[:, chunk(2 * a + oc)], lambda c: wt[k][:, c, chunk(oc)],
                                       lambda c: xnT[:, c, :])
                last.then_inc(s["qk_ready"], 1)

            def values(n):
                after(pe, s["s2c_kept"], n - 1)
                product(ps_v[:, 0:D], lambda c: xnT[:, c, :], lambda c: wt["Wv_c_T"][:, c, :]).then_inc(s["v_ready"], 1)

            def fold_queries(n):
                pe.wait_ge(s["qkT_ready"], n)
                after(pe, s["pcT_ready"], n - 1)
                for oc in range(C):
                    product(ps_f[:, chunk(oc)], lambda c: wt["Wk_s"][:, c, chunk(oc)], lambda c: qT[:, c, :])
                product(ps_f[:, D:D + 1], lambda c: qT[:, c, :], lambda c: cols["bk_s"][:, c:c + 1]).then_inc(
                    s["folded_ready"], 1)

            def scores(n):
                after(pe, s["ip_kept"], n - 1)
                wait(pe, s["sel_kept"], n)
                for b in range(BT):
                    last = product(ps_x[64 * (b % 2):64 * (b % 2) + 64, S * (b // 2):S * (b // 2) + S],
                                   lambda c: selT[:, c, SEL * b:SEL * b + SEL], lambda c: kT[:, c, S * b:S * b + S])
                last.then_inc(s["s2_ready"], 1)
                pe.wait_ge(s["ctx_loaded"], n * (16 * C))
                wait(pe, s["folded_kept"], n)
                for b in range(BT):
                    at = slice(S * b, S * b + S)
                    last = product(ps_s1[at, 0:KEYS], lambda c: folded[:, c, at], lambda c: ctxT[:, c, b, :])
                last.then_inc(s["s1_ready"], 1)

            def interpolate(n):
                after(pe, s["z_kept"], n - 1)
                wait(pe, s["probs2_ready"], n)
                for b in range(BT):
                    half = slice(64 * (b % 2), 64 * (b % 2) + 64)
                    last = nc.tensor.matmul((ps_x if b % 2 == 0 else ps_y)[S * b:S * b + S, 0:S],
                                            probs2[half, b // 2, :], core.table("interpolate")[half, :],
                                            start=True, stop=True)
                last.then_inc(s["ip_ready"], 1)

            def turn_probs(n, ahead):
                pe.wait_ge(s["exp1_ready"], n)
                if ahead:
                    pe.wait_ge(s["qkT_ready"], n + 1)
                for kc in range(2):
                    nc.tensor.transpose(ps_qk[:, chunk(kc)], probs1[:, chunk(kc)], ident)
                nc.tensor.transpose(ps_qk[0:1, chunk(2)], probs1[:, K2:KEYS], ident).then_inc(s["probs1_turned"], 1)

            def context_attention(n):
                pe.wait_ge(s["v_kept"], n)
                pe.wait_ge(s["ip_kept"], n)
                nc.tensor.matmul(ps_v[:, 0:D], ip[:], v[:], start=True, stop=True).then_inc(s["s2c_ready"], 1)

            def weighed_context(n):
                pe.wait_ge(s["rows_loaded"], n * (16 * (BT + 1)))
                wait(pe, s["probs1T_ready"], n)
                for oc in range(C):
                    for b in range(BT):
                        at = slice(S * b, S * b + S)
                        dst = ps_f[:, oc * P + S * b:oc * P + S * b + S]
                        for kc in range(2):
                            nc.tensor.matmul(dst, ctx_rows[:, b, kc, chunk(oc)], probs1T[:, kc, at],
                                             start=(kc == 0), stop=False)
                        last = nc.tensor.matmul(dst, ctx_last[0:1, b, chunk(oc)], probs1T[0:1, 2, at],
                                                start=False, stop=True)
                last.then_inc(s["pc_ready"], 1)

            def latent_attention(n):
                pe.wait_ge(s["pcT_ready"], n)
                pe.sem_inc(s["rows_used"], 1)
                product(ps_t[:, 0:D], lambda c: pcT[:, c, :], lambda c: wt["Wv_s_T"][:, c, :]).then_inc(
                    s["c2s_ready"], 1)

            def turn_gate_in(n, ahead):
                if ahead:
                    pe.wait_ge(s["sel_kept"], n + 1)
                pe.wait_ge(s["s2c_kept"], n)
                pe.wait_ge(s["c2s_kept"], n)
                for c in range(C):
                    nc.tensor.transpose(ps_sel[:, chunk(c)], c2s[:, chunk(c)], ident)
                for c in range(C):
                    last = nc.tensor.transpose(ps_sel[:, chunk(C + c)], s2c[:, chunk(c)], ident)
                last.then_inc(s["gate_in_turned"], 1)

            def gate_product(n):
                pe.wait_ge(s["ip_kept"], n)
                pe.wait_ge(s["gate_in_ready"], n)
                product(ps_y[:, 0:D], lambda c: gate_in[:, c, :], lambda c: wg[:, c, :], 2 * C).then_inc(
                    s["z_ready"], 1)

            def turn(i, now, ahead, ahead2):
                n = i + 1
                if now:
                    scores(n)
                if ahead:
                    turn_xn(n + 1)
                if now and not_first(i):
                    gate_product(n - 1)
                if ahead:
                    context_queries(n + 1)
                    queries_and_keys(n + 1)
                if now:
                    interpolate(n)
                    turn_probs(n, ahead)
                    context_attention(n)
                    weighed_context(n)
                if ahead:
                    values(n + 1)
                if now:
                    latent_attention(n)
                if ahead:
                    fold_queries(n + 1)
                if now:
                    turn_gate_in(n, ahead)

            staged_tiles(pe, turn)
            gate_product(NT)

        @block.scalar
        def _(act):
            act.wait_ge(s["weights_loaded"], 16 * n_loads)

            def with_bias(dst, src, column):
                return nc.scalar.activation(dst, src, ACT.Identity, bias=column)

            def keep_xnT(n):
                act.wait_ge(s["xn_turned"], n)
                nc.scalar.copy(xnT[:].rearrange("p c n -> p (c n)"), ps_t[:, 0:D]).then_inc(s["xnT_ready"], 1)

            def keep_selected(n):
                after(act, s["s2_ready"], n - 1)
                act.wait_ge(s["sel_ready"], n + 1)
                for c in range(C):
                    last = with_bias(selT[:, c, :], ps_sel[:, c * 256:c * 256 + 256], cols["bq_s"][:, c:c + 1])
                last.then_inc(s["sel_kept"], 1)

            def keep_queries_and_keys(n):
                act.wait_ge(s["qk_ready"], n)
                for a, (dst, k) in enumerate(((qT, "bq_c"), (kT, "bk_c"))):
                    for c in range(C):
                        last = with_bias(dst[:, c, :], ps_qk[:, (2 * a + c) * P:(2 * a + c + 1) * P],
                                         cols[k][:, c:c + 1])
                last.then_inc(s["qkT_ready"], 1)

            def keep_folded(n):
                act.wait_ge(s["folded_ready"], n)
                act.wait_ge(s["s1_ready"], n)
                after(act, s["bias1_ready"], n - 1)
                nc.scalar.copy(q_bk[:], ps_f[:, D:D + 1])
                nc.scalar.copy(folded[:].rearrange("p c n -> p (c n)"), ps_f[:, 0:D]).then_inc(s["folded_kept"], 1)

            def context_exps(n):
                act.wait_ge(s["bias2_ready"], n)
                for j in range(2):
                    last = nc.scalar.activation(probs2[:, j, :], ps_x[:, S * j:S * j + S], ACT.Exp, scale=scale,
                                                bias=bias2[:, j:j + 1], accum_out=rsum2[:, j:j + 1])
                last.then_inc(s["exp2_ready"], 1)

            def latent_exps(n):
                act.wait_ge(s["bias1_ready"], n)
                nc.scalar.activation(probs1[:], ps_s1[:, 0:KEYS], ACT.Exp, scale=scale, bias=bias1[:],
                                     accum_out=rsum1[:]).then_inc(s["exp1_ready"], 1)

            def keep_probs(n):
                after(act, s["pc_ready"], n - 1)
                act.wait_ge(s["probs1_turned"], n)
                nc.scalar.copy(probs1T[:, 0:2].rearrange("p k n -> p (k n)"), ps_qk[:, 0:2 * P])
                nc.scalar.copy(probs1T[0:1, 2, :], ps_qk[0:1, 2 * P:3 * P]).then_inc(s["probs1T_ready"], 1)

            def keep_context(n):
                after(act, s["c2s_ready"], n - 1)
                act.wait_ge(s["pc_ready"], n)
                nc.scalar.copy(pcT[:].rearrange("p c n -> p (c n)"), ps_f[:, 0:D]).then_inc(s["pcT_ready"], 1)

            def keep_gate_in(n):
                after(act, s["z_ready"], n - 1)
                act.wait_ge(s["gate_in_turned"], n)
                nc.scalar.copy(gate_in[:].rearrange("p c n -> p (c n)"), ps_sel[:]).then_inc(s["gate_in_ready"], 1)

            def gate_exps(n):
                act.wait_ge(s["z_kept"], n)
                nc.scalar.activation(e[:], z[:], ACT.Exp, scale=-1.0).then_inc(s["e_ready"], 1)

            def turn(i, now, ahead, ahead2):
                n = i + 1
                if now:
                    context_exps(n)
                    latent_exps(n)
                if ahead:
                    keep_xnT(n + 1)
                if now and not_first(i):
                    gate_exps(n - 1)
                if ahead:
                    keep_selected(n + 1)
                    keep_queries_and_keys(n + 1)
                if now:
                    keep_probs(n)
                    keep_context(n)
                if ahead:
                    keep_folded(n + 1)
                if now:
                    keep_gate_in(n)

            staged_tiles(act, turn)
            gate_exps(NT)

        @block.vector
        def _(dve):
            nc.vector.memset(ip[:], 0.0).then_inc(s["cleared"], 1)
            dve.wait_ge(s["cleared"], 1)
            dve.wait_ge(s["weights_loaded"], 16 * n_loads)

            def then(ins, name, n):
                ins.then_inc(s[name], 1)
                dve.wait_ge(s[name], n)

            def context_maxima(n):
                dve.wait_ge(s["s2_ready"], n)
                then(nc.vector.tensor_reduce(big2[:], ps_x[:, 0:2 * S].rearrange("p (j k) -> p j k", j=2), X, ALU.max,
                                             negate=True), "max2_ready", n)
                nc.vector.tensor_scalar(bias2[:], big2[:], scale, None, ALU.mult).then_inc(s["bias2_ready"], 1)

            def context_probs(n):
                dve.wait_ge(s["exp2_ready"], n)
                then(nc.vector.reciprocal(rinv2[:], rsum2[:]), "inv2_ready", n)
                nc.vector.tensor_tensor(probs2[:], probs2[:], rinv2[:].unsqueeze(2).broadcast_to([P, 2, S]),
                                        ALU.mult).then_inc(s["probs2_ready"], 1)

            def latent_maxima(n):
                dve.wait_ge(s["s1_ready"], n + 1)
                then(nc.vector.tensor_reduce(big1[:], ps_s1[:, 0:KEYS], X, ALU.max), "max1_ready", n)
                dve.wait_ge(s["folded_kept"], n)
                then(nc.vector.tensor_tensor(sum1[:], big1[:], q_bk[:], ALU.add), "shift1_ready", n)
                nc.vector.tensor_scalar(bias1[:], q_bk[:], sum1[:], scale, ALU.subtract, ALU.mult).then_inc(
                    s["bias1_ready"], 1)

            def keep_interpolated(n):
                after(dve, s["s2c_ready"], n - 1)
                dve.wait_ge(s["ip_ready"], n)
                for b in range(BT):
                    at = slice(S * b, S * b + S)
                    last = nc.vector.tensor_copy(ip[at, at], (ps_x if b % 2 == 0 else ps_y)[at, 0:S])
                last.then_inc(s["ip_kept"], 1)

            def keep_values(n):
                after(dve, s["s2c_ready"], n - 1)
                dve.wait_ge(s["v_ready"], n)
                nc.vector.tensor_tensor(v[:], ps_v[:, 0:D], rows["bv_c"][:], ALU.add).then_inc(s["v_kept"], 1)

            def keep_context_attention(n):
                after(dve, s["gate_in_turned"], n - 1)
                dve.wait_ge(s["s2c_ready"], n)
                nc.vector.tensor_copy(s2c[:], ps_v[:, 0:D]).then_inc(s["s2c_kept"], 1)

            def keep_latent_attention(i, n):
                dve.wait_ge(s["exp1_ready"], n)
                then(nc.vector.reciprocal(rinv1[:], rsum1[:]), "inv1_ready", n)
                dve.wait_ge(s["c2s_ready"], n)
                then(nc.vector.scalar_tensor_tensor(c2s[:], ps_t[:, 0:D], rinv1[:], rows["bv_s"][:], ALU.mult,
                                                    ALU.add), "c2s_kept", n)
                dve.wait_ge(s["s2c_kept"], n)
                nc.vector.tensor_tensor(diff[:], c2s[:], s2c[:], ALU.subtract).then_inc(s["diff_ready"], 1)
                nc.vector.tensor_tensor(core.x[:, i, :], core.x[:, i, :], s2c[:], ALU.add).then_inc(s["x_plus"], 1)

            def keep_gate(n):
                after(dve, s["e_ready"], n - 1)
                dve.wait_ge(s["z_ready"], n)
                nc.vector.tensor_tensor(z[:], ps_y[:, 0:D], rows["bg"][:], ALU.add).then_inc(s["z_kept"], 1)

            def apply_gate(i, n):
                dve.wait_ge(s["e_ready"], n)
                then(nc.vector.tensor_scalar(e[:], e[:], 1.0, None, ALU.add), "one_plus", n)
                then(nc.vector.reciprocal(e[:], e[:]), "gate_ready", n)
                dve.wait_ge(s["diff_ready"], n)
                then(nc.vector.tensor_tensor(diff[:], diff[:], e[:], ALU.mult), "mixed", n)
                dve.wait_ge(s["x_plus"], n)
                nc.vector.tensor_tensor(core.x[:, i, :], core.x[:, i, :], diff[:], ALU.add).then_inc(s["x_done"], 1)

            def turn(i, now, ahead, ahead2):
                n = i + 1
                if now:
                    context_maxima(n)
                    latent_maxima(n)
                    context_probs(n)
                if now and not_first(i):
                    keep_gate(n - 1)
                if now:
                    keep_interpolated(n)
                if ahead2:
                    norm_stats(dve, nc, s, n + 2, core.x[:, i + 2, :], stats[:], mean[:])
                if now:
                    keep_context_attention(n)
                if now and not_first(i):
                    apply_gate(i - 1, n - 1)
                if ahead:
                    keep_values(n + 1)
                if now:
                    keep_latent_attention(i, n)
                if ahead2:
                    after(dve, s["xn_turned"], n + 1)
                    normed(dve, nc, s, n + 2, core.x[:, i + 2, :], xn[:], mean[:], rstd[:])

            staged_tiles(dve, turn)
            keep_gate(NT)
            apply_gate(NT - 1, NT)


def fixed_experts_ffn(core, tag):
    nc = core.nc
    E, HID = 8, 4 * D
    HC = HID // P
    U = NT // E
    N = U * P
    w = "L0_ffn_"
    with ExitStack() as ctx:
        def sb(name, shape, dt=F32):
            return ctx.enter_context(nc.sbuf_tensor(f"{tag}_{name}", shape, dt))

        def ps(name, shape):
            return ctx.enter_context(nc.psum_tensor(f"{tag}_{name}", shape, F32))

        s = semaphores(nc, tag, """weights_loaded w1_loaded w2_loaded w1_used w2_used ps_t_used flatT_ready
            xn2T_ready attn_ready xaT_ready out_ready eoT_ready y_ready y_kept gelu_ready x_done""")
        ln = [[semaphores(nc, f"{tag}_ln{a}{u}", LN_SEMS) for u in range(U)] for a in range(2)]
        turned = [nc.alloc_semaphore(f"{tag}_turned{u}") for u in range(U)]
        half_read = [nc.alloc_semaphore(f"{tag}_half_read{u}") for u in range(U)]
        flat_read = [nc.alloc_semaphore(f"{tag}_flat_read{u}") for u in range(U)]
        h_ready = [nc.alloc_semaphore(f"{tag}_h_ready{k}") for k in range(HC // 2)]
        h_kept = [nc.alloc_semaphore(f"{tag}_h_kept{k}") for k in range(HC // 2)]
        attn_w, next_w = sb("attn_w", [P, C, D]), sb("next_w", [P, C, D])
        cols = {k: sb(k, [P, C]) for k in ("ln_scale", "ln_bias", "attn_b")}
        next_b = sb("next_b", [P, D])
        w1, w2 = sb("w1", [P, C, HID]), sb("w2", [P, HC, D])
        b1, b2 = sb("b1", [P, HC]), sb("b2", [P, C])
        stats, mean, rstd = sb("stats", [P, 2, U, 6]), sb("mean", [P, 2, U, 2]), sb("rstd", [P, 2, U])
        flat, xn2 = sb("flat", [P, U, D]), sb("xn2", [P, U, D])
        flatT, xn2T, xaT = sb("flatT", [P, C, N]), sb("xn2T", [P, C, N]), sb("xaT", [P, C, N])
        hT = sb("hT", [P, HC, N])
        eoT = sb("eoT", [P, C, N])
        y = sb("y", [P, U, D])
        ps_t, ps_a = ps("ps_t", [P, 4, P]), ps("ps_a", [P, C, N])
        ps_h = ps("ps_h", [P, HC // 2, 2, N])
        ps_e, ps_y = ps("ps_e", [P, C, N]), ps("ps_y", [P, U, D])
        ident = core.table("ident")
        block = ctx.enter_context(nc.Block())

        @block.sync
        def _(sp):
            for t, k in ((attn_w, "attn_w_T"), (next_w, "next_w_T")):
                sp.dma_start(t[:], core.weight(w + k)).then_inc(s["weights_loaded"], 16)
            for k in cols:
                sp.dma_start(cols[k][:], core.column(w + k)).then_inc(s["weights_loaded"], 16)
            sp.dma_start(next_b[:], core.rows(w + "next_b")).then_inc(s["weights_loaded"], 16)
            w1_by_expert = core.inputs[w + "w1"].rearrange("e (c p) n -> e p c n", p=P)
            w2_by_expert = core.inputs[w + "w2"].rearrange("e (c p) n -> e p c n", p=P)
            with sp.Fori(0, E) as e:
                wait(sp, s["w1_used"], e + 1)
                sp.dma_start(w1[:], w1_by_expert[e]).then_inc(s["w1_loaded"], 16)
                sp.dma_start(b1[:], core.inputs[w + "b1_col"][e]).then_inc(s["w1_loaded"], 16)
                wait(sp, s["w2_used"], e + 1)
                sp.dma_start(w2[:], w2_by_expert[e]).then_inc(s["w2_loaded"], 16)
                sp.dma_start(b2[:], core.inputs[w + "b2_col"][e]).then_inc(s["w2_loaded"], 16)

        @block.gpsimd
        def _(pool):
            def turn(e, now, ahead, ahead2):
                if ahead2:
                    for a in range(2):
                        for u in range(U):
                            layer_norm_root(pool, nc, ln[a][u], e + 3, mean[:, a, u], rstd[:, a, u:u + 1],
                                            core.table("minus_half"))

            staged_tiles(pool, turn, E)

        @block.tensor
        def _(pe):
            pe.wait_ge(s["weights_loaded"], 16 * 6)

            def turn_normed(n, u):
                if u:
                    pe.wait_ge(half_read[u - 1], n)
                    pe.wait_ge(flat_read[u - 1], n)
                else:
                    after(pe, half_read[U - 1], n - 1)
                    after(pe, flat_read[U - 1], n - 1)
                pe.wait_ge(ln[1][u]["xn_ready"], n)
                for c in range(C):
                    nc.tensor.transpose(ps_t[:, c, :], flat[:, u, c * P:c * P + P], ident)
                for c in range(C):
                    last = nc.tensor.transpose(ps_t[:, C + c, :], xn2[:, u, c * P:c * P + P], ident)
                last.then_inc(turned[u], 1)

            def projection(n):
                after(pe, s["xaT_ready"], n - 1)
                pe.wait_ge(half_read[U - 1], n)
                for oc in range(C):
                    for c in range(C):
                        last = nc.tensor.matmul(ps_a[:, oc, :], attn_w[:, c, oc * P:oc * P + P], xn2T[:, c, :],
                                                start=(c == 0), stop=(c == C - 1))
                last.then_inc(s["attn_ready"], 1)

            def first_layer(n):
                pe.wait_ge(s["w1_loaded"], n * 32)
                pe.wait_ge(s["xaT_ready"], n)
                for k in range(HC // 2):
                    after(pe, h_kept[k], n - 1)
                    for hc in (2 * k, 2 * k + 1):
                        for c in range(C):
                            last = nc.tensor.matmul(ps_h[:, k, hc % 2, :], w1[:, c, hc * P:hc * P + P], xaT[:, c, :],
                                                    start=(c == 0), stop=(c == C - 1))
                    last.then_inc(h_ready[k], 1)

            def second_layer(n):
                pe.wait_ge(s["w2_loaded"], n * 32)
                after(pe, s["eoT_ready"], n - 1)
                for oc in range(C):
                    for hc in range(HC):
                        if oc == 0 and hc % 2 == 0:
                            pe.wait_ge(h_kept[hc // 2], n)
                        last = nc.tensor.matmul(ps_e[:, oc, :], w2[:, hc, oc * P:oc * P + P], hT[:, hc, :],
                                                start=(hc == 0), stop=(hc == HC - 1))
                last.then_inc(s["out_ready"], 1)

            def next_projection(n):
                after(pe, s["y_kept"], n - 1)
                pe.wait_ge(s["eoT_ready"], n)
                for u in range(U):
                    for c in range(C):
                        last = nc.tensor.matmul(ps_y[:, u, :], eoT[:, c, u * P:u * P + P], next_w[:, c, :],
                                                start=(c == 0), stop=(c == C - 1))
                last.then_inc(s["y_ready"], 1)

            def turn(e, now, ahead, ahead2):
                if now:
                    first_layer(e + 1)
                if ahead:
                    turn_normed(e + 2, 0)
                if now:
                    second_layer(e + 1)
                if ahead:
                    turn_normed(e + 2, 1)
                    projection(e + 2)
                if now:
                    next_projection(e + 1)

            staged_tiles(pe, turn, E)

        @block.scalar
        def _(act):
            act.sem_inc(s["w1_used"], 1)
            act.sem_inc(s["w2_used"], 1)
            act.wait_ge(s["weights_loaded"], 16 * 6)

            def keep_turned(n, u):
                after(act, s["xaT_ready"], n - 1)
                act.wait_ge(turned[u], n)
                for c in range(C):
                    last = nc.scalar.copy(flatT[:, c, u * P:u * P + P], ps_t[:, c, :])
                last.then_inc(flat_read[u], 1)
                for c in range(C):
                    last = nc.scalar.activation(xn2T[:, c, u * P:u * P + P], ps_t[:, C + c, :], ACT.Identity,
                                                bias=cols["ln_bias"][:, c:c + 1], scale=cols["ln_scale"][:, c:c + 1])
                last.then_inc(half_read[u], 1)

            def gelus(n):
                after(act, s["out_ready"], n - 1)
                for k in range(HC // 2):
                    act.wait_ge(h_ready[k], n)
                    if k == 0:
                        act.wait_ge(s["w1_loaded"], n * 32)
                    for hc in (2 * k, 2 * k + 1):
                        last = nc.scalar.activation(hT[:, hc, :], ps_h[:, k, hc % 2, :], ACT.Gelu,
                                                    bias=b1[:, hc:hc + 1])
                    last.then_inc(h_kept[k], 1)
                act.wait_ge(h_kept[HC // 2 - 1], n)
                act.sem_inc(s["w1_used"], 1)

            def keep_expert_output(n):
                after(act, s["y_ready"], n - 1)
                act.wait_ge(s["out_ready"], n)
                act.wait_ge(s["w2_loaded"], n * 32)
                for c in range(C):
                    last = nc.scalar.activation(eoT[:, c, :], ps_e[:, c, :], ACT.Identity, bias=b2[:, c:c + 1])
                last.then_inc(s["eoT_ready"], 1)
                act.wait_ge(s["eoT_ready"], n)
                act.sem_inc(s["w2_used"], 1)

            def turn(e, now, ahead, ahead2):
                if now:
                    gelus(e + 1)
                if ahead:
                    keep_turned(e + 2, 0)
                if now:
                    keep_expert_output(e + 1)
                if ahead:
                    keep_turned(e + 2, 1)
                if now:
                    act.wait_ge(s["y_kept"], e + 1)
                    nc.scalar.activation(y[:], y[:], ACT.Gelu).then_inc(s["gelu_ready"], 1)

            staged_tiles(act, turn, E)

        @block.vector
        def _(dve):
            dve.wait_ge(s["weights_loaded"], 16 * 6)

            def norms(e, n):
                for u in range(U):
                    norm_stats(dve, nc, ln[0][u], n, core.x[:, e + E * u, :], stats[:, 0, u], mean[:, 0, u])
                for u in range(U):
                    after(dve, turned[u], n - 1)
                    normed(dve, nc, ln[0][u], n, core.x[:, e + E * u, :], flat[:, u], mean[:, 0, u],
                           rstd[:, 0, u:u + 1])
                for u in range(U):
                    dve.wait_ge(ln[0][u]["xn_ready"], n)
                    norm_stats(dve, nc, ln[1][u], n, flat[:, u], stats[:, 1, u], mean[:, 1, u])
                for u in range(U):
                    normed(dve, nc, ln[1][u], n, flat[:, u], xn2[:, u], mean[:, 1, u], rstd[:, 1, u:u + 1])

            def add_projection(n):
                dve.wait_ge(s["attn_ready"], n)
                dve.wait_ge(flat_read[U - 1], n)
                after(dve, h_ready[HC // 2 - 1], n - 1)
                for c in range(C):
                    last = nc.vector.scalar_tensor_tensor(xaT[:, c, :], ps_a[:, c, :], cols["attn_b"][:, c:c + 1],
                                                          flatT[:, c, :], ALU.add, ALU.add)
                last.then_inc(s["xaT_ready"], 1)

            def keep_y(n):
                after(dve, s["x_done"], n - 1)
                dve.wait_ge(s["y_ready"], n)
                nc.vector.tensor_tensor(y[:], ps_y[:], next_b[:].unsqueeze(1).broadcast_to([P, U, D]), ALU.add).then_inc(
                    s["y_kept"], 1)

            def add_output(e, n):
                dve.wait_ge(s["gelu_ready"], n)
                for u in range(U):
                    last = nc.vector.tensor_tensor(core.x[:, e + E * u, :], core.x[:, e + E * u, :], y[:, u],
                                                   ALU.add)
                last.then_inc(s["x_done"], 1)

            def turn(e, now, ahead, ahead2):
                if ahead:
                    add_projection(e + 2)
                if now:
                    keep_y(e + 1)
                if ahead2:
                    norms(e + 2, e + 3)
                if now:
                    add_output(e, e + 1)

            staged_tiles(dve, turn, E)


def normed_features(core, tag, xnT_all, router=None):
    nc = core.nc
    E = 8
    with ExitStack() as ctx:
        def sb(name, shape, dt=F32):
            return ctx.enter_context(nc.sbuf_tensor(f"{tag}_{name}", shape, dt))

        def ps(name, shape):
            return ctx.enter_context(nc.psum_tensor(f"{tag}_{name}", shape, F32))

        s = semaphores(nc, tag, LN_SEMS + """ weights_loaded xn_turned xnT_ready bank_read logits_ready
            logits_kept""")
        stats, mean, rstd = sb("stats", [P, 6]), sb("mean", [P, 2]), sb("rstd", [P, 1])
        xn, xnT = sb("xn", [P, D]), sb("xnT", [P, C, P])
        ps_t = ps("ps_t", [P, C, P])
        if router:
            weights, bias_row, kind, gates = router
            rw, rb = sb("rw", [P, C, E]), sb("rb", [P, E])
            ps_r = ps("ps_r", [P, E])
            logits, by, e = sb("logits", [P, NT, E]), sb("by", [P, NT, E]), sb("e", [P, NT, E])
            sig = sb("sig", [P, NT, E])
            top, place = sb("top", [P, NT, E]), sb("place", [P, NT, E], U32)
            place_f = sb("place_f", [P, NT, 2])
            weigh, share = sb("weigh", [P, NT, 2]), sb("share", [P, NT, 2])
            one_hot = sb("one_hot", [P, 2, NT, E])
            total, enough = sb("total", [P, NT]), sb("enough", [P, NT])
            then = semaphores(nc, tag + "g", """exp_ready one_plus sigmoid_ready chosen_by top_ready place_ready
                placed hot ones gap exps picked_1 picked_2 weigh_1 weigh_2 total enough total_plus inverse
                share shifted masked shared weighed""")
        ident = core.table("ident")
        block = ctx.enter_context(nc.Block())

        @block.sync
        def _(sp):
            if router:
                sp.dma_start(rw[:], core.inputs[weights]).then_inc(s["weights_loaded"], 16)
                sp.dma_start(rb[:], core.rows(bias_row)).then_inc(s["weights_loaded"], 16)

        @block.gpsimd
        def _(pool):
            def turn(i, now, ahead, ahead2):
                if ahead2:
                    layer_norm_root(pool, nc, s, i + 3, mean[:], rstd[:], core.table("minus_half"))

            staged_tiles(pool, turn)

        @block.tensor
        def _(pe):
            if router:
                pe.wait_ge(s["weights_loaded"], 32)

            def turn_xn(n):
                pe.wait_ge(s["xn_ready"], n)
                after(pe, s["bank_read"], n - 1)
                for c in range(C):
                    last = nc.tensor.transpose(ps_t[:, c, :], xn[:, c * P:c * P + P], ident)
                last.then_inc(s["xn_turned"], 1)

            def router_logits(n):
                after(pe, s["logits_kept"], n - 1)
                pe.wait_ge(s["xnT_ready"], n)
                for c in range(C):
                    last = nc.tensor.matmul(ps_r[:], xnT[:, c, :], rw[:, c, :], start=(c == 0), stop=(c == C - 1))
                last.then_inc(s["logits_ready"], 1)

            def turn(i, now, ahead, ahead2):
                if now and router:
                    router_logits(i + 1)
                if ahead:
                    turn_xn(i + 2)

            staged_tiles(pe, turn)

        @block.scalar
        def _(act):
            def turn(i, now, ahead, ahead2):
                if ahead:
                    act.wait_ge(s["xn_turned"], i + 2)
                    if router:
                        after(act, s["logits_ready"], i + 1)
                        nc.scalar.copy(xnT[:], ps_t[:]).then_inc(s["xnT_ready"], 1)
                    nc.scalar.copy(xnT_all[:, :, bass.ts(i + 1, P)], ps_t[:]).then_inc(s["bank_read"], 1)

            staged_tiles(act, turn)
            if router and kind == "sigmoid":
                act.wait_ge(s["logits_kept"], NT)
                nc.scalar.activation(e[:], logits[:], ACT.Exp, scale=-1.0).then_inc(then["exp_ready"], 1)
            if router and kind == "softmax":
                act.wait_ge(then["gap"], 1)
                nc.scalar.activation(weigh[:, :, 1], weigh[:, :, 1], ACT.Exp).then_inc(then["exps"], 1)

        @block.vector
        def _(dve):
            if router:
                dve.wait_ge(s["weights_loaded"], 32)

            def turn(i, now, ahead, ahead2):
                if ahead:
                    after(dve, s["xn_turned"], i + 1)
                    normed(dve, nc, s, i + 2, core.x[:, i + 1, :], xn[:], mean[:], rstd[:])
                if ahead2:
                    norm_stats(dve, nc, s, i + 3, core.x[:, i + 2, :], stats[:], mean[:])
                if now and router:
                    dve.wait_ge(s["logits_ready"], i + 1)
                    nc.vector.tensor_copy(logits[:, i, :], ps_r[:]).then_inc(s["logits_kept"], 1)

            staged_tiles(dve, turn)
            if not router:
                return

            def step(ins, name):
                ins.then_inc(then[name], 1)
                wait(dve, then[name], 1)

            dve.wait_ge(s["logits_kept"], NT)
            chosen = logits
            if kind == "sigmoid":
                dve.wait_ge(then["exp_ready"], 1)
                step(nc.vector.tensor_scalar(e[:], e[:], 1.0, None, ALU.add), "one_plus")
                step(nc.vector.reciprocal(sig[:], e[:]), "sigmoid_ready")
                chosen = sig
            step(nc.vector.tensor_tensor(by[:], chosen[:], rb[:].unsqueeze(1).broadcast_to([P, NT, E]), ALU.add),
                 "chosen_by")
            for t in range(NT):
                last = nc.vector.max(top[:, t, :], by[:, t, :])
            step(last, "top_ready")
            for t in range(NT):
                last = nc.vector.max_index(place[:, t, :], top[:, t, :], by[:, t, :])
            step(last, "place_ready")
            step(nc.vector.tensor_copy(place_f[:], place[:, :, 0:2]), "placed")
            for k in range(2):
                last = nc.vector.tensor_tensor(one_hot[:, k], place_f[:, :, k].unsqueeze(2).broadcast_to([P, NT, E]),
                                               core.table("iota")[:, 0:E].unsqueeze(1).broadcast_to([P, NT, E]),
                                               ALU.is_equal)
            step(last, "hot")
            if kind == "softmax":
                step(nc.vector.memset(weigh[:, :, 0], 1.0), "ones")
                step(nc.vector.tensor_tensor(weigh[:, :, 1], top[:, :, 1], top[:, :, 0], ALU.subtract), "gap")
                dve.wait_ge(then["exps"], 1)
            else:
                for k in range(2):
                    step(nc.vector.tensor_tensor(gates[:, :, 0:E], one_hot[:, k], sig[:], ALU.mult),
                         f"picked_{k + 1}")
                    step(nc.vector.tensor_reduce(weigh[:, :, k], gates[:, :, 0:E], X, ALU.add), f"weigh_{k + 1}")
            step(nc.vector.tensor_tensor(total[:], weigh[:, :, 0], weigh[:, :, 1], ALU.add), "total")
            if kind == "sigmoid":
                step(nc.vector.tensor_scalar(enough[:], total[:], 1e-9, None, ALU.is_gt), "enough")
                step(nc.vector.tensor_scalar(total[:], total[:], 1e-9, None, ALU.add), "total_plus")
            step(nc.vector.reciprocal(total[:], total[:]), "inverse")
            step(nc.vector.tensor_tensor(share[:], weigh[:], total[:].unsqueeze(2).broadcast_to([P, NT, 2]),
                                         ALU.mult), "share")
            if kind == "sigmoid":
                step(nc.vector.tensor_scalar(share[:], share[:], 0.5, None, ALU.subtract), "shifted")
                step(nc.vector.tensor_tensor(share[:], share[:], enough[:].unsqueeze(2).broadcast_to([P, NT, 2]),
                                             ALU.mult), "masked")
                step(nc.vector.tensor_scalar(share[:], share[:], 0.5, None, ALU.add), "shared")
            for k in range(2):
                last = nc.vector.tensor_tensor(one_hot[:, k], one_hot[:, k],
                                               share[:, :, k].unsqueeze(2).broadcast_to([P, NT, E]), ALU.mult)
            step(last, "weighed")
            nc.vector.tensor_tensor(gates[:, :, 0:E], one_hot[:, 0], one_hot[:, 1], ALU.add)
            nc.vector.memset(gates[:, :, E], 1.0)


def dense_experts(core, tag, xnT_all, gates, first, count, hidden, names, swiglu):
    nc = core.nc
    HC = hidden // P
    TB = 512
    NB = T // TB
    TT = TB // P
    ups = 2 if swiglu else 1
    slots = 2 if count > 1 else 1
    with ExitStack() as ctx:
        def sb(name, shape, dt=F32):
            return ctx.enter_context(nc.sbuf_tensor(f"{tag}_{name}", shape, dt))

        def ps(name, shape):
            return ctx.enter_context(nc.psum_tensor(f"{tag}_{name}", shape, F32))

        s = semaphores(nc, tag, "up_ready activated hidden_ready out_ready x_done gate_ready")
        loaded = [nc.alloc_semaphore(f"{tag}_loaded{k}") for k in range(slots)]
        used = [nc.alloc_semaphore(f"{tag}_used{k}") for k in range(slots)]
        w_up = sb("w_up", [P, slots, ups, C, hidden])
        w_down = sb("w_down", [P, slots, HC, D])
        act_out = sb("act_out", [P, 2, TB])
        hiddenT = sb("hiddenT", [P, 2, HC, TB])
        gate = sb("gate", [P, NT])
        ps_up = ps("ps_up", [P, 2, ups, TB])
        ps_d = ps("ps_d", [P, 2, TT, D])
        block = ctx.enter_context(nc.Block())
        per_load = 16 * (ups + 1)

        def each(engine, body):
            if count >= 2:
                with engine.Fori(0, count // 2) as i:
                    body(0, i * 2, i + 1)
                    body(1, i * 2 + 1, i + 1)
            if count % 2:
                body(0, count - 1, count // 2 + 1)

        @block.sync
        def _(sp):
            views = [core.inputs[k].rearrange("e (c p) n -> e p c n", p=P) for k in names]

            def load(slot, e, turn):
                wait(sp, used[slot], turn)
                for k in range(ups):
                    sp.dma_start(w_up[:, slot, k], views[k][e]).then_inc(loaded[slot], 16)
                sp.dma_start(w_down[:, slot], views[ups][e]).then_inc(loaded[slot], 16)

            each(sp, load)

        @block.tensor
        def _(pe):
            for slot in range(slots):
                pe.sem_inc(used[slot], 1)
            pe.sem_inc(s["out_ready"], 2)

            def expert(slot, e, turn):
                pe.wait_ge(loaded[slot], turn * per_load)

                def up(tb, hc):
                    k = (tb * HC + hc) % 2
                    pe.wait_ge(s["hidden_ready"], e * (NB * HC) + (tb * HC + hc + 1))
                    for a in range(ups):
                        for c in range(C):
                            last = nc.tensor.matmul(ps_up[:, k, a, :], w_up[:, slot, a, c, hc * P:hc * P + P],
                                                    xnT_all[:, c, tb * TB:tb * TB + TB],
                                                    start=(c == 0), stop=(c == C - 1))
                    last.then_inc(s["up_ready"], 1)

                def down(tb):
                    pe.wait_ge(s["hidden_ready"], e * (NB * HC) + (tb * HC + HC + 2))
                    pe.wait_ge(s["x_done"], e * NB + (tb + 1))
                    for tt in range(TT):
                        for hc in range(HC):
                            last = nc.tensor.matmul(ps_d[:, tb % 2, tt, :], hiddenT[:, tb % 2, hc, tt * P:tt * P + P],
                                                    w_down[:, slot, hc, :], start=(hc == 0), stop=(hc == HC - 1))
                    last.then_inc(s["out_ready"], 1)

                for tb in range(NB):
                    for hc in range(HC):
                        up(tb, hc)
                        if hc == 1 and tb:
                            down(tb - 1)
                down(NB - 1)
                pe.wait_ge(s["out_ready"], e * NB + (NB + 2))
                pe.sem_inc(used[slot], 1)

            each(pe, expert)

        @block.scalar
        def _(act):
            def expert(slot, e, turn):
                for tb in range(NB):
                    for hc in range(HC):
                        k = (tb * HC + hc) % 2
                        if swiglu:
                            act.wait_ge(s["hidden_ready"], e * (NB * HC) + (tb * HC + hc + 1))
                        elif hc == 0:
                            act.wait_ge(s["out_ready"], e * NB + (tb + 1))
                        act.wait_ge(s["up_ready"], e * (NB * HC) + (tb * HC + hc + 1))
                        if swiglu:
                            nc.scalar.activation(act_out[:, k, :], ps_up[:, k, 0, :], ACT.Silu).then_inc(
                                s["activated"], 1)
                        else:
                            nc.scalar.activation(hiddenT[:, tb % 2, hc, :], ps_up[:, k, 0, :], ACT.Gelu).then_inc(
                                s["hidden_ready"], 1)

            if not swiglu:
                act.sem_inc(s["hidden_ready"], 2)
            each(act, expert)

        @block.vector
        def _(dve):
            if swiglu:
                dve.sem_inc(s["hidden_ready"], 2)
            dve.sem_inc(s["x_done"], 2)

            def expert(slot, e, turn):
                wait(dve, s["x_done"], e * NB + 2)
                nc.vector.tensor_copy(gate[:], gates[:, :, first + e]).then_inc(s["gate_ready"], 1)
                dve.wait_ge(s["gate_ready"], e + 1)

                def add(tb):
                    dve.wait_ge(s["out_ready"], e * NB + (tb + 3))
                    for tt in range(TT):
                        t = tb * TT + tt
                        last = nc.vector.scalar_tensor_tensor(core.x[:, t, :], ps_d[:, tb % 2, tt, :], gate[:, t:t + 1],
                                                              core.x[:, t, :], ALU.mult, ALU.add)
                    last.then_inc(s["x_done"], 1)

                for tb in range(NB):
                    for hc in range(HC):
                        if swiglu:
                            k = (tb * HC + hc) % 2
                            if hc == 0:
                                dve.wait_ge(s["out_ready"], e * NB + (tb + 1))
                            dve.wait_ge(s["activated"], e * (NB * HC) + (tb * HC + hc + 1))
                            nc.vector.tensor_tensor(hiddenT[:, tb % 2, hc, :], act_out[:, k, :], ps_up[:, k, 1, :],
                                                    ALU.mult).then_inc(s["hidden_ready"], 1)
                        if hc == 1 and tb:
                            add(tb - 1)
                add(NB - 1)

            each(dve, expert)


def routed_ffn(core, tag, router, parts):
    with ExitStack() as ctx:
        xnT_all = ctx.enter_context(core.nc.sbuf_tensor(f"{tag}_xnT_all", [P, C, T], F32))
        gates = ctx.enter_context(core.nc.sbuf_tensor(f"{tag}_gates", [P, NT, 9], F32))
        normed_features(core, tag + "n", xnT_all, (*router, gates))
        for k, (first, count, hidden, names, swiglu) in enumerate(parts):
            dense_experts(core, f"{tag}e{k}", xnT_all, gates, first, count, hidden, names, swiglu)


PH = 8
NK = 64
K8 = 8
EN = PH * K8


def product_key_ffn(core, tag):
    nc = core.nc
    w = "L1_ffn_"
    with ExitStack() as whole:
        def keep(name, shape, dt=F32):
            return whole.enter_context(nc.sbuf_tensor(f"{tag}_{name}", shape, dt))

        xnT_all = keep("xnT_all", [P, C, T])
        norm_scale, norm_bias = keep("norm_scale", [P, C]), keep("norm_bias", [P, C])
        normed_features(core, tag + "n", xnT_all)
        folded = keep("folded", [P, C, 2 * PH * NK])
        fold_keys(core, tag + "f", xnT_all, folded, norm_scale, norm_bias)
        chosen_units(core, tag + "u", xnT_all, folded, norm_scale, norm_bias)


def fold_keys(core, tag, xnT_all, folded, norm_scale, norm_bias):
    nc = core.nc
    PARTS = T // 512
    with ExitStack() as ctx:
        def sb(name, shape, dt=F32):
            return ctx.enter_context(nc.sbuf_tensor(f"{tag}_{name}", shape, dt))

        s = semaphores(nc, tag, """weights_loaded folded_ready stats_ready mean_ready var_ready rstd_ready
            scale_ready shift_ready bias_ready""")
        w_q = sb("w_q", [P, 2 * PH, D])
        keys = sb("keys", [P, 2 * PH, NK])
        gamma, beta = sb("gamma", [P, C]), sb("beta", [P, C])
        stats, mean, rstd = sb("stats", [P, C, PARTS, 6]), sb("mean", [P, C, 2]), sb("rstd", [P, C])
        shift = sb("shift", [P, C])
        ps_f = ctx.enter_context(nc.psum_tensor(f"{tag}_ps_f", [P, C, 2 * PH * NK], F32))
        block = ctx.enter_context(nc.Block())

        @block.sync
        def _(sp):
            sp.dma_start(w_q[:], core.inputs["L1_ffn_w_q"].rearrange("(a p) d -> p a d", p=P)).then_inc(
                s["weights_loaded"], 16)
            sp.dma_start(keys[:], core.inputs["L1_ffn_keys_by_dim"]).then_inc(s["weights_loaded"], 16)
            sp.dma_start(gamma[:], core.column("L1_ffn_gamma")).then_inc(s["weights_loaded"], 16)
            sp.dma_start(beta[:], core.column("L1_ffn_beta")).then_inc(s["weights_loaded"], 16)

        @block.tensor
        def _(pe):
            pe.wait_ge(s["weights_loaded"], 64)
            for c in range(C):
                for a in range(2 * PH):
                    last = nc.tensor.matmul(ps_f[:, c, a * NK:a * NK + NK], w_q[:, a, c * P:c * P + P], keys[:, a, :],
                                            start=True, stop=True)
            last.then_inc(s["folded_ready"], 1)

        @block.scalar
        def _(act):
            act.wait_ge(s["folded_ready"], 1)
            for c in range(C):
                nc.scalar.copy(folded[:, c, :], ps_f[:, c, :])

        @block.gpsimd
        def _(pool):
            pool.wait_ge(s["mean_ready"], C)
            nc.gpsimd.tensor_scalar(mean[:, :, 1], mean[:, :, 1], EPS, None, ALU.add).then_inc(s["var_ready"], 1)
            pool.wait_ge(s["var_ready"], 1)
            nc.gpsimd.tensor_tensor(rstd[:], mean[:, :, 1], core.table("minus_half").broadcast_to([P, C]),
                                    ALU.pow).then_inc(s["rstd_ready"], 1)

        @block.vector
        def _(dve):
            for c in range(C):
                for k in range(PARTS):
                    last = nc.vector.bn_stats(stats[:, c, k], xnT_all[:, c, k * 512:k * 512 + 512])
            last.then_inc(s["stats_ready"], 1)
            dve.wait_ge(s["stats_ready"], 1)
            for c in range(C):
                nc.vector.bn_aggr(mean[:, c], stats[:, c].rearrange("p k n -> p (k n)")).then_inc(s["mean_ready"], 1)
            dve.wait_ge(s["weights_loaded"], 64)
            dve.wait_ge(s["rstd_ready"], 1)
            nc.vector.tensor_tensor(norm_scale[:], rstd[:], gamma[:], ALU.mult).then_inc(s["scale_ready"], 1)
            dve.wait_ge(s["scale_ready"], 1)
            nc.vector.tensor_tensor(shift[:], mean[:, :, 0], norm_scale[:], ALU.mult).then_inc(s["shift_ready"], 1)
            dve.wait_ge(s["shift_ready"], 1)
            nc.vector.tensor_tensor(norm_bias[:], beta[:], shift[:], ALU.subtract).then_inc(s["bias_ready"], 1)


def chosen_units(core, tag, xnT_all, folded, norm_scale, norm_bias):
    nc = core.nc
    J = NK // 2
    K = 8
    TC = NK // K
    JS = J // K
    W3 = 3
    with ExitStack() as ctx:
        def sb(name, shape, dt=F32):
            return ctx.enter_context(nc.sbuf_tensor(f"{tag}_{name}", shape, dt))

        def ps(name, shape):
            return ctx.enter_context(nc.psum_tensor(f"{tag}_{name}", shape, F32))

        s = semaphores(nc, tag, """weights_loaded part_ready first_ready second_hot second_ready plane_ready
            plane_kept units_ready activated weighed step_done x_done
            normed sim_ready sim_kept top_ready place_ready place_f_ready sums_ready best_ready
            rank_ready rows_ready digits_ready hot_ready weighed_ready picked_ready
            gap_ready exp_ready total_ready inv_ready weight_ready upper_ready split_ready doubled turned entries_kept""")
        key_in = sb("key_in", [P, C, J, P])
        key_out = sb("key_out", [P, J, D])
        entries = sb("entries", [P, 2, 3, NK])
        parts, rest = sb("parts", [P, 2, W3, NK], BF16), sb("rest", [P, 2, NK])
        first = sb("first", [P, 2, TC, P], BF16)
        second = sb("second", [P, 2, TC, J], BF16)
        second_weighed = sb("second_weighed", [P, 2, W3, TC, J], BF16)
        plane = sb("plane", [P, 2, P, J])
        act_out, weighed = sb("act_out", [P, 2, JS, P]), sb("weighed", [P, 2, JS, P])
        xbT = sb("xbT", [P, C, P])
        sim = sb("sim", [P, 2 * PH, NK])
        top, place = sb("top", [P, 2 * PH, K8]), sb("place", [P, 2 * PH, K8], U32)
        place_f = sb("place_f", [P, 2 * PH, K8])
        sums = sb("sums", [P, PH, K8, K8])
        best, rank = sb("best", [P, PH, K8]), sb("rank", [P, PH, K8], U32)
        digit = sb("digit", [P, 2, PH, K8], U32)
        digit_f = sb("digit_f", [P, 2, PH, K8])
        hot = sb("hot", [P, 2, PH, K8, K8])
        trio = sb("trio", [P, 3, EN])
        upper = sb("upper", [P, EN])
        gap, total, inv = sb("gap", [P, PH, K8]), sb("total", [P, PH]), sb("inv", [P, PH])
        doubled = sb("doubled", [P, 3, 2, EN])
        ps_p = ps("ps_p", [P, 2, 512])[:, :, 0:TC * J].rearrange("p h (n j) -> p h n j", j=J)
        ps_u = ps("ps_u", [P, 2, JS, P])
        ps_y = ps("ps_y", [P, 512])[:, 0:D]
        ps_sim = ps("ps_sim", [P, 2, 512])
        ps_e = ps("ps_e", [P, 4, P])
        ident = core.table("ident")
        iota8 = core.table("iota")[:, 0:K8]

        def iota(n):
            return core.table("iota")[:, 0:n].unsqueeze(1).broadcast_to([P, TC, n])
        block = ctx.enter_context(nc.Block())

        def all_turns(engine, turn):
            turn(-2, 0, True, False, False)
            turn(-1, 1, True, True, False)
            with engine.Fori(0, NT // 2 - 1) as g:
                turn(g * 2, 0, True, True, True)
                turn(g * 2 + 1, 1, True, True, True)
            turn(NT - 2, 0, False, True, True)
            turn(NT - 1, 1, False, False, True)

        def spread(par, value, k, n):
            return entries[:, par, value, TC * k:TC * k + TC].unsqueeze(2).broadcast_to([P, TC, n])

        @block.sync
        def _(sp):
            sp.dma_start(key_in[:], core.inputs["L1_ffn_key_in_by_expert"].rearrange("(c p) j m -> p c j m", p=P)
                         ).then_inc(s["weights_loaded"], 16)
            sp.dma_start(key_out[:], core.inputs["L1_ffn_key_out_by_expert"]).then_inc(s["weights_loaded"], 16)

        @block.gpsimd
        def _(pool):
            def turn(t, par, choose, build, units):
                if build:
                    for k in range(K):
                        pool.wait_ge(s["second_hot"], (t + 1) * K + (k + 1))
                        after(pool, s["plane_ready"], (t + 1) * K + (k - 1))
                        for part in range(W3):
                            last = nc.gpsimd.tensor_tensor(
                                second_weighed[:, k % 2, part], second[:, k % 2],
                                parts[:, 1 - par, part, TC * k:TC * k + TC].unsqueeze(2).broadcast_to([P, TC, J]),
                                ALU.mult)
                        last.then_inc(s["second_ready"], 1)

            all_turns(pool, turn)

        @block.tensor
        def _(pe):
            pe.sem_inc(s["step_done"], 2)

            def similarities(tile):
                pe.wait_ge(s["normed"], tile + 1)
                after(pe, s["sim_kept"], tile)
                for k in range(2):
                    for c in range(C):
                        last = nc.tensor.matmul(ps_sim[:, k, :], xbT[:, c, :], folded[:, c, k * 512:k * 512 + 512],
                                                start=(c == 0), stop=(c == C - 1))
                last.then_inc(s["sim_ready"], 1)

            def turn_entries(tile):
                pe.wait_ge(s["doubled"], tile + 1)
                after(pe, s["entries_kept"], tile)
                for k in range(3):
                    last = nc.tensor.transpose(ps_e[:, k, :], doubled[:, k].rearrange("p r e -> p (r e)"), ident)
                last.then_inc(s["turned"], 1)

            def build_plane(tile, k):
                pe.wait_ge(s["first_ready"], tile * K + (k + 1))
                after(pe, s["plane_kept"], tile * K + k)
                wait(pe, s["second_ready"], tile * K + (k + 1))
                for token in range(TC):
                    for half in range(2):
                        rows = slice(EN * half, EN * half + EN)
                        for part in range(W3):
                            last = nc.tensor.matmul(ps_p[:, half, token, :], first[rows, k % 2, token, :],
                                                    second_weighed[rows, k % 2, part, token, :],
                                                    start=(part == 0), stop=(part == W3 - 1))
                last.then_inc(s["plane_ready"], 1)

            def hidden(tile, k):
                pe.wait_ge(s["activated"], tile * K + (k + 1))
                for j in range(JS):
                    for c in range(C):
                        last = nc.tensor.matmul(ps_u[:, k % 2, j, :], key_in[:, c, JS * k + j, :],
                                                xnT_all[:, c, bass.ts(tile, P)], start=(c == 0), stop=(c == C - 1))
                last.then_inc(s["units_ready"], 1)

            def outputs(tile, k):
                if k == 0:
                    pe.wait_ge(s["x_done"], tile + 1)
                pe.wait_ge(s["weighed"], tile * K + (k + 3))
                for j in range(JS):
                    last = nc.tensor.matmul(ps_y, weighed[:, k % 2, j, :], key_out[:, JS * k + j, :],
                                            start=(k + j == 0), stop=(k == K - 1 and j == JS - 1))
                last.then_inc(s["step_done"], 1)

            def turn(t, par, choose, build, units):
                if units:
                    hidden(t, 0)
                for k in range(K):
                    if units and k + 1 < K:
                        hidden(t, k + 1)
                    if build:
                        build_plane(t + 1, k)
                    if units:
                        outputs(t, k)
                    if choose and k == 0:
                        similarities(t + 2)
                    if choose and k == K - 1:
                        turn_entries(t + 2)
                if build and not units:
                    pe.wait_ge(s["weights_loaded"], 32)

            all_turns(pe, turn)

        @block.scalar
        def _(act):
            act.sem_inc(s["activated"], 2)

            def normed(tile):
                after(act, s["sim_ready"], tile, alone=True)
                for c in range(C):
                    last = nc.scalar.activation(xbT[:, c, :], xnT_all[:, c, bass.ts(tile, P)], ACT.Identity,
                                                bias=norm_bias[:, c:c + 1], scale=norm_scale[:, c:c + 1])
                last.then_inc(s["normed"], 1)

            def keep_similarities(tile):
                act.wait_ge(s["sim_ready"], tile + 1)
                after(act, s["place_ready"], tile)
                nc.scalar.copy(sim[:].rearrange("p a k -> p (a k)"), ps_sim[:].rearrange("p a k -> p (a k)")).then_inc(
                    s["sim_kept"], 1)

            def exps(tile):
                act.wait_ge(s["gap_ready"], tile + 1)
                nc.scalar.activation(gap[:], gap[:], ACT.Exp).then_inc(s["exp_ready"], 1)

            def keep_entries(tile, par):
                after(act, s["plane_ready"], tile * K - K)
                wait(act, s["turned"], tile + 1)
                for half in range(2):
                    at = slice(EN * half, EN * half + EN)
                    last = nc.scalar.copy(entries[at, par], ps_e[at, 0:3, NK * half:NK * half + NK])
                last.then_inc(s["entries_kept"], 1)

            def keep_plane(tile, par, k):
                if k == 0:
                    after(act, s["weighed"], tile * K + (2 - K))
                act.wait_ge(s["plane_ready"], tile * K + (k + 1))
                nc.scalar.copy(
                    plane[:, par].rearrange("p (h n) j -> p h (n j)", h=2)[:, :, TC * J * k:TC * J * k + TC * J],
                    ps_p.rearrange("p h n j -> p h (n j)")).then_inc(s["plane_kept"], 1)

            def gelus(tile, k):
                act.wait_ge(s["units_ready"], tile * K + (k + 1))
                act.wait_ge(s["weighed"], tile * K + (k + 1))
                nc.scalar.activation(act_out[:, k % 2], ps_u[:, k % 2], ACT.Gelu).then_inc(s["activated"], 1)

            def turn(t, par, choose, build, units):
                if choose:
                    normed(t + 2)
                if units:
                    gelus(t, 0)
                for k in range(K):
                    if units and k + 1 < K:
                        gelus(t, k + 1)
                    if build:
                        keep_plane(t + 1, 1 - par, k)
                    if choose and k == 0:
                        keep_similarities(t + 2)
                    if choose and k == 5:
                        exps(t + 2)
                    if choose and k == K - 1:
                        keep_entries(t + 2, par)

            all_turns(act, turn)

        @block.vector
        def _(dve):
            dve.sem_inc(s["weighed"], 2)
            dve.sem_inc(s["x_done"], 1)

            def choose_step(tile, k):
                n = tile + 1

                def then(ins, name):
                    ins.then_inc(s[name], 1)
                    wait(dve, s[name], n)

                if k == 1:
                    wait(dve, s["sim_kept"], n)
                    for a in range(2 * PH):
                        last = nc.vector.max(top[:, a, :], sim[:, a, :])
                    then(last, "top_ready")
                if k == 2:
                    for a in range(2 * PH):
                        last = nc.vector.max_index(place[:, a, :], top[:, a, :], sim[:, a, :])
                    then(last, "place_ready")
                if k == 3:
                    nc.vector.tensor_copy(place_f[:], place[:]).then_inc(s["place_f_ready"], 1)
                    then(nc.vector.tensor_tensor(sums[:], top[:, 0:PH, :].unsqueeze(3).broadcast_to([P, PH, K8, K8]),
                                                 top[:, PH:, :].unsqueeze(2).broadcast_to([P, PH, K8, K8]), ALU.add),
                         "sums_ready")
                    for h in range(PH):
                        last = nc.vector.max(best[:, h, :], sums[:, h].rearrange("p a b -> p (a b)"))
                    then(last, "best_ready")
                if k == 4:
                    for h in range(PH):
                        last = nc.vector.max_index(rank[:, h, :], best[:, h, :],
                                                   sums[:, h].rearrange("p a b -> p (a b)"))
                    then(last, "rank_ready")
                    nc.vector.tensor_tensor(gap[:], best[:], best[:, :, 0:1].broadcast_to([P, PH, K8]),
                                            ALU.subtract).then_inc(s["gap_ready"], 1)
                    nc.vector.tensor_scalar(digit[:, 0], rank[:], 3, None, ALU.logical_shift_right)
                    then(nc.vector.tensor_scalar(digit[:, 1], rank[:], 7, None, ALU.bitwise_and), "rows_ready")
                    then(nc.vector.tensor_copy(digit_f[:], digit[:]), "digits_ready")
                if k == 5:
                    for p in range(2):
                        last = nc.vector.tensor_tensor(
                            hot[:, p], digit_f[:, p].unsqueeze(3).broadcast_to([P, PH, K8, K8]),
                            iota8.unsqueeze(1).unsqueeze(1).broadcast_to([P, PH, K8, K8]), ALU.is_equal)
                    then(last, "hot_ready")
                    dve.wait_ge(s["place_f_ready"], n)
                    for p in range(2):
                        last = nc.vector.tensor_tensor(
                            hot[:, p], hot[:, p], place_f[:, PH * p:PH * p + PH, :].unsqueeze(2).broadcast_to(
                                [P, PH, K8, K8]), ALU.mult)
                    then(last, "weighed_ready")
                if k == 6:
                    for p in range(2):
                        last = nc.vector.tensor_reduce(trio[:, p].rearrange("p (h k) -> p h k", h=PH), hot[:, p], X,
                                                       ALU.add)
                    last.then_inc(s["picked_ready"], 1)
                    dve.wait_ge(s["exp_ready"], n)
                    then(nc.vector.tensor_reduce(total[:], gap[:], X, ALU.add), "total_ready")
                    then(nc.vector.reciprocal(inv[:], total[:]), "inv_ready")
                    then(nc.vector.tensor_tensor(trio[:, 2].rearrange("p (h k) -> p h k", h=PH), gap[:],
                                                 inv[:].unsqueeze(2).broadcast_to([P, PH, K8]), ALU.mult),
                         "weight_ready")
                    dve.wait_ge(s["picked_ready"], n)
                    then(nc.vector.tensor_scalar(upper[:], trio[:, 1], float(J), float(J), ALU.is_ge, ALU.mult),
                         "upper_ready")
                    nc.vector.scalar_tensor_tensor(trio[:, 0], upper[:], NK / J, trio[:, 0], ALU.mult, ALU.add)
                    then(nc.vector.tensor_tensor(trio[:, 1], trio[:, 1], upper[:], ALU.subtract), "split_ready")
                    after(dve, s["turned"], tile, alone=True)
                    nc.vector.tensor_copy(doubled[:], trio[:].unsqueeze(2).broadcast_to([P, 3, 2, EN])).then_inc(
                        s["doubled"], 1)

            def one_hot_rows(tile, par, k):
                if k == 0:
                    dve.wait_ge(s["entries_kept"], tile + 1)
                    left = entries[:, par, 2]
                    for part in range(W3):
                        nc.vector.tensor_copy(parts[:, par, part], left).then_inc(s["part_ready"], 1)
                        dve.wait_ge(s["part_ready"], tile * (2 * W3 - 1) + (2 * part + 1))
                        if part < W3 - 1:
                            nc.vector.tensor_tensor(rest[:, part], left, parts[:, par, part],
                                                    ALU.subtract).then_inc(s["part_ready"], 1)
                            dve.wait_ge(s["part_ready"], tile * (2 * W3 - 1) + (2 * part + 2))
                            left = rest[:, part]
                after(dve, s["plane_ready"], tile * K + (k - 1))
                nc.vector.tensor_tensor(first[:, k % 2], spread(par, 0, k, P), iota(P), ALU.is_equal).then_inc(
                    s["first_ready"], 1)
                after(dve, s["second_ready"], tile * K + (k - 1))
                nc.vector.tensor_tensor(second[:, k % 2], spread(par, 1, k, J), iota(J), ALU.is_equal).then_inc(
                    s["second_hot"], 1)

            def weigh(tile, par, k):
                if k == 0:
                    dve.wait_ge(s["plane_kept"], tile * K + K)
                dve.wait_ge(s["activated"], tile * K + (k + 3))
                dve.wait_ge(s["step_done"], tile * K + (k + 1))
                nc.vector.tensor_tensor(weighed[:, k % 2], act_out[:, k % 2],
                                        plane[:, par, :, JS * k:JS * k + JS].rearrange("p n j -> p j n"),
                                        ALU.mult).then_inc(s["weighed"], 1)

            def add_outputs(tile):
                wait(dve, s["step_done"], tile * K + (K + 2))
                nc.vector.tensor_tensor(core.x[:, tile, :], core.x[:, tile, :], ps_y, ALU.add).then_inc(s["x_done"], 1)

            def turn(t, par, choose, build, units):
                if build:
                    one_hot_rows(t + 1, 1 - par, 0)
                for k in range(K):
                    if units:
                        weigh(t, par, k)
                    if build and k + 1 < K:
                        one_hot_rows(t + 1, 1 - par, k + 1)
                    if choose:
                        choose_step(t + 2, k)
                if units:
                    add_outputs(t)

            all_turns(dve, turn)


SUBLAYERS = range(12)


def perceiver(nc, inputs, where, out):
    with ExitStack() as ctx:
        x_sb = ctx.enter_context(nc.sbuf_tensor("x_sb", [P, NT, D], F32))
        const = ctx.enter_context(nc.sbuf_tensor("const", [P, inputs["const"].shape[1]], F32))
        core = Core(nc, inputs, x_sb, const, where)
        with nc.semaphore("x_loaded") as x_loaded, nc.Block() as block:
            @block.sync
            def _(sp):
                sp.dma_start(const[:], inputs["const"]).then_inc(x_loaded, 16)
                sp.dma_start(x_sb[:], inputs["x"].rearrange("(t p) d -> p t d", p=P)).then_inc(x_loaded, 16)
                sp.wait_ge(x_loaded, 32)
        for n in SUBLAYERS:
            with nc.cleanup_on_exit():
                sublayer(core, n)
        with nc.semaphore("x_stored") as x_stored, nc.Block() as block:
            @block.sync
            def _(sp):
                sp.dma_start(out.rearrange("(t p) d -> p t d", p=P), x_sb[:]).then_inc(x_stored, 16)
                sp.wait_ge(x_stored, 16)


def sublayer(core, n):
    if n == 1:
        self_attention(core, "l0a", dict(q="L0_attn_w_q_T", k="L0_attn_w_k_T", v="L0_attn_w_v_T", o="L0_attn_w_o_T",
                                         bo="L0_attn_b_o"))
    if n == 0:
        gated_cross_attention(core, "l0x")
    if n == 4:
        complex_attention(core, "l1a", dict(q="L1_attn_Wq_T", k="L1_attn_Wk_T", v="L1_attn_Wv_T", o="L1_attn_Wo_T",
                                            bq="L1_attn_bq", bk="L1_attn_bk", bv="L1_attn_bv", bo="L1_attn_bo"))
    if n == 2:
        fixed_experts_ffn(core, "l0f")
    if n == 5:
        product_key_ffn(core, "l1f")
    if n == 8:
        routed_ffn(core, "l2f", ("L2_ffn_router", "L2_ffn_experts_bias", "softmax"), [
            (0, 9, 512, ("L2_ffn_w1_all", "L2_ffn_w3_all", "L2_ffn_w2_all"), True)])
    if n == 11:
        routed_ffn(core, "l3f", ("L3_ffn_router", "L3_ffn_router_bias", "sigmoid"), [
            (0, 8, 256, ("L3_ffn_ew1", "L3_ffn_ew2"), False),
            (8, 1, 512, ("L3_ffn_sw1", "L3_ffn_sw3", "L3_ffn_sw2"), True)])
    if n == 3:
        cross_attention(core, "l1x", dict(q="L1_xattn_Wq_T", k="L1_xattn_Wk_T", v="L1_xattn_Wv_T", o="L1_xattn_o",
                                          bq="L1_xattn_bq", bk="L1_xattn_bk", bv="L1_xattn_bv", bo="L1_xattn_bo"),
                        mask="mask_int", mask_type=I32)
    if n == 6:
        cross_attention(core, "l2x", dict(q="L2_xattn_Wq_T", k="L2_xattn_Wk_T", v="L2_xattn_Wv_T", o="L2_xattn_o",
                                          bq="L2_xattn_bq", bk="L2_xattn_bk", bv="L2_xattn_bv", bo="L2_xattn_bo"),
                        mask="mask_bool", mask_type=U8)
    if n == 9:
        cross_attention(core, "l3x", dict(q="L3_xattn_Wq", k="L3_xattn_Wk", v="L3_xattn_Wv", o="L3_xattn_o"),
                        bias_rows="fside")
    if n == 7:
        self_attention(core, "l2a", dict(
            q="L2_attn_q_w_T", k="L2_attn_k_w_T", v="L2_attn_v_w_T", o="L2_attn_o_w_T", bq="L2_attn_q_b",
            bk="L2_attn_k_b", bv="L2_attn_v_b", bo="L2_attn_o_b", qr="L2_attn_q_w_rot", kr="L2_attn_k_w_rot",
            bqr="L2_attn_q_b_rot", bkr="L2_attn_k_b_rot"), rope=True)
    if n == 10:
        self_attention(core, "l3a", dict(
            q="L3_attn_W_q", k="L3_attn_W_k", v="L3_attn_W_v", o="L3_attn_W_proj", bq="L3_attn_b_q",
            bk="L3_attn_b_k", bv="L3_attn_b_v", bo="L3_attn_b_proj"), alibi="L3_attn_slopes")


COLUMNS = ["L1_ffn_gamma", "L1_ffn_beta", "L0_ffn_ln_scale", "L0_ffn_ln_bias", "L0_ffn_attn_b", "L0_xattn_bq_c", "L0_xattn_bk_c", "L0_xattn_bk_s", "L0_xattn_bq_s",
           "L1_attn_bq", "L1_attn_bk", "L1_attn_bv", "L1_xattn_bq", "L1_xattn_bk", "L2_xattn_bq", "L2_xattn_bk",
           "L2_attn_q_b", "L2_attn_k_b", "L2_attn_v_b", "L2_attn_q_b_rot", "L2_attn_k_b_rot",
           "L3_attn_b_q", "L3_attn_b_k", "L3_attn_b_v"]


def laid_out(inputs):
    a = {k: np.asarray(v) for k, v in inputs.items()}
    table, where, rows = constant_tables()
    d = dict(const=table)
    d["x"] = a["x"].reshape(T, D)
    for n in ("L0_attn_w_q", "L0_attn_w_k", "L0_attn_w_v", "L0_attn_w_o",
              "L2_attn_q_w", "L2_attn_k_w", "L2_attn_v_w", "L2_attn_o_w"):
        d[n + "_T"] = a[n].T
    other = np.arange(D).reshape(H, 2, HD // 2)[:, ::-1].reshape(-1)
    for n in ("L2_attn_q", "L2_attn_k"):
        d[n + "_w_rot"] = a[n + "_w"][other].T
        d[n + "_b_rot"] = a[n + "_b"][other]
    for j, n in enumerate("kqv"):
        d["L3_attn_W_" + n] = a["L3_attn_W_kqv"][:, j * D:j * D + D]
        d["L3_attn_b_" + n] = a["L3_attn_b_kqv"][j * D:j * D + D]
    for n in ("L0_attn_b_o", "L2_attn_o_b", "L3_attn_W_proj", "L3_attn_b_proj"):
        d[n] = a[n]
    context = a["ctx_1024"].transpose(2, 0, 1)
    d["ctx_T"] = context.reshape(D, -1)
    d["ctx"] = a["ctx_1024"]
    d["ctx_sel_T"] = context[:, :, rows].reshape(D, -1)
    for n in ("Wq_c", "Wk_c", "Wv_c", "Wv_s", "Wq_s", "Wg"):
        d[f"L0_xattn_{n}_T"] = a["L0_xattn_" + n].T
    for n in ("Wk_s", "bv_c", "bv_s", "bg"):
        d["L0_xattn_" + n] = a["L0_xattn_" + n]
    for n in ("Wq", "Wk", "Wv", "Wo"):
        d[f"L1_attn_{n}_T"] = a["L1_attn_" + n].T
    d["L1_attn_bo"] = a["L1_attn_bo"]
    d["ctx_tail"] = context[:, :, KEYS - 1]
    d["mask_int"] = a["mask_BxS2_ik0"].reshape(-1)
    d["mask_bool"] = a["mask_Bx1x1xS2_bf1"].view(np.uint8).reshape(-1)
    d["fside"] = a["fside_1x1xSxS2_0"].reshape(S, KEYS)
    for n in ("L1_xattn_", "L2_xattn_"):
        for k in "qkv":
            d[n + "W" + k + "_T"] = a[n + "W" + k].T
        d[n + "o"] = a[n + "Wo"].T.reshape(G, HG, HD, D).transpose(0, 2, 1, 3).reshape(GD, HG, D)
        d[n + "bv"], d[n + "bo"] = a[n + "bv"], a[n + "bo"]
    for k in "qkv":
        d["L3_xattn_W" + k] = a["L3_xattn_W" + k].reshape(D, D)
    d["L3_xattn_o"] = a["L3_xattn_Wo"].reshape(G, HG, HD, D).transpose(0, 2, 1, 3).reshape(GD, HG, D)
    for n in ("attn_w", "next_w"):
        d[f"L0_ffn_{n}_T"] = a["L0_ffn_" + n].T
    for n in ("next_b", "w1", "w2"):
        d["L0_ffn_" + n] = a["L0_ffn_" + n]
    for n in ("b1", "b2"):
        d[f"L0_ffn_{n}_col"] = a["L0_ffn_" + n].reshape(8, -1, P).transpose(0, 2, 1)
    for n in ("L2_ffn_router", "L3_ffn_router"):
        d[n] = a[n + "_w"].T.reshape(C, P, 8).transpose(1, 0, 2)
    for n in ("L2_ffn_experts_bias", "L3_ffn_router_bias", "L3_ffn_ew1", "L3_ffn_ew2"):
        d[n] = a[n]
    for n in ("w1", "w3", "w2"):
        d[f"L2_ffn_{n}_all"] = np.concatenate([a["L2_ffn_" + n], a["L2_ffn_s" + n]])
        d["L3_ffn_s" + n] = a["L3_ffn_s" + n][None]
    d["L1_ffn_w_q"] = a["L1_ffn_w_q"]
    d["L1_ffn_keys_by_dim"] = a["L1_ffn_keys"].transpose(3, 2, 0, 1).reshape(P, 2 * PH, NK)
    experts = a["L1_ffn_key_in"].reshape(NK, 2, NK // 2, D)
    d["L1_ffn_key_in_by_expert"] = experts.transpose(3, 2, 1, 0).reshape(D, NK // 2, P)
    experts = a["L1_ffn_key_out"].reshape(NK, 2, NK // 2, D)
    d["L1_ffn_key_out_by_expert"] = experts.transpose(1, 0, 2, 3).reshape(P, NK // 2, D)
    for n in COLUMNS:
        v = d.pop(n) if n in d else a[n]
        d[n + "_col"] = v.reshape(-1, P).T
    d["L3_attn_slopes_by_head"] = a["L3_attn_slopes"].reshape(G, HG).T
    return {k: np.ascontiguousarray(v) for k, v in d.items()}, where


def kernel(**inputs):
    import concourse.bacc as bacc
    from concourse.bass_utils import run_bass_kernel_spmd

    nc = bacc.Bacc("TRN2", target_bir_lowering=False, num_devices=1)
    arrays, where = laid_out(inputs)
    aps, fed = {}, {}
    for name, a in arrays.items():
        fed[f"in_{name}_dram"] = a
        aps[name] = nc.dram_tensor(f"in_{name}_dram", a.shape, mybir.dt.from_np(a.dtype), kind="ExternalInput").ap()
    out = nc.dram_tensor("out_0_dram", (T, D), F32, kind="ExternalOutput").ap()
    perceiver(nc, aps, where, out)
    r = run_bass_kernel_spmd(nc, [fed], core_ids=[0])
    return r.results[0]["out_0_dram"].reshape(B, S, D)
```

```python
from contextlib import ExitStack

import numpy as np

import concourse.bass as bass
from concourse import mybir
from concourse.alu_op_type import AluOpType as ALU

ACT = mybir.ActivationFunctionType
F32 = mybir.dt.float32
BF16 = mybir.dt.bfloat16
I32 = mybir.dt.int32
U8 = mybir.dt.uint8
U32 = mybir.dt.uint32
X = mybir.AxisListType.X

P = 128
D = 256
C = D // P
B = 64
S = 32
KEYS = 257
T = B * S
NT = T // P
BT = P // S
H = 16
HD = D // H
G = 4
HG = H // G
GD = HG * HD
MASKED = -3.4028234663852886e38
EPS = 1e-5


def constant_tables():
    p = np.arange(P)
    parts = {
        "ident": np.eye(P),
        "minus_half": np.full((P, 1), -0.5),
        "head_of_feature": 0.25 * ((p[:, None] % GD) // HD == np.arange(HG)[None]),
        "quarter": (p[:, None] // S == np.arange(4)[None]),
        "relative": np.minimum(np.arange(S)[None] - (p % S)[:, None], 0),
        "later": np.where(np.arange(S)[None] > (p % S)[:, None], -1e30, 0.0),
        "iota": np.broadcast_to(np.arange(P), (P, P)),
        "group_rows": np.repeat((p[:, None] % S == (np.arange(G) % 2 * 2 + np.arange(G) // 2)[None]), GD, axis=1),
    }
    inv = (1.0 / 10000.0 ** (np.arange(0, HD, 2, dtype=np.float32) / HD)).astype(np.float32)
    freq = np.arange(S, dtype=np.float32)[:, None] * inv[None]
    emb = np.concatenate([freq, freq], axis=-1).astype(np.float32)
    sign = np.where(np.arange(HD) < HD // 2, -1.0, 1.0)
    parts["cosine"] = np.cos(emb).T[p % HD]
    parts["sine"] = (np.sin(emb).T * sign[:, None])[p % HD]
    pos = np.clip((np.arange(S, dtype=np.float32) + 0.5) * np.float32(KEYS / S) - 0.5, 0.0, KEYS - 1)
    lo = np.floor(pos).astype(np.int64)
    hi = np.minimum(lo + 1, KEYS - 1)
    w = (pos - lo).astype(np.float32)
    inter = np.zeros((64, S), np.float32)
    inter[2 * np.arange(S), np.arange(S)] = 1 - w
    inter[2 * np.arange(S) + 1, np.arange(S)] = w
    parts["interpolate"] = np.concatenate([inter, inter], axis=0)
    where, at = {}, 0
    for name, a in parts.items():
        where[name] = (at, a.shape[1])
        at += a.shape[1]
    table = np.concatenate([np.asarray(a, np.float32) for a in parts.values()], axis=1)
    return np.ascontiguousarray(table), where, np.stack([lo, hi], axis=1).reshape(-1)


class Core:

    def __init__(self, nc, inputs, x_sb, const, where, packs):
        self.nc, self.inputs, self.x, self.const, self.where = nc, inputs, x_sb, const, where
        self.packs, self.loading = packs, set()
        self.pack_loaded = {n: nc.alloc_semaphore(f"pack_loaded{n}") for n in PACKED if n in SUBLAYERS}
        self.number, self.group, self.arenas = None, (), ()

    def table(self, name, rows=P):
        at, n = self.where[name]
        return self.const[0:rows, at:at + n]

    def rows(self, name, n=P):
        a = self.inputs[name].rearrange("(a d) -> a d", a=1)
        return a.broadcast_to([n, a.shape[1]])

    def pack(self, tag):
        tile = self.arenas[self.number % 2]
        return {key: view(tile[:, at:at + n]) for key, (at, n, view) in self.packs[tag].items()}

    def load_packs(self, sp):
        for number in (self.number, self.number + 1):
            if number in self.group and PACKED.get(number) and number not in self.loading:
                tag = PACKED[number]
                source = self.inputs[tag + "_pack"]
                sp.dma_start(self.arenas[number % 2][:, 0:source.shape[1]], source).then_inc(
                    self.pack_loaded[number], 16)
                self.loading.add(number)

    def wait_for_pack(self, engine):
        engine.wait_ge(self.pack_loaded[self.number], 16)


def semaphores(nc, tag, names):
    return {n: nc.alloc_semaphore(f"{tag}_{n}") for n in names.split()}


LN_SEMS = "var_ready stats_ready mean_ready rstd_ready xn_ready"


def wait(engine, sem, n):
    engine.wait_ge(sem, n)
    engine.nop(nofuse=True)


def layer_norm_root(pool, nc, s, n, mean, rstd, minus_half):
    wait(pool, s["mean_ready"], n)
    nc.gpsimd.tensor_scalar(mean[:, 1:2], mean[:, 1:2], EPS, None, ALU.add).then_inc(s["var_ready"], 1)
    pool.wait_ge(s["var_ready"], n)
    nc.gpsimd.tensor_tensor(rstd, mean[:, 1:2], minus_half, ALU.pow).then_inc(s["rstd_ready"], 1)


def after(engine, sem, count, alone=False):
    if isinstance(count, int) and count < 1:
        return
    if alone:
        wait(engine, sem, count)
    else:
        engine.wait_ge(sem, count)


def staged_tiles(engine, turn, count=NT):
    turn(-2, False, False, True)
    turn(-1, False, True, True)
    turn(0, True, True, True)
    with engine.Fori(1, count - 2) as i:
        turn(i, True, True, True)
    turn(count - 2, True, True, False)
    turn(count - 1, True, False, False)


def not_first(i):
    return not (isinstance(i, int) and i == 0)


def norm_stats(dve, nc, s, n, x_tile, stats, mean):
    nc.vector.bn_stats(stats, x_tile).then_inc(s["stats_ready"], 1)
    wait(dve, s["stats_ready"], n)
    nc.vector.bn_aggr(mean, stats).then_inc(s["mean_ready"], 1)


def normed(dve, nc, s, n, x_tile, xn, mean, rstd):
    dve.wait_ge(s["rstd_ready"], n)
    nc.vector.tensor_scalar(xn, x_tile, mean[:, 0:1], rstd, ALU.subtract, ALU.mult).then_inc(s["xn_ready"], 1)


def layer_norm(dve, nc, s, n, x_tile, xn, stats, mean, rstd):
    norm_stats(dve, nc, s, n, x_tile, stats, mean)
    normed(dve, nc, s, n, x_tile, xn, mean, rstd)


def self_attention(core, tag, rope=False, alibi=False):
    nc = core.nc
    with ExitStack() as ctx:
        def sb(name, shape, dt=F32):
            return ctx.enter_context(nc.sbuf_tensor(f"{tag}_{name}", shape, dt))

        def ps(name, shape):
            return ctx.enter_context(nc.psum_tensor(f"{tag}_{name}", shape, F32))

        s = semaphores(nc, tag, LN_SEMS + """ xn_turned xnT_ready xnT4_ready qk_ready v_ready
            qT_ready kT_ready qk_kept q_spread v_spread scores_ready biased_ready max_ready shifted_ready exp_ready
            sum_ready inv_ready probs_ready probs_turned ctx_ready ctxT_ready y_ready x_biased x_done
            cleared bias_1 bias_2 rot_1 rot_2 rot_3 rot_4 rot_ready rotq_mult rotk_mult""")
        pack = core.pack(tag)
        wt = {k: pack[k] for k in ("q", "k", "v", "o", "qr", "kr") if k in pack}
        cols = {k: pack[k] for k in ("bq", "bk", "bv", "bqr", "bkr") if k in pack}
        bo = pack["bo"]
        stats, mean, rstd = sb("stats", [P, 6]), sb("mean", [P, 2]), sb("rstd", [P, 1])
        xn = sb("xn", [P, D])
        xnT = sb("xnT", [P, C, P])
        xnT_four = sb("xnT_four", [P, C, BT, HG, S])
        qT, kT = sb("qT", [P, C, P]), sb("kT", [P, C, P]) if rope else None
        k_by_half = sb("k_by_half", [P, C, BT, 2, S])
        q_by_head = sb("q_by_head", [P, C, BT, HG, S])
        v_by_head = sb("v_by_head", [P, BT, G, HG, HD])
        biased = sb("biased", [P, BT * G, S])
        big, rsum, rinv = sb("big", [P, BT * G]), sb("rsum", [P, BT * G]), sb("rinv", [P, BT * G])
        shifted = sb("shifted", [P, BT * G, S])
        probs = sb("probs", [P, BT * G, S])
        probsT = sb("probsT", [P, BT * G, S])
        ctxT = sb("ctxT", [P, C, P])
        x_plus_bo = sb("x_plus_bo", [P, D])
        if rope:
            qrot, krot = sb("qrot", [P, C, P]), sb("krot", [P, C, P])
        if alibi:
            slope = pack["slope"]
            bias = sb("bias", [P, G, S])
        ps_t = ps("ps_t", [P, C, P])
        ps_qk = ps("ps_qk", [P, 2, C, P])
        ps_qkr = ps("ps_qkr", [P, 2, C, P]) if rope else None
        ps_v = ps("ps_v", [P, BT, D])
        ps_s = ps("ps_s", [P, BT * G, S])
        ps_oy = ps("ps_oy", [P, 2, C, P])
        ps_o, ps_y = ps_oy[:, 0], ps_oy[:, 1].rearrange("p c n -> p (c n)")
        ident = core.table("ident")
        head_of_feature = core.table("head_of_feature")
        quarter = core.table("quarter")
        block = ctx.enter_context(nc.Block())

        @block.sync
        def _(sp):
            core.load_packs(sp)

        def turns(name):
            return core.table(name).unsqueeze(1).broadcast_to([P, C * BT, S])

        def flat(t):
            return t[:].rearrange("p c (b q) -> p (c b) q", b=BT)

        @block.gpsimd
        def _(pool):
            def turn(i, now, ahead, ahead2):
                if ahead and not now:
                    core.wait_for_pack(pool)
                if ahead2:
                    layer_norm_root(pool, nc, s, i + 3, mean[:], rstd[:], core.table("minus_half"))
                if now:
                    after(pool, s["x_done"], i)
                    nc.gpsimd.tensor_tensor(x_plus_bo[:], core.x[:, i, :], bo[:], ALU.add).then_inc(s["x_biased"], 1)
                if ahead and rope:
                    pool.wait_ge(s["rotk_mult"], i + 2)
                    nc.gpsimd.tensor_tensor(flat(kT), flat(kT), turns("cosine"), ALU.mult)
                    pool.wait_ge(s["rotq_mult"], i + 2)
                    nc.gpsimd.tensor_tensor(flat(krot), flat(krot), turns("sine"), ALU.mult).then_inc(s["rot_2"], 1)

            staged_tiles(pool, turn)

        @block.tensor
        def _(pe):
            def turn_xn(n):
                after(pe, s["xnT4_ready"], n - 1)
                pe.wait_ge(s["xn_ready"], n)
                nc.tensor.transpose(ps_t[:, 0, :], xn[:, 0:P], ident)
                nc.tensor.transpose(ps_t[:, 1, :], xn[:, P:D], ident).then_inc(s["xn_turned"], 1)

            def queries_and_keys(n):
                after(pe, s["qk_kept"], n - 1)
                pe.wait_ge(s["xnT_ready"], n)
                for a, k in enumerate(("q", "k")):
                    for dst, kk in ((ps_qk, k), (ps_qkr, k + "r")):
                        if kk in wt:
                            for o in range(C):
                                for c in range(C):
                                    last = nc.tensor.matmul(dst[:, a, o, :], wt[kk][:, c, o * P:o * P + P],
                                                            xnT[:, c, :], start=(c == 0), stop=(c == C - 1))
                last.then_inc(s["qk_ready"], 1)

            def values(n):
                after(pe, s["v_spread"], n - 1)
                pe.wait_ge(s["xnT4_ready"], n)
                for b in range(BT):
                    for c in range(C):
                        last = nc.tensor.matmul(ps_v[:, b, :], xnT_four[:, c, b, :, :], wt["v"][:, c, :],
                                                start=(c == 0), stop=(c == C - 1))
                last.then_inc(s["v_ready"], 1)

            def scores(n):
                after(pe, s["biased_ready"] if alibi else s["shifted_ready"], n - 1)
                pe.wait_ge(s["kT_ready"], n)
                pe.wait_ge(s["q_spread"], n)
                for b in range(BT):
                    for c in range(C):
                        g = b * G + 2 * c
                        last = nc.tensor.matmul(ps_s[:, g:g + 2, :], q_by_head[:, c, b, :, :],
                                                k_by_half[:, c, b, :, :], start=True, stop=True)
                last.then_inc(s["scores_ready"], 1)

            def weighed_values(n):
                after(pe, s["x_done"], n - 1)
                pe.wait_ge(s["v_spread"], n)
                wait(pe, s["probs_turned"], n)
                for b in range(BT):
                    for g in range(G):
                        at = slice(GD * (g % 2), GD * (g % 2) + GD)
                        last = nc.tensor.matmul(ps_o[at, g // 2, S * b:S * b + S], v_by_head[:, b, g, :, :],
                                                probsT[:, b * G + g, :], start=True, stop=True)
                last.then_inc(s["ctx_ready"], 1)

            def output(n):
                pe.wait_ge(s["ctxT_ready"], n)
                for c in range(C):
                    last = nc.tensor.matmul(ps_y[:], ctxT[:, c, :], wt["o"][:, c, :], start=(c == 0), stop=(c == C - 1))
                last.then_inc(s["y_ready"], 1)

            def turn(i, now, ahead, ahead2):
                if ahead and not now:
                    core.wait_for_pack(pe)
                if now:
                    scores(i + 1)
                if now and not_first(i):
                    output(i)
                if ahead:
                    queries_and_keys(i + 2)
                    values(i + 2)
                if now:
                    weighed_values(i + 1)
                if ahead2:
                    turn_xn(i + 3)

            staged_tiles(pe, turn)
            output(NT)

        @block.scalar
        def _(act):
            def keep_xnT(n):
                after(act, s["v_ready"], n - 1)
                act.wait_ge(s["xn_turned"], n)
                nc.scalar.copy(xnT[:], ps_t[:]).then_inc(s["xnT_ready"], 1)
                for c in range(C):
                    last = nc.scalar.copy(xnT_four[:, c], ps_t[:, c, :].rearrange("p (b k) -> p b k", b=BT)
                                          .unsqueeze(2).broadcast_to([P, BT, HG, S]))
                last.then_inc(s["xnT4_ready"], 1)

            def kept(dst, src, column, at=slice(0, P)):
                if column in cols:
                    return lambda c: nc.scalar.activation(dst(c), src(c), ACT.Identity,
                                                          bias=cols[column][at, c:c + 1])
                return lambda c: nc.scalar.copy(dst(c), src(c))

            def keep_queries_and_keys(n):
                after(act, s["q_spread"], n - 1)
                after(act, s["kT_ready"] if rope else s["scores_ready"], n - 1)
                act.wait_ge(s["qk_ready"], n)
                for c in range(C):
                    last = kept(lambda c: qT[:, c, :], lambda c: ps_qk[:, 0, c, :], "bq")(c)
                last.then_inc(s["qT_ready"], 1)
                for c in range(C):
                    if rope:
                        last = kept(lambda c: kT[:, c, :], lambda c: ps_qk[:, 1, c, :], "bk")(c)
                    else:
                        for half in range(2):
                            at = slice(GD * half, GD * half + GD)
                            last = kept(lambda c: k_by_half[at, c, :, half, :],
                                        lambda c: ps_qk[at, 1, c, :].rearrange("p (b k) -> p b k", b=BT), "bk",
                                        at)(c)
                last.then_inc(s["rotk_mult"] if rope else s["kT_ready"], 1)
                if rope:
                    for a, (dst, column) in enumerate(((qrot, "bqr"), (krot, "bkr"))):
                        for c in range(C):
                            last = kept(lambda c: dst[:, c, :], lambda c: ps_qkr[:, a, c, :], column)(c)
                    last.then_inc(s["rotq_mult"], 1)
                wait(act, s["rotq_mult"] if rope else s["kT_ready"], n)
                act.sem_inc(s["qk_kept"], 1)

            def exps(n):
                act.wait_ge(s["shifted_ready"], n)
                nc.scalar.activation(shifted[:], shifted[:], ACT.Exp).then_inc(s["exp_ready"], 1)

            def spread_values(n):
                after(act, s["ctx_ready"], n - 1)
                act.wait_ge(s["v_ready"], n)
                for h in range(HG):
                    last = nc.scalar.activation(
                        v_by_head[:, :, :, h, :], ps_v[:].rearrange("p b (g h d) -> p b g h d", g=G, h=HG)[:, :, :, h, :],
                        ACT.Copy, scale=quarter[:, h:h + 1])
                last.then_inc(s["v_spread"], 1)

            def keep_context(n):
                after(act, s["y_ready"], n - 1)
                act.wait_ge(s["ctx_ready"], n)
                for c in range(C):
                    last = kept(lambda c: ctxT[:, c, :], lambda c: ps_o[:, c, :], "bv")(c)
                last.then_inc(s["ctxT_ready"], 1)

            def turn(i, now, ahead, ahead2):
                if ahead and not now:
                    core.wait_for_pack(act)
                if now:
                    exps(i + 1)
                if ahead:
                    keep_queries_and_keys(i + 2)
                if now:
                    keep_context(i + 1)
                if ahead:
                    spread_values(i + 2)
                if ahead2:
                    keep_xnT(i + 3)

            act.wait_ge(s["cleared"], 1)
            staged_tiles(act, turn)

        @block.vector
        def _(dve):
            nc.vector.memset(k_by_half[:], 0.0).then_inc(s["cleared"], 1)
            dve.wait_ge(s["cleared"], 1)
            if alibi:
                core.wait_for_pack(dve)
                for g in range(G):
                    last = nc.vector.tensor_scalar(bias[:, g, :], core.table("relative"), slope[:, g:g + 1], None,
                                                   ALU.mult)
                last.then_inc(s["bias_1"], 1)
                dve.wait_ge(s["bias_1"], 1)
                nc.vector.tensor_tensor(bias[:], bias[:], core.table("later").unsqueeze(1).broadcast_to([P, G, S]),
                                        ALU.add).then_inc(s["bias_2"], 1)
                dve.wait_ge(s["bias_2"], 1)

            def rotate(n):
                dve.wait_ge(s["rotq_mult"], n)
                nc.vector.tensor_tensor(flat(qT), flat(qT), turns("cosine"), ALU.mult)
                nc.vector.tensor_tensor(flat(qrot), flat(qrot), turns("sine"), ALU.mult).then_inc(s["rot_1"], 1)
                dve.wait_ge(s["rot_2"], n)
                after(dve, s["scores_ready"], n - 1)
                for half in range(2):
                    at = slice(GD * half, GD * half + GD)
                    last = nc.vector.tensor_tensor(k_by_half[at, :, :, half, :],
                                                   kT[at].rearrange("p c (b k) -> p c b k", b=BT),
                                                   krot[at].rearrange("p c (b k) -> p c b k", b=BT), ALU.add)
                last.then_inc(s["kT_ready"], 1)
                dve.wait_ge(s["rot_1"], n)
                nc.vector.tensor_tensor(qT[:], qT[:], qrot[:], ALU.add).then_inc(s["rot_3"], 1)
                dve.wait_ge(s["rot_3"], n)

            def spread_queries(n):
                dve.wait_ge(s["qT_ready"], n)
                if rope:
                    rotate(n)
                after(dve, s["scores_ready"], n - 1)
                for c in range(C):
                    last = nc.vector.tensor_tensor(
                        q_by_head[:, c], qT[:, c, :].rearrange("p (b q) -> p b q", b=BT).unsqueeze(2).broadcast_to(
                            [P, BT, HG, S]),
                        head_of_feature.unsqueeze(1).unsqueeze(3).broadcast_to([P, BT, HG, S]), ALU.mult)
                last.then_inc(s["q_spread"], 1)

            def less_maximum(n):
                dve.wait_ge(s["scores_ready"], n)
                scores = ps_s[:]
                if alibi:
                    nc.vector.tensor_tensor(
                        biased[:].rearrange("p (b g) k -> p b (g k)", b=BT), ps_s[:].rearrange("p (b g) k -> p b (g k)", b=BT),
                        bias[:].rearrange("p g k -> p (g k)").unsqueeze(1).broadcast_to([P, BT, G * S]),
                        ALU.add).then_inc(s["biased_ready"], 1)
                    dve.wait_ge(s["biased_ready"], n)
                    scores = biased[:]
                nc.vector.tensor_reduce(big[:], scores, X, ALU.max).then_inc(s["max_ready"], 1)
                dve.wait_ge(s["max_ready"], n)
                nc.vector.tensor_tensor(shifted[:], scores, big[:].unsqueeze(2).broadcast_to([P, BT * G, S]),
                                        ALU.subtract).then_inc(s["shifted_ready"], 1)

            def probabilities(n):
                dve.wait_ge(s["exp_ready"], n)
                nc.vector.tensor_reduce(rsum[:], shifted[:], X, ALU.add).then_inc(s["sum_ready"], 1)
                dve.wait_ge(s["sum_ready"], n)
                nc.vector.reciprocal(rinv[:], rsum[:]).then_inc(s["inv_ready"], 1)
                dve.wait_ge(s["inv_ready"], n)
                nc.vector.tensor_tensor(probs[:], shifted[:], rinv[:].unsqueeze(2).broadcast_to([P, BT * G, S]),
                                        ALU.mult).then_inc(s["probs_ready"], 1)
                dve.wait_ge(s["probs_ready"], n)
                after(dve, s["ctx_ready"], n - 1)
                nc.vector.transpose(probsT[:].rearrange("p a k -> p (a k)"),
                                    probs[:].rearrange("p a k -> p (a k)")).then_inc(s["probs_turned"], 1)

            def add_output(i, n):
                dve.wait_ge(s["y_ready"], n)
                dve.wait_ge(s["x_biased"], n)
                nc.vector.tensor_tensor(core.x[:, i, :], ps_y[:], x_plus_bo[:], ALU.add).then_inc(s["x_done"], 1)

            def turn(i, now, ahead, ahead2):
                if now:
                    less_maximum(i + 1)
                if now and not_first(i):
                    add_output(i - 1, i)
                if ahead2:
                    norm_stats(dve, nc, s, i + 3, core.x[:, i + 2, :], stats[:], mean[:])
                if now:
                    probabilities(i + 1)
                if ahead2:
                    after(dve, s["xn_turned"], i + 2)
                    normed(dve, nc, s, i + 3, core.x[:, i + 2, :], xn[:], mean[:], rstd[:])
                if ahead:
                    spread_queries(i + 2)

            staged_tiles(dve, turn)
            add_output(NT - 1, NT)


def cross_attention(core, tag, mask=None, mask_type=None):
    nc = core.nc
    K2 = KEYS - 1
    with ExitStack() as ctx:
        def sb(name, shape, dt=F32):
            return ctx.enter_context(nc.sbuf_tensor(f"{tag}_{name}", shape, dt))

        def ps(name, shape):
            return ctx.enter_context(nc.psum_tensor(f"{tag}_{name}", shape, F32))

        s = semaphores(nc, tag, LN_SEMS + """ xn_turned xnT_ready q_ready
            qT_ready q_spread tail_copied tail_cleared tail_keys_ready tail_keys tail_values_ready tail_values tail_half
            tail_scores_ready tail_scores y_ready x_biased x_done mask_loaded mask_bias_ready mask_read""")
        per_batch = {k: [nc.alloc_semaphore(f"{tag}_{k}{b}") for b in range(BT)] for k in
                     """ctx_loaded ctx_used k_ready kT_ready v_ready v_kept scores_ready biased_ready row_ready max_ready
                     exp_ready inv_ready probs_turned_1 probs_turned probsT_1 probsT_2 o_ready o_kept oT_ready
                     oT_kept""".split()}
        pack = core.pack(tag)
        wt, wo = {k: pack[k] for k in "qkv"}, pack["o"]
        cols = {k: pack[k] for k in ("bq", "bk") if k in pack}
        rows = {k: pack[k] for k in ("bv", "bo") if k in pack}
        ctx_tail = pack["ctx_tail"]
        ctx_sb = sb("ctx_sb", [P, BT, C, K2])
        stats, mean, rstd = sb("stats", [P, 6]), sb("mean", [P, 2]), sb("rstd", [P, 1])
        xn, xnT, qT = sb("xn", [P, D]), sb("xnT", [P, C, P]), sb("qT", [P, C, P])
        q_by_head = sb("q_by_head", [P, C, BT, HG, S])
        tail_rep = sb("tail_rep", [P, C, BT, S])
        k_tail = sb("k_tail", [P, C, BT, 2])
        s_tail = sb("s_tail", [P, BT, G])
        v_tail = sb("v_tail", [P, D])
        kT = sb("kT", [P, 2, C, K2])
        v = sb("v", [P, BT, 2, D])
        scores = sb("scores", [P, BT, G, KEYS])
        bias = sb("bias", [P, BT, KEYS]) if mask else pack["bias"]
        mask_raw = sb("mask_raw", [P, BT, KEYS], mask_type) if mask else None
        minus_big, rsum, rinv = sb("minus_big", [P, BT, G]), sb("rsum", [P, BT, G]), sb("rinv", [P, BT, G])
        probsT = sb("probsT", [P, 2, G, P])
        probsT_tail = sb("probsT_tail", [P, P])
        o = sb("o", [P, BT, G, HD])
        oT = sb("oT", [GD, HG, BT, S])
        x_plus_bo = sb("x_plus_bo", [P, D])
        ps_s = ps("ps_s", [P, 2, 2, K2])
        ps_k = ps("ps_k", [P, C, K2])
        ps_v = ps("ps_v", [P, 2, D])
        ps_p = ps("ps_p", [P, 2, G, P])
        ps_a = ps("ps_a", [P, 512])
        ps_o, ps_oT, ps_pt = ps_a[:, 0:256], ps_a[0:GD, 256:384], ps_a[:, 384:512]
        ps_b = ps("ps_b", [P, 512])
        ps_t, ps_vt = ps_b[:, 0:256], ps_b[:, 256:512]
        ident = core.table("ident")
        block = ctx.enter_context(nc.Block())

        def j_of(g):
            return (g % 2) * 2 + g // 2

        @block.sync
        def _(sp):
            core.load_packs(sp)
            context = core.inputs["ctx_T"].rearrange("(c p) (t b k) -> p t b c k", p=P, b=BT, k=KEYS)
            if mask:
                mask_rows = core.inputs[mask].rearrange("(t n) -> t n", n=BT * KEYS)
            with sp.Fori(0, NT) as i:
                if mask:
                    wait(sp, s["mask_read"], i + 1)
                    sp.dma_start(mask_raw[:].rearrange("p b k -> p (b k)"),
                                 mask_rows[bass.ds(i, 1), :].broadcast_to([P, BT * KEYS])).then_inc(s["mask_loaded"], 16)
                for b in range(BT):
                    wait(sp, per_batch["ctx_used"][b], i + 1)
                    sp.dma_start(ctx_sb[:, b], context[:, i, b, :, 0:K2]).then_inc(
                        per_batch["ctx_loaded"][b], 16)

        def all_tiles(engine, turn):
            turn(0, first=True, last=False)
            with engine.Fori(1, NT - 1) as i:
                turn(i, first=False, last=False)
            turn(NT - 1, first=False, last=True)

        def batch(t, n, first, last):
            if (t < 0 and first) or (t >= BT and last):
                return None
            return t % BT, n + t // BT

        @block.gpsimd
        def _(pool):
            if mask:
                pool.sem_inc(s["mask_read"], 1)

            def front(i, n):
                layer_norm_root(pool, nc, s, n, mean[:], rstd[:], core.table("minus_half"))
                if isinstance(n, int) and n == 1:
                    core.wait_for_pack(pool)
                after(pool, s["tail_values_ready"], n - 1)
                for c in range(C):
                    last = nc.gpsimd.tensor_copy(tail_rep[:, c], ctx_tail[:, c, bass.ds(i * BT, BT)].unsqueeze(2)
                                                 .broadcast_to([P, BT, S]))
                last.then_inc(s["tail_copied"], 1)

            def mask_bias(n):
                if mask:
                    after(pool, per_batch["biased_ready"][BT - 1], n - 1)
                    wait(pool, s["mask_loaded"], n * 16)
                    nc.gpsimd.tensor_scalar(bias[:], mask_raw[:], 0.0, MASKED, ALU.is_equal, ALU.mult).then_inc(
                        s["mask_bias_ready"], 1)
                    wait(pool, s["mask_bias_ready"], n)
                    pool.sem_inc(s["mask_read"], 1)

            def turn(i, first, last):
                n = i + 1
                if not last:
                    front(i + 1, n + 1)
                if "bo" in rows:
                    after(pool, s["x_done"], n - 1)
                    nc.gpsimd.tensor_tensor(x_plus_bo[:], core.x[:, i, :], rows["bo"][:], ALU.add).then_inc(
                        s["x_biased"], 1)
                if not last:
                    mask_bias(n + 1)

            front(0, 1)
            mask_bias(1)
            all_tiles(pool, turn)

        @block.tensor
        def _(pe):
            for b in range(BT):
                pe.sem_inc(per_batch["ctx_used"][b], 1)

            def turn_xn(n):
                after(pe, s["x_done"], n - 2)
                after(pe, s["tail_values"], n - 1)
                pe.wait_ge(s["xn_ready"], n)
                nc.tensor.transpose(ps_t[:, 0:P], xn[:, 0:P], ident)
                nc.tensor.transpose(ps_t[:, P:D], xn[:, P:D], ident).then_inc(s["xn_turned"], 1)

            def queries(n):
                pe.wait_ge(s["xnT_ready"], n)
                for oc in range(C):
                    for c in range(C):
                        last = nc.tensor.matmul(ps_t[:, oc * P:oc * P + P], wt["q"][:, c, oc * P:oc * P + P],
                                                xnT[:, c, :], start=(c == 0), stop=(c == C - 1))
                last.then_inc(s["q_ready"], 1)

            def tail_keys(n):
                pe.wait_ge(s["tail_copied"], n)
                pe.wait_ge(s["qT_ready"], n)
                for oc in range(C):
                    for c in range(C):
                        last = nc.tensor.matmul(ps_vt[:, oc * BT:oc * BT + BT], wt["k"][:, c, oc * P:oc * P + P],
                                                tail_rep[:, c, :, 0], start=(c == 0), stop=(c == C - 1))
                last.then_inc(s["tail_keys_ready"], 1)

            def tail_scores(n):
                pe.wait_ge(s["q_spread"], n)
                wait(pe, s["tail_keys"], n)
                for b in range(BT):
                    for c in range(C):
                        last = nc.tensor.matmul(ps_vt[:, (b * C + c) * 2:(b * C + c) * 2 + 2],
                                                q_by_head[:, c, b, :, :], k_tail[:, c, b, :], start=True, stop=True)
                last.then_inc(s["tail_scores_ready"], 1)

            def tail_values(n):
                pe.wait_ge(s["tail_scores"], n)
                for c in range(C):
                    last = nc.tensor.matmul(ps_vt, tail_rep[:, c, :, :], wt["v"][:, c, :],
                                            start=(c == 0), stop=(c == C - 1))
                last.then_inc(s["tail_values_ready"], 1)

            def keys_and_values(at, before):
                b, n = at
                pe.wait_ge(per_batch["ctx_loaded"][b], n * 16)
                if before:
                    pe.wait_ge(per_batch["kT_ready"][before[0]], before[1])
                for oc in range(C):
                    for c in range(C):
                        last = nc.tensor.matmul(ps_k[:, oc, :], wt["k"][:, c, oc * P:oc * P + P],
                                                ctx_sb[:, b, c, :], start=(c == 0), stop=(c == C - 1))
                last.then_inc(per_batch["k_ready"][b], 1)
                if before:
                    pe.wait_ge(per_batch["v_kept"][before[0]], before[1])
                for kc in range(2):
                    for c in range(C):
                        last = nc.tensor.matmul(ps_v[:, kc, :], ctx_sb[:, b, c, kc * P:kc * P + P],
                                                wt["v"][:, c, :], start=(c == 0), stop=(c == C - 1))
                last.then_inc(per_batch["v_ready"][b], 1)

            def score(at, before):
                b, n = at
                if before:
                    pe.wait_ge(per_batch["biased_ready"][before[0]], before[1])
                pe.wait_ge(s["q_spread"], n)
                wait(pe, per_batch["kT_ready"][b], n)
                for g in range(G):
                    rows_g = slice(GD * (g % 2), GD * (g % 2) + GD)
                    last = nc.tensor.matmul(ps_s[:, g % 2, g // 2, :], q_by_head[rows_g, g // 2, b, :, :],
                                            kT[rows_g, b % 2, g // 2, :], start=True, stop=True)
                last.then_inc(per_batch["scores_ready"][b], 1)

            def turn_probs(at, before):
                b, n = at
                pe.wait_ge(per_batch["exp_ready"][b], n)
                if before:
                    pe.wait_ge(per_batch["probsT_2"][before[0]], before[1])
                    pe.wait_ge(per_batch["probsT_1"][before[0]], before[1])
                for kc in range(2):
                    for j in range(G):
                        last = nc.tensor.transpose(ps_p[:, kc, j, :], scores[:, b, j, kc * P:kc * P + P], ident)
                    if kc == 0:
                        last.then_inc(per_batch["probs_turned_1"][b], 1)
                if before:
                    pe.wait_ge(per_batch["oT_kept"][before[0]], before[1])
                nc.tensor.matmul(ps_pt[S * b:S * b + G, :], scores[:, b, :, K2], ident, start=True,
                                 stop=True).then_inc(per_batch["probs_turned"][b], 1)

            def outputs(at):
                b, n = at
                pe.wait_ge(s["tail_values"], n)
                pe.wait_ge(per_batch["v_kept"][b], n)
                pe.wait_ge(per_batch["probsT_1"][b], n)
                wait(pe, per_batch["probsT_2"][b], n)
                nc.tensor.matmul(ps_o, probsT_tail[S * b:S * b + G, :], v_tail[S * b:S * b + G, :],
                                 start=True, stop=False, skip_group_check=True, tile_position=(S * b, 0))
                for g in range(G):
                    for kc in range(2):
                        last = nc.tensor.matmul(ps_o[:, g * GD:g * GD + GD], probsT[:, kc, j_of(g), :],
                                                v[:, b, kc, g * GD:g * GD + GD], start=False,
                                                stop=(kc == 1), skip_group_check=True)
                last.then_inc(per_batch["o_ready"][b], 1)

            def turn_outputs(at):
                b, n = at
                wait(pe, per_batch["o_kept"][b], n)
                nc.tensor.transpose(ps_oT, o[:, b].rearrange("p g d -> p (g d)"), ident).then_inc(
                    per_batch["oT_ready"][b], 1)

            def tile_output(n):
                pe.wait_ge(per_batch["oT_kept"][BT - 1], n)
                for h in range(HG):
                    last = nc.tensor.matmul(ps_t, oT[:, h, :, :], wo[:, h, :], start=(h == 0), stop=(h == HG - 1))
                last.then_inc(s["y_ready"], 1)

            def turn(i, first, last):
                n = i + 1
                for t in range(BT):
                    now, before, ahead, ahead2 = (batch(t + k, n, first, last) for k in (0, -1, 1, 2))
                    if ahead:
                        score(ahead, now)
                    if before:
                        turn_outputs(before)
                    if t == 0:
                        tail_values(n)
                    if not last and t == 1:
                        turn_xn(n + 1)
                    if not last and t == 2:
                        tail_keys(n + 1)
                    if not last and t == 3:
                        tail_scores(n + 1)
                    turn_probs(now, before)
                    if ahead2:
                        keys_and_values(ahead2, ahead)
                    if not last and t == 1:
                        queries(n + 1)
                    if not first and t == 0:
                        wait(pe, s["tail_values"], n)
                        tile_output(n - 1)
                    outputs(now)
                    if ahead2:
                        wait(pe, per_batch["v_ready"][ahead2[0]], ahead2[1])
                        pe.sem_inc(per_batch["ctx_used"][ahead2[0]], 1)

            turn_xn(1)
            core.wait_for_pack(pe)
            queries(1)
            keys_and_values((0, 1), None)
            keys_and_values((1, 1), (0, 1))
            for b in range(2):
                wait(pe, per_batch["v_ready"][b], 1)
                pe.sem_inc(per_batch["ctx_used"][b], 1)
            tail_keys(1)
            score((0, 1), None)
            tail_scores(1)
            all_tiles(pe, turn)
            turn_outputs((BT - 1, NT))
            tile_output(NT)

        @block.scalar
        def _(act):
            nc.scalar.activation(k_tail[:], core.table("iota")[:, 0:C * BT * 2], ACT.Copy, scale=0.0).then_inc(s["tail_cleared"], 1)
            act.wait_ge(s["tail_cleared"], 1)

            def keep_xnT(n):
                act.wait_ge(s["xn_turned"], n)
                nc.scalar.copy(xnT[:].rearrange("p c n -> p (c n)"), ps_t).then_inc(s["xnT_ready"], 1)

            def keep_q(n):
                act.wait_ge(s["q_ready"], n)
                for c in range(C):
                    if "bq" in cols:
                        last = nc.scalar.activation(qT[:, c, :], ps_t[:, c * P:c * P + P], ACT.Identity,
                                                    bias=cols["bq"][:, c:c + 1])
                    else:
                        last = nc.scalar.copy(qT[:, c, :], ps_t[:, c * P:c * P + P])
                last.then_inc(s["qT_ready"], 1)

            def keep_tail_keys(n):
                act.wait_ge(s["tail_keys_ready"], n)
                for c in range(C):
                    for half in range(2):
                        at = slice(GD * half, GD * half + GD)
                        if "bk" in cols:
                            last = nc.scalar.activation(k_tail[at, c, :, half], ps_vt[at, c * BT:c * BT + BT],
                                                        ACT.Identity, bias=cols["bk"][at, c:c + 1])
                        else:
                            last = nc.scalar.copy(k_tail[at, c, :, half], ps_vt[at, c * BT:c * BT + BT])
                last.then_inc(s["tail_keys"], 1)

            def keep_keys(at, used):
                b, n = at
                act.wait_ge(per_batch["k_ready"][b], n)
                if used:
                    act.wait_ge(per_batch["scores_ready"][used[0]], used[1])
                for c in range(C):
                    if "bk" in cols:
                        last = nc.scalar.activation(kT[:, b % 2, c, :], ps_k[:, c, :], ACT.Identity,
                                                    bias=cols["bk"][:, c:c + 1])
                    else:
                        last = nc.scalar.copy(kT[:, b % 2, c, :], ps_k[:, c, :])
                last.then_inc(per_batch["kT_ready"][b], 1)

            def exps(at):
                b, n = at
                act.wait_ge(per_batch["max_ready"][b], n)
                for j in range(G):
                    last = nc.scalar.activation(scores[:, b, j, :], scores[:, b, j, :], ACT.Exp,
                                                bias=minus_big[:, b, j:j + 1], accum_out=rsum[:, b, j:j + 1])
                last.then_inc(per_batch["exp_ready"][b], 1)

            def keep_probs(at, before):
                b, n = at
                act.wait_ge(per_batch["probs_turned_1"][b], n)
                if before:
                    act.wait_ge(per_batch["o_ready"][before[0]], before[1])
                nc.scalar.copy(probsT[:, 0], ps_p[:, 0]).then_inc(per_batch["probsT_1"][b], 1)

            def keep_outputs(at):
                b, n = at
                if b == 0:
                    after(act, s["y_ready"], n - 1)
                act.wait_ge(per_batch["oT_ready"][b], n)
                nc.scalar.copy(oT[:, :, b, :], ps_oT.rearrange("p (h q) -> p h q", h=HG)).then_inc(
                    per_batch["oT_kept"][b], 1)

            def turn(i, first, last):
                n = i + 1
                for t in range(BT):
                    now, before, ahead, ahead2 = (batch(t + k, n, first, last) for k in (0, -1, 1, 2))
                    if before:
                        keep_outputs(before)
                    if not last and t == 1:
                        keep_xnT(n + 1)
                    if not last and t == 2:
                        keep_tail_keys(n + 1)
                    keep_probs(now, before)
                    if ahead:
                        exps(ahead)
                    if ahead2:
                        keep_keys(ahead2, now)
                    if not last and t == 1:
                        keep_q(n + 1)

            keep_xnT(1)
            core.wait_for_pack(act)
            keep_q(1)
            keep_keys((0, 1), None)
            keep_keys((1, 1), None)
            keep_tail_keys(1)
            exps((0, 1))
            all_tiles(act, turn)
            keep_outputs((BT - 1, NT))

        @block.vector
        def _(dve):
            def tile_stats(i, n):
                norm_stats(dve, nc, s, n, core.x[:, i, :], stats[:], mean[:])

            def tile_normed(i, n):
                normed(dve, nc, s, n, core.x[:, i, :], xn[:], mean[:], rstd[:])

            def spread_q(n):
                dve.wait_ge(s["qT_ready"], n)
                after(dve, per_batch["scores_ready"][BT - 1], n - 1)
                for c in range(C):
                    last = nc.vector.tensor_tensor(
                        q_by_head[:, c], qT[:, c, :].rearrange("p (b q) -> p b q", b=BT).unsqueeze(2).broadcast_to(
                            [P, BT, HG, S]),
                        core.table("head_of_feature").unsqueeze(1).unsqueeze(3).broadcast_to([P, BT, HG, S]),
                        ALU.mult)
                last.then_inc(s["q_spread"], 1)

            def keep_tail_scores(n):
                if mask:
                    dve.wait_ge(s["mask_bias_ready"], n)
                dve.wait_ge(s["tail_scores_ready"], n)
                raw = ps_vt[:, 0:BT * G].rearrange("p (b c j) -> p b j c", b=BT, j=2)
                kept = s_tail[:].rearrange("p b (j c) -> p b j c", j=2)
                if bias is None:
                    last = nc.vector.tensor_copy(kept, raw)
                else:
                    of_tail = bias[:, :, K2:KEYS] if mask else bias[:, K2:KEYS].unsqueeze(1).broadcast_to([P, BT, 1])
                    last = nc.vector.tensor_tensor(kept, raw, of_tail.unsqueeze(3).broadcast_to([P, BT, 2, C]),
                                                   ALU.add)
                last.then_inc(s["tail_scores"], 1)

            def keep_tail_values(n):
                dve.wait_ge(s["tail_values_ready"], n)
                after(dve, per_batch["o_ready"][BT - 1], n - 1)
                if "bv" in rows:
                    nc.vector.tensor_tensor(v_tail[:], ps_vt, rows["bv"][:], ALU.add).then_inc(s["tail_half"], 1)
                else:
                    nc.vector.tensor_copy(v_tail[:], ps_vt).then_inc(s["tail_half"], 1)
                dve.wait_ge(s["tail_half"], n)
                nc.vector.tensor_tensor(v_tail[:], v_tail[:], core.table("group_rows"), ALU.mult).then_inc(
                    s["tail_values"], 1)

            def maxima(at):
                b, n = at
                dve.wait_ge(per_batch["scores_ready"][b], n)
                after(dve, per_batch["probs_turned"][b], n - 1)
                nc.vector.tensor_tensor(
                    scores[:, b, :, 0:K2], ps_s[:].rearrange("p j c k -> p (j c) k"),
                    (bias[:, b, 0:K2] if mask else bias[:, 0:K2]).unsqueeze(1).broadcast_to([P, G, K2]), ALU.add).then_inc(
                        per_batch["biased_ready"][b], 1)
                dve.wait_ge(s["tail_scores"], n)
                nc.vector.tensor_copy(scores[:, b, :, K2], s_tail[:, b, :]).then_inc(per_batch["row_ready"][b], 1)
                dve.wait_ge(per_batch["biased_ready"][b], n)
                dve.wait_ge(per_batch["row_ready"][b], n)
                nc.vector.tensor_reduce(minus_big[:, b, :], scores[:, b], X, ALU.max, negate=True).then_inc(
                    per_batch["max_ready"][b], 1)

            def keep_values(at):
                b, n = at
                dve.wait_ge(per_batch["v_ready"][b], n)
                after(dve, per_batch["o_ready"][b], n - 1)
                if "bv" in rows:
                    last = nc.vector.tensor_tensor(v[:, b], ps_v[:], rows["bv"][:].unsqueeze(1).broadcast_to(
                        [P, 2, D]), ALU.add)
                else:
                    last = nc.vector.tensor_copy(v[:, b], ps_v[:])
                last.then_inc(per_batch["v_kept"][b], 1)

            def keep_probs(at, before):
                b, n = at
                dve.wait_ge(per_batch["probs_turned"][b], n)
                if before:
                    dve.wait_ge(per_batch["o_ready"][before[0]], before[1])
                nc.vector.tensor_copy(probsT_tail[S * b:S * b + G, :], ps_pt[S * b:S * b + G, :])
                nc.vector.tensor_copy(probsT[:, 1], ps_p[:, 1]).then_inc(per_batch["probsT_2"][b], 1)

            def keep_outputs(at):
                b, n = at
                dve.wait_ge(per_batch["exp_ready"][b], n)
                nc.vector.reciprocal(rinv[:, b, :], rsum[:, b, :]).then_inc(per_batch["inv_ready"][b], 1)
                dve.wait_ge(per_batch["o_ready"][b], n)
                dve.wait_ge(per_batch["inv_ready"][b], n)
                for h in range(HG):
                    at_h = slice(S * h, S * h + S)
                    last = nc.vector.tensor_tensor(
                        o[at_h, b].rearrange("p (c j) d -> p c j d", j=2),
                        ps_o[at_h, :].rearrange("p (c j h d) -> p c j h d", c=C, j=2, h=HG)[:, :, :, h, :],
                        rinv[at_h, b, :].rearrange("p (j c) -> p c j", j=2).unsqueeze(3).broadcast_to(
                            [S, C, 2, HD]), ALU.mult)
                last.then_inc(per_batch["o_kept"][b], 1)

            def add_output(i, n):
                dve.wait_ge(s["y_ready"], n)
                if "bo" in rows:
                    dve.wait_ge(s["x_biased"], n)
                    nc.vector.tensor_tensor(core.x[:, i, :], ps_t, x_plus_bo[:], ALU.add).then_inc(s["x_done"], 1)
                else:
                    nc.vector.tensor_tensor(core.x[:, i, :], ps_t, core.x[:, i, :], ALU.add).then_inc(s["x_done"], 1)

            def turn(i, first, last):
                n = i + 1
                for t in range(BT):
                    now, before, ahead, ahead2 = (batch(t + k, n, first, last) for k in (0, -1, 1, 2))
                    if before:
                        keep_outputs(before)
                    if not last and t == 0:
                        tile_stats(i + 1, n + 1)
                    if not last and t == 3:
                        keep_tail_scores(n + 1)
                    if ahead:
                        maxima(ahead)
                    if t == 0:
                        keep_tail_values(n)
                    keep_probs(now, before)
                    if not last and t == 2:
                        spread_q(n + 1)
                    if ahead2:
                        keep_values(ahead2)
                    if not first and t == 0:
                        add_output(i - 1, n - 1)
                    if not last and t == 0:
                        tile_normed(i + 1, n + 1)

            tile_stats(0, 1)
            tile_normed(0, 1)
            core.wait_for_pack(dve)
            spread_q(1)
            keep_values((0, 1))
            keep_values((1, 1))
            keep_tail_scores(1)
            maxima((0, 1))
            all_tiles(dve, turn)
            keep_outputs((BT - 1, NT))
            add_output(NT - 1, NT)


def complex_attention(core, tag):
    nc = core.nc
    E = 2 * D
    CE = E // P
    scale = 1.0 / np.sqrt(D)
    with ExitStack() as ctx:
        def sb(name, shape, dt=F32):
            return ctx.enter_context(nc.sbuf_tensor(f"{tag}_{name}", shape, dt))

        def ps(name, shape):
            return ctx.enter_context(nc.psum_tensor(f"{tag}_{name}", shape, F32))

        s = semaphores(nc, tag, LN_SEMS + """ cleared xn_turned xnT_ready q_ready k_ready v_ready
            qT_ready kT_ready v_kept scores_ready max_ready bias_ready exp_ready inv_ready probs_ready probs_turned
            o_ready oT_ready y_ready x_biased x_done""")
        pack = core.pack(tag)
        wt, wo = {k: pack[k] for k in "qkv"}, pack["o"]
        cols, bo = {k: pack[k] for k in ("bq", "bk", "bv")}, pack["bo"]
        stats, mean, rstd = sb("stats", [P, 6]), sb("mean", [P, 2]), sb("rstd", [P, 1])
        xn, xnT = sb("xn", [P, D]), sb("xnT", [P, C, P])
        qT, kT, v = sb("qT", [P, CE, P]), sb("kT", [P, CE, P]), sb("v", [P, E])
        big, minus_big = sb("big", [P, 1]), sb("minus_big", [P, 1])
        rsum, rinv = sb("rsum", [P, 1]), sb("rinv", [P, 1])
        probs, probsT = sb("probs", [P, S]), sb("probsT", [P, P])
        oT = sb("oT", [P, CE, P])
        x_plus_bo = sb("x_plus_bo", [P, D])
        ps_t, ps_q, ps_k = ps("ps_t", [P, D]), ps("ps_q", [P, CE, P]), ps("ps_k", [P, CE, P])
        ps_v, ps_s, ps_o, ps_y = ps("ps_v", [P, E]), ps("ps_s", [P, S]), ps("ps_o", [P, CE, P]), ps("ps_y", [P, D])
        ident = core.table("ident")
        block = ctx.enter_context(nc.Block())

        @block.sync
        def _(sp):
            core.load_packs(sp)

        @block.gpsimd
        def _(pool):
            def turn(i, now, ahead, ahead2):
                if ahead and not now:
                    core.wait_for_pack(pool)
                if ahead2:
                    layer_norm_root(pool, nc, s, i + 3, mean[:], rstd[:], core.table("minus_half"))
                if now:
                    after(pool, s["x_done"], i)
                    nc.gpsimd.tensor_tensor(x_plus_bo[:], core.x[:, i, :], bo[:], ALU.add).then_inc(s["x_biased"], 1)

            staged_tiles(pool, turn)

        @block.tensor
        def _(pe):
            def turn_xn(n):
                after(pe, s["xnT_ready"], n - 1)
                pe.wait_ge(s["xn_ready"], n)
                for c in range(C):
                    last = nc.tensor.transpose(ps_t[:, c * P:c * P + P], xn[:, c * P:c * P + P], ident)
                last.then_inc(s["xn_turned"], 1)

            def queries_and_keys(n):
                pe.wait_ge(s["xnT_ready"], n)
                for k, dst in (("q", ps_q), ("k", ps_k)):
                    after(pe, s[k + "T_ready"], n - 1)
                    for oc in range(CE):
                        for c in range(C):
                            last = nc.tensor.matmul(dst[:, oc, :], wt[k][:, c, oc * P:oc * P + P], xnT[:, c, :],
                                                    start=(c == 0), stop=(c == C - 1))
                    last.then_inc(s[k + "_ready"], 1)

            def values(n):
                after(pe, s["v_kept"], n - 1)
                for c in range(C):
                    last = nc.tensor.matmul(ps_v[:], xnT[:, c, :], wt["v"][:, c, :], start=(c == 0), stop=(c == C - 1))
                last.then_inc(s["v_ready"], 1)

            def scores(n):
                after(pe, s["exp_ready"], n - 1)
                pe.wait_ge(s["qT_ready"], n)
                wait(pe, s["kT_ready"], n)
                for b in range(BT):
                    at = slice(S * b, S * b + S)
                    for c in range(CE):
                        last = nc.tensor.matmul(ps_s[at, :], qT[:, c, at], kT[:, c, at],
                                                start=(c == 0), stop=(c == CE - 1))
                last.then_inc(s["scores_ready"], 1)

            def weighed_values(n):
                pe.wait_ge(s["v_kept"], n)
                pe.wait_ge(s["probs_turned"], n)
                after(pe, s["oT_ready"], n - 1)
                for c in range(CE):
                    last = nc.tensor.matmul(ps_o[:, c, :], v[:, c * P:c * P + P], probsT[:], start=True, stop=True)
                last.then_inc(s["o_ready"], 1)

            def output(n):
                after(pe, s["x_done"], n - 1)
                pe.wait_ge(s["oT_ready"], n)
                for c in range(CE):
                    last = nc.tensor.matmul(ps_y[:], oT[:, c, :], wo[:, c, :], start=(c == 0), stop=(c == CE - 1))
                last.then_inc(s["y_ready"], 1)

            def turn(i, now, ahead, ahead2):
                if ahead and not now:
                    core.wait_for_pack(pe)
                if now:
                    scores(i + 1)
                if ahead:
                    queries_and_keys(i + 2)
                if now:
                    weighed_values(i + 1)
                if ahead:
                    values(i + 2)
                if ahead2:
                    turn_xn(i + 3)
                if now:
                    output(i + 1)

            staged_tiles(pe, turn)

        @block.scalar
        def _(act):
            def keep_xnT(n):
                after(act, s["v_ready"], n - 1)
                act.wait_ge(s["xn_turned"], n)
                nc.scalar.copy(xnT[:].rearrange("p c n -> p (c n)"), ps_t[:]).then_inc(s["xnT_ready"], 1)

            def keep_queries_and_keys(n):
                after(act, s["scores_ready"], n - 1)
                for k, dst, src in (("q", qT, ps_q), ("k", kT, ps_k)):
                    act.wait_ge(s[k + "_ready"], n)
                    for c in range(CE):
                        last = nc.scalar.activation(dst[:, c, :], src[:, c, :], ACT.Identity,
                                                    bias=cols["b" + k][:, c:c + 1])
                    last.then_inc(s[k + "T_ready"], 1)

            def exps(n):
                act.wait_ge(s["bias_ready"], n)
                nc.scalar.activation(probs[:], ps_s[:], ACT.Exp, bias=minus_big[:], scale=float(scale),
                                     accum_out=rsum[:]).then_inc(s["exp_ready"], 1)

            def keep_context(n):
                after(act, s["y_ready"], n - 1)
                act.wait_ge(s["o_ready"], n)
                for c in range(CE):
                    last = nc.scalar.activation(oT[:, c, :], ps_o[:, c, :], ACT.Identity, bias=cols["bv"][:, c:c + 1])
                last.then_inc(s["oT_ready"], 1)

            def turn(i, now, ahead, ahead2):
                if ahead and not now:
                    core.wait_for_pack(act)
                if now:
                    exps(i + 1)
                if ahead:
                    keep_queries_and_keys(i + 2)
                if now:
                    keep_context(i + 1)
                if ahead2:
                    keep_xnT(i + 3)

            staged_tiles(act, turn)

        @block.vector
        def _(dve):
            nc.vector.memset(probsT[:], 0.0).then_inc(s["cleared"], 1)
            dve.wait_ge(s["cleared"], 1)

            def maxima(n):
                dve.wait_ge(s["scores_ready"], n)
                nc.vector.tensor_reduce(big[:], ps_s[:], X, ALU.max, negate=True).then_inc(s["max_ready"], 1)
                dve.wait_ge(s["max_ready"], n)
                nc.vector.tensor_scalar(minus_big[:], big[:], float(scale), None, ALU.mult).then_inc(s["bias_ready"], 1)

            def probabilities(n):
                dve.wait_ge(s["exp_ready"], n)
                nc.vector.reciprocal(rinv[:], rsum[:]).then_inc(s["inv_ready"], 1)
                dve.wait_ge(s["inv_ready"], n)
                nc.vector.tensor_scalar(probs[:], probs[:], rinv[:], None, ALU.mult).then_inc(s["probs_ready"], 1)
                dve.wait_ge(s["probs_ready"], n)
                after(dve, s["o_ready"], n - 1)
                for b in range(BT):
                    at = slice(S * b, S * b + S)
                    last = nc.vector.transpose(probsT[at, at], probs[at, :])
                last.then_inc(s["probs_turned"], 1)

            def keep_values(n):
                dve.wait_ge(s["v_ready"], n)
                after(dve, s["o_ready"], n - 1)
                nc.vector.tensor_copy(v[:], ps_v[:]).then_inc(s["v_kept"], 1)

            def add_output(i, n):
                dve.wait_ge(s["y_ready"], n)
                dve.wait_ge(s["x_biased"], n)
                nc.vector.tensor_tensor(core.x[:, i, :], ps_y[:], x_plus_bo[:], ALU.add).then_inc(s["x_done"], 1)

            def turn(i, now, ahead, ahead2):
                if now:
                    maxima(i + 1)
                if ahead2:
                    norm_stats(dve, nc, s, i + 3, core.x[:, i + 2, :], stats[:], mean[:])
                if now:
                    probabilities(i + 1)
                if ahead2:
                    after(dve, s["xn_turned"], i + 2)
                    normed(dve, nc, s, i + 3, core.x[:, i + 2, :], xn[:], mean[:], rstd[:])
                if ahead:
                    keep_values(i + 2)
                if now:
                    add_output(i, i + 1)

            staged_tiles(dve, turn)


SEL = 2 * S


def gated_cross_attention(core, tag):
    nc = core.nc
    K2 = KEYS - 1
    scale = float(1.0 / np.sqrt(D))
    with ExitStack() as ctx:
        def sb(name, shape, dt=F32):
            return ctx.enter_context(nc.sbuf_tensor(f"{tag}_{name}", shape, dt))

        def ps(name):
            return ctx.enter_context(nc.psum_tensor(f"{tag}_{name}", [P, 512], F32))

        s = semaphores(nc, tag, LN_SEMS + """ cleared tail_spread sel_loaded ctx_loaded
            rows_loaded rows_used xn_turned xnT_ready
            qk_ready qkT_ready v_ready v_kept folded_ready folded_kept sel_ready sel_kept s1_ready max1_ready
            shift1_ready bias1_ready exp1_ready inv1_ready probs1_turned probs1T_ready pc_ready pcT_ready c2s_ready
            c2s_kept s2_ready max2_ready bias2_ready exp2_ready inv2_ready probs2_ready ip_ready ip_kept s2c_ready
            s2c_kept diff_ready gate_in_turned gate_in_ready z_ready z_kept e_ready one_plus gate_ready mixed x_plus
            x_done""")
        wt = core.pack(tag)
        wg = wt["Wg"]
        cols = {k: wt[k] for k in ("bq_c", "bk_c", "bk_s", "bq_s")}
        rows = {k: wt[k] for k in ("bv_c", "bv_s", "bg")}
        ctxT = sb("ctxT", [P, C, BT, KEYS])
        ctx_rows = sb("ctx_rows", [P, BT, 2, D])
        ctx_last = sb("ctx_last", [BT, D])
        tail_by_batch = sb("tail_by_batch", [P, BT])
        ctx_sel = sb("ctx_sel", [P, C, BT * SEL])
        stats, mean, rstd = sb("stats", [P, 6]), sb("mean", [P, 2]), sb("rstd", [P, 1])
        xn, xnT = sb("xn", [P, D]), sb("xnT", [P, C, P])
        qT, kT, v = sb("qT", [P, C, P]), sb("kT", [P, C, P]), sb("v", [P, D])
        folded = sb("folded", [P, C, P])
        q_bk = sb("q_bk", [P, 1])
        selT = sb("selT", [P, C, BT * SEL])
        big1, sum1, bias1, rsum1, rinv1 = (sb(k, [P, 1]) for k in ("big1", "sum1", "bias1", "rsum1", "rinv1"))
        probs1, probs1T = sb("probs1", [P, KEYS]), sb("probs1T", [P, 3, P])
        pcT = sb("pcT", [P, C, P])
        c2s, s2c = sb("c2s", [P, D]), sb("s2c", [P, D])
        big2, bias2, rsum2, rinv2 = (sb(k, [P, 2]) for k in ("big2", "bias2", "rsum2", "rinv2"))
        probs2 = sb("probs2", [P, 2, S])
        ip = sb("ip", [P, P])
        gate_in = sb("gate_in", [P, 2 * C, P])
        z, e, diff = sb("z", [P, D]), sb("e", [P, D]), sb("diff", [P, D])
        ps_t, ps_qk, ps_s1, ps_v, ps_f, ps_sel, ps_x, ps_y = (ps(f"bank{k}") for k in range(8))
        ident = core.table("ident")
        block = ctx.enter_context(nc.Block())

        @block.sync
        def _(sp):
            core.load_packs(sp)
            by_feature = core.inputs["ctx_T"].rearrange("(c p) (t n) -> p t c n", p=P, n=BT * KEYS)
            by_row = core.inputs["ctx"].rearrange("(t b) k d -> t b k d", b=BT)
            selected = core.inputs["ctx_sel_T"].rearrange("(c p) (t n) -> p t c n", p=P, n=BT * SEL)
            with sp.Fori(0, NT) as i:
                wait(sp, s["sel_ready"], i + 1)
                for c in range(C):
                    sp.dma_start(ctx_sel[:, c, :], selected[:, i, c, :]).then_inc(s["sel_loaded"], 16)
                wait(sp, s["s1_ready"], i + 1)
                for c in range(C):
                    sp.dma_start(ctxT[:, c].rearrange("p b k -> p (b k)"), by_feature[:, i, c, :]).then_inc(
                        s["ctx_loaded"], 16)
                wait(sp, s["rows_used"], i + 1)
                for b in range(BT):
                    sp.dma_start(ctx_rows[:, b], by_row[i, b, 0:K2, :].rearrange("(k p) d -> p k d", p=P)).then_inc(
                        s["rows_loaded"], 16)
                sp.dma_start(ctx_last[:], by_row[i, :, K2, :]).then_inc(s["rows_loaded"], 16)

        @block.gpsimd
        def _(pool):
            def turn(i, now, ahead, ahead2):
                if ahead2:
                    layer_norm_root(pool, nc, s, i + 3, mean[:], rstd[:], core.table("minus_half"))

            staged_tiles(pool, turn)

        @block.tensor
        def _(pe):
            for k in ("sel_ready", "s1_ready", "rows_used"):
                pe.sem_inc(s[k], 1)
            core.wait_for_pack(pe)

            def product(dst, lhsT, rhs, count=C):
                for c in range(count):
                    last = nc.tensor.matmul(dst, lhsT(c), rhs(c), start=(c == 0), stop=(c == count - 1))
                return last

            def chunk(oc):
                return slice(oc * P, oc * P + P)

            def turn_xn(n):
                after(pe, s["c2s_kept"], n - 2)
                pe.wait_ge(s["xn_ready"], n)
                for c in range(C):
                    last = nc.tensor.transpose(ps_t[:, chunk(c)], xn[:, chunk(c)], ident)
                last.then_inc(s["xn_turned"], 1)

            def context_queries(n):
                after(pe, s["gate_in_ready"], n - 2)
                pe.wait_ge(s["sel_loaded"], n * (16 * C))
                for oc in range(C):
                    last = product(ps_sel[:, oc * 256:oc * 256 + 256], lambda c: wt["Wq_s_T"][:, c, chunk(oc)],
                                   lambda c: ctx_sel[:, c, :])
                last.then_inc(s["sel_ready"], 1)

            def queries_and_keys(n):
                after(pe, s["probs1T_ready"], n - 2)
                pe.wait_ge(s["xnT_ready"], n)
                for a, k in enumerate(("Wq_c_T", "Wk_c_T")):
                    for oc in range(C):
                        last = product(ps_qk[:, chunk(2 * a + oc)], lambda c: wt[k][:, c, chunk(oc)],
                                       lambda c: xnT[:, c, :])
                last.then_inc(s["qk_ready"], 1)

            def values(n):
                after(pe, s["s2c_kept"], n - 1)
                product(ps_v[:, 0:D], lambda c: xnT[:, c, :], lambda c: wt["Wv_c_T"][:, c, :]).then_inc(s["v_ready"], 1)

            def fold_queries(n):
                pe.wait_ge(s["qkT_ready"], n)
                after(pe, s["pcT_ready"], n - 1)
                for oc in range(C):
                    product(ps_f[:, chunk(oc)], lambda c: wt["Wk_s"][:, c, chunk(oc)], lambda c: qT[:, c, :])
                product(ps_f[:, D:D + 1], lambda c: qT[:, c, :], lambda c: cols["bk_s"][:, c:c + 1]).then_inc(
                    s["folded_ready"], 1)

            def scores(n):
                after(pe, s["ip_kept"], n - 1)
                wait(pe, s["sel_kept"], n)
                for b in range(BT):
                    last = product(ps_x[64 * (b % 2):64 * (b % 2) + 64, S * (b // 2):S * (b // 2) + S],
                                   lambda c: selT[:, c, SEL * b:SEL * b + SEL], lambda c: kT[:, c, S * b:S * b + S])
                last.then_inc(s["s2_ready"], 1)
                pe.wait_ge(s["ctx_loaded"], n * (16 * C))
                wait(pe, s["folded_kept"], n)
                for b in range(BT):
                    at = slice(S * b, S * b + S)
                    last = product(ps_s1[at, 0:KEYS], lambda c: folded[:, c, at], lambda c: ctxT[:, c, b, :])
                last.then_inc(s["s1_ready"], 1)

            def interpolate(n):
                after(pe, s["z_kept"], n - 1)
                wait(pe, s["probs2_ready"], n)
                for b in range(BT):
                    half = slice(64 * (b % 2), 64 * (b % 2) + 64)
                    last = nc.tensor.matmul((ps_x if b % 2 == 0 else ps_y)[S * b:S * b + S, 0:S],
                                            probs2[half, b // 2, :], core.table("interpolate")[half, :],
                                            start=True, stop=True)
                last.then_inc(s["ip_ready"], 1)

            def turn_probs(n, ahead):
                pe.wait_ge(s["tail_spread"], n)
                if ahead:
                    pe.wait_ge(s["qkT_ready"], n + 1)
                for kc in range(2):
                    nc.tensor.transpose(ps_qk[:, chunk(kc)], probs1[:, chunk(kc)], ident)
                nc.tensor.matmul(ps_qk[0:BT, chunk(2)], tail_by_batch[:], ident, start=True, stop=True).then_inc(
                    s["probs1_turned"], 1)

            def context_attention(n):
                pe.wait_ge(s["v_kept"], n)
                pe.wait_ge(s["ip_kept"], n)
                nc.tensor.matmul(ps_v[:, 0:D], ip[:], v[:], start=True, stop=True).then_inc(s["s2c_ready"], 1)

            def weighed_context(n):
                pe.wait_ge(s["rows_loaded"], n * (16 * (BT + 1)))
                wait(pe, s["probs1T_ready"], n)
                for oc in range(C):
                    nc.tensor.matmul(ps_f[:, chunk(oc)], ctx_last[:, chunk(oc)], probs1T[0:BT, 2, :],
                                     start=(oc == 0), stop=False, skip_group_check=True)
                for oc in range(C):
                    for b in range(BT):
                        at = slice(S * b, S * b + S)
                        for kc in range(2):
                            last = nc.tensor.matmul(ps_f[:, oc * P + S * b:oc * P + S * b + S],
                                                    ctx_rows[:, b, kc, chunk(oc)], probs1T[:, kc, at],
                                                    start=False, stop=(kc == 1), skip_group_check=True)
                last.then_inc(s["pc_ready"], 1)

            def latent_attention(n):
                pe.wait_ge(s["pcT_ready"], n)
                pe.sem_inc(s["rows_used"], 1)
                product(ps_t[:, 0:D], lambda c: pcT[:, c, :], lambda c: wt["Wv_s_T"][:, c, :]).then_inc(
                    s["c2s_ready"], 1)

            def turn_gate_in(n, ahead):
                if ahead:
                    pe.wait_ge(s["sel_kept"], n + 1)
                pe.wait_ge(s["s2c_kept"], n)
                pe.wait_ge(s["c2s_kept"], n)
                for c in range(C):
                    nc.tensor.transpose(ps_sel[:, chunk(c)], c2s[:, chunk(c)], ident)
                for c in range(C):
                    last = nc.tensor.transpose(ps_sel[:, chunk(C + c)], s2c[:, chunk(c)], ident)
                last.then_inc(s["gate_in_turned"], 1)

            def gate_product(n):
                pe.wait_ge(s["ip_kept"], n)
                pe.wait_ge(s["gate_in_ready"], n)
                product(ps_y[:, 0:D], lambda c: gate_in[:, c, :], lambda c: wg[:, c, :], 2 * C).then_inc(
                    s["z_ready"], 1)

            def turn(i, now, ahead, ahead2):
                n = i + 1
                if now:
                    scores(n)
                if ahead:
                    turn_xn(n + 1)
                if now and not_first(i):
                    gate_product(n - 1)
                if ahead:
                    queries_and_keys(n + 1)
                if now:
                    interpolate(n)
                if ahead:
                    context_queries(n + 1)
                if now:
                    turn_probs(n, ahead)
                    context_attention(n)
                    weighed_context(n)
                if ahead:
                    values(n + 1)
                if now:
                    latent_attention(n)
                if ahead:
                    fold_queries(n + 1)
                if now:
                    turn_gate_in(n, ahead)

            staged_tiles(pe, turn)
            gate_product(NT)

        @block.scalar
        def _(act):
            core.wait_for_pack(act)

            def with_bias(dst, src, column):
                return nc.scalar.activation(dst, src, ACT.Identity, bias=column)

            def keep_xnT(n):
                act.wait_ge(s["xn_turned"], n)
                nc.scalar.copy(xnT[:].rearrange("p c n -> p (c n)"), ps_t[:, 0:D]).then_inc(s["xnT_ready"], 1)

            def keep_selected(n):
                after(act, s["s2_ready"], n - 1)
                act.wait_ge(s["sel_ready"], n + 1)
                for c in range(C):
                    last = with_bias(selT[:, c, :], ps_sel[:, c * 256:c * 256 + 256], cols["bq_s"][:, c:c + 1])
                last.then_inc(s["sel_kept"], 1)

            def keep_queries_and_keys(n):
                act.wait_ge(s["qk_ready"], n)
                for a, (dst, k) in enumerate(((qT, "bq_c"), (kT, "bk_c"))):
                    for c in range(C):
                        last = with_bias(dst[:, c, :], ps_qk[:, (2 * a + c) * P:(2 * a + c + 1) * P],
                                         cols[k][:, c:c + 1])
                last.then_inc(s["qkT_ready"], 1)

            def keep_folded(n):
                act.wait_ge(s["folded_ready"], n)
                act.wait_ge(s["s1_ready"], n)
                after(act, s["bias1_ready"], n - 1)
                nc.scalar.copy(q_bk[:], ps_f[:, D:D + 1])
                nc.scalar.copy(folded[:].rearrange("p c n -> p (c n)"), ps_f[:, 0:D]).then_inc(s["folded_kept"], 1)

            def context_exps(n):
                act.wait_ge(s["bias2_ready"], n)
                for j in range(2):
                    last = nc.scalar.activation(probs2[:, j, :], ps_x[:, S * j:S * j + S], ACT.Exp, scale=scale,
                                                bias=bias2[:, j:j + 1], accum_out=rsum2[:, j:j + 1])
                last.then_inc(s["exp2_ready"], 1)

            def latent_exps(n):
                act.wait_ge(s["bias1_ready"], n)
                nc.scalar.activation(probs1[:], ps_s1[:, 0:KEYS], ACT.Exp, scale=scale, bias=bias1[:],
                                     accum_out=rsum1[:]).then_inc(s["exp1_ready"], 1)

            def keep_probs(n):
                after(act, s["pc_ready"], n - 1)
                act.wait_ge(s["probs1_turned"], n)
                nc.scalar.copy(probs1T[:, 0:2].rearrange("p k n -> p (k n)"), ps_qk[:, 0:2 * P])
                nc.scalar.copy(probs1T[0:BT, 2, :], ps_qk[0:BT, 2 * P:3 * P]).then_inc(s["probs1T_ready"], 1)

            def keep_context(n):
                after(act, s["c2s_ready"], n - 1)
                act.wait_ge(s["pc_ready"], n)
                nc.scalar.copy(pcT[:].rearrange("p c n -> p (c n)"), ps_f[:, 0:D]).then_inc(s["pcT_ready"], 1)

            def keep_gate_in(n):
                after(act, s["z_ready"], n - 1)
                act.wait_ge(s["gate_in_turned"], n)
                nc.scalar.copy(gate_in[:].rearrange("p c n -> p (c n)"), ps_sel[:]).then_inc(s["gate_in_ready"], 1)

            def gate_exps(n):
                act.wait_ge(s["z_kept"], n)
                nc.scalar.activation(e[:], z[:], ACT.Exp, scale=-1.0).then_inc(s["e_ready"], 1)

            def turn(i, now, ahead, ahead2):
                n = i + 1
                if now:
                    context_exps(n)
                    latent_exps(n)
                if ahead:
                    keep_xnT(n + 1)
                if now and not_first(i):
                    gate_exps(n - 1)
                if ahead:
                    keep_queries_and_keys(n + 1)
                    keep_selected(n + 1)
                if now:
                    keep_probs(n)
                    keep_context(n)
                if ahead:
                    keep_folded(n + 1)
                if now:
                    keep_gate_in(n)

            staged_tiles(act, turn)
            gate_exps(NT)

        @block.vector
        def _(dve):
            nc.vector.memset(ip[:], 0.0).then_inc(s["cleared"], 1)
            dve.wait_ge(s["cleared"], 1)

            def then(ins, name, n):
                ins.then_inc(s[name], 1)
                dve.wait_ge(s[name], n)

            def context_maxima(n):
                dve.wait_ge(s["s2_ready"], n)
                then(nc.vector.tensor_reduce(big2[:], ps_x[:, 0:2 * S].rearrange("p (j k) -> p j k", j=2), X, ALU.max,
                                             negate=True), "max2_ready", n)
                nc.vector.tensor_scalar(bias2[:], big2[:], scale, None, ALU.mult).then_inc(s["bias2_ready"], 1)

            def context_probs(n):
                dve.wait_ge(s["exp2_ready"], n)
                then(nc.vector.reciprocal(rinv2[:], rsum2[:]), "inv2_ready", n)
                nc.vector.tensor_tensor(probs2[:], probs2[:], rinv2[:].unsqueeze(2).broadcast_to([P, 2, S]),
                                        ALU.mult).then_inc(s["probs2_ready"], 1)

            def latent_maxima(n):
                dve.wait_ge(s["s1_ready"], n + 1)
                then(nc.vector.tensor_reduce(big1[:], ps_s1[:, 0:KEYS], X, ALU.max), "max1_ready", n)
                dve.wait_ge(s["folded_kept"], n)
                then(nc.vector.tensor_tensor(sum1[:], big1[:], q_bk[:], ALU.add), "shift1_ready", n)
                nc.vector.tensor_scalar(bias1[:], q_bk[:], sum1[:], scale, ALU.subtract, ALU.mult).then_inc(
                    s["bias1_ready"], 1)

            def spread_tail(n):
                after(dve, s["probs1_turned"], n - 1)
                dve.wait_ge(s["exp1_ready"], n)
                nc.vector.tensor_scalar(tail_by_batch[:], core.table("quarter"), probs1[:, K2:KEYS], None,
                                        ALU.mult).then_inc(s["tail_spread"], 1)

            def keep_interpolated(n):
                after(dve, s["s2c_ready"], n - 1)
                dve.wait_ge(s["ip_ready"], n)
                for b in range(BT):
                    at = slice(S * b, S * b + S)
                    last = nc.vector.tensor_copy(ip[at, at], (ps_x if b % 2 == 0 else ps_y)[at, 0:S])
                last.then_inc(s["ip_kept"], 1)

            def keep_values(n):
                after(dve, s["s2c_ready"], n - 1)
                dve.wait_ge(s["v_ready"], n)
                nc.vector.tensor_tensor(v[:], ps_v[:, 0:D], rows["bv_c"][:], ALU.add).then_inc(s["v_kept"], 1)

            def keep_context_attention(n):
                after(dve, s["gate_in_turned"], n - 1)
                dve.wait_ge(s["s2c_ready"], n)
                nc.vector.tensor_copy(s2c[:], ps_v[:, 0:D]).then_inc(s["s2c_kept"], 1)

            def keep_latent_attention(i, n):
                dve.wait_ge(s["exp1_ready"], n)
                then(nc.vector.reciprocal(rinv1[:], rsum1[:]), "inv1_ready", n)
                dve.wait_ge(s["c2s_ready"], n)
                then(nc.vector.scalar_tensor_tensor(c2s[:], ps_t[:, 0:D], rinv1[:], rows["bv_s"][:], ALU.mult,
                                                    ALU.add), "c2s_kept", n)
                dve.wait_ge(s["s2c_kept"], n)
                nc.vector.tensor_tensor(diff[:], c2s[:], s2c[:], ALU.subtract).then_inc(s["diff_ready"], 1)
                nc.vector.tensor_tensor(core.x[:, i, :], core.x[:, i, :], s2c[:], ALU.add).then_inc(s["x_plus"], 1)

            def keep_gate(n):
                after(dve, s["e_ready"], n - 1)
                dve.wait_ge(s["z_ready"], n)
                nc.vector.tensor_tensor(z[:], ps_y[:, 0:D], rows["bg"][:], ALU.add).then_inc(s["z_kept"], 1)

            def apply_gate(i, n):
                dve.wait_ge(s["e_ready"], n)
                then(nc.vector.tensor_scalar(e[:], e[:], 1.0, None, ALU.add), "one_plus", n)
                then(nc.vector.reciprocal(e[:], e[:]), "gate_ready", n)
                dve.wait_ge(s["diff_ready"], n)
                then(nc.vector.tensor_tensor(diff[:], diff[:], e[:], ALU.mult), "mixed", n)
                dve.wait_ge(s["x_plus"], n)
                nc.vector.tensor_tensor(core.x[:, i, :], core.x[:, i, :], diff[:], ALU.add).then_inc(s["x_done"], 1)

            def turn(i, now, ahead, ahead2):
                n = i + 1
                if ahead and not now:
                    core.wait_for_pack(dve)
                if now:
                    context_maxima(n)
                    latent_maxima(n)
                    context_probs(n)
                    spread_tail(n)
                if now and not_first(i):
                    keep_gate(n - 1)
                if now:
                    keep_interpolated(n)
                if ahead2:
                    norm_stats(dve, nc, s, n + 2, core.x[:, i + 2, :], stats[:], mean[:])
                if now:
                    keep_context_attention(n)
                if now and not_first(i):
                    apply_gate(i - 1, n - 1)
                if ahead:
                    keep_values(n + 1)
                if now:
                    keep_latent_attention(i, n)
                if ahead2:
                    after(dve, s["xn_turned"], n + 1)
                    normed(dve, nc, s, n + 2, core.x[:, i + 2, :], xn[:], mean[:], rstd[:])

            staged_tiles(dve, turn)
            keep_gate(NT)
            apply_gate(NT - 1, NT)


def fixed_experts_ffn(core, tag):
    nc = core.nc
    E, HID = 8, 4 * D
    HC = HID // P
    U = NT // E
    N = U * P
    w = "L0_ffn_"
    with ExitStack() as ctx:
        def sb(name, shape, dt=F32):
            return ctx.enter_context(nc.sbuf_tensor(f"{tag}_{name}", shape, dt))

        def ps(name, shape):
            return ctx.enter_context(nc.psum_tensor(f"{tag}_{name}", shape, F32))

        s = semaphores(nc, tag, """w1_loaded w2_loaded w1_used w2_used ps_t_used flatT_ready
            xn2T_ready attn_ready xaT_ready out_ready eoT_ready y_ready y_kept gelu_ready x_done""")
        ln = [[semaphores(nc, f"{tag}_ln{a}{u}", LN_SEMS) for u in range(U)] for a in range(2)]
        turned = [nc.alloc_semaphore(f"{tag}_turned{u}") for u in range(U)]
        half_read = [nc.alloc_semaphore(f"{tag}_half_read{u}") for u in range(U)]
        flat_read = [nc.alloc_semaphore(f"{tag}_flat_read{u}") for u in range(U)]
        h_ready = [nc.alloc_semaphore(f"{tag}_h_ready{k}") for k in range(HC // 2)]
        h_kept = [nc.alloc_semaphore(f"{tag}_h_kept{k}") for k in range(HC // 2)]
        pack = core.pack(tag)
        attn_w, next_w, next_b = pack["attn_w"], pack["next_w"], pack["next_b"]
        cols = {k: pack[k] for k in ("ln_scale", "ln_bias", "attn_b")}
        w1, w2 = sb("w1", [P, C, HID]), sb("w2", [P, HC, D])
        b1, b2 = sb("b1", [P, HC]), sb("b2", [P, C])
        stats, mean, rstd = sb("stats", [P, 2, U, 6]), sb("mean", [P, 2, U, 2]), sb("rstd", [P, 2, U])
        flat, xn2 = sb("flat", [P, U, D]), sb("xn2", [P, U, D])
        flatT, xn2T, xaT = sb("flatT", [P, C, N]), sb("xn2T", [P, C, N]), sb("xaT", [P, C, N])
        hT = sb("hT", [P, HC, N])
        eoT = sb("eoT", [P, C, N])
        y = sb("y", [P, U, D])
        ps_t, ps_a = ps("ps_t", [P, 4, P]), ps("ps_a", [P, C, N])
        ps_h = ps("ps_h", [P, HC // 2, 2, N])
        ps_e, ps_y = ps("ps_e", [P, C, N]), ps("ps_y", [P, U, D])
        ident = core.table("ident")
        block = ctx.enter_context(nc.Block())

        @block.sync
        def _(sp):
            core.load_packs(sp)
            w1_by_expert = core.inputs[w + "w1"].rearrange("e (c p) n -> e p c n", p=P)
            w2_by_expert = core.inputs[w + "w2"].rearrange("e (c p) n -> e p c n", p=P)
            with sp.Fori(0, E) as e:
                wait(sp, s["w1_used"], e + 1)
                sp.dma_start(w1[:], w1_by_expert[e]).then_inc(s["w1_loaded"], 16)
                sp.dma_start(b1[:], core.inputs[w + "b1_col"][e]).then_inc(s["w1_loaded"], 16)
                wait(sp, s["w2_used"], e + 1)
                sp.dma_start(w2[:], w2_by_expert[e]).then_inc(s["w2_loaded"], 16)
                sp.dma_start(b2[:], core.inputs[w + "b2_col"][e]).then_inc(s["w2_loaded"], 16)

        @block.gpsimd
        def _(pool):
            def turn(e, now, ahead, ahead2):
                if ahead2:
                    for a in range(2):
                        for u in range(U):
                            layer_norm_root(pool, nc, ln[a][u], e + 3, mean[:, a, u], rstd[:, a, u:u + 1],
                                            core.table("minus_half"))

            staged_tiles(pool, turn, E)

        @block.tensor
        def _(pe):
            def turn_normed(n, u):
                if u:
                    pe.wait_ge(half_read[u - 1], n)
                    pe.wait_ge(flat_read[u - 1], n)
                else:
                    after(pe, half_read[U - 1], n - 1)
                    after(pe, flat_read[U - 1], n - 1)
                pe.wait_ge(ln[1][u]["xn_ready"], n)
                for c in range(C):
                    nc.tensor.transpose(ps_t[:, c, :], flat[:, u, c * P:c * P + P], ident)
                for c in range(C):
                    last = nc.tensor.transpose(ps_t[:, C + c, :], xn2[:, u, c * P:c * P + P], ident)
                last.then_inc(turned[u], 1)

            def projection(n):
                after(pe, s["xaT_ready"], n - 1)
                pe.wait_ge(half_read[U - 1], n)
                for oc in range(C):
                    for c in range(C):
                        last = nc.tensor.matmul(ps_a[:, oc, :], attn_w[:, c, oc * P:oc * P + P], xn2T[:, c, :],
                                                start=(c == 0), stop=(c == C - 1))
                last.then_inc(s["attn_ready"], 1)

            def first_layer(n):
                pe.wait_ge(s["w1_loaded"], n * 32)
                pe.wait_ge(s["xaT_ready"], n)
                for k in range(HC // 2):
                    after(pe, h_kept[k], n - 1)
                    for hc in (2 * k, 2 * k + 1):
                        for c in range(C):
                            last = nc.tensor.matmul(ps_h[:, k, hc % 2, :], w1[:, c, hc * P:hc * P + P], xaT[:, c, :],
                                                    start=(c == 0), stop=(c == C - 1))
                    last.then_inc(h_ready[k], 1)

            def second_layer(n):
                pe.wait_ge(s["w2_loaded"], n * 32)
                after(pe, s["eoT_ready"], n - 1)
                for oc in range(C):
                    for hc in range(HC):
                        if oc == 0 and hc % 2 == 0:
                            pe.wait_ge(h_kept[hc // 2], n)
                        last = nc.tensor.matmul(ps_e[:, oc, :], w2[:, hc, oc * P:oc * P + P], hT[:, hc, :],
                                                start=(hc == 0), stop=(hc == HC - 1))
                last.then_inc(s["out_ready"], 1)

            def next_projection(n):
                after(pe, s["y_kept"], n - 1)
                pe.wait_ge(s["eoT_ready"], n)
                for u in range(U):
                    for c in range(C):
                        last = nc.tensor.matmul(ps_y[:, u, :], eoT[:, c, u * P:u * P + P], next_w[:, c, :],
                                                start=(c == 0), stop=(c == C - 1))
                last.then_inc(s["y_ready"], 1)

            def turn(e, now, ahead, ahead2):
                if ahead and not now:
                    core.wait_for_pack(pe)
                if now:
                    first_layer(e + 1)
                if ahead:
                    turn_normed(e + 2, 0)
                if now:
                    second_layer(e + 1)
                if ahead:
                    turn_normed(e + 2, 1)
                    projection(e + 2)
                if now:
                    next_projection(e + 1)

            staged_tiles(pe, turn, E)

        @block.scalar
        def _(act):
            act.sem_inc(s["w1_used"], 1)
            act.sem_inc(s["w2_used"], 1)
            core.wait_for_pack(act)

            def keep_turned(n, u):
                after(act, s["xaT_ready"], n - 1)
                act.wait_ge(turned[u], n)
                for c in range(C):
                    last = nc.scalar.copy(flatT[:, c, u * P:u * P + P], ps_t[:, c, :])
                last.then_inc(flat_read[u], 1)
                for c in range(C):
                    last = nc.scalar.activation(xn2T[:, c, u * P:u * P + P], ps_t[:, C + c, :], ACT.Identity,
                                                bias=cols["ln_bias"][:, c:c + 1], scale=cols["ln_scale"][:, c:c + 1])
                last.then_inc(half_read[u], 1)

            def gelus(n):
                after(act, s["out_ready"], n - 1)
                for k in range(HC // 2):
                    act.wait_ge(h_ready[k], n)
                    if k == 0:
                        act.wait_ge(s["w1_loaded"], n * 32)
                    for hc in (2 * k, 2 * k + 1):
                        last = nc.scalar.activation(hT[:, hc, :], ps_h[:, k, hc % 2, :], ACT.Gelu,
                                                    bias=b1[:, hc:hc + 1])
                    last.then_inc(h_kept[k], 1)
                act.wait_ge(h_kept[HC // 2 - 1], n)
                act.sem_inc(s["w1_used"], 1)

            def keep_expert_output(n):
                after(act, s["y_ready"], n - 1)
                act.wait_ge(s["out_ready"], n)
                act.wait_ge(s["w2_loaded"], n * 32)
                for c in range(C):
                    last = nc.scalar.activation(eoT[:, c, :], ps_e[:, c, :], ACT.Identity, bias=b2[:, c:c + 1])
                last.then_inc(s["eoT_ready"], 1)
                act.wait_ge(s["eoT_ready"], n)
                act.sem_inc(s["w2_used"], 1)

            def turn(e, now, ahead, ahead2):
                if now:
                    gelus(e + 1)
                if ahead:
                    keep_turned(e + 2, 0)
                if now:
                    keep_expert_output(e + 1)
                if ahead:
                    keep_turned(e + 2, 1)
                if now:
                    act.wait_ge(s["y_kept"], e + 1)
                    nc.scalar.activation(y[:], y[:], ACT.Gelu).then_inc(s["gelu_ready"], 1)

            staged_tiles(act, turn, E)

        @block.vector
        def _(dve):
            def norms(e, n):
                for u in range(U):
                    norm_stats(dve, nc, ln[0][u], n, core.x[:, e + E * u, :], stats[:, 0, u], mean[:, 0, u])
                for u in range(U):
                    after(dve, turned[u], n - 1)
                    normed(dve, nc, ln[0][u], n, core.x[:, e + E * u, :], flat[:, u], mean[:, 0, u],
                           rstd[:, 0, u:u + 1])
                for u in range(U):
                    dve.wait_ge(ln[0][u]["xn_ready"], n)
                    norm_stats(dve, nc, ln[1][u], n, flat[:, u], stats[:, 1, u], mean[:, 1, u])
                for u in range(U):
                    normed(dve, nc, ln[1][u], n, flat[:, u], xn2[:, u], mean[:, 1, u], rstd[:, 1, u:u + 1])

            def add_projection(n):
                dve.wait_ge(s["attn_ready"], n)
                dve.wait_ge(flat_read[U - 1], n)
                after(dve, h_ready[HC // 2 - 1], n - 1)
                for c in range(C):
                    last = nc.vector.scalar_tensor_tensor(xaT[:, c, :], ps_a[:, c, :], cols["attn_b"][:, c:c + 1],
                                                          flatT[:, c, :], ALU.add, ALU.add)
                last.then_inc(s["xaT_ready"], 1)

            def keep_y(n):
                after(dve, s["x_done"], n - 1)
                dve.wait_ge(s["y_ready"], n)
                nc.vector.tensor_tensor(y[:], ps_y[:], next_b[:].unsqueeze(1).broadcast_to([P, U, D]), ALU.add).then_inc(
                    s["y_kept"], 1)

            def add_output(e, n):
                dve.wait_ge(s["gelu_ready"], n)
                for u in range(U):
                    last = nc.vector.tensor_tensor(core.x[:, e + E * u, :], core.x[:, e + E * u, :], y[:, u],
                                                   ALU.add)
                last.then_inc(s["x_done"], 1)

            def turn(e, now, ahead, ahead2):
                if ahead and not now:
                    core.wait_for_pack(dve)
                if ahead:
                    add_projection(e + 2)
                if now:
                    keep_y(e + 1)
                if ahead2:
                    norms(e + 2, e + 3)
                if now:
                    add_output(e, e + 1)

            staged_tiles(dve, turn, E)


def tiles_led(engine, lead, trail):
    def step(slot, i):
        lead(1 - slot, i + 1)
        trail(slot, i)

    lead(0, 0)
    for i in range(2):
        step(i, i)
    with engine.Fori(1, NT // 2 - 1) as g:
        for slot in range(2):
            step(slot, g * 2 + slot)
    step(0, NT - 2)
    trail(1, NT - 1)


def normed_features(core, tag, xnT_all, router=None, prefetch=None):
    nc = core.nc
    E = 8
    with ExitStack() as ctx:
        def sb(name, shape, dt=F32):
            return ctx.enter_context(nc.sbuf_tensor(f"{tag}_{name}", shape, dt))

        def ps(name, shape):
            return ctx.enter_context(nc.psum_tensor(f"{tag}_{name}", shape, F32))

        s = semaphores(nc, tag, """stats_ready mean_ready var_ready rstd_ready xn_ready weights_loaded
            xn_turned xnT_ready bank_read logits_ready logits_kept""")
        stats, mean, rstd = sb("stats", [P, NT, 6]), sb("mean", [P, NT, 2]), sb("rstd", [P, NT])
        xn, xnT = sb("xn", [P, 2, D]), sb("xnT", [P, 2, C, P])
        ps_t = ps("ps_t", [P, 2, 512])[:, :, 0:C * P].rearrange("p k (c n) -> p k c n", c=C)
        if router:
            weights, bias_row, kind, gates = router
            rw, rb = sb("rw", [P, C, E]), sb("rb", [P, E])
            ps_r = ps("ps_r", [P, 2, 512])[:, :, 0:E]
            logits, by, e = sb("logits", [P, NT, E]), sb("by", [P, NT, E]), sb("e", [P, NT, E])
            sig = sb("sig", [P, NT, E])
            top, place = sb("top", [P, NT, E]), sb("place", [P, NT, E], U32)
            place_f = sb("place_f", [P, NT, 2])
            weigh, share = sb("weigh", [P, NT, 2]), sb("share", [P, NT, 2])
            one_hot = sb("one_hot", [P, 2, NT, E])
            total, enough = sb("total", [P, NT]), sb("enough", [P, NT])
            then = semaphores(nc, tag + "g", """exp_ready one_plus sigmoid_ready chosen_by top_ready place_ready
                placed hot ones gap exps picked_1 picked_2 weigh_1 weigh_2 total enough total_plus inverse
                share shifted masked shared weighed""")
        ident = core.table("ident")
        block = ctx.enter_context(nc.Block())

        @block.sync
        def _(sp):
            if router:
                sp.dma_start(rw[:], core.inputs[weights]).then_inc(s["weights_loaded"], 16)
                sp.dma_start(rb[:], core.rows(bias_row)).then_inc(s["weights_loaded"], 16)
            if prefetch:
                prefetch(sp)

        @block.gpsimd
        def _(pool):
            wait(pool, s["mean_ready"], NT)
            nc.gpsimd.tensor_scalar(mean[:, :, 1], mean[:, :, 1], EPS, None, ALU.add).then_inc(s["var_ready"], 1)
            pool.wait_ge(s["var_ready"], 1)
            nc.gpsimd.tensor_tensor(rstd[:], mean[:, :, 1], core.table("minus_half").broadcast_to([P, NT]),
                                    ALU.pow).then_inc(s["rstd_ready"], 1)

        @block.tensor
        def _(pe):
            if router:
                pe.wait_ge(s["weights_loaded"], 32)

            def turn_xn(slot, i):
                pe.wait_ge(s["xn_ready"], i + 1)
                after(pe, s["bank_read"], i - 1)
                for c in range(C):
                    last = nc.tensor.transpose(ps_t[:, slot, c, :], xn[:, slot, c * P:c * P + P], ident)
                last.then_inc(s["xn_turned"], 1)

            def router_logits(slot, i):
                if router:
                    after(pe, s["logits_kept"], i - 1)
                    pe.wait_ge(s["xnT_ready"], i + 1)
                    for c in range(C):
                        last = nc.tensor.matmul(ps_r[:, slot], xnT[:, slot, c, :], rw[:, c, :], start=(c == 0),
                                                stop=(c == C - 1))
                    last.then_inc(s["logits_ready"], 1)

            tiles_led(pe, turn_xn, router_logits)

        @block.scalar
        def _(act):
            def keep_xnT(slot, i):
                act.wait_ge(s["xn_turned"], i + 1)
                if router:
                    after(act, s["logits_ready"], i - 1)
                    nc.scalar.copy(xnT[:, slot], ps_t[:, slot]).then_inc(s["xnT_ready"], 1)
                nc.scalar.copy(xnT_all[:, :, bass.ts(i, P)], ps_t[:, slot]).then_inc(s["bank_read"], 1)

            def keep_logits(slot, i):
                if router:
                    act.wait_ge(s["logits_ready"], i + 1)
                    nc.scalar.copy(logits[:, i, :], ps_r[:, slot]).then_inc(s["logits_kept"], 1)

            tiles_led(act, keep_xnT, keep_logits)
            if router and kind == "sigmoid":
                act.wait_ge(s["logits_kept"], NT)
                nc.scalar.activation(e[:], logits[:], ACT.Exp, scale=-1.0).then_inc(then["exp_ready"], 1)
            if router and kind == "softmax":
                act.wait_ge(then["gap"], 1)
                nc.scalar.activation(weigh[:, :, 1], weigh[:, :, 1], ACT.Exp).then_inc(then["exps"], 1)

        @block.vector
        def _(dve):
            for i in range(NT):
                nc.vector.bn_stats(stats[:, i, :], core.x[:, i, :]).then_inc(s["stats_ready"], 1)
            for i in range(NT):
                dve.wait_ge(s["stats_ready"], i + 1)
                nc.vector.bn_aggr(mean[:, i, :], stats[:, i, :]).then_inc(s["mean_ready"], 1)
            wait(dve, s["rstd_ready"], 1)

            def normed_tile(slot, i):
                after(dve, s["xn_turned"], i - 1)
                nc.vector.tensor_scalar(xn[:, slot, :], core.x[:, i, :], mean[:, i, 0:1], rstd[:, bass.ds(i, 1)],
                                        ALU.subtract, ALU.mult).then_inc(s["xn_ready"], 1)

            tiles_led(dve, normed_tile, lambda slot, i: None)
            if router:
                dve.wait_ge(s["weights_loaded"], 32)
            if not router:
                return

            def step(ins, name):
                ins.then_inc(then[name], 1)
                wait(dve, then[name], 1)

            dve.wait_ge(s["logits_kept"], NT)
            chosen = logits
            if kind == "sigmoid":
                dve.wait_ge(then["exp_ready"], 1)
                step(nc.vector.tensor_scalar(e[:], e[:], 1.0, None, ALU.add), "one_plus")
                step(nc.vector.reciprocal(sig[:], e[:]), "sigmoid_ready")
                chosen = sig
            step(nc.vector.tensor_tensor(by[:], chosen[:], rb[:].unsqueeze(1).broadcast_to([P, NT, E]), ALU.add),
                 "chosen_by")
            for t in range(NT):
                last = nc.vector.max(top[:, t, :], by[:, t, :])
            step(last, "top_ready")
            for t in range(NT):
                last = nc.vector.max_index(place[:, t, :], top[:, t, :], by[:, t, :])
            step(last, "place_ready")
            step(nc.vector.tensor_copy(place_f[:], place[:, :, 0:2]), "placed")
            for k in range(2):
                last = nc.vector.tensor_tensor(one_hot[:, k], place_f[:, :, k].unsqueeze(2).broadcast_to([P, NT, E]),
                                               core.table("iota")[:, 0:E].unsqueeze(1).broadcast_to([P, NT, E]),
                                               ALU.is_equal)
            step(last, "hot")
            if kind == "softmax":
                step(nc.vector.memset(weigh[:, :, 0], 1.0), "ones")
                step(nc.vector.tensor_tensor(weigh[:, :, 1], top[:, :, 1], top[:, :, 0], ALU.subtract), "gap")
                dve.wait_ge(then["exps"], 1)
            else:
                for k in range(2):
                    step(nc.vector.tensor_tensor(gates[:, :, 0:E], one_hot[:, k], sig[:], ALU.mult),
                         f"picked_{k + 1}")
                    step(nc.vector.tensor_reduce(weigh[:, :, k], gates[:, :, 0:E], X, ALU.add), f"weigh_{k + 1}")
            step(nc.vector.tensor_tensor(total[:], weigh[:, :, 0], weigh[:, :, 1], ALU.add), "total")
            if kind == "sigmoid":
                step(nc.vector.tensor_scalar(enough[:], total[:], 1e-9, None, ALU.is_gt), "enough")
                step(nc.vector.tensor_scalar(total[:], total[:], 1e-9, None, ALU.add), "total_plus")
            step(nc.vector.reciprocal(total[:], total[:]), "inverse")
            step(nc.vector.tensor_tensor(share[:], weigh[:], total[:].unsqueeze(2).broadcast_to([P, NT, 2]),
                                         ALU.mult), "share")
            if kind == "sigmoid":
                step(nc.vector.tensor_scalar(share[:], share[:], 0.5, None, ALU.subtract), "shifted")
                step(nc.vector.tensor_tensor(share[:], share[:], enough[:].unsqueeze(2).broadcast_to([P, NT, 2]),
                                             ALU.mult), "masked")
                step(nc.vector.tensor_scalar(share[:], share[:], 0.5, None, ALU.add), "shared")
            for k in range(2):
                last = nc.vector.tensor_tensor(one_hot[:, k], one_hot[:, k],
                                               share[:, :, k].unsqueeze(2).broadcast_to([P, NT, E]), ALU.mult)
            step(last, "weighed")
            nc.vector.tensor_tensor(gates[:, :, 0:E], one_hot[:, 0], one_hot[:, 1], ALU.add)
            nc.vector.memset(gates[:, :, E], 1.0)


class ExpertWeights:

    def __init__(self, core, ctx, tag, count, hidden, names, swiglu):
        nc = core.nc
        self.ups = 2 if swiglu else 1
        self.slots = 2 if count > 1 else 1
        self.loaded = [nc.alloc_semaphore(f"{tag}_loaded{k}") for k in range(self.slots)]
        self.up = ctx.enter_context(nc.sbuf_tensor(f"{tag}_w_up", [P, self.slots, self.ups, C, hidden], F32))
        self.down = ctx.enter_context(nc.sbuf_tensor(f"{tag}_w_down", [P, self.slots, hidden // P, D], F32))
        self.views = [core.inputs[k].rearrange("e (c p) n -> e p c n", p=P) for k in names]

    def load(self, sp, slot, e):
        for k in range(self.ups):
            sp.dma_start(self.up[:, slot, k], self.views[k][e]).then_inc(self.loaded[slot], 16)
        sp.dma_start(self.down[:, slot], self.views[self.ups][e]).then_inc(self.loaded[slot], 16)

    def load_first(self, sp):
        for slot in range(self.slots):
            self.load(sp, slot, slot)


def dense_experts(core, tag, xnT_all, gates, weights, first, count, hidden, swiglu):
    nc = core.nc
    HC = hidden // P
    TB = 512
    NB = T // TB
    TT = TB // P
    ups, slots, loaded, w_up, w_down = weights.ups, weights.slots, weights.loaded, weights.up, weights.down
    with ExitStack() as ctx:
        def sb(name, shape, dt=F32):
            return ctx.enter_context(nc.sbuf_tensor(f"{tag}_{name}", shape, dt))

        def ps(name, shape):
            return ctx.enter_context(nc.psum_tensor(f"{tag}_{name}", shape, F32))

        s = semaphores(nc, tag, "up_ready activated hidden_ready out_ready x_done gate_ready")
        used = [nc.alloc_semaphore(f"{tag}_used{k}") for k in range(slots)]
        act_out = sb("act_out", [P, 2, TB])
        hiddenT = sb("hiddenT", [P, 2, HC, TB])
        gate = sb("gate", [P, NT])
        ps_up = ps("ps_up", [P, 2, ups, TB])
        ps_d = ps("ps_d", [P, 2, TT, D])
        block = ctx.enter_context(nc.Block())
        per_load = 16 * (ups + 1)

        def each(engine, body):
            if count >= 2:
                with engine.Fori(0, count // 2) as i:
                    body(0, i * 2, i + 1)
                    body(1, i * 2 + 1, i + 1)
            if count % 2:
                body(0, count - 1, count // 2 + 1)

        @block.sync
        def _(sp):
            def load(slot, e, turn):
                wait(sp, used[slot], turn)
                weights.load(sp, slot, e)

            if count >= 4:
                with sp.Fori(1, count // 2) as i:
                    load(0, i * 2, i)
                    load(1, i * 2 + 1, i)
            if count % 2 and count > 1:
                load(0, count - 1, count // 2)

        @block.tensor
        def _(pe):
            pe.sem_inc(s["out_ready"], 2)

            def expert(slot, e, turn):
                pe.wait_ge(loaded[slot], turn * per_load)

                def up(tb, hc):
                    k = (tb * HC + hc) % 2
                    pe.wait_ge(s["hidden_ready"], e * (NB * HC) + (tb * HC + hc + 1))
                    for a in range(ups):
                        for c in range(C):
                            last = nc.tensor.matmul(ps_up[:, k, a, :], w_up[:, slot, a, c, hc * P:hc * P + P],
                                                    xnT_all[:, c, tb * TB:tb * TB + TB],
                                                    start=(c == 0), stop=(c == C - 1))
                    last.then_inc(s["up_ready"], 1)

                def down(tb):
                    pe.wait_ge(s["hidden_ready"], e * (NB * HC) + (tb * HC + HC + 2))
                    pe.wait_ge(s["x_done"], e * NB + (tb + 1))
                    for tt in range(TT):
                        for hc in range(HC):
                            last = nc.tensor.matmul(ps_d[:, tb % 2, tt, :], hiddenT[:, tb % 2, hc, tt * P:tt * P + P],
                                                    w_down[:, slot, hc, :], start=(hc == 0), stop=(hc == HC - 1))
                    last.then_inc(s["out_ready"], 1)

                for tb in range(NB):
                    for hc in range(HC):
                        up(tb, hc)
                        if hc == 1 and tb:
                            down(tb - 1)
                down(NB - 1)
                pe.wait_ge(s["out_ready"], e * NB + (NB + 2))
                pe.sem_inc(used[slot], 1)

            each(pe, expert)

        @block.scalar
        def _(act):
            def expert(slot, e, turn):
                for tb in range(NB):
                    for hc in range(HC):
                        k = (tb * HC + hc) % 2
                        if swiglu:
                            act.wait_ge(s["hidden_ready"], e * (NB * HC) + (tb * HC + hc + 1))
                        elif hc == 0:
                            act.wait_ge(s["out_ready"], e * NB + (tb + 1))
                        act.wait_ge(s["up_ready"], e * (NB * HC) + (tb * HC + hc + 1))
                        if swiglu:
                            nc.scalar.activation(act_out[:, k, :], ps_up[:, k, 0, :], ACT.Silu).then_inc(
                                s["activated"], 1)
                        else:
                            nc.scalar.activation(hiddenT[:, tb % 2, hc, :], ps_up[:, k, 0, :], ACT.Gelu).then_inc(
                                s["hidden_ready"], 1)

            if not swiglu:
                act.sem_inc(s["hidden_ready"], 2)
            each(act, expert)

        @block.vector
        def _(dve):
            if swiglu:
                dve.sem_inc(s["hidden_ready"], 2)
            dve.sem_inc(s["x_done"], 2)

            def expert(slot, e, turn):
                wait(dve, s["x_done"], e * NB + 2)
                nc.vector.tensor_copy(gate[:], gates[:, :, first + e]).then_inc(s["gate_ready"], 1)
                dve.wait_ge(s["gate_ready"], e + 1)

                def add(tb):
                    dve.wait_ge(s["out_ready"], e * NB + (tb + 3))
                    for tt in range(TT):
                        t = tb * TT + tt
                        last = nc.vector.scalar_tensor_tensor(core.x[:, t, :], ps_d[:, tb % 2, tt, :], gate[:, t:t + 1],
                                                              core.x[:, t, :], ALU.mult, ALU.add)
                    last.then_inc(s["x_done"], 1)

                for tb in range(NB):
                    for hc in range(HC):
                        if swiglu:
                            k = (tb * HC + hc) % 2
                            if hc == 0:
                                dve.wait_ge(s["out_ready"], e * NB + (tb + 1))
                            dve.wait_ge(s["activated"], e * (NB * HC) + (tb * HC + hc + 1))
                            nc.vector.tensor_tensor(hiddenT[:, tb % 2, hc, :], act_out[:, k, :], ps_up[:, k, 1, :],
                                                    ALU.mult).then_inc(s["hidden_ready"], 1)
                        if hc == 1 and tb:
                            add(tb - 1)
                add(NB - 1)

            each(dve, expert)


def routed_ffn(core, tag, router, parts):
    with ExitStack() as ctx:
        xnT_all = ctx.enter_context(core.nc.sbuf_tensor(f"{tag}_xnT_all", [P, C, T], F32))
        gates = ctx.enter_context(core.nc.sbuf_tensor(f"{tag}_gates", [P, NT, 9], F32))
        weights = [ExpertWeights(core, ctx, f"{tag}e{k}", count, hidden, names, swiglu)
                   for k, (first, count, hidden, names, swiglu) in enumerate(parts)]

        def prefetch(sp):
            for w in weights:
                w.load_first(sp)
            core.load_packs(sp)

        normed_features(core, tag + "n", xnT_all, (*router, gates), prefetch)
        for k, (first, count, hidden, names, swiglu) in enumerate(parts):
            dense_experts(core, f"{tag}e{k}", xnT_all, gates, weights[k], first, count, hidden, swiglu)


PH = 8
NK = 64
K8 = 8
EN = PH * K8


def product_key_ffn(core, tag):
    nc = core.nc
    w = "L1_ffn_"
    with ExitStack() as whole:
        def keep(name, shape, dt=F32):
            return whole.enter_context(nc.sbuf_tensor(f"{tag}_{name}", shape, dt))

        xnT_all = keep("xnT_all", [P, C, T])
        norm_scale, norm_bias = keep("norm_scale", [P, C]), keep("norm_bias", [P, C])
        folded = keep("folded", [P, C, 2 * PH * NK])
        with ExitStack() as ctx:
            w_q = ctx.enter_context(nc.sbuf_tensor(f"{tag}_w_q", [P, 2 * PH, D], F32))
            keys = ctx.enter_context(nc.sbuf_tensor(f"{tag}_keys", [P, 2 * PH, NK], F32))
            loaded = nc.alloc_semaphore(f"{tag}_w_q_loaded")

            def prefetch(sp):
                sp.dma_start(w_q[:], core.inputs["L1_ffn_w_q"].rearrange("(a p) d -> p a d", p=P)).then_inc(loaded, 16)
                sp.dma_start(keys[:], core.inputs["L1_ffn_keys_by_dim"]).then_inc(loaded, 16)

            normed_features(core, tag + "n", xnT_all, prefetch=prefetch)
            fold_keys(core, tag + "f", xnT_all, w_q, keys, loaded, folded, norm_scale, norm_bias)
        chosen_units(core, tag + "u", xnT_all, folded, norm_scale, norm_bias)


def fold_keys(core, tag, xnT_all, w_q, keys, loaded, folded, norm_scale, norm_bias):
    nc = core.nc
    PARTS = T // 512
    with ExitStack() as ctx:
        def sb(name, shape, dt=F32):
            return ctx.enter_context(nc.sbuf_tensor(f"{tag}_{name}", shape, dt))

        s = semaphores(nc, tag, """weights_loaded folded_ready stats_ready mean_ready var_ready rstd_ready
            scale_ready shift_ready bias_ready""")
        gamma, beta = sb("gamma", [P, C]), sb("beta", [P, C])
        stats, mean, rstd = sb("stats", [P, C, PARTS, 6]), sb("mean", [P, C, 2]), sb("rstd", [P, C])
        shift = sb("shift", [P, C])
        ps_f = ctx.enter_context(nc.psum_tensor(f"{tag}_ps_f", [P, C, 2 * PH * NK], F32))
        block = ctx.enter_context(nc.Block())

        @block.sync
        def _(sp):
            sp.dma_start(gamma[:], core.inputs["L1_ffn_gamma_col"]).then_inc(s["weights_loaded"], 16)
            sp.dma_start(beta[:], core.inputs["L1_ffn_beta_col"]).then_inc(s["weights_loaded"], 16)

        @block.tensor
        def _(pe):
            pe.wait_ge(loaded, 32)
            for c in range(C):
                for a in range(2 * PH):
                    last = nc.tensor.matmul(ps_f[:, c, a * NK:a * NK + NK], w_q[:, a, c * P:c * P + P], keys[:, a, :],
                                            start=True, stop=True)
            last.then_inc(s["folded_ready"], 1)

        @block.scalar
        def _(act):
            act.wait_ge(s["folded_ready"], 1)
            for c in range(C):
                nc.scalar.copy(folded[:, c, :], ps_f[:, c, :])

        @block.gpsimd
        def _(pool):
            pool.wait_ge(s["mean_ready"], C)
            nc.gpsimd.tensor_scalar(mean[:, :, 1], mean[:, :, 1], EPS, None, ALU.add).then_inc(s["var_ready"], 1)
            pool.wait_ge(s["var_ready"], 1)
            nc.gpsimd.tensor_tensor(rstd[:], mean[:, :, 1], core.table("minus_half").broadcast_to([P, C]),
                                    ALU.pow).then_inc(s["rstd_ready"], 1)

        @block.vector
        def _(dve):
            for c in range(C):
                for k in range(PARTS):
                    last = nc.vector.bn_stats(stats[:, c, k], xnT_all[:, c, k * 512:k * 512 + 512])
            last.then_inc(s["stats_ready"], 1)
            dve.wait_ge(s["stats_ready"], 1)
            for c in range(C):
                nc.vector.bn_aggr(mean[:, c], stats[:, c].rearrange("p k n -> p (k n)")).then_inc(s["mean_ready"], 1)
            dve.wait_ge(s["weights_loaded"], 32)
            dve.wait_ge(s["rstd_ready"], 1)
            nc.vector.tensor_tensor(norm_scale[:], rstd[:], gamma[:], ALU.mult).then_inc(s["scale_ready"], 1)
            dve.wait_ge(s["scale_ready"], 1)
            nc.vector.tensor_tensor(shift[:], mean[:, :, 0], norm_scale[:], ALU.mult).then_inc(s["shift_ready"], 1)
            dve.wait_ge(s["shift_ready"], 1)
            nc.vector.tensor_tensor(norm_bias[:], beta[:], shift[:], ALU.subtract).then_inc(s["bias_ready"], 1)


def chosen_units(core, tag, xnT_all, folded, norm_scale, norm_bias):
    nc = core.nc
    J = NK // 2
    K = 8
    TC = NK // K
    JS = J // K
    W3 = 3
    with ExitStack() as ctx:
        def sb(name, shape, dt=F32):
            return ctx.enter_context(nc.sbuf_tensor(f"{tag}_{name}", shape, dt))

        def ps(name, shape):
            return ctx.enter_context(nc.psum_tensor(f"{tag}_{name}", shape, F32))

        s = semaphores(nc, tag, """weights_loaded part_ready first_ready second_hot second_ready plane_ready
            plane_kept units_ready activated weighed step_done x_done
            normed sim_ready sim_kept top_ready place_ready place_f_ready sums_ready best_ready
            rank_ready rows_ready digits_ready hot_ready weighed_ready picked_ready
            gap_ready exp_ready total_ready inv_ready weight_ready upper_ready split_ready doubled turned entries_kept""")
        key_in = sb("key_in", [P, C, J, P])
        key_out = sb("key_out", [P, J, D])
        entries = sb("entries", [P, 2, 3, NK])
        parts, rest = sb("parts", [P, 2, W3, NK], BF16), sb("rest", [P, 2, NK])
        first = sb("first", [P, 2, TC, P], BF16)
        second = sb("second", [P, 2, TC, J], BF16)
        second_weighed = sb("second_weighed", [P, 2, W3, TC, J], BF16)
        plane = sb("plane", [P, 2, P, J])
        act_out, weighed = sb("act_out", [P, 2, JS, P]), sb("weighed", [P, 2, JS, P])
        xbT = sb("xbT", [P, C, P])
        sim = sb("sim", [P, 2 * PH, NK])
        top, place = sb("top", [P, 2 * PH, K8]), sb("place", [P, 2 * PH, K8], U32)
        place_f = sb("place_f", [P, 2 * PH, K8])
        sums = sb("sums", [P, PH, K8, K8])
        best, rank = sb("best", [P, PH, K8]), sb("rank", [P, PH, K8], U32)
        digit = sb("digit", [P, 2, PH, K8], U32)
        digit_f = sb("digit_f", [P, 2, PH, K8])
        hot = sb("hot", [P, 2, PH, K8, K8])
        trio = sb("trio", [P, 3, EN])
        upper = sb("upper", [P, EN])
        gap, total, inv = sb("gap", [P, PH, K8]), sb("total", [P, PH]), sb("inv", [P, PH])
        doubled = sb("doubled", [P, 3, 2, EN])
        ps_p = ps("ps_p", [P, 2, 512])[:, :, 0:TC * J].rearrange("p h (n j) -> p h n j", j=J)
        ps_u = ps("ps_u", [P, 2, JS, P])
        ps_y = ps("ps_y", [P, 512])[:, 0:D]
        ps_sim = ps("ps_sim", [P, 2, 512])
        ps_e = ps("ps_e", [P, 4, P])
        ident = core.table("ident")
        iota8 = core.table("iota")[:, 0:K8]

        def iota(n):
            return core.table("iota")[:, 0:n].unsqueeze(1).broadcast_to([P, TC, n])
        block = ctx.enter_context(nc.Block())

        def all_turns(engine, turn):
            turn(-2, 0, True, False, False)
            turn(-1, 1, True, True, False)
            with engine.Fori(0, NT // 2 - 1) as g:
                turn(g * 2, 0, True, True, True)
                turn(g * 2 + 1, 1, True, True, True)
            turn(NT - 2, 0, False, True, True)
            turn(NT - 1, 1, False, False, True)

        def spread(par, value, k, n):
            return entries[:, par, value, TC * k:TC * k + TC].unsqueeze(2).broadcast_to([P, TC, n])

        @block.sync
        def _(sp):
            sp.dma_start(key_in[:], core.inputs["L1_ffn_key_in_by_expert"].rearrange("(c p) j m -> p c j m", p=P)
                         ).then_inc(s["weights_loaded"], 16)
            sp.dma_start(key_out[:], core.inputs["L1_ffn_key_out_by_expert"]).then_inc(s["weights_loaded"], 16)

        @block.gpsimd
        def _(pool):
            def turn(t, par, choose, build, units):
                if build:
                    for k in range(K):
                        pool.wait_ge(s["second_hot"], (t + 1) * K + (k + 1))
                        after(pool, s["plane_ready"], (t + 1) * K + (k - 1))
                        for part in range(W3):
                            last = nc.gpsimd.tensor_tensor(
                                second_weighed[:, k % 2, part], second[:, k % 2],
                                parts[:, 1 - par, part, TC * k:TC * k + TC].unsqueeze(2).broadcast_to([P, TC, J]),
                                ALU.mult)
                        last.then_inc(s["second_ready"], 1)

            all_turns(pool, turn)

        @block.tensor
        def _(pe):
            pe.sem_inc(s["step_done"], 2)

            def similarities(tile):
                pe.wait_ge(s["normed"], tile + 1)
                after(pe, s["sim_kept"], tile)
                for k in range(2):
                    for c in range(C):
                        last = nc.tensor.matmul(ps_sim[:, k, :], xbT[:, c, :], folded[:, c, k * 512:k * 512 + 512],
                                                start=(c == 0), stop=(c == C - 1))
                last.then_inc(s["sim_ready"], 1)

            def turn_entries(tile):
                pe.wait_ge(s["doubled"], tile + 1)
                after(pe, s["entries_kept"], tile)
                for k in range(3):
                    last = nc.tensor.transpose(ps_e[:, k, :], doubled[:, k].rearrange("p r e -> p (r e)"), ident)
                last.then_inc(s["turned"], 1)

            def build_plane(tile, k):
                pe.wait_ge(s["first_ready"], tile * K + (k + 1))
                after(pe, s["plane_kept"], tile * K + k)
                wait(pe, s["second_ready"], tile * K + (k + 1))
                for token in range(TC):
                    for half in range(2):
                        rows = slice(EN * half, EN * half + EN)
                        for part in range(W3):
                            last = nc.tensor.matmul(ps_p[:, half, token, :], first[rows, k % 2, token, :],
                                                    second_weighed[rows, k % 2, part, token, :],
                                                    start=(part == 0), stop=(part == W3 - 1))
                last.then_inc(s["plane_ready"], 1)

            def hidden(tile, k):
                pe.wait_ge(s["activated"], tile * K + (k + 1))
                for j in range(JS):
                    for c in range(C):
                        last = nc.tensor.matmul(ps_u[:, k % 2, j, :], key_in[:, c, JS * k + j, :],
                                                xnT_all[:, c, bass.ts(tile, P)], start=(c == 0), stop=(c == C - 1))
                last.then_inc(s["units_ready"], 1)

            def outputs(tile, k):
                if k == 0:
                    pe.wait_ge(s["x_done"], tile + 1)
                pe.wait_ge(s["weighed"], tile * K + (k + 3))
                for j in range(JS):
                    last = nc.tensor.matmul(ps_y, weighed[:, k % 2, j, :], key_out[:, JS * k + j, :],
                                            start=(k + j == 0), stop=(k == K - 1 and j == JS - 1))
                last.then_inc(s["step_done"], 1)

            def turn(t, par, choose, build, units):
                if units:
                    hidden(t, 0)
                for k in range(K):
                    if units and k + 1 < K:
                        hidden(t, k + 1)
                    if choose and k == K - 1:
                        turn_entries(t + 2)
                    if build:
                        build_plane(t + 1, k)
                    if units:
                        outputs(t, k)
                    if choose and k == 0:
                        similarities(t + 2)
                if build and not units:
                    pe.wait_ge(s["weights_loaded"], 32)

            all_turns(pe, turn)

        @block.scalar
        def _(act):
            act.sem_inc(s["activated"], 2)

            def normed(tile):
                after(act, s["sim_ready"], tile, alone=True)
                for c in range(C):
                    last = nc.scalar.activation(xbT[:, c, :], xnT_all[:, c, bass.ts(tile, P)], ACT.Identity,
                                                bias=norm_bias[:, c:c + 1], scale=norm_scale[:, c:c + 1])
                last.then_inc(s["normed"], 1)

            def keep_similarities(tile):
                act.wait_ge(s["sim_ready"], tile + 1)
                after(act, s["place_ready"], tile)
                nc.scalar.copy(sim[:].rearrange("p a k -> p (a k)"), ps_sim[:].rearrange("p a k -> p (a k)")).then_inc(
                    s["sim_kept"], 1)

            def exps(tile):
                act.wait_ge(s["gap_ready"], tile + 1)
                nc.scalar.activation(gap[:], gap[:], ACT.Exp).then_inc(s["exp_ready"], 1)

            def keep_entries(tile, par):
                after(act, s["plane_ready"], tile * K - K)
                wait(act, s["turned"], tile + 1)
                for half in range(2):
                    at = slice(EN * half, EN * half + EN)
                    last = nc.scalar.copy(entries[at, par], ps_e[at, 0:3, NK * half:NK * half + NK])
                last.then_inc(s["entries_kept"], 1)

            def keep_plane(tile, par, k):
                if k == 0:
                    after(act, s["weighed"], tile * K + (2 - K))
                act.wait_ge(s["plane_ready"], tile * K + (k + 1))
                nc.scalar.copy(
                    plane[:, par].rearrange("p (h n) j -> p h (n j)", h=2)[:, :, TC * J * k:TC * J * k + TC * J],
                    ps_p.rearrange("p h n j -> p h (n j)")).then_inc(s["plane_kept"], 1)

            def gelus(tile, k):
                act.wait_ge(s["units_ready"], tile * K + (k + 1))
                act.wait_ge(s["weighed"], tile * K + (k + 1))
                nc.scalar.activation(act_out[:, k % 2], ps_u[:, k % 2], ACT.Gelu).then_inc(s["activated"], 1)

            def turn(t, par, choose, build, units):
                if choose:
                    normed(t + 2)
                if units:
                    gelus(t, 0)
                for k in range(K):
                    if units and k + 1 < K:
                        gelus(t, k + 1)
                    if choose and k == K - 1:
                        keep_entries(t + 2, par)
                    if build:
                        keep_plane(t + 1, 1 - par, k)
                    if choose and k == 0:
                        keep_similarities(t + 2)
                    if choose and k == 5:
                        exps(t + 2)

            all_turns(act, turn)

        @block.vector
        def _(dve):
            dve.sem_inc(s["weighed"], 2)
            dve.sem_inc(s["x_done"], 1)

            def choose_step(tile, k):
                n = tile + 1

                def then(ins, name):
                    ins.then_inc(s[name], 1)
                    wait(dve, s[name], n)

                if k == 1:
                    wait(dve, s["sim_kept"], n)
                    for a in range(2 * PH):
                        last = nc.vector.max(top[:, a, :], sim[:, a, :])
                    then(last, "top_ready")
                if k == 2:
                    for a in range(2 * PH):
                        last = nc.vector.max_index(place[:, a, :], top[:, a, :], sim[:, a, :])
                    then(last, "place_ready")
                if k == 3:
                    nc.vector.tensor_copy(place_f[:], place[:]).then_inc(s["place_f_ready"], 1)
                    then(nc.vector.tensor_tensor(sums[:], top[:, 0:PH, :].unsqueeze(3).broadcast_to([P, PH, K8, K8]),
                                                 top[:, PH:, :].unsqueeze(2).broadcast_to([P, PH, K8, K8]), ALU.add),
                         "sums_ready")
                    for h in range(PH):
                        last = nc.vector.max(best[:, h, :], sums[:, h].rearrange("p a b -> p (a b)"))
                    then(last, "best_ready")
                if k == 4:
                    for h in range(PH):
                        last = nc.vector.max_index(rank[:, h, :], best[:, h, :],
                                                   sums[:, h].rearrange("p a b -> p (a b)"))
                    then(last, "rank_ready")
                    nc.vector.tensor_tensor(gap[:], best[:], best[:, :, 0:1].broadcast_to([P, PH, K8]),
                                            ALU.subtract).then_inc(s["gap_ready"], 1)
                    nc.vector.tensor_scalar(digit[:, 0], rank[:], 3, None, ALU.logical_shift_right)
                    then(nc.vector.tensor_scalar(digit[:, 1], rank[:], 7, None, ALU.bitwise_and), "rows_ready")
                    then(nc.vector.tensor_copy(digit_f[:], digit[:]), "digits_ready")
                if k == 5:
                    for p in range(2):
                        last = nc.vector.tensor_tensor(
                            hot[:, p], digit_f[:, p].unsqueeze(3).broadcast_to([P, PH, K8, K8]),
                            iota8.unsqueeze(1).unsqueeze(1).broadcast_to([P, PH, K8, K8]), ALU.is_equal)
                    then(last, "hot_ready")
                    dve.wait_ge(s["place_f_ready"], n)
                    for p in range(2):
                        last = nc.vector.tensor_tensor(
                            hot[:, p], hot[:, p], place_f[:, PH * p:PH * p + PH, :].unsqueeze(2).broadcast_to(
                                [P, PH, K8, K8]), ALU.mult)
                    then(last, "weighed_ready")
                if k == 6:
                    for p in range(2):
                        last = nc.vector.tensor_reduce(trio[:, p].rearrange("p (h k) -> p h k", h=PH), hot[:, p], X,
                                                       ALU.add)
                    last.then_inc(s["picked_ready"], 1)
                    dve.wait_ge(s["exp_ready"], n)
                    then(nc.vector.tensor_reduce(total[:], gap[:], X, ALU.add), "total_ready")
                    then(nc.vector.reciprocal(inv[:], total[:]), "inv_ready")
                    then(nc.vector.tensor_tensor(trio[:, 2].rearrange("p (h k) -> p h k", h=PH), gap[:],
                                                 inv[:].unsqueeze(2).broadcast_to([P, PH, K8]), ALU.mult),
                         "weight_ready")
                    dve.wait_ge(s["picked_ready"], n)
                    then(nc.vector.tensor_scalar(upper[:], trio[:, 1], float(J), float(J), ALU.is_ge, ALU.mult),
                         "upper_ready")
                    nc.vector.scalar_tensor_tensor(trio[:, 0], upper[:], NK / J, trio[:, 0], ALU.mult, ALU.add)
                    then(nc.vector.tensor_tensor(trio[:, 1], trio[:, 1], upper[:], ALU.subtract), "split_ready")
                    after(dve, s["turned"], tile, alone=True)
                    nc.vector.tensor_copy(doubled[:], trio[:].unsqueeze(2).broadcast_to([P, 3, 2, EN])).then_inc(
                        s["doubled"], 1)

            def one_hot_rows(tile, par, k):
                if k == 0:
                    dve.wait_ge(s["entries_kept"], tile + 1)
                    left = entries[:, par, 2]
                    for part in range(W3):
                        nc.vector.tensor_copy(parts[:, par, part], left).then_inc(s["part_ready"], 1)
                        dve.wait_ge(s["part_ready"], tile * (2 * W3 - 1) + (2 * part + 1))
                        if part < W3 - 1:
                            nc.vector.tensor_tensor(rest[:, part], left, parts[:, par, part],
                                                    ALU.subtract).then_inc(s["part_ready"], 1)
                            dve.wait_ge(s["part_ready"], tile * (2 * W3 - 1) + (2 * part + 2))
                            left = rest[:, part]
                after(dve, s["plane_ready"], tile * K + (k - 1))
                nc.vector.tensor_tensor(first[:, k % 2], spread(par, 0, k, P), iota(P), ALU.is_equal).then_inc(
                    s["first_ready"], 1)
                after(dve, s["second_ready"], tile * K + (k - 1))
                nc.vector.tensor_tensor(second[:, k % 2], spread(par, 1, k, J), iota(J), ALU.is_equal).then_inc(
                    s["second_hot"], 1)

            def weigh(tile, par, k):
                if k == 0:
                    dve.wait_ge(s["plane_kept"], tile * K + K)
                dve.wait_ge(s["activated"], tile * K + (k + 3))
                dve.wait_ge(s["step_done"], tile * K + (k + 1))
                nc.vector.tensor_tensor(weighed[:, k % 2], act_out[:, k % 2],
                                        plane[:, par, :, JS * k:JS * k + JS].rearrange("p n j -> p j n"),
                                        ALU.mult).then_inc(s["weighed"], 1)

            def add_outputs(tile):
                wait(dve, s["step_done"], tile * K + (K + 2))
                nc.vector.tensor_tensor(core.x[:, tile, :], core.x[:, tile, :], ps_y, ALU.add).then_inc(s["x_done"], 1)

            def turn(t, par, choose, build, units):
                for k in range(K):
                    if units:
                        weigh(t, par, k)
                    if build and k + 1 < K:
                        one_hot_rows(t + 1, 1 - par, k + 1)
                    if choose:
                        choose_step(t + 2, k)
                if choose:
                    one_hot_rows(t + 2, par, 0)
                if units:
                    add_outputs(t)

            all_turns(dve, turn)


SUBLAYERS = range(12)

PACKED = {0: "l0x", 1: "l0a", 2: "l0f", 3: "l1x", 4: "l1a", 6: "l2x", 7: "l2a", 9: "l3x", 10: "l3a"}
GROUPS = (range(0, 5), range(5, 6), range(6, 12))


def cross_pack(w, names="q k v bq bk bv bo"):
    kinds = dict(q="matrix", k="matrix", v="matrix", bq="column", bk="column", bv="row", bo="row")
    ending = dict(q="Wq_T", k="Wk_T", v="Wv_T")
    return [(k, kinds[k], w + ending.get(k, k)) for k in names.split()] + [
        ("o", "rows", w + "o"), ("ctx_tail", "matrix", "ctx_tail")]


PACKS = {
    "l0x": [(k, "matrix", "L0_xattn_" + k) for k in ("Wq_c_T", "Wk_c_T", "Wv_c_T", "Wk_s", "Wv_s_T", "Wq_s_T")]
    + [("Wg", "matrix", "L0_xattn_Wg_T")]
    + [(k, "column", "L0_xattn_" + k) for k in ("bq_c", "bk_c", "bk_s", "bq_s")]
    + [(k, "row", "L0_xattn_" + k) for k in ("bv_c", "bv_s", "bg")],
    "l0a": [(k, "matrix", f"L0_attn_w_{k}_T") for k in "qkvo"] + [("bo", "row", "L0_attn_b_o")],
    "l0f": [(k, "matrix", f"L0_ffn_{k}_T") for k in ("attn_w", "next_w")]
    + [(k, "column", "L0_ffn_" + k) for k in ("ln_scale", "ln_bias", "attn_b")] + [("next_b", "row", "L0_ffn_next_b")],
    "l1x": cross_pack("L1_xattn_"),
    "l1a": [(k, "matrix", f"L1_attn_W{k}_T") for k in "qkvo"]
    + [("b" + k, "column", "L1_attn_b" + k) for k in "qkv"] + [("bo", "row", "L1_attn_bo")],
    "l2x": cross_pack("L2_xattn_"),
    "l2a": [(k, "matrix", f"L2_attn_{k}_w_T") for k in "qkvo"]
    + [(k + "r", "matrix", f"L2_attn_{k}_w_rot") for k in "qk"]
    + [("b" + k, "column", f"L2_attn_{k}_b") for k in "qkv"]
    + [("b" + k + "r", "column", f"L2_attn_{k}_b_rot") for k in "qk"] + [("bo", "row", "L2_attn_o_b")],
    "l3x": cross_pack("L3_xattn_", "q k v") + [("bias", "tiles", "fside")],
    "l3a": [(k, "matrix", "L3_attn_W_" + k) for k in "qkv"] + [("o", "matrix", "L3_attn_W_proj")]
    + [("b" + k, "column", "L3_attn_b_" + k) for k in "qkv"] + [("bo", "row", "L3_attn_b_proj"),
                                                               ("slope", "tiles", "L3_attn_slopes")],
}


def packed(d):
    where, used = {}, set()
    for tag, items in PACKS.items():
        at, arrays, where[tag] = 0, [], {}
        for key, kind, name in items:
            a = d[name]
            used.add(name)
            if kind == "matrix":
                a = a.reshape(-1, P, a.shape[1]).transpose(1, 0, 2)
            elif kind == "column":
                a = a.reshape(-1, P).T
            elif kind == "row":
                a = np.broadcast_to(a, (P, a.shape[0]))
            elif kind == "rows":
                a = np.concatenate([a, np.zeros((P - a.shape[0], *a.shape[1:]), a.dtype)])
            else:
                a = np.tile(a, (P // a.shape[0], 1))
            n = int(np.prod(a.shape[1:]))
            rows = d[name].shape[0] if kind == "rows" else P
            if a.ndim == 3:
                def view(ap, c=a.shape[1], rows=rows):
                    return ap[0:rows].rearrange("p (c n) -> p c n", c=c)
            else:
                def view(ap):
                    return ap
            where[tag][key] = (at, n, view)
            arrays.append(a.reshape(P, n))
            at += n
        d[tag + "_pack"] = np.concatenate(arrays, axis=1)
    for name in used:
        del d[name]
    return where


def perceiver(nc, inputs, where, packs, out):
    with ExitStack() as ctx:
        x_sb = ctx.enter_context(nc.sbuf_tensor("x_sb", [P, NT, D], F32))
        const = ctx.enter_context(nc.sbuf_tensor("const", [P, inputs["const"].shape[1]], F32))
        core = Core(nc, inputs, x_sb, const, where, packs)
        with nc.semaphore("x_loaded") as x_loaded, nc.Block() as block:
            @block.sync
            def _(sp):
                sp.dma_start(const[:], inputs["const"]).then_inc(x_loaded, 16)
                sp.dma_start(x_sb[:], inputs["x"].rearrange("(t p) d -> p t d", p=P)).then_inc(x_loaded, 16)
                sp.wait_ge(x_loaded, 32)
        for group in GROUPS:
            numbers = [n for n in SUBLAYERS if n in group]
            with ExitStack() as arenas:
                width = max([inputs[PACKED[n] + "_pack"].shape[1] for n in numbers if n in PACKED], default=0)
                if width:
                    core.arenas = [arenas.enter_context(nc.sbuf_tensor(f"weights{numbers[0]}_{k}", [P, width], F32))
                                   for k in range(2)]
                core.group = numbers
                for n in numbers:
                    core.number = n
                    with nc.cleanup_on_exit():
                        sublayer(core, n)
        with nc.semaphore("x_stored") as x_stored, nc.Block() as block:
            @block.sync
            def _(sp):
                sp.dma_start(out.rearrange("(t p) d -> p t d", p=P), x_sb[:]).then_inc(x_stored, 16)
                sp.wait_ge(x_stored, 16)


def sublayer(core, n):
    if n == 0:
        gated_cross_attention(core, "l0x")
    if n == 1:
        self_attention(core, "l0a")
    if n == 2:
        fixed_experts_ffn(core, "l0f")
    if n == 3:
        cross_attention(core, "l1x", mask="mask_int", mask_type=I32)
    if n == 4:
        complex_attention(core, "l1a")
    if n == 5:
        product_key_ffn(core, "l1f")
    if n == 6:
        cross_attention(core, "l2x", mask="mask_bool", mask_type=U8)
    if n == 7:
        self_attention(core, "l2a", rope=True)
    if n == 8:
        routed_ffn(core, "l2f", ("L2_ffn_router", "L2_ffn_experts_bias", "softmax"), [
            (0, 9, 512, ("L2_ffn_w1_all", "L2_ffn_w3_all", "L2_ffn_w2_all"), True)])
    if n == 9:
        cross_attention(core, "l3x")
    if n == 10:
        self_attention(core, "l3a", alibi=True)
    if n == 11:
        routed_ffn(core, "l3f", ("L3_ffn_router", "L3_ffn_router_bias", "sigmoid"), [
            (0, 8, 256, ("L3_ffn_ew1", "L3_ffn_ew2"), False),
            (8, 1, 512, ("L3_ffn_sw1", "L3_ffn_sw3", "L3_ffn_sw2"), True)])


def laid_out(inputs):
    a = {k: np.asarray(v) for k, v in inputs.items()}
    table, where, rows = constant_tables()
    d = dict(const=table)
    d["x"] = a["x"].reshape(T, D)
    for n in ("L0_attn_w_q", "L0_attn_w_k", "L0_attn_w_v", "L0_attn_w_o",
              "L2_attn_q_w", "L2_attn_k_w", "L2_attn_v_w", "L2_attn_o_w"):
        d[n + "_T"] = a[n].T
    other = np.arange(D).reshape(H, 2, HD // 2)[:, ::-1].reshape(-1)
    for n in ("L2_attn_q", "L2_attn_k"):
        d[n + "_w_rot"] = a[n + "_w"][other].T
        d[n + "_b_rot"] = a[n + "_b"][other]
    for j, n in enumerate("kqv"):
        d["L3_attn_W_" + n] = a["L3_attn_W_kqv"][:, j * D:j * D + D]
        d["L3_attn_b_" + n] = a["L3_attn_b_kqv"][j * D:j * D + D]
    for n in ("L0_attn_b_o", "L2_attn_o_b", "L3_attn_W_proj", "L3_attn_b_proj"):
        d[n] = a[n]
    context = a["ctx_1024"].transpose(2, 0, 1)
    d["ctx_T"] = context.reshape(D, -1)
    d["ctx"] = a["ctx_1024"]
    d["ctx_sel_T"] = context[:, :, rows].reshape(D, -1)
    for n in ("Wq_c", "Wk_c", "Wv_c", "Wv_s", "Wq_s", "Wg"):
        d[f"L0_xattn_{n}_T"] = a["L0_xattn_" + n].T
    for n in ("Wk_s", "bv_c", "bv_s", "bg"):
        d["L0_xattn_" + n] = a["L0_xattn_" + n]
    for n in ("Wq", "Wk", "Wv", "Wo"):
        d[f"L1_attn_{n}_T"] = a["L1_attn_" + n].T
    d["L1_attn_bo"] = a["L1_attn_bo"]
    d["ctx_tail"] = context[:, :, KEYS - 1]
    d["mask_int"] = a["mask_BxS2_ik0"].reshape(-1)
    d["mask_bool"] = a["mask_Bx1x1xS2_bf1"].view(np.uint8).reshape(-1)
    d["fside"] = a["fside_1x1xSxS2_0"].reshape(S, KEYS)
    for n in ("L1_xattn_", "L2_xattn_"):
        for k in "qkv":
            d[n + "W" + k + "_T"] = a[n + "W" + k].T
        d[n + "o"] = a[n + "Wo"].T.reshape(G, HG, HD, D).transpose(0, 2, 1, 3).reshape(GD, HG, D)
        d[n + "bv"], d[n + "bo"] = a[n + "bv"], a[n + "bo"]
    for k in "qkv":
        d[f"L3_xattn_W{k}_T"] = a["L3_xattn_W" + k].reshape(D, D)
    d["L3_xattn_o"] = a["L3_xattn_Wo"].reshape(G, HG, HD, D).transpose(0, 2, 1, 3).reshape(GD, HG, D)
    for n in ("attn_w", "next_w"):
        d[f"L0_ffn_{n}_T"] = a["L0_ffn_" + n].T
    for n in ("next_b", "w1", "w2"):
        d["L0_ffn_" + n] = a["L0_ffn_" + n]
    for n in ("b1", "b2"):
        d[f"L0_ffn_{n}_col"] = a["L0_ffn_" + n].reshape(8, -1, P).transpose(0, 2, 1)
    for n in ("L2_ffn_router", "L3_ffn_router"):
        d[n] = a[n + "_w"].T.reshape(C, P, 8).transpose(1, 0, 2)
    for n in ("L2_ffn_experts_bias", "L3_ffn_router_bias", "L3_ffn_ew1", "L3_ffn_ew2"):
        d[n] = a[n]
    for n in ("w1", "w3", "w2"):
        d[f"L2_ffn_{n}_all"] = np.concatenate([a["L2_ffn_" + n], a["L2_ffn_s" + n]])
        d["L3_ffn_s" + n] = a["L3_ffn_s" + n][None]
    d["L1_ffn_w_q"] = a["L1_ffn_w_q"]
    d["L1_ffn_keys_by_dim"] = a["L1_ffn_keys"].transpose(3, 2, 0, 1).reshape(P, 2 * PH, NK)
    experts = a["L1_ffn_key_in"].reshape(NK, 2, NK // 2, D)
    d["L1_ffn_key_in_by_expert"] = experts.transpose(3, 2, 1, 0).reshape(D, NK // 2, P)
    experts = a["L1_ffn_key_out"].reshape(NK, 2, NK // 2, D)
    d["L1_ffn_key_out_by_expert"] = experts.transpose(1, 0, 2, 3).reshape(P, NK // 2, D)
    for n in ("L1_ffn_gamma", "L1_ffn_beta"):
        d[n + "_col"] = a[n].reshape(-1, P).T
    d["L3_attn_slopes"] = np.repeat(a["L3_attn_slopes"].reshape(G, HG).T, S, axis=0)
    for items in PACKS.values():
        for key, kind, name in items:
            if name not in d:
                d[name] = a[name]
    packs = packed(d)
    return {k: np.ascontiguousarray(v) for k, v in d.items()}, where, packs


def kernel(**inputs):
    import concourse.bacc as bacc
    from concourse.bass_utils import run_bass_kernel_spmd

    nc = bacc.Bacc("TRN2", target_bir_lowering=False, num_devices=1)
    arrays, where, packs = laid_out(inputs)
    aps, fed = {}, {}
    for name, a in arrays.items():
        fed[f"in_{name}_dram"] = a
        aps[name] = nc.dram_tensor(f"in_{name}_dram", a.shape, mybir.dt.from_np(a.dtype), kind="ExternalInput").ap()
    out = nc.dram_tensor("out_0_dram", (T, D), F32, kind="ExternalOutput").ap()
    perceiver(nc, aps, where, packs, out)
    r = run_bass_kernel_spmd(nc, [fed], core_ids=[0])
    return r.results[0]["out_0_dram"].reshape(B, S, D)
```
